# Optimizing a Trainium2 kernel written in Bass

```python
import numpy as np
import jax
import jax.numpy as jnp

def _softmax(x, axis=-1):
    return jax.nn.softmax(x, axis=axis)

def _gelu(x):
    return jax.nn.gelu(x, approximate=True)

def _silu(x):
    return jax.nn.silu(x)

def _sigmoid(x):
    return jax.nn.sigmoid(x)

def _layernorm(x, axis=-1, eps=1e-05):
    m = jnp.mean(x, axis=axis, keepdims=True)
    v = jnp.var(x, axis=axis, keepdims=True)
    return (x - m) / jnp.sqrt(v + eps)

def _scatter_add(tgt, idx, src, axis=0):
    return tgt.at[idx].add(src)

def _segment_sum(src, seg, n):
    return jax.ops.segment_sum(src, seg, n)
kernel_name = 'mk_decoder_postln_d4_seqx_r4_d59472'

def setup_inputs(seed: int=0):
    np.random.seed(seed)
    _w = jnp.asarray

    def _rec_inputs():
        import jax
        import jax.numpy as jnp
        _rk = jax.random.key(seed)
        x = -0.0002928 + 1 * jax.random.normal(jax.random.fold_in(_rk, 1), (4, 512, 256), jnp.float32)
        _lenS = 512 - jax.random.randint(jax.random.fold_in(_rk, 7), (4,), 0, max(1, 512 // 4) + 1, jnp.int32)
        _lenS2 = 512 - jax.random.randint(jax.random.fold_in(_rk, 8), (4,), 0, max(1, 512 // 4) + 1, jnp.int32)
        _ctx_1024P = jax.random.normal(jax.random.fold_in(_rk, 11), (4, 16, 256), jnp.float32)
        _ctx_1024c = jax.random.dirichlet(jax.random.fold_in(_rk, 511), 0.3 * jnp.ones((16,), jnp.float32), (4, 512))
        _ctx_1024t = jnp.einsum('bsk,bkd->bsd', _ctx_1024c, _ctx_1024P)
        _ctx_1024t = _ctx_1024t * jax.lax.rsqrt(jnp.mean(jnp.square(_ctx_1024t)) + 1e-12) * 0.953939
        ctx_1024 = -1.39393e-06 + 0.999914 * (_ctx_1024t + 0.3 * jax.random.normal(jax.random.fold_in(_rk, 611), (4, 512, 256), jnp.float32))
        _validS = jnp.arange(512)[None, :] < _lenS[:, None]
        _validS2 = jnp.arange(512)[None, :] < _lenS2[:, None]
        _causal = jnp.tril(jnp.ones((512, 512), dtype=bool))
        mask_BxS2_bf1 = jnp.ones((4, 512), dtype=bool)
        return (x, ctx_1024, mask_BxS2_bf1)
    x, ctx_1024, mask_BxS2_bf1 = _rec_inputs()

    def _L0_attn_setup():
        import jax, jax.numpy as jnp
        import numpy as np
        DIM = 256
        HEADS = 16
        HEAD_DIM = DIM // HEADS

        def _feature_map(z, W, b):
            p = jnp.einsum('bhtd,ed->bhte', z, W) + b
            return jnp.concatenate([jax.nn.softmax(p, axis=-1), jax.nn.softmax(-p, axis=-1)], axis=-1)
        key = jax.random.key(seed)
        ks = jax.random.split(key, 7)
        s = 0.02
        x = jax.random.normal(ks[0], (1, 256, DIM), dtype=jnp.float32)
        w_qkv = jax.random.normal(ks[1], (3 * DIM, DIM), dtype=jnp.float32) * s
        wq_map = jnp.eye(HEAD_DIM, dtype=jnp.float32) + jax.random.normal(ks[2], (HEAD_DIM, HEAD_DIM), dtype=jnp.float32) * s
        bq_map = jax.random.normal(ks[3], (HEAD_DIM,), dtype=jnp.float32) * s
        wk_map = jnp.eye(HEAD_DIM, dtype=jnp.float32) + jax.random.normal(ks[4], (HEAD_DIM, HEAD_DIM), dtype=jnp.float32) * s
        bk_map = jax.random.normal(ks[5], (HEAD_DIM,), dtype=jnp.float32) * s
        w_out = jax.random.normal(ks[6], (DIM, DIM), dtype=jnp.float32) * s
        return {'x': x, 'w_qkv': w_qkv, 'wq_map': wq_map, 'bq_map': bq_map, 'wk_map': wk_map, 'bk_map': bk_map, 'w_out': w_out}
    _L0_attn_all = _L0_attn_setup()
    _L0_attn_in = {k: v for k, v in _L0_attn_all.items() if k in ('w_qkv', 'wq_map', 'bq_map', 'wk_map', 'bk_map', 'w_out')}
    del _L0_attn_all

    def _L0_xattn_setup():
        import jax, jax.numpy as jnp
        import numpy as np
        D_MODEL = 256
        NUM_HEADS = 16
        HEAD_DIM = D_MODEL // NUM_HEADS
        key = jax.random.key(seed)
        ks = jax.random.split(key, 11)
        B, S = (2, 512)
        inp = {'query': jax.random.normal(ks[0], (B, S, D_MODEL), jnp.float32), 'key': jax.random.normal(ks[1], (B, S, D_MODEL), jnp.float32), 'value': jax.random.normal(ks[2], (B, S, D_MODEL), jnp.float32), 'mask': 1, 'w_q': jax.random.normal(ks[3], (D_MODEL, D_MODEL), jnp.float32) / np.sqrt(D_MODEL), 'b_q': jax.random.normal(ks[4], (D_MODEL,), jnp.float32) * 0.02, 'w_k': jax.random.normal(ks[5], (D_MODEL, D_MODEL), jnp.float32) / np.sqrt(D_MODEL), 'b_k': jax.random.normal(ks[6], (D_MODEL,), jnp.float32) * 0.02, 'w_v': jax.random.normal(ks[7], (D_MODEL, D_MODEL), jnp.float32) / np.sqrt(D_MODEL), 'b_v': jax.random.normal(ks[8], (D_MODEL,), jnp.float32) * 0.02, 'w_o': jax.random.normal(ks[9], (D_MODEL, D_MODEL), jnp.float32) / np.sqrt(D_MODEL), 'b_o': jax.random.normal(ks[10], (D_MODEL,), jnp.float32) * 0.02}
        return inp
    _L0_xattn_all = _L0_xattn_setup()
    _L0_xattn_in = {k: v for k, v in _L0_xattn_all.items() if k in ('w_q', 'b_q', 'w_k', 'b_k', 'w_v', 'b_v', 'w_o', 'b_o')}
    del _L0_xattn_all

    def _L0_ffn_setup():
        import jax, jax.numpy as jnp
        import numpy as np
        B, S, D, H, E, K = (4, 512, 256, 512, 8, 2)
        TEMP = 5.0
        EPS = 1e-09
        key = jax.random.key(seed)
        k_x, k_wg, k_w1, k_w2 = jax.random.split(key, 4)
        scale = 0.02
        return {'x': jax.random.normal(k_x, (B, S, D), dtype=jnp.float32), 'Wg': jax.random.normal(k_wg, (D, E), dtype=jnp.float32) * scale, 'bg': jnp.zeros((E,), dtype=jnp.float32), 'W1': jax.random.normal(k_w1, (E, D, H), dtype=jnp.float32) * scale, 'b1': jnp.zeros((E, H), dtype=jnp.float32), 'W2': jax.random.normal(k_w2, (E, H, D), dtype=jnp.float32) * scale, 'b2': jnp.zeros((E, D), dtype=jnp.float32)}
    _L0_ffn_all = _L0_ffn_setup()
    _L0_ffn_in = {k: v for k, v in _L0_ffn_all.items() if k in ('Wg', 'bg', 'W1', 'b1', 'W2', 'b2')}
    del _L0_ffn_all

    def _L1_attn_setup():
        import jax, jax.numpy as jnp
        import numpy as np
        OUT_DIM = 256
        key = jax.random.key(seed)
        k1, k2, k3, k4 = jax.random.split(key, 4)
        B, N, D = (4, 512, 256)
        s = 1.0 / np.sqrt(D)
        return {'x': jax.random.normal(k1, (B, N, D), dtype=jnp.float32), 'W_query': jax.random.normal(k2, (D, OUT_DIM), dtype=jnp.float32) * s, 'W_key': jax.random.normal(k3, (D, OUT_DIM), dtype=jnp.float32) * s, 'W_value': jax.random.normal(k4, (D, OUT_DIM), dtype=jnp.float32) * s}
    _L1_attn_all = _L1_attn_setup()
    _L1_attn_in = {k: v for k, v in _L1_attn_all.items() if k in ('W_query', 'W_key', 'W_value')}
    del _L1_attn_all

    def _L1_xattn_setup():
        import jax, jax.numpy as jnp
        import numpy as np
        E, TPE, H, F = (64, 64, 256, 256)
        key = jax.random.key(seed)
        k1, k2, k3, k4 = jax.random.split(key, 4)
        scale = 1.0 / np.sqrt(H)
        return {'x': jax.random.normal(k1, (E, TPE, H), dtype=jnp.float32), 'w1': jax.random.normal(k2, (E, F, H), dtype=jnp.float32) * scale, 'v1': jax.random.normal(k3, (E, F, H), dtype=jnp.float32) * scale, 'w2': jax.random.normal(k4, (E, F, H), dtype=jnp.float32) * scale}
    _L1_xattn_all = _L1_xattn_setup()
    _L1_xattn_in = {k: v for k, v in _L1_xattn_all.items() if k in ()}
    del _L1_xattn_all

    def _L1_ffn_setup():
        import jax, jax.numpy as jnp
        import numpy as np
        LORA_DIM = 16
        LORA_TOKEN_INDEX = 1
        B, S, D, H = (4, 512, 256, 1024)
        key = jax.random.key(seed)
        ks = jax.random.split(key, 6)
        x = jax.random.normal(ks[0], (B, S, D), dtype=jnp.float32)
        W1 = jax.random.normal(ks[1], (H, D), dtype=jnp.float32) * 0.02
        b1 = jnp.zeros((H,), dtype=jnp.float32)
        W2 = jax.random.normal(ks[2], (D, H), dtype=jnp.float32) * 0.02
        b2 = jnp.zeros((D,), dtype=jnp.float32)
        scale = jnp.asarray(0.001, dtype=jnp.float32)
        return {'x': x, 'W1': W1, 'b1': b1, 'W2': W2, 'b2': b2, 'scale': scale}
    _L1_ffn_all = _L1_ffn_setup()
    _L1_ffn_in = {k: v for k, v in _L1_ffn_all.items() if k in ('W1', 'b1', 'W2', 'b2', 'scale')}
    del _L1_ffn_all

    def _L2_attn_setup():
        import jax, jax.numpy as jnp
        import numpy as np
        D_MODEL = 256
        D_QK = 256
        NUM_HEADS = 16
        HEAD_DIM = D_QK // NUM_HEADS
        V_DIM = D_MODEL // NUM_HEADS
        B, S = (2, 512)
        key = jax.random.key(seed)
        ks = jax.random.split(key, 9)
        sc = 0.02
        return {'x': jax.random.normal(ks[0], (B, S, D_MODEL), dtype=jnp.float32), 'Wqk': jax.random.normal(ks[1], (D_MODEL, 2 * D_QK), dtype=jnp.float32) * sc, 'bqk': jax.random.normal(ks[2], (2 * D_QK,), dtype=jnp.float32) * sc, 'Wv': jax.random.normal(ks[3], (D_MODEL, D_MODEL), dtype=jnp.float32) * sc, 'bv': jax.random.normal(ks[4], (D_MODEL,), dtype=jnp.float32) * sc, 'Wn': jax.random.normal(ks[5], (D_MODEL, NUM_HEADS), dtype=jnp.float32) * sc, 'bn': jax.random.normal(ks[6], (NUM_HEADS,), dtype=jnp.float32) * sc, 'Wo': jax.random.normal(ks[7], (D_MODEL, D_MODEL), dtype=jnp.float32) * sc, 'bo': jax.random.normal(ks[8], (D_MODEL,), dtype=jnp.float32) * sc}
    _L2_attn_all = _L2_attn_setup()
    _L2_attn_in = {k: v for k, v in _L2_attn_all.items() if k in ('Wqk', 'bqk', 'Wv', 'bv', 'Wn', 'bn', 'Wo', 'bo')}
    del _L2_attn_all

    def _L2_xattn_setup():
        import jax, jax.numpy as jnp
        import numpy as np
        DIM = 256
        HEADS = 16
        DIM_HEAD = 64
        INNER = HEADS * DIM_HEAD
        B, F, Q = (16, 1024, 64)
        EPS = 1e-05
        SCALE = DIM_HEAD ** (-0.5)

        def _layernorm(x, gamma, beta):
            mu = jnp.mean(x, axis=-1, keepdims=True)
            var = jnp.var(x, axis=-1, keepdims=True)
            return (x - mu) * jax.lax.rsqrt(var + EPS) * gamma + beta
        key = jax.random.key(seed)
        ks = jax.random.split(key, 8)
        features = jax.random.normal(ks[0], (B, F, DIM), dtype=jnp.float32)
        masks = jnp.ones((B, F), dtype=bool)
        latents = jax.random.normal(ks[1], (B, Q, DIM), dtype=jnp.float32)
        Wq = jax.random.normal(ks[2], (DIM, INNER), dtype=jnp.float32) / np.sqrt(DIM)
        Wk = jax.random.normal(ks[3], (DIM, INNER), dtype=jnp.float32) / np.sqrt(DIM)
        Wv = jax.random.normal(ks[4], (DIM, INNER), dtype=jnp.float32) / np.sqrt(DIM)
        Wo = jax.random.normal(ks[5], (INNER, DIM), dtype=jnp.float32) / np.sqrt(INNER)
        gm = jnp.ones((DIM,), jnp.float32)
        bm = jnp.zeros((DIM,), jnp.float32)
        gl = jnp.ones((DIM,), jnp.float32)
        bl = jnp.zeros((DIM,), jnp.float32)
        return {'features': features, 'masks': masks, 'latents': latents, 'gm': gm, 'bm': bm, 'gl': gl, 'bl': bl, 'Wq': Wq, 'Wk': Wk, 'Wv': Wv, 'Wo': Wo}
    _L2_xattn_all = _L2_xattn_setup()
    _L2_xattn_in = {k: v for k, v in _L2_xattn_all.items() if k in ('gm', 'bm', 'gl', 'bl', 'Wq', 'Wk', 'Wv', 'Wo')}
    del _L2_xattn_all

    def _L2_ffn_setup():
        import jax, jax.numpy as jnp
        import numpy as np
        QP = 127.0
        MIN_RANGE = 1e-06

        def _ste_round(x):
            return x + jax.lax.stop_gradient(jnp.round(x) - x)

        def _quant_per_tensor(x):
            scale = jnp.maximum(jnp.max(jnp.abs(x)), MIN_RANGE) / QP
            return (_ste_round(x / scale), scale)

        def _qlinear(x2d, w, b):
            xq, sx = _quant_per_tensor(x2d)
            wq, sw = _quant_per_tensor(w)
            out = jnp.matmul(xq, wq.T) + b[None, :]
            return out * (sw * sx)
        key = jax.random.key(seed)
        k = jax.random.split(key, 5)
        B, N, D, H = (8, 256, 256, 1024)
        return {'x': jax.random.normal(k[0], (B, N, D), dtype=jnp.float32), 'w1': jax.random.normal(k[1], (H, D), dtype=jnp.float32) * 0.02, 'b1': jax.random.normal(k[2], (H,), dtype=jnp.float32) * 0.02, 'w2': jax.random.normal(k[3], (D, H), dtype=jnp.float32) * 0.02, 'b2': jax.random.normal(k[4], (D,), dtype=jnp.float32) * 0.02}
    _L2_ffn_all = _L2_ffn_setup()
    _L2_ffn_in = {k: v for k, v in _L2_ffn_all.items() if k in ('w1', 'b1', 'w2', 'b2')}
    del _L2_ffn_all

    def _L3_attn_setup():
        import jax, jax.numpy as jnp
        import numpy as np
        import math
        N_HEADS = 16

        def _rope_tables(seq_len, head_dim):
            pos = jnp.arange(seq_len, dtype=jnp.float32)
            freqs = jnp.exp(jnp.arange(0, head_dim, 2, dtype=jnp.float32) * (-math.log(10000.0) / head_dim))
            angles = pos[:, None] * freqs[None, :]
            cos_emb = jnp.zeros((seq_len, head_dim), jnp.float32).at[:, 0::2].set(jnp.cos(angles))
            sin_emb = jnp.zeros((seq_len, head_dim), jnp.float32).at[:, 1::2].set(jnp.sin(angles))
            return (cos_emb, sin_emb)
        key = jax.random.key(seed)
        ks = jax.random.split(key, 5)
        B, S, D = (2, 512, 256)
        scale = 1.0 / math.sqrt(D)
        return {'x': jax.random.normal(ks[0], (B, S, D), jnp.float32), 'Wq': jax.random.normal(ks[1], (D, D), jnp.float32) * scale, 'Wk': jax.random.normal(ks[2], (D, D), jnp.float32) * scale, 'Wv': jax.random.normal(ks[3], (D, D), jnp.float32) * scale, 'Wo': jax.random.normal(ks[4], (D, D), jnp.float32) * scale}
    _L3_attn_all = _L3_attn_setup()
    _L3_attn_in = {k: v for k, v in _L3_attn_all.items() if k in ('Wq', 'Wk', 'Wv', 'Wo')}
    del _L3_attn_all

    def _L3_xattn_setup():
        import jax, jax.numpy as jnp
        import numpy as np
        DIM = 256
        H = 16
        D = 64
        INNER = H * D
        EPS = 1e-05

        def layernorm(x, w, b):
            mu = jnp.mean(x, axis=-1, keepdims=True)
            var = jnp.var(x, axis=-1, keepdims=True)
            return (x - mu) * jax.lax.rsqrt(var + EPS) * w + b
        key = jax.random.key(seed)
        ks = jax.random.split(key, 8)
        B, N, S = (4, 64, 2048)
        s = 1.0 / np.sqrt(DIM)
        return {'latents': jax.random.normal(ks[0], (B, N, DIM), jnp.float32), 'context': jax.random.normal(ks[1], (B, S, DIM), jnp.float32), 'ln_l_w': jnp.ones((DIM,), jnp.float32), 'ln_l_b': jnp.zeros((DIM,), jnp.float32), 'ln_c_w': jnp.ones((DIM,), jnp.float32), 'ln_c_b': jnp.zeros((DIM,), jnp.float32), 'Wq': jax.random.normal(ks[2], (DIM, INNER), jnp.float32) * s, 'Wkv': jax.random.normal(ks[3], (DIM, 2 * INNER), jnp.float32) * s, 'Wo': jax.random.normal(ks[4], (INNER, DIM), jnp.float32) * (1.0 / np.sqrt(INNER)), 'bo': jnp.zeros((DIM,), jnp.float32)}
    _L3_xattn_all = _L3_xattn_setup()
    _L3_xattn_in = {k: v for k, v in _L3_xattn_all.items() if k in ('ln_l_w', 'ln_l_b', 'ln_c_w', 'ln_c_b', 'Wq', 'Wkv', 'Wo', 'bo')}
    del _L3_xattn_all

    def _L3_ffn_setup():
        import jax, jax.numpy as jnp
        import numpy as np
        D_MODEL = 256
        EXPANSION = 4
        D_HIDDEN = D_MODEL * EXPANSION
        NUM_STAGES = int(np.log2(D_HIDDEN))

        def butterfly(y, weights, dim):
            lead = y.shape[:-1]
            for stage in range(weights.shape[0]):
                s = 2 ** stage
                nb = dim // (2 * s)
                yr = y.reshape(*lead, nb, 2, s)
                a = yr[..., 0, :]
                b = yr[..., 1, :]
                w = weights[stage].reshape(nb, s, 2, 2)
                na = w[..., 0, 0] * a + w[..., 0, 1] * b
                nb2 = w[..., 1, 0] * a + w[..., 1, 1] * b
                y = jnp.stack([na, nb2], axis=-2).reshape(*lead, dim)
            return y
        key = jax.random.key(seed)
        ks = jax.random.split(key, 6)
        B, S = (4, 512)
        x = jax.random.normal(ks[0], (B, S, D_MODEL), jnp.float32)
        W_exp = jax.random.normal(ks[1], (D_MODEL, D_HIDDEN), jnp.float32) * 0.02
        b_exp = jnp.zeros((D_HIDDEN,), jnp.float32)
        up_weights = jax.random.normal(ks[2], (NUM_STAGES, D_HIDDEN // 2, 2, 2), jnp.float32) * 0.02
        up_bias = jnp.zeros((D_HIDDEN,), jnp.float32)
        down_weights = jax.random.normal(ks[3], (NUM_STAGES, D_HIDDEN // 2, 2, 2), jnp.float32) * 0.02
        W_con = jax.random.normal(ks[4], (D_HIDDEN, D_MODEL), jnp.float32) * 0.02
        b_con = jnp.zeros((D_MODEL,), jnp.float32)
        down_bias = jnp.zeros((D_MODEL,), jnp.float32)
        return dict(x=x, W_exp=W_exp, b_exp=b_exp, up_weights=up_weights, up_bias=up_bias, down_weights=down_weights, W_con=W_con, b_con=b_con, down_bias=down_bias)
    _L3_ffn_all = _L3_ffn_setup()
    _L3_ffn_in = {k: v for k, v in _L3_ffn_all.items() if k in ('W_exp', 'b_exp', 'up_weights', 'up_bias', 'down_weights', 'W_con', 'b_con', 'down_bias')}
    del _L3_ffn_all
    return {'x': x, 'ctx_1024': ctx_1024, 'mask_BxS2_bf1': mask_BxS2_bf1, 'L0_attn_w_qkv': _L0_attn_in['w_qkv'], 'L0_attn_wq_map': _L0_attn_in['wq_map'], 'L0_attn_bq_map': _L0_attn_in['bq_map'], 'L0_attn_wk_map': _L0_attn_in['wk_map'], 'L0_attn_bk_map': _L0_attn_in['bk_map'], 'L0_attn_w_out': _L0_attn_in['w_out'], 'L0_xattn_w_q': _L0_xattn_in['w_q'], 'L0_xattn_b_q': _L0_xattn_in['b_q'], 'L0_xattn_w_k': _L0_xattn_in['w_k'], 'L0_xattn_b_k': _L0_xattn_in['b_k'], 'L0_xattn_w_v': _L0_xattn_in['w_v'], 'L0_xattn_b_v': _L0_xattn_in['b_v'], 'L0_xattn_w_o': _L0_xattn_in['w_o'], 'L0_xattn_b_o': _L0_xattn_in['b_o'], 'L0_ffn_Wg': _L0_ffn_in['Wg'], 'L0_ffn_bg': _L0_ffn_in['bg'], 'L0_ffn_W1': _L0_ffn_in['W1'], 'L0_ffn_b1': _L0_ffn_in['b1'], 'L0_ffn_W2': _L0_ffn_in['W2'], 'L0_ffn_b2': _L0_ffn_in['b2'], 'L1_attn_W_query': _L1_attn_in['W_query'], 'L1_attn_W_key': _L1_attn_in['W_key'], 'L1_attn_W_value': _L1_attn_in['W_value'], 'L1_ffn_W1': _L1_ffn_in['W1'], 'L1_ffn_b1': _L1_ffn_in['b1'], 'L1_ffn_W2': _L1_ffn_in['W2'], 'L1_ffn_b2': _L1_ffn_in['b2'], 'L1_ffn_scale': _L1_ffn_in['scale'], 'L2_attn_Wqk': _L2_attn_in['Wqk'], 'L2_attn_bqk': _L2_attn_in['bqk'], 'L2_attn_Wv': _L2_attn_in['Wv'], 'L2_attn_bv': _L2_attn_in['bv'], 'L2_attn_Wn': _L2_attn_in['Wn'], 'L2_attn_bn': _L2_attn_in['bn'], 'L2_attn_Wo': _L2_attn_in['Wo'], 'L2_attn_bo': _L2_attn_in['bo'], 'L2_xattn_gm': _L2_xattn_in['gm'], 'L2_xattn_bm': _L2_xattn_in['bm'], 'L2_xattn_gl': _L2_xattn_in['gl'], 'L2_xattn_bl': _L2_xattn_in['bl'], 'L2_xattn_Wq': _L2_xattn_in['Wq'], 'L2_xattn_Wk': _L2_xattn_in['Wk'], 'L2_xattn_Wv': _L2_xattn_in['Wv'], 'L2_xattn_Wo': _L2_xattn_in['Wo'], 'L2_ffn_w1': _L2_ffn_in['w1'], 'L2_ffn_b1': _L2_ffn_in['b1'], 'L2_ffn_w2': _L2_ffn_in['w2'], 'L2_ffn_b2': _L2_ffn_in['b2'], 'L3_attn_Wq': _L3_attn_in['Wq'], 'L3_attn_Wk': _L3_attn_in['Wk'], 'L3_attn_Wv': _L3_attn_in['Wv'], 'L3_attn_Wo': _L3_attn_in['Wo'], 'L3_xattn_ln_l_w': _L3_xattn_in['ln_l_w'], 'L3_xattn_ln_l_b': _L3_xattn_in['ln_l_b'], 'L3_xattn_ln_c_w': _L3_xattn_in['ln_c_w'], 'L3_xattn_ln_c_b': _L3_xattn_in['ln_c_b'], 'L3_xattn_Wq': _L3_xattn_in['Wq'], 'L3_xattn_Wkv': _L3_xattn_in['Wkv'], 'L3_xattn_Wo': _L3_xattn_in['Wo'], 'L3_xattn_bo': _L3_xattn_in['bo'], 'L3_ffn_W_exp': _L3_ffn_in['W_exp'], 'L3_ffn_b_exp': _L3_ffn_in['b_exp'], 'L3_ffn_up_weights': _L3_ffn_in['up_weights'], 'L3_ffn_up_bias': _L3_ffn_in['up_bias'], 'L3_ffn_down_weights': _L3_ffn_in['down_weights'], 'L3_ffn_W_con': _L3_ffn_in['W_con'], 'L3_ffn_b_con': _L3_ffn_in['b_con'], 'L3_ffn_down_bias': _L3_ffn_in['down_bias']}

def reference(x, ctx_1024, mask_BxS2_bf1, L0_attn_w_qkv, L0_attn_wq_map, L0_attn_bq_map, L0_attn_wk_map, L0_attn_bk_map, L0_attn_w_out, L0_xattn_w_q, L0_xattn_b_q, L0_xattn_w_k, L0_xattn_b_k, L0_xattn_w_v, L0_xattn_b_v, L0_xattn_w_o, L0_xattn_b_o, L0_ffn_Wg, L0_ffn_bg, L0_ffn_W1, L0_ffn_b1, L0_ffn_W2, L0_ffn_b2, L1_attn_W_query, L1_attn_W_key, L1_attn_W_value, L1_ffn_W1, L1_ffn_b1, L1_ffn_W2, L1_ffn_b2, L1_ffn_scale, L2_attn_Wqk, L2_attn_bqk, L2_attn_Wv, L2_attn_bv, L2_attn_Wn, L2_attn_bn, L2_attn_Wo, L2_attn_bo, L2_xattn_gm, L2_xattn_bm, L2_xattn_gl, L2_xattn_bl, L2_xattn_Wq, L2_xattn_Wk, L2_xattn_Wv, L2_xattn_Wo, L2_ffn_w1, L2_ffn_b1, L2_ffn_w2, L2_ffn_b2, L3_attn_Wq, L3_attn_Wk, L3_attn_Wv, L3_attn_Wo, L3_xattn_ln_l_w, L3_xattn_ln_l_b, L3_xattn_ln_c_w, L3_xattn_ln_c_b, L3_xattn_Wq, L3_xattn_Wkv, L3_xattn_Wo, L3_xattn_bo, L3_ffn_W_exp, L3_ffn_b_exp, L3_ffn_up_weights, L3_ffn_up_bias, L3_ffn_down_weights, L3_ffn_W_con, L3_ffn_b_con, L3_ffn_down_bias):
    import jax
    import jax.numpy as jnp

    def _L0_attn_ref(x, w_qkv, wq_map, bq_map, wk_map, bk_map, w_out):
        import jax, jax.numpy as jnp
        import numpy as np
        DIM = 256
        HEADS = 16
        HEAD_DIM = DIM // HEADS

        def _feature_map(z, W, b):
            p = jnp.einsum('bhtd,ed->bhte', z, W) + b
            return jnp.concatenate([jax.nn.softmax(p, axis=-1), jax.nn.softmax(-p, axis=-1)], axis=-1)
        b, t, dim = x.shape
        h, hd = (HEADS, HEAD_DIM)
        qkv = (x @ w_qkv.T).reshape(b, t, 3, h, hd)
        q, k, v = [jnp.transpose(qkv[:, :, i], (0, 2, 1, 3)) for i in range(3)]
        q = _feature_map(q, wq_map, bq_map)
        k = _feature_map(k, wk_map, bk_map)
        k_prefix = jnp.cumsum(k, axis=2)
        kv_prefix = jnp.cumsum(jnp.einsum('bhtf,bhtd->bhtfd', k, v), axis=2)
        numer = jnp.einsum('bhtf,bhtfd->bhtd', q, kv_prefix)
        denom = jnp.maximum(jnp.einsum('bhtf,bhtf->bht', q, k_prefix)[..., None], 1e-06)
        y = jnp.transpose(numer / denom, (0, 2, 1, 3)).reshape(b, t, dim)
        return y @ w_out.T

    def _L0_xattn_ref(query, key, value, mask, w_q, b_q, w_k, b_k, w_v, b_v, w_o, b_o):
        import jax, jax.numpy as jnp
        import numpy as np
        D_MODEL = 256
        NUM_HEADS = 16
        HEAD_DIM = D_MODEL // NUM_HEADS
        B, S, _ = query.shape
        H, Dh = (NUM_HEADS, HEAD_DIM)
        q = (query @ w_q + b_q).reshape(B, S, H, Dh).transpose(0, 2, 1, 3)
        k = (key @ w_k + b_k).reshape(B, S, H, Dh).transpose(0, 2, 1, 3)
        v = (value @ w_v + b_v).reshape(B, S, H, Dh).transpose(0, 2, 1, 3)
        scale = 1.0 / jnp.sqrt(jnp.asarray(Dh, q.dtype))
        scores = jnp.einsum('bhqd,bhkd->bhqk', q, k) * scale
        if mask:
            causal = jnp.tril(jnp.ones((S, S), dtype=bool))
            scores = jnp.where(causal, scores, jnp.asarray(-1000000000.0, scores.dtype))
        attn = jax.nn.softmax(scores, axis=-1)
        x = jnp.einsum('bhqk,bhkd->bhqd', attn, v)
        x = x.transpose(0, 2, 1, 3).reshape(B, S, H * Dh)
        return x @ w_o + b_o

    def _L0_ffn_ref(x, Wg, bg, W1, b1, W2, b2):
        import jax, jax.numpy as jnp
        import numpy as np
        B, S, D, H, E, K = (4, 512, 256, 512, 8, 2)
        TEMP = 5.0
        EPS = 1e-09
        logits = jnp.einsum('bsd,de->bse', x, Wg) + bg
        probs = jax.nn.softmax(logits / TEMP, axis=-1)
        vals, idx = jax.lax.top_k(probs, K)
        onehot = jax.nn.one_hot(idx, E, dtype=x.dtype)
        mask = jnp.einsum('bske,bsk->bse', onehot, vals)
        gates = mask / (jnp.sum(mask, axis=-1, keepdims=True) + EPS)
        h = jax.nn.gelu(jnp.einsum('bsd,edh->besh', x, W1) + b1[None, :, None, :], approximate=False)
        out = jnp.einsum('besh,ehd->besd', h, W2) + b2[None, :, None, :]
        y = jnp.einsum('bse,besd->bsd', gates, out)
        return y

    def _L1_attn_ref(x, W_query, W_key, W_value):
        import jax, jax.numpy as jnp
        import numpy as np
        OUT_DIM = 256
        q = jnp.einsum('bnd,de->bne', x, W_query)
        k = jnp.einsum('bnd,de->bne', x, W_key)
        v = jnp.einsum('bnd,de->bne', x, W_value)
        sqrt_d = jnp.sqrt(jnp.asarray(OUT_DIM, dtype=jnp.float32))
        scores = jnp.einsum('bie,bje->bij', q, k) / sqrt_d
        attn = jax.nn.softmax(scores, axis=1)
        return jnp.einsum('bij,bie->bje', attn, v)

    def _L1_xattn_ref(x, w1, v1, w2):
        import jax, jax.numpy as jnp
        import numpy as np
        E, TPE, H, F = (64, 64, 256, 256)
        h1 = jnp.einsum('eth,efh->etf', x, w1)
        h2 = jnp.einsum('eth,efh->etf', x, v1)
        g = jax.nn.gelu(h1, approximate=False) * h2
        return jnp.einsum('etf,efh->eth', g, w2)

    def _L1_ffn_ref(x, W1, b1, W2, b2, scale):
        import jax, jax.numpy as jnp
        import numpy as np
        LORA_DIM = 16
        LORA_TOKEN_INDEX = 1
        B, S, D, H = (4, 512, 256, 1024)
        Bx, Sx, Dx = x.shape
        Hx = W1.shape[0]
        lt = jax.lax.dynamic_slice_in_dim(x, LORA_TOKEN_INDEX, LORA_DIM, axis=1)
        even = lt[:, ::2, :]
        odd = lt[:, 1::2, :]
        m1 = (even[:, :4, :, None] * odd[:, :4, None, :]).reshape(Bx, Hx, Dx)
        m2 = (even[:, 4:, :, None] * odd[:, 4:, None, :]).reshape(Bx, Dx, Hx)
        h = jnp.einsum('bsd,hd->bsh', x, W1) + scale * jnp.einsum('bsd,bhd->bsh', x, m1) + b1
        h = jax.nn.gelu(h, approximate=False)
        out = jnp.einsum('bsh,oh->bso', h, W2) + scale * jnp.einsum('bsh,boh->bso', h, m2) + b2
        return out

    def _L2_attn_ref(x, Wqk, bqk, Wv, bv, Wn, bn, Wo, bo):
        import jax, jax.numpy as jnp
        import numpy as np
        D_MODEL = 256
        D_QK = 256
        NUM_HEADS = 16
        HEAD_DIM = D_QK // NUM_HEADS
        V_DIM = D_MODEL // NUM_HEADS
        B, S = (2, 512)
        b, s, _ = x.shape
        qk = x @ Wqk + bqk
        v = x @ Wv + bv
        n = x @ Wn + bn
        qk = qk.reshape(b, s, 2, NUM_HEADS, HEAD_DIM)
        q, k = (qk[:, :, 0], qk[:, :, 1])
        v = v.reshape(b, s, NUM_HEADS, V_DIM)
        scores = jnp.einsum('bthd,bshd->bhts', q, k)
        mask = jnp.tril(jnp.ones((s, s), dtype=scores.dtype))
        n_exp = jnp.exp(jnp.transpose(n, (0, 2, 1)))
        attn = scores * mask / n_exp[:, :, :, None]
        ctx = jnp.einsum('bhts,bshd->bthd', attn, v)
        ctx = ctx.reshape(b, s, D_MODEL)
        return ctx @ Wo + bo

    def _L2_xattn_ref(features, masks, latents, gm, bm, gl, bl, Wq, Wk, Wv, Wo):
        import jax, jax.numpy as jnp
        import numpy as np
        DIM = 256
        HEADS = 16
        DIM_HEAD = 64
        INNER = HEADS * DIM_HEAD
        B, F, Q = (16, 1024, 64)
        EPS = 1e-05
        SCALE = DIM_HEAD ** (-0.5)

        def _layernorm(x, gamma, beta):
            mu = jnp.mean(x, axis=-1, keepdims=True)
            var = jnp.var(x, axis=-1, keepdims=True)
            return (x - mu) * jax.lax.rsqrt(var + EPS) * gamma + beta
        b, f, d = features.shape
        q_len = latents.shape[1]
        x = _layernorm(features, gm, bm)
        lat = _layernorm(latents, gl, bl)
        q = (lat @ Wq).reshape(b, q_len, HEADS, DIM_HEAD).transpose(0, 2, 1, 3)
        kv_input = jnp.concatenate([x, lat], axis=1)
        kv_mask = jnp.concatenate([masks, jnp.ones((b, q_len), dtype=bool)], axis=1)
        kv_mask = kv_mask[:, None, None, :]
        k = (kv_input @ Wk).reshape(b, f + q_len, HEADS, DIM_HEAD).transpose(0, 2, 1, 3)
        v = (kv_input @ Wv).reshape(b, f + q_len, HEADS, DIM_HEAD).transpose(0, 2, 1, 3)
        q = q * SCALE
        sim = jnp.einsum('bhqd,bhfd->bhqf', q, k)
        sim = sim - jax.lax.stop_gradient(jnp.max(sim, axis=-1, keepdims=True))
        sim = jnp.where(kv_mask, sim, -jnp.inf)
        alphas = jax.nn.softmax(sim, axis=-1)
        out = jnp.einsum('bhqf,bhfd->bhqd', alphas, v)
        out = out.transpose(0, 2, 1, 3).reshape(b, q_len, INNER)
        return out @ Wo

    def _L2_ffn_ref(x, w1, b1, w2, b2):
        import jax, jax.numpy as jnp
        import numpy as np
        QP = 127.0
        MIN_RANGE = 1e-06

        def _ste_round(x):
            return x + jax.lax.stop_gradient(jnp.round(x) - x)

        def _quant_per_tensor(x):
            scale = jnp.maximum(jnp.max(jnp.abs(x)), MIN_RANGE) / QP
            return (_ste_round(x / scale), scale)

        def _qlinear(x2d, w, b):
            xq, sx = _quant_per_tensor(x2d)
            wq, sw = _quant_per_tensor(w)
            out = jnp.matmul(xq, wq.T) + b[None, :]
            return out * (sw * sx)
        B, N, D = x.shape
        h = _qlinear(x.reshape(-1, D), w1, b1)
        h = jax.nn.gelu(h, approximate=False)
        o = _qlinear(h, w2, b2)
        return o.reshape(B, N, -1)

    def _L3_attn_ref(x, Wq, Wk, Wv, Wo):
        import jax, jax.numpy as jnp
        import numpy as np
        import math
        N_HEADS = 16

        def _rope_tables(seq_len, head_dim):
            pos = jnp.arange(seq_len, dtype=jnp.float32)
            freqs = jnp.exp(jnp.arange(0, head_dim, 2, dtype=jnp.float32) * (-math.log(10000.0) / head_dim))
            angles = pos[:, None] * freqs[None, :]
            cos_emb = jnp.zeros((seq_len, head_dim), jnp.float32).at[:, 0::2].set(jnp.cos(angles))
            sin_emb = jnp.zeros((seq_len, head_dim), jnp.float32).at[:, 1::2].set(jnp.sin(angles))
            return (cos_emb, sin_emb)
        B, S, D = x.shape
        H = N_HEADS
        hd = D // H
        q = (x @ Wq.T).reshape(B, S, H, hd)
        k = (x @ Wk.T).reshape(B, S, H, hd)
        v = (x @ Wv.T).reshape(B, S, H, hd)
        cos_emb, sin_emb = _rope_tables(S, hd)
        cos = cos_emb[None, :, None, :]
        sin = sin_emb[None, :, None, :]
        q = q * cos - jnp.roll(q, 1, axis=-1) * sin
        k = k * cos - jnp.roll(k, 1, axis=-1) * sin
        q = q.transpose(0, 2, 1, 3)
        k = k.transpose(0, 2, 1, 3)
        v = v.transpose(0, 2, 1, 3)
        scores = jnp.einsum('bhqd,bhkd->bhqk', q, k) / math.sqrt(hd)
        attn = jax.nn.softmax(scores, axis=-1)
        ctx = jnp.einsum('bhqk,bhkd->bhqd', attn, v)
        ctx = ctx.transpose(0, 2, 1, 3).reshape(B, S, D)
        return ctx @ Wo.T

    def _L3_xattn_ref(latents, context, ln_l_w, ln_l_b, ln_c_w, ln_c_b, Wq, Wkv, Wo, bo):
        import jax, jax.numpy as jnp
        import numpy as np
        DIM = 256
        H = 16
        D = 64
        INNER = H * D
        EPS = 1e-05

        def layernorm(x, w, b):
            mu = jnp.mean(x, axis=-1, keepdims=True)
            var = jnp.var(x, axis=-1, keepdims=True)
            return (x - mu) * jax.lax.rsqrt(var + EPS) * w + b
        b, n, _ = latents.shape
        s = context.shape[1]
        lat = layernorm(latents, ln_l_w, ln_l_b)
        ctx = layernorm(context, ln_c_w, ln_c_b)
        q = (lat @ Wq).reshape(b, n, H, D).transpose(0, 2, 1, 3)
        kv = ctx @ Wkv
        k, v = jnp.split(kv, 2, axis=-1)
        k = k.reshape(b, s, H, D).transpose(0, 2, 1, 3)
        v = v.reshape(b, s, H, D).transpose(0, 2, 1, 3)
        scale = D ** (-0.5)
        attn = jnp.einsum('bhnd,bhsd->bhns', q, k) * scale
        attn = jnp.clip(attn, -11.0, 11.0)
        attn = jax.nn.softmax(attn, axis=-1)
        out = jnp.einsum('bhns,bhsd->bhnd', attn, v)
        out = out.transpose(0, 2, 1, 3).reshape(b, n, INNER)
        return out @ Wo + bo

    def _L3_ffn_ref(x, W_exp, b_exp, up_weights, up_bias, down_weights, W_con, b_con, down_bias):
        import jax, jax.numpy as jnp
        import numpy as np
        D_MODEL = 256
        EXPANSION = 4
        D_HIDDEN = D_MODEL * EXPANSION
        NUM_STAGES = int(np.log2(D_HIDDEN))

        def butterfly(y, weights, dim):
            lead = y.shape[:-1]
            for stage in range(weights.shape[0]):
                s = 2 ** stage
                nb = dim // (2 * s)
                yr = y.reshape(*lead, nb, 2, s)
                a = yr[..., 0, :]
                b = yr[..., 1, :]
                w = weights[stage].reshape(nb, s, 2, 2)
                na = w[..., 0, 0] * a + w[..., 0, 1] * b
                nb2 = w[..., 1, 0] * a + w[..., 1, 1] * b
                y = jnp.stack([na, nb2], axis=-2).reshape(*lead, dim)
            return y
        h = jnp.einsum('bsd,dh->bsh', x, W_exp) + b_exp
        h = butterfly(h, up_weights, D_HIDDEN)
        h = jax.nn.gelu(h + up_bias, approximate=False)
        h = butterfly(h, down_weights, D_HIDDEN)
        y = jnp.einsum('bsh,hd->bsd', h, W_con) + b_con
        return y + down_bias
    x = _layernorm(x + _L0_attn_ref(x, L0_attn_w_qkv, L0_attn_wq_map, L0_attn_bq_map, L0_attn_wk_map, L0_attn_bk_map, L0_attn_w_out), axis=-1)
    x = _layernorm(x + _L0_xattn_ref(x, ctx_1024, ctx_1024, 1, L0_xattn_w_q, L0_xattn_b_q, L0_xattn_w_k, L0_xattn_b_k, L0_xattn_w_v, L0_xattn_b_v, L0_xattn_w_o, L0_xattn_b_o), axis=-1)
    x = _layernorm(x + _L0_ffn_ref(x, L0_ffn_Wg, L0_ffn_bg, L0_ffn_W1, L0_ffn_b1, L0_ffn_W2, L0_ffn_b2), axis=-1)
    x = _layernorm(x + _L1_attn_ref(x, L1_attn_W_query, L1_attn_W_key, L1_attn_W_value), axis=-1)
    x = _layernorm(x + _L1_xattn_ref(x, ctx_1024, ctx_1024, ctx_1024), axis=-1)
    x = _layernorm(x + _L1_ffn_ref(x, L1_ffn_W1, L1_ffn_b1, L1_ffn_W2, L1_ffn_b2, L1_ffn_scale), axis=-1)
    x = _layernorm(x + _L2_attn_ref(x, L2_attn_Wqk, L2_attn_bqk, L2_attn_Wv, L2_attn_bv, L2_attn_Wn, L2_attn_bn, L2_attn_Wo, L2_attn_bo), axis=-1)
    x = _layernorm(x + _L2_xattn_ref(ctx_1024, mask_BxS2_bf1, x, L2_xattn_gm, L2_xattn_bm, L2_xattn_gl, L2_xattn_bl, L2_xattn_Wq, L2_xattn_Wk, L2_xattn_Wv, L2_xattn_Wo), axis=-1)
    x = _layernorm(x + _L2_ffn_ref(x, L2_ffn_w1, L2_ffn_b1, L2_ffn_w2, L2_ffn_b2), axis=-1)
    x = _layernorm(x + _L3_attn_ref(x, L3_attn_Wq, L3_attn_Wk, L3_attn_Wv, L3_attn_Wo), axis=-1)
    x = _layernorm(x + _L3_xattn_ref(x, ctx_1024, L3_xattn_ln_l_w, L3_xattn_ln_l_b, L3_xattn_ln_c_w, L3_xattn_ln_c_b, L3_xattn_Wq, L3_xattn_Wkv, L3_xattn_Wo, L3_xattn_bo), axis=-1)
    x = _layernorm(x + _L3_ffn_ref(x, L3_ffn_W_exp, L3_ffn_b_exp, L3_ffn_up_weights, L3_ffn_up_bias, L3_ffn_down_weights, L3_ffn_W_con, L3_ffn_b_con, L3_ffn_down_bias), axis=-1)
    return x

_drawn_inputs = setup_inputs


def setup_inputs(seed=0):
    import zlib

    import numpy as np

    out = dict(_drawn_inputs(seed))
    spreads = {'L0_ffn_bg': (0.0, 0.302),
     'L0_ffn_b1': (0.0, 0.624),
     'L0_ffn_b2': (0.0, 0.1),
     'L1_ffn_b1': (0.0, 0.1),
     'L1_ffn_b2': (0.0, 0.1),
     'L2_xattn_gm': (1.0, 0.2),
     'L2_xattn_bm': (0.0, 0.1),
     'L2_xattn_gl': (1.0, 0.2),
     'L2_xattn_bl': (0.0, 0.1),
     'L3_xattn_ln_l_w': (1.0, 0.2),
     'L3_xattn_ln_l_b': (0.0, 0.465),
     'L3_xattn_ln_c_w': (1.0, 0.2),
     'L3_xattn_ln_c_b': (0.0, 0.1),
     'L3_xattn_bo': (0.0, 0.1),
     'L3_ffn_b_exp': (0.0, 0.1),
     'L3_ffn_up_bias': (0.0, 0.1),
     'L3_ffn_b_con': (0.0, 0.1),
     'L3_ffn_down_bias': (0.0, 0.1)}
    factors = {'L0_attn_w_qkv': 4.721,
     'L0_attn_wq_map': 8.0,
     'L0_attn_bq_map': 32.808,
     'L0_attn_wk_map': 8.0,
     'L0_attn_bk_map': 42.321,
     'L0_attn_w_out': 4.898,
     'L0_xattn_b_q': 8.0,
     'L0_xattn_b_k': 64.0,
     'L0_xattn_b_v': 2.86,
     'L2_attn_bn': 3.908,
     'L2_attn_bo': 8.0,
     'L2_ffn_b1': 64.0,
     'L2_ffn_b2': 64.0}
    for name, (base, spread) in spreads.items():
        noise = np.random.default_rng([zlib.crc32(name.encode()), seed]).standard_normal(out[name].shape)
        drawn = base * np.exp(spread * noise) if base else spread * noise
        out[name] = jnp.asarray(drawn.astype(out[name].dtype))
    for name, factor in factors.items():
        out[name] = (out[name] * factor).astype(out[name].dtype)
    return out
```

```python
from contextlib import ExitStack

import numpy as np

import concourse.bass as bass
from concourse import mybir

F32 = mybir.dt.float32
BF16 = mybir.dt.bfloat16
ALU = mybir.AluOpType
ACT = mybir.ActivationFunctionType
AX = mybir.AxisListType.X
RMAX = bass.bass_isa.ReduceOp.max

P = 128
B, S, D = 4, 512, 256
T = S // P
KD = D // P
H = 16
NG = 4
EPS = 1e-5
SLOTS = 2
MAGIC = 12582912.0
PHASES = range(0, 12)


class Ring:

    def __init__(self, nc, ctx, short, name, psum):
        self.full = ctx.enter_context(nc.semaphore(f"{name}_full"))
        self.empty = ctx.enter_context(nc.semaphore(f"{name}_empty"))
        self.psum, self.base, self.short = psum, 0, short

    def begin(self, per_batch):
        assert per_batch % SLOTS == 0, per_batch
        self.n, self.keys, self.taken = per_batch, [], 0

    def end(self):
        assert len(self.keys) == self.taken == self.n, (len(self.keys), self.taken, self.n)
        self.base += B * self.n

    def vacant(self, b, key):
        self.keys.append(key)
        return b * self.n + (self.base + len(self.keys))

    def filled(self, b, key):
        assert self.keys[self.taken] == key, (key, self.keys[self.taken])
        self.taken += 1
        return b * self.n + (self.base + self.taken)

    def copied(self, b, key):
        return b * self.n + (self.base + self.keys.index(key) + 1 + SLOTS)

    def slot(self, key):
        return self.psum[:, self.keys.index(key) % SLOTS, :]


class Signal:

    def __init__(self, nc, ctx, name):
        self.sem = ctx.enter_context(nc.semaphore(name))
        self.base, self.n = 0, 0

    def begin(self, per_batch):
        self.n = per_batch

    def end(self):
        self.base += B * self.n
        self.n = 0

    def at(self, b, k):
        return b * self.n + (self.base + k)


class Core:
    pass


def allocator(nc, ctx, layer):
    def sb(name, shape, dt=F32):
        return ctx.enter_context(nc.sbuf_tensor(f"{layer}_{name}", shape, dt))
    return sb


def alone(c, eng):
    eng.sem_inc(c.marker, 1)


def mm(pe, out, pairs, start=True):
    for i, (lhsT, rhs) in enumerate(pairs):
        last = pe.matmul(out, lhsT, rhs, start=start and i == 0, stop=i == len(pairs) - 1)
    return last


def begin(c, **counts):
    for ring in (c.A, c.V, c.O):
        ring.begin(counts.pop(ring.short))
    for name, n in counts.items():
        c.signals[name].begin(n)



def act_fetch_x(c, act, b):
    alone(c, act)
    act.activation(c.xn[:, :, :], c.x[:, bass.ds(b * T, T), :], ACT.Copy).then_inc(c.x_here.sem, 1)


def pe_transpose_x(c, pe, b):
    pe.wait_ge(c.A.empty, c.A.vacant(b, "xT"))
    out = c.A.slot("xT")
    pe.wait_ge(c.x_here.sem, c.x_here.at(b, 1))
    for k in range(KD):
        for t in range(T):
            last = pe.transpose(out[:, k * S + t * P:k * S + (t + 1) * P], c.xn[:, t, k * P:(k + 1) * P], c.ident[:, :])
    last.then_inc(c.A.full, 1)


def pe_transpose_x_halves(c, pe, b):
    for k in range(KD):
        pe.wait_ge(c.A.empty, c.A.vacant(b, ("xT", k)))
        out = c.A.slot(("xT", k))
        pe.wait_ge(c.x_here.sem, c.x_here.at(b, 1))
        for t in range(T):
            last = pe.transpose(out[:, t * P:(t + 1) * P], c.xn[:, t, k * P:(k + 1) * P], c.ident[:, :])
        last.then_inc(c.A.full, 1)


def act_transposed_x(c, act, b):
    act.wait_ge(c.A.full, c.A.filled(b, "xT"))
    act.activation(c.xT[:, :, :].rearrange("p k s -> p (k s)"), c.A.slot("xT"), ACT.Copy).then_inc(c.A.empty, 1)


def pe_transpose_ctx(c, pe, b):
    pe.wait_ge(c.A.empty, c.A.vacant(b, "cT"))
    out = c.A.slot("cT")
    pe.wait_ge(c.ctx_here.sem, c.ctx_here.at(b, 1))
    for k in range(KD):
        for t in range(T):
            last = pe.transpose(out[:, k * S + t * P:k * S + (t + 1) * P], c.ctxn[:, t, k * P:(k + 1) * P], c.ident[:, :])
    last.then_inc(c.A.full, 1)


def act_fetch_ctx(c, act, b):
    alone(c, act)
    act.activation(c.ctxn[:, :, :], c.ctx[:, bass.ds(b * T, T), :], ACT.Copy).then_inc(c.ctx_here.sem, 1)


def act_transposed_ctx(c, act, b):
    act.wait_ge(c.A.full, c.A.filled(b, "cT"))
    act.activation(c.cT[:, :, :].rearrange("p k s -> p (k s)"), c.A.slot("cT"), ACT.Copy).then_inc(c.A.empty, 1)


def dve_norm(c, dve, b, j, src, dst):
    for t in range(T):
        dve.bn_stats(c.stats[:, t, :], src[:, t, :])
    dve.drain()
    for t in range(T):
        dve.bn_aggr(c.meanvar[:, t, :], c.stats[:, t, :])
    dve.drain()
    dve.tensor_scalar(c.vareps[:, :], c.meanvar[:, :, 1], EPS, None, ALU.add).then_inc(c.var_ready.sem, 1)
    dve.wait_ge(c.rstd_ready.sem, c.rstd_ready.at(b, j + 1))
    alone(c, dve)
    for t in range(T):
        last = dve.tensor_scalar(dst[:, t, :], src[:, t, :], c.meanvar[:, t, 0:1], c.rstd[:, t:t + 1],
                                 ALU.subtract, ALU.mult)
    return last


def pool_rstd(c, pool, b, j):
    pool.wait_ge(c.var_ready.sem, c.var_ready.at(b, j + 1))
    alone(c, pool)
    pool.tensor_tensor(c.rstd[:, :], c.vareps[:, :], c.minus_half[:, :], ALU.pow).then_inc(c.rstd_ready.sem, 1)


def dve_residual_norm(c, dve, b, norm=0):
    dve.drain()
    for i in range(2):
        dve.wait_ge(c.V.full, c.V.filled(b, ("y", i)))
        y = c.V.slot(("y", i)).rearrange("p (t d) -> p t d", d=D)
        last = dve.tensor_tensor(c.r[:, 2 * i:2 * i + 2, :], y, c.x[:, bass.ds(b * T + 2 * i, 2), :], ALU.add)
        last.then_inc(c.V.empty, 1)
    dve.drain()
    dve_norm(c, dve, b, norm, c.r, c.x[:, bass.ds(b * T, T), :])


def pe_project_out(c, pe, b, lhs, rhs, bias=None):
    for i in range(2):
        pe.wait_ge(c.V.empty, c.V.vacant(b, ("y", i)))
        out = c.V.slot(("y", i))
        for t in (2 * i, 2 * i + 1):
            pairs = [(l(t), r) for l, r in zip(lhs, rhs)]
            if bias is not None:
                pairs += [(c.ones[0:1, 0:P], v) for v in bias]
            last = mm(pe, out[:, (t - 2 * i) * D:(t - 2 * i + 1) * D], pairs)
        last.then_inc(c.V.full, 1)


def pe_transpose_attn(c, pe, b, on, width):
    for m in range(width // P // 2):
        pe.wait_ge(c.A.empty, c.A.vacant(b, ("oT", m)))
        out = c.A.slot(("oT", m))
        if m == 0:
            pe.wait_ge(c.heads_ready.sem, c.heads_ready.at(b, H // c.per_o))
        for k in range(2):
            for t in range(T):
                last = pe.transpose(out[:, k * S + t * P:k * S + (t + 1) * P],
                                    on[:, t, (2 * m + k) * P:(2 * m + k + 1) * P], c.ident[:, :])
        last.then_inc(c.A.full, 1)


def act_transposed_attn(c, act, b, oT, width):
    for m in range(width // P // 2):
        act.wait_ge(c.A.full, c.A.filled(b, ("oT", m)))
        src = c.A.slot(("oT", m))
        act.activation(oT[:, 2 * m:2 * m + 2, :].rearrange("p k s -> p (k s)"), src, ACT.Copy).then_inc(c.A.empty, 1)


OFF_AT = {0: 0, 2: 384, 1: 512}
OFF_LEN = 768


def causal_at(kt, qt):
    return qt * P if kt == qt else S + OFF_AT[kt] + (qt - kt - 1) * P


def pe_causal_scores(c, pe, b, h, kh, qh, diag_ring, softmax):
    pe.wait_ge(diag_ring.empty, diag_ring.vacant(b, ("d", h)))
    out = diag_ring.slot(("d", h))
    if softmax:
        pe.matmul(out[:, 0:S], c.ident16[:, :], c.causal_kq[:, :], start=True, stop=False)
        pe.matmul(out[:, 0:S], c.selh(h), c.shifth(h), start=False, stop=False)
    for t in range(T):
        cols = slice(t * P, (t + 1) * P)
        last = pe.matmul(out[:, cols], kh[:, cols], qh[:, cols], start=not softmax, stop=not softmax or t == T - 1)
    last.then_inc(diag_ring.full, 1)
    pe.wait_ge(c.A.empty, c.A.vacant(b, ("o", h)))
    out = c.A.slot(("o", h))
    for kts in ((0, 2), (1,)):
        if softmax:
            for kt in kts:
                n = S - (kt + 1) * P
                pe.matmul(out[:, OFF_AT[kt]:OFF_AT[kt] + n], c.selh(h), c.shifth(h)[:, S - n:S], start=kt == kts[0],
                          stop=False)
        for kt in kts:
            n = S - (kt + 1) * P
            last = pe.matmul(out[:, OFF_AT[kt]:OFF_AT[kt] + n], kh[:, kt * P:(kt + 1) * P], qh[:, S - n:S],
                             start=not softmax, stop=not softmax or kt == kts[-1])
    last.then_inc(c.A.full, 1)


def pe_scores(c, pe, b, h, kh, qh, kts):
    for j in range(kts // 2):
        pe.wait_ge(c.A.empty, c.A.vacant(b, ("s", h, j)))
        out = c.A.slot(("s", h, j))
        for i in range(2):
            kt = 2 * j + i
            pe.matmul(out[:, i * S:(i + 1) * S], c.selh(h), c.shifth(h), start=True, stop=False)
            last = pe.matmul(out[:, i * S:(i + 1) * S], kh[:, kt * P:(kt + 1) * P], qh, start=False, stop=True)
        last.then_inc(c.A.full, 1)


def pe_values(c, pe, b, h, e, v, vw, causal, last_jobs):
    g, i = divmod(h, c.per_o)
    if i == 0:
        pe.wait_ge(c.O.empty, c.O.vacant(b, ("O", g)))
        c.o_slot = c.O.slot(("O", g))
    for ring, key in last_jobs:
        pe.wait_ge(ring.empty, ring.copied(b, key))
    for qt in range(T):
        kts = range(qt + 1) if causal else range(v.shape[1])
        at = (qt * c.per_o + i) * vw
        for kt in kts:
            w = e[:, causal_at(kt, qt):causal_at(kt, qt) + P] if causal else e[:, kt * S + qt * P:kt * S + (qt + 1) * P]
            last = pe.matmul(c.o_slot[:, at:at + vw], w, v[:, kt, h, 0:vw], start=kt == 0, stop=kt == kts[-1])
    if i == c.per_o - 1:
        last.then_inc(c.O.full, 1)


def pe_max_scores(c, pe, b, h, qt, kh, qh, parts, by_register=False):
    pe.wait_ge(c.V.empty, c.V.vacant(b, ("m", h, qt, parts[0][1])))
    out = c.V.slot(("m", h, qt, parts[0][1]))
    if by_register:
        alone(c, pe)
    for at, k0, n, hide in parts:
        if hide is not None:
            pe.matmul(out[:, at:at + n], hide[0], hide[1], start=True, stop=False)
        last = pe.matmul(out[:, at:at + n], qh[:, qt * P:(qt + 1) * P], kh[:, k0:k0 + n], start=hide is None, stop=True)
    last.then_inc(c.V.full, 1)


def pe_project_values(c, pe, b, xT, wv, bias=None):
    for i in range(2):
        pe.wait_ge(c.V.empty, c.V.vacant(b, ("v", i)))
        out = c.V.slot(("v", i))
        for t in (2 * i, 2 * i + 1):
            pairs = [(xT[:, k, t * P:(t + 1) * P], wv[:, k, :]) for k in range(KD)]
            if bias is not None:
                pairs.append((c.ones[0:1, 0:P], bias))
            last = mm(pe, out[:, (t - 2 * i) * D:(t - 2 * i + 1) * D], pairs)
        last.then_inc(c.V.full, 1)


def dve_values(c, dve, b):
    for i in range(2):
        dve.wait_ge(c.V.full, c.V.filled(b, ("v", i)))
        src = c.V.slot(("v", i)).rearrange("p (t h d) -> p t h d", t=2, d=16)
        for t in range(2):
            last = dve.tensor_copy(c.v[:, 2 * i + t, :, 0:16], src[:, t, :, :])
        last.then_inc(c.V.empty, 1)


def dve_shift_parts(c, dve):
    nmax, hi = c.nmax, c.nmax16
    dve.tensor_reduce(nmax[:, :, :], c.mraw[:, :, :, :], AX, ALU.max, negate=True)
    dve.drain()
    dve.tensor_copy(hi[:, :, :], nmax[:, :, :])
    dve.drain()
    dst = c.parts[:, :, :].rearrange("p t (c w) -> p t c w", w=32)
    for cc in range(4):
        dve.tensor_copy(dst[:, :, cc, 0:H], hi[:, :, :])
        last = dve.tensor_tensor(dst[:, :, cc, H:2 * H], nmax[:, :, :], hi[:, :, :], ALU.subtract)
    last.then_inc(c.parts_ready.sem, 1)


def pe_transpose_shift(c, pe, b):
    pe.wait_ge(c.A.empty, c.A.vacant(b, "shift"))
    out = c.A.slot("shift")
    pe.wait_ge(c.parts_ready.sem, c.parts_ready.at(b, 1))
    for t in range(T):
        last = pe.transpose(out[:, t * P:(t + 1) * P], c.parts[:, t, :], c.ident[:, :])
    last.then_inc(c.A.full, 1)


def act_transposed_shift(c, act, b):
    act.wait_ge(c.A.full, c.A.filled(b, "shift"))
    act.activation(c.shift[:, :], c.A.slot("shift")[:, 0:S], ACT.Copy).then_inc(c.A.empty, 1)


def head16(tile, h):
    return tile[32 * (h % 4):32 * (h % 4) + 32, h // 4, :]


def head64(tile, h):
    return tile[64 * (h % 2):64 * (h % 2) + 64, h // 2, :]


def alloc_attention(c, sb, e_len, vw, kts, o_width, softmax, k=32):
    c.e = [sb(f"e{i}", [P, e_len]) for i in range(2)]
    c.v = sb("v", [P, kts, H, vw])
    c.on = sb("on", [P, T, o_width])
    c.rec = sb("rec", [P, T, H])
    if softmax:
        c.nmax = sb("nmax", [P, T, H])
        c.nmax16 = sb("nmax16", [P, T, H], BF16)
        c.parts = sb("parts", [P, T, P])
        c.shift = sb("shift", [P, S], BF16)
        sel = c.sel = sb("sel", [P, H, P], BF16)
        c.selh = lambda h: sel[k * (h % (P // k)):k * (h % (P // k)) + k, h, :]
        c.shifth = lambda h: c.shift[k * (h % (P // k)):k * (h % (P // k)) + k, :]


def dve_heads_out(c, dve, b, g, hd, vw, floor=None, given=None):
    n = c.per_o
    dve.wait_ge(c.O.full, c.O.filled(b, ("O", g)))
    o = c.O.slot(("O", g))[:, 0:T * n * vw].rearrange("p (t i w) -> p t i w", i=n, w=vw)
    hs = slice(g * n, (g + 1) * n)
    if given is None:
        rec = c.rec[:, :, hs]
        if floor is not None:
            dve.tensor_scalar(rec, o[:, :, :, hd], floor, None, ALU.max)
            dve.drain()
            dve.reciprocal(rec, rec)
        else:
            dve.reciprocal(rec, o[:, :, :, hd])
        dve.drain()
    else:
        rec = given[:, :, hs]
    for t in range(T):
        dst = c.on[:, t, g * n * hd:(g + 1) * n * hd].rearrange("p (i d) -> p i d", d=hd)
        last = dve.tensor_tensor(dst, o[:, t, :, 0:hd], rec[:, t, :].unsqueeze(2).to_broadcast([P, n, hd]), ALU.mult)
    last.then_inc(c.O.empty, 1)
    dve.drain().then_inc(c.heads_ready.sem, 1)



def layer_l0_attn(nc, c, ins):
    with ExitStack() as ctx:
        sb = allocator(nc, ctx, "l0_attn")
        FW = 2 * 2 * D
        wqk = sb("wqk", [P, 4, D])
        maps = sb("maps", [P, 2, P])
        wv = sb("wv", [P, KD, D])
        wo = sb("wo", [P, KD, D])
        fbias = sb("fbias", [1, 2 * D])
        wc = sb("wc", [P, KD, 2 * D])
        feat = sb("feat", [P, T, FW])
        hi = sb("hi", [P, T, 2 * H])
        lo = sb("lo", [P, T, 2 * H])
        fsum = sb("fsum", [P, T, 4 * H])
        fT = sb("fT", [P, 2, NG, S])
        oT = sb("oT", [P, KD, S])
        c.causal01 = sb("causal01", [P, S])
        alloc_attention(c, sb, S + OFF_LEN, 17, T, D, False)
        c.per_o = 4
        begin(c, A=1 + NG + H + 1, V=T + 2 + H + 2, O=NG, x_here=1, var_ready=1, rstd_ready=1, heads_ready=NG,
              exp_in=T, exp_ready=T, feat_ready=T)
        c.expect_setup(2)
        c.setup_fulls += 1

        with nc.Block() as block:
            @block.sync
            def _(sp):
                for dst, name in ((wqk, "wqk0"), (maps, "maps0"), (wv, "wv0"), (wo, "wo0"), (fbias, "fbias0"),
                                  (c.causal01, "causal01")):
                    c.load(sp, dst, ins[name])

            @block.tensor
            def _(pe):
                pe.wait_ge(c.loaded, c.load_count)
                for m in range(4):
                    for k in range(KD):
                        last = pe.matmul(c.psO[:, k, m * P:(m + 1) * P], wqk[:, m, k * P:(k + 1) * P],
                                         maps[:, m // 2, :], start=True, stop=True)
                last.then_inc(c.setup_full, 1)
                pe.wait_ge(c.setup_done, c.setup_dones)
                with pe.Fori(0, B) as b:
                    pe_transpose_x(c, pe, b)
                    pe.wait_ge(c.A.empty, c.A.copied(b, "xT"))
                    for t in range(T):
                        pe.wait_ge(c.V.empty, c.V.vacant(b, ("p", t)))
                        out = c.V.slot(("p", t))
                        mm(pe, out, [(c.xT[:, k, t * P:(t + 1) * P], wc[:, k, :]) for k in range(KD)]
                                      + [(c.ones[0:1, 0:P], fbias[0:1, :])]).then_inc(c.V.full, 1)
                    pe_project_values(c, pe, b, c.xT, wv)
                    for g in range(NG):
                        pe.wait_ge(c.A.empty, c.A.vacant(b, ("fT", g)))
                        out = c.A.slot(("fT", g))
                        if g == 0:
                            pe.wait_ge(c.feat_ready.sem, c.feat_ready.at(b, T))
                        for w in range(2):
                            for t in range(T):
                                last = pe.transpose(out[:, w * S + t * P:w * S + (t + 1) * P],
                                                    feat[:, t, (w * NG + g) * P:(w * NG + g + 1) * P], c.ident[:, :])
                        last.then_inc(c.A.full, 1)
                    for h in range(H + 1):
                        if h < H:
                            if h % 4 == 0:
                                pe.wait_ge(c.A.empty, c.A.copied(b, ("fT", h // 4)))
                            pe_causal_scores(c, pe, b, h, head16(fT[:, 1], h), head16(fT[:, 0], h), c.V, False)
                        if h:
                            pe_values(c, pe, b, h - 1, c.e[(h - 1) % 2], c.v, 17, True,
                                      [(c.V, ("d", h - 1)), (c.A, ("o", h - 1))])
                    pe_transpose_attn(c, pe, b, c.on, D)
                    pe.wait_ge(c.A.empty, c.A.copied(b, ("oT", 0)))
                    pe_project_out(c, pe, b, [lambda t, k=k: oT[:, k, t * P:(t + 1) * P] for k in range(KD)],
                                   [wo[:, k, :] for k in range(KD)])

            @block.vector
            def _(dve):
                dve.wait_ge(c.setup_full, 1)
                dve.tensor_copy(wc[:, :, :], c.psO[:, :, :]).then_inc(c.setup_done, 1)
                with dve.Fori(0, B) as b:
                    for t in range(T):
                        dve.wait_ge(c.V.full, c.V.filled(b, ("p", t)))
                        p = c.V.slot(("p", t)).rearrange("p (h d) -> p h d", d=16)
                        f = feat[:, t, :].rearrange("p (h d) -> p h d", d=32)
                        dve.tensor_reduce(hi[:, t, :], p, AX, ALU.max)
                        dve.tensor_reduce(lo[:, t, :], p, AX, ALU.min)
                        dve.drain()
                        shape = [P, 2 * H, 16]
                        dve.tensor_tensor(f[:, :, 0:16], p, hi[:, t, :].unsqueeze(2).to_broadcast(shape), ALU.subtract)
                        last = dve.tensor_tensor(f[:, :, 16:32], lo[:, t, :].unsqueeze(2).to_broadcast(shape), p,
                                                 ALU.subtract)
                        last.then_inc(c.V.empty, 1)
                        dve.drain().then_inc(c.exp_in.sem, 1)
                    dve_values(c, dve, b)
                    for t in range(T):
                        f = feat[:, t, :].rearrange("p (h d) -> p h d", d=16)
                        dve.wait_ge(c.exp_ready.sem, c.exp_ready.at(b, t + 1))
                        dve.tensor_reduce(fsum[:, t, :], f, AX, ALU.add)
                        dve.drain()
                        dve.reciprocal(fsum[:, t, :], fsum[:, t, :])
                        dve.drain()
                        dve.tensor_tensor(
                            f, f, fsum[:, t, :].unsqueeze(2).to_broadcast([P, 4 * H, 16]), ALU.mult).then_inc(c.feat_ready.sem, 1)
                    for h in range(H):
                        dve.wait_ge(c.V.full, c.V.filled(b, ("d", h)))
                        d = c.V.slot(("d", h))
                        dve.tensor_tensor(c.e[h % 2][:, 0:S], d, c.causal01[:, :], ALU.mult).then_inc(c.V.empty, 1)
                        if h % 4 == 0 and h:
                            dve_heads_out(c, dve, b, h // 4 - 1, 16, 17, floor=1e-6)
                    dve_heads_out(c, dve, b, 3, 16, 17, floor=1e-6)
                    dve_residual_norm(c, dve, b)

            @block.scalar
            def _(act):
                with act.Fori(0, B) as b:
                    act_fetch_x(c, act, b)
                    act_transposed_x(c, act, b)
                    for t in range(T):
                        act.wait_ge(c.exp_in.sem, c.exp_in.at(b, t + 1))
                        act.activation(feat[:, t, :], feat[:, t, :], ACT.Exp).then_inc(c.exp_ready.sem, 1)
                    for g in range(NG):
                        act.wait_ge(c.A.full, c.A.filled(b, ("fT", g)))
                        src = c.A.slot(("fT", g))
                        act.activation(fT[:, :, g, :], src.rearrange("p (w s) -> p w s", s=S), ACT.Copy).then_inc(c.A.empty, 1)
                    for h in range(H):
                        act.wait_ge(c.A.full, c.A.filled(b, ("o", h)))
                        src = c.A.slot(("o", h))
                        act.activation(c.e[h % 2][:, S:S + OFF_LEN], src[:, 0:OFF_LEN], ACT.Copy).then_inc(c.A.empty, 1)
                    act_transposed_attn(c, act, b, oT, D)

            @block.gpsimd
            def _(pool):
                pool.memset(c.v[:, :, :, 16:17], 1.0).then_inc(c.setup_done, 1)
                with pool.Fori(0, B) as b:
                    pool_rstd(c, pool, b, 0)
        c.finish()



def layer_l0_xattn(nc, c, ins):
    with ExitStack() as ctx:
        sb = allocator(nc, ctx, "l0_xattn")
        wq, wk = sb("wq", [P, KD, NG * P]), sb("wk", [P, KD, NG * P])
        wv, wo = sb("wv", [P, KD, D]), sb("wo", [P, KD, D])
        qbias, kbias = sb("qbias", [P, NG]), sb("kbias", [P, NG])
        vbias, obias = sb("vbias", [1, D]), sb("obias", [1, D])
        qT, kT = sb("qT", [P, NG, S]), sb("kT", [P, NG, S])
        oT = sb("oT", [P, KD, S])
        alloc_attention(c, sb, S + OFF_LEN, 17, T, D, True)
        c.mraw = sb("mraw", [P, T, H, 1])
        c.per_o = 4
        begin(c, A=2 + 2 + 1 + 2 * H + 1, V=NG + 2 + H * T + 2, O=NG,
              x_here=1, ctx_here=1, var_ready=1, rstd_ready=1, heads_ready=NG, parts_ready=1)
        c.expect_setup(1)

        with nc.Block() as block:
            @block.sync
            def _(sp):
                for dst, name in ((wq, "wq1"), (wk, "wk1"), (wv, "wv1"), (wo, "wo1"), (qbias, "qbias1"),
                                  (kbias, "kbias1"), (vbias, "vbias1"), (obias, "obias1"),
                                  (c.sel, "sel32")):
                    c.load(sp, dst, ins[name])

            @block.tensor
            def _(pe):
                pe.wait_ge(c.loaded, c.load_count)
                pe.wait_ge(c.setup_done, c.setup_dones)
                with pe.Fori(0, B) as b:
                    pe_transpose_x(c, pe, b)
                    pe_transpose_ctx(c, pe, b)
                    pe.wait_ge(c.A.empty, c.A.copied(b, "xT"))
                    for g in range(NG):
                        pe.wait_ge(c.V.empty, c.V.vacant(b, ("q", g)))
                        out = c.V.slot(("q", g))
                        mm(pe, out, [(wq[:, k, g * P:(g + 1) * P], c.xT[:, k, :]) for k in range(KD)]).then_inc(c.V.full, 1)
                    pe.wait_ge(c.A.empty, c.A.copied(b, "cT"))
                    for i in range(2):
                        pe.wait_ge(c.A.empty, c.A.vacant(b, ("k", i)))
                        out = c.A.slot(("k", i))
                        for g in (2 * i, 2 * i + 1):
                            last = mm(pe, out[:, (g - 2 * i) * S:(g - 2 * i + 1) * S],
                                      [(wk[:, k, g * P:(g + 1) * P], c.cT[:, k, :]) for k in range(KD)])
                        last.then_inc(c.A.full, 1)
                    pe_project_values(c, pe, b, c.cT, wv, vbias[0:1, :])
                    for h in range(H):
                        if h == 0:
                            pe.wait_ge(c.V.empty, c.V.copied(b, ("q", NG - 1)))
                        if h % 8 == 0:
                            pe.wait_ge(c.A.empty, c.A.copied(b, ("k", h // 8)))
                        for qt in range(T):
                            parts = [(0, 0, qt * P, None)] if qt else []
                            parts.append((qt * P, qt * P, P, (c.ident16[:, :], c.causal_qk[:, :])))
                            pe_max_scores(c, pe, b, h, qt, head16(kT, h), head16(qT, h), parts)
                    pe_transpose_shift(c, pe, b)
                    pe.wait_ge(c.A.empty, c.A.copied(b, "shift"))
                    pe.wait_ge(c.V.empty, c.V.copied(b, ("v", 1)))
                    for h in range(H + 1):
                        if h < H:
                            pe_causal_scores(c, pe, b, h, head16(kT, h), head16(qT, h), c.A, True)
                        if h:
                            pe_values(c, pe, b, h - 1, c.e[(h - 1) % 2], c.v, 17, True, [(c.A, ("o", h - 1))])
                    pe_transpose_attn(c, pe, b, c.on, D)
                    pe.wait_ge(c.A.empty, c.A.copied(b, ("oT", 0)))
                    pe_project_out(c, pe, b, [lambda t, k=k: oT[:, k, t * P:(t + 1) * P] for k in range(KD)],
                                   [wo[:, k, :] for k in range(KD)], [obias[0:1, :]])

            @block.vector
            def _(dve):
                dve.wait_ge(c.loaded, c.load_count)
                dve.memset(c.parts[:, :, :], 0.0)
                dve.memset(c.v[:, :, :, 16:17], 1.0)
                dve.drain().then_inc(c.setup_done, 1)
                with dve.Fori(0, B) as b:
                    for g in range(NG):
                        dve.wait_ge(c.V.full, c.V.filled(b, ("q", g)))
                        q = c.V.slot(("q", g))
                        dve.tensor_scalar(qT[:, g, :], q, qbias[:, g:g + 1], None, ALU.add).then_inc(c.V.empty, 1)
                    dve_values(c, dve, b)
                    for h in range(H):
                        for qt in range(T):
                            dve.wait_ge(c.V.full, c.V.filled(b, ("m", h, qt, 0)))
                            s = c.V.slot(("m", h, qt, 0))[:, 0:(qt + 1) * P]
                            dve.tensor_reduce(c.mraw[:, qt, h, :], s, AX, ALU.max).then_inc(c.V.empty, 1)
                    dve.drain()
                    dve_shift_parts(c, dve)
                    for g in range(NG):
                        dve_heads_out(c, dve, b, g, 16, 17)
                    dve_residual_norm(c, dve, b)

            @block.scalar
            def _(act):
                with act.Fori(0, B) as b:
                    act_fetch_x(c, act, b)
                    act_fetch_ctx(c, act, b)
                    act_transposed_x(c, act, b)
                    act_transposed_ctx(c, act, b)
                    for i in range(2):
                        act.wait_ge(c.A.full, c.A.filled(b, ("k", i)))
                        src = c.A.slot(("k", i))
                        for g in (2 * i, 2 * i + 1):
                            last = act.activation(kT[:, g, :], src[:, (g - 2 * i) * S:(g - 2 * i + 1) * S],
                                                  ACT.Identity, bias=kbias[:, g:g + 1])
                        last.then_inc(c.A.empty, 1)
                    act_transposed_shift(c, act, b)
                    for h in range(H):
                        act.wait_ge(c.A.full, c.A.filled(b, ("d", h)))
                        src = c.A.slot(("d", h))
                        act.activation(c.e[h % 2][:, 0:S], src[:, 0:S], ACT.Exp, scale=0.25).then_inc(c.A.empty, 1)
                        act.wait_ge(c.A.full, c.A.filled(b, ("o", h)))
                        src = c.A.slot(("o", h))
                        act.activation(c.e[h % 2][:, S:S + OFF_LEN], src[:, 0:OFF_LEN], ACT.Exp, scale=0.25).then_inc(c.A.empty, 1)
                    act_transposed_attn(c, act, b, oT, D)

            @block.gpsimd
            def _(pool):
                with pool.Fori(0, B) as b:
                    pool_rstd(c, pool, b, 0)
        c.finish()



def layer_l0_ffn(nc, c, ins):
    with ExitStack() as ctx:
        sb = allocator(nc, ctx, "l0_ffn")
        E, FT = 8, 4
        w1, w2 = sb("w1", [P, E, KD, FT * P]), sb("w2", [P, E, FT, D])
        wg, gbias = sb("wg", [P, KD, E]), sb("gbias", [1, E])
        b1, b2 = sb("b1", [P, E * FT]), sb("b2", [E, D])
        rank = sb("rank", [P, T, E])
        hT = [sb(f"hT{i}", [P, FT, S]) for i in range(2)]
        logits, probs, left = sb("logits", [P, T, E]), sb("probs", [P, T, E]), sb("left", [P, T, E])
        key, pick, mask = sb("key", [P, T, E]), sb("pick", [P, T, E]), sb("mask", [P, T, E])
        top = sb("top", [P, T])
        gates, gatesT, mixed_b2 = sb("gates", [P, T, P]), sb("gatesT", [P, S]), sb("mixed_b2", [P, T, D])
        begin(c, A=4 + 2 * E, V=2 * E, O=0, x_here=1, var_ready=1, rstd_ready=1, exp_in=1, exp_ready=1, vec_ready=1)
        c.expect_setup(0)

        with nc.Block() as block:
            @block.sync
            def _(sp):
                for dst, name in ((wg, "wg2"), (gbias, "gbias2"), (rank, "rank2"), (b1, "b1_2"), (b2, "b2_2"),
                                  (w1, "w1_2"), (w2, "w2_2")):
                    c.load(sp, dst, ins[name])

            @block.tensor
            def _(pe):
                pe.wait_ge(c.loaded, c.load_count)
                with pe.Fori(0, B) as b:
                    pe_transpose_x(c, pe, b)
                    pe.wait_ge(c.A.empty, c.A.copied(b, "xT"))
                    pe.wait_ge(c.A.empty, c.A.vacant(b, "logits"))
                    out = c.A.slot("logits")
                    for t in range(T):
                        last = mm(pe, out[:, t * E:(t + 1) * E],
                                  [(c.xT[:, k, t * P:(t + 1) * P], wg[:, k, :]) for k in range(KD)]
                                  + [(c.ones[0:1, 0:P], gbias[0:1, :])])
                    last.then_inc(c.A.full, 1)

                    def up(e):
                        for i in range(2):
                            pe.wait_ge(c.A.empty, c.A.vacant(b, ("h", e, i)))
                            out = c.A.slot(("h", e, i))
                            for m in (2 * i, 2 * i + 1):
                                last = mm(pe, out[:, (m - 2 * i) * S:(m - 2 * i + 1) * S],
                                          [(w1[:, e, k, m * P:(m + 1) * P], c.xT[:, k, :]) for k in range(KD)])
                            last.then_inc(c.A.full, 1)

                    def down(e):
                        pe.wait_ge(c.A.empty, c.A.copied(b, ("h", e, 1)))
                        for i in range(2):
                            pe.wait_ge(c.V.empty, c.V.vacant(b, ("o", e, i)))
                            out = c.V.slot(("o", e, i))
                            for t in (2 * i, 2 * i + 1):
                                last = mm(pe, out[:, (t - 2 * i) * D:(t - 2 * i + 1) * D],
                                          [(hT[e % 2][:, f, t * P:(t + 1) * P], w2[:, e, f, :]) for f in range(FT)])
                            last.then_inc(c.V.full, 1)

                    up(0)
                    pe.wait_ge(c.A.empty, c.A.vacant(b, "gatesT"))
                    out = c.A.slot("gatesT")
                    pe.wait_ge(c.vec_ready.sem, c.vec_ready.at(b, 1))
                    for t in range(T):
                        last = pe.transpose(out[:, t * P:(t + 1) * P], gates[:, t, :], c.ident[:, :])
                    last.then_inc(c.A.full, 1)
                    pe.wait_ge(c.A.empty, c.A.vacant(b, "mixed_b2"))
                    out = c.A.slot("mixed_b2")
                    pe.wait_ge(c.A.empty, c.A.copied(b, "gatesT"))
                    for t in range(T):
                        last = pe.matmul(out[:, t * D:(t + 1) * D], gatesT[0:E, t * P:(t + 1) * P], b2[0:E, :],
                                         start=True, stop=True)
                    last.then_inc(c.A.full, 1)
                    for e in range(E):
                        if e + 1 < E:
                            up(e + 1)
                        down(e)

            @block.vector
            def _(dve):
                dve.wait_ge(c.loaded, c.load_count)
                dve.memset(gates[:, :, :], 0.0)
                with dve.Fori(0, B) as b:
                    wide = [P, T, E]
                    dve.wait_ge(c.A.empty, c.A.copied(b, "logits"))
                    dve.tensor_reduce(top[:, :], logits[:, :, :], AX, ALU.max)
                    dve.drain()
                    dve.tensor_tensor(logits[:, :, :], logits[:, :, :],
                                                  top[:, :].unsqueeze(2).to_broadcast(wide), ALU.subtract).then_inc(c.exp_in.sem, 1)
                    dve.wait_ge(c.exp_ready.sem, c.exp_ready.at(b, 1))
                    dve.tensor_reduce(top[:, :], probs[:, :, :], AX, ALU.add)
                    dve.drain()
                    dve.reciprocal(top[:, :], top[:, :])
                    dve.drain()
                    dve.tensor_tensor(probs[:, :, :], probs[:, :, :], top[:, :].unsqueeze(2).to_broadcast(wide), ALU.mult)
                    dve.drain()
                    for i in range(2):
                        src = probs if i == 0 else left
                        dve.tensor_reduce(top[:, :], src[:, :, :], AX, ALU.max)
                        dve.drain()
                        dve.tensor_tensor(key[:, :, :], src[:, :, :], top[:, :].unsqueeze(2).to_broadcast(wide), ALU.is_equal)
                        dve.drain()
                        dve.tensor_tensor(key[:, :, :], key[:, :, :], rank[:, :, :], ALU.mult)
                        dve.drain()
                        dve.tensor_reduce(top[:, :], key[:, :, :], AX, ALU.max)
                        dve.drain()
                        dst = mask if i == 0 else pick
                        dve.tensor_tensor(dst[:, :, :], key[:, :, :], top[:, :].unsqueeze(2).to_broadcast(wide), ALU.is_equal)
                        dve.drain()
                        if i == 0:
                            dve.scalar_tensor_tensor(left[:, :, :], mask[:, :, :], -2.0, probs[:, :, :], ALU.mult, ALU.add)
                            dve.drain()
                    dve.tensor_tensor(mask[:, :, :], mask[:, :, :], pick[:, :, :], ALU.add)
                    dve.drain()
                    dve.tensor_tensor(mask[:, :, :], mask[:, :, :], probs[:, :, :], ALU.mult)
                    dve.drain()
                    dve.tensor_reduce(top[:, :], mask[:, :, :], AX, ALU.add)
                    dve.drain()
                    dve.tensor_scalar(top[:, :], top[:, :], 1e-9, None, ALU.add)
                    dve.drain()
                    dve.reciprocal(top[:, :], top[:, :])
                    dve.drain()
                    dve.tensor_tensor(gates[:, :, 0:E], mask[:, :, :],
                                                     top[:, :].unsqueeze(2).to_broadcast(wide), ALU.mult).then_inc(c.vec_ready.sem, 1)
                    dve.wait_ge(c.A.empty, c.A.copied(b, "mixed_b2"))
                    dve.tensor_tensor(c.r[:, :, :], mixed_b2[:, :, :], c.x[:, bass.ds(b * T, T), :], ALU.add)
                    dve.drain()
                    for e in range(E):
                        for i in range(2):
                            dve.wait_ge(c.V.full, c.V.filled(b, ("o", e, i)))
                            o = c.V.slot(("o", e, i))
                            for t in (2 * i, 2 * i + 1):
                                last = dve.scalar_tensor_tensor(c.r[:, t, :], o[:, (t - 2 * i) * D:(t - 2 * i + 1) * D],
                                                                gates[:, t, e:e + 1], c.r[:, t, :], ALU.mult, ALU.add)
                            last.then_inc(c.V.empty, 1)
                        dve.drain()
                    dve_norm(c, dve, b, 0, c.r, c.x[:, bass.ds(b * T, T), :])

            @block.scalar
            def _(act):
                with act.Fori(0, B) as b:
                    act_fetch_x(c, act, b)
                    act_transposed_x(c, act, b)
                    act.wait_ge(c.A.full, c.A.filled(b, "logits"))
                    src = c.A.slot("logits")
                    act.activation(logits[:, :, :].rearrange("p t e -> p (t e)"), src[:, 0:T * E], ACT.Copy).then_inc(c.A.empty, 1)
                    act.wait_ge(c.exp_in.sem, c.exp_in.at(b, 1))
                    act.activation(probs[:, :, :], logits[:, :, :], ACT.Exp, scale=0.2).then_inc(c.exp_ready.sem, 1)

                    def gelu(e):
                        for i in range(2):
                            act.wait_ge(c.A.full, c.A.filled(b, ("h", e, i)))
                            src = c.A.slot(("h", e, i))
                            for m in (2 * i, 2 * i + 1):
                                last = act.activation(hT[e % 2][:, m, :], src[:, (m - 2 * i) * S:(m - 2 * i + 1) * S],
                                                      ACT.Gelu, bias=b1[:, e * FT + m:e * FT + m + 1])
                            last.then_inc(c.A.empty, 1)

                    gelu(0)
                    act.wait_ge(c.A.full, c.A.filled(b, "gatesT"))
                    src = c.A.slot("gatesT")
                    act.activation(gatesT[:, :], src[:, 0:S], ACT.Copy).then_inc(c.A.empty, 1)
                    act.wait_ge(c.A.full, c.A.filled(b, "mixed_b2"))
                    src = c.A.slot("mixed_b2")
                    act.activation(mixed_b2[:, :, :].rearrange("p t d -> p (t d)"), src, ACT.Copy).then_inc(c.A.empty, 1)
                    for e in range(1, E):
                        gelu(e)

            @block.gpsimd
            def _(pool):
                with pool.Fori(0, B) as b:
                    pool_rstd(c, pool, b, 0)
        c.finish()



def layer_l1_attn(nc, c, ins):
    with ExitStack() as ctx:
        sb = allocator(nc, ctx, "l1_attn")
        wq, wk, wv = (sb(n, [P, KD, D]) for n in ("wq", "wk", "wv"))
        qT, kT, v = sb("qT", [P, KD, S]), sb("kT", [P, KD, S]), sb("v", [P, T, D])
        e, eT = sb("e", [P, T, S]), sb("eT", [P, T, S])
        nmax, rsum = sb("nmax", [P, T]), sb("rsum", [P, T])
        begin(c, A=6, V=6, O=0, x_here=1, var_ready=1, rstd_ready=1, exp_in=T, exp_ready=T)
        c.expect_setup(0)

        with nc.Block() as block:
            @block.sync
            def _(sp):
                for dst, name in ((wq, "wq3"), (wk, "wk3"), (wv, "wv3")):
                    c.load(sp, dst, ins[name])

            @block.tensor
            def _(pe):
                pe.wait_ge(c.loaded, c.load_count)
                with pe.Fori(0, B) as b:
                    pe_transpose_x(c, pe, b)
                    pe.wait_ge(c.A.empty, c.A.copied(b, "xT"))
                    for name, w in (("q", wq), ("k", wk)):
                        pe.wait_ge(c.A.empty, c.A.vacant(b, name))
                        out = c.A.slot(name)
                        for m in range(KD):
                            last = mm(pe, out[:, m * S:(m + 1) * S],
                                      [(w[:, k, m * P:(m + 1) * P], c.xT[:, k, :]) for k in range(KD)])
                        last.then_inc(c.A.full, 1)
                    pe.wait_ge(c.A.empty, c.A.vacant(b, "v"))
                    out = c.A.slot("v")
                    for t in range(T):
                        last = mm(pe, out[:, t * D:(t + 1) * D],
                                  [(c.xT[:, k, t * P:(t + 1) * P], wv[:, k, :]) for k in range(KD)])
                    last.then_inc(c.A.full, 1)
                    pe.wait_ge(c.A.empty, c.A.copied(b, "k"))
                    for t in range(T):
                        pe.wait_ge(c.V.empty, c.V.vacant(b, ("s", t)))
                        out = c.V.slot(("s", t))
                        mm(pe, out, [(kT[:, k, t * P:(t + 1) * P], qT[:, k, :]) for k in range(KD)]).then_inc(c.V.full, 1)
                    for i in range(2):
                        pe.wait_ge(c.A.empty, c.A.vacant(b, ("eT", i)))
                        out = c.A.slot(("eT", i))
                        if i == 0:
                            pe.wait_ge(c.exp_ready.sem, c.exp_ready.at(b, T))
                        for q in (2 * i, 2 * i + 1):
                            for t in range(T):
                                last = pe.transpose(out[:, (q - 2 * i) * S + t * P:(q - 2 * i) * S + (t + 1) * P],
                                                    e[:, t, q * P:(q + 1) * P], c.ident[:, :])
                        last.then_inc(c.A.full, 1)
                    pe.wait_ge(c.A.empty, c.A.copied(b, ("eT", 1)))
                    pe_project_out(c, pe, b, [lambda t, q=q: eT[:, q, t * P:(t + 1) * P] for q in range(T)],
                                   [v[:, q, :] for q in range(T)])

            @block.vector
            def _(dve):
                with dve.Fori(0, B) as b:
                    for t in range(T):
                        dve.wait_ge(c.V.full, c.V.filled(b, ("s", t)))
                        s = c.V.slot(("s", t))
                        dve.tensor_reduce(nmax[:, t:t + 1], s, AX, ALU.max)
                        dve.drain()
                        dve.tensor_scalar(e[:, t, :], s, nmax[:, t:t + 1], None, ALU.subtract).then_inc(c.V.empty, 1)
                        dve.drain().then_inc(c.exp_in.sem, 1)
                    for t in range(T):
                        dve.wait_ge(c.exp_ready.sem, c.exp_ready.at(b, t + 1))
                        dve.tensor_reduce(rsum[:, t:t + 1], e[:, t, :], AX, ALU.add)
                    dve.drain()
                    dve.reciprocal(rsum[:, :], rsum[:, :])
                    dve.drain()
                    for i in range(2):
                        dve.wait_ge(c.V.full, c.V.filled(b, ("y", i)))
                        y = c.V.slot(("y", i))
                        for t in (2 * i, 2 * i + 1):
                            last = dve.tensor_scalar(c.r[:, t, :], y[:, (t - 2 * i) * D:(t - 2 * i + 1) * D],
                                                     rsum[:, t:t + 1], None, ALU.mult)
                        last.then_inc(c.V.empty, 1)
                    dve.drain()
                    dve.tensor_tensor(c.r[:, :, :], c.r[:, :, :], c.x[:, bass.ds(b * T, T), :], ALU.add)
                    dve.drain()
                    dve_norm(c, dve, b, 0, c.r, c.x[:, bass.ds(b * T, T), :])

            @block.scalar
            def _(act):
                with act.Fori(0, B) as b:
                    act_fetch_x(c, act, b)
                    act_transposed_x(c, act, b)
                    for name, dst in (("q", qT), ("k", kT), ("v", v)):
                        act.wait_ge(c.A.full, c.A.filled(b, name))
                        src = c.A.slot(name)
                        act.activation(dst[:, :, :].rearrange("p a s -> p (a s)"), src, ACT.Copy).then_inc(c.A.empty, 1)
                    for t in range(T):
                        act.wait_ge(c.exp_in.sem, c.exp_in.at(b, t + 1))
                        act.activation(e[:, t, :], e[:, t, :], ACT.Exp, scale=1.0 / 16).then_inc(c.exp_ready.sem, 1)
                    for i in range(2):
                        act.wait_ge(c.A.full, c.A.filled(b, ("eT", i)))
                        src = c.A.slot(("eT", i))
                        act.activation(eT[:, 2 * i:2 * i + 2, :].rearrange("p a s -> p (a s)"), src, ACT.Copy).then_inc(c.A.empty, 1)

            @block.gpsimd
            def _(pool):
                with pool.Fori(0, B) as b:
                    pool_rstd(c, pool, b, 0)
        c.finish()



def layer_l1_xattn(nc, c, ins):
    with ExitStack() as ctx:
        sb = allocator(nc, ctx, "l1_xattn")
        lin, gate = sb("lin", [P, T, S]), sb("gate", [P, T, S])
        begin(c, A=4, V=2, O=0, x_here=1, ctx_here=1, var_ready=1, rstd_ready=1, vec_ready=2)

        with nc.Block() as block:
            @block.tensor
            def _(pe):
                with pe.Fori(0, B) as b:
                    pe_transpose_x(c, pe, b)
                    pe_transpose_ctx(c, pe, b)
                    pe.wait_ge(c.A.empty, c.A.copied(b, "cT"))
                    for i in range(2):
                        pe.wait_ge(c.A.empty, c.A.vacant(b, ("h", i)))
                        out = c.A.slot(("h", i))
                        for f in (2 * i, 2 * i + 1):
                            last = mm(pe, out[:, (f - 2 * i) * S:(f - 2 * i + 1) * S],
                                      [(c.cT[:, k, f * P:(f + 1) * P], c.xT[:, k, :]) for k in range(KD)])
                        last.then_inc(c.A.full, 1)
                    pe.wait_ge(c.vec_ready.sem, c.vec_ready.at(b, 2))
                    alone(c, pe)
                    pe_project_out(c, pe, b, [lambda t, f=f: gate[:, f, t * P:(t + 1) * P] for f in range(T)],
                                   [c.ctx[:, bass.ds(b * T + f, 1), :] for f in range(T)])

            @block.vector
            def _(dve):
                with dve.Fori(0, B) as b:
                    for i in range(2):
                        dve.wait_ge(c.A.empty, c.A.copied(b, ("h", i)))
                        sl = slice(2 * i, 2 * i + 2)
                        dve.tensor_tensor(gate[:, sl, :], gate[:, sl, :], lin[:, sl, :], ALU.mult).then_inc(c.vec_ready.sem, 1)
                    dve_residual_norm(c, dve, b)

            @block.scalar
            def _(act):
                with act.Fori(0, B) as b:
                    act_fetch_x(c, act, b)
                    act_fetch_ctx(c, act, b)
                    act_transposed_x(c, act, b)
                    act_transposed_ctx(c, act, b)
                    for i in range(2):
                        act.wait_ge(c.A.full, c.A.filled(b, ("h", i)))
                        src = c.A.slot(("h", i))
                        sl = slice(2 * i, 2 * i + 2)
                        act.activation(gate[:, sl, :].rearrange("p a s -> p (a s)"), src, ACT.Gelu)
                        act.activation(lin[:, sl, :].rearrange("p a s -> p (a s)"), src, ACT.Copy).then_inc(c.A.empty, 1)

            @block.gpsimd
            def _(pool):
                with pool.Fori(0, B) as b:
                    pool_rstd(c, pool, b, 0)
        c.finish()



def layer_l1_ffn(nc, c, ins):
    with ExitStack() as ctx:
        sb = allocator(nc, ctx, "l1_ffn")
        FT = 8
        w1, w2 = sb("w1", [P, KD, FT * P]), sb("w2", [P, FT, D])
        w1b, w2b = sb("w1b", [P, KD, FT * P]), sb("w2b", [P, FT, D])
        b1, b2 = sb("b1", [P, FT]), sb("b2", [1, D])
        shiftm, tokens, scale = sb("shiftm", [P, P]), sb("tokens", [P, 8]), sb("scale", [P, 1])
        before = sb("before", [P, D])
        outer1, outer2 = sb("outer1", [P, 4, D]), sb("outer2", [P, 4, 4, D // 4])
        hT = sb("hT", [P, FT, S])
        begin(c, A=6, V=10, O=0, x_here=1, var_ready=1, rstd_ready=1, vec_ready=2)
        c.expect_setup(0)

        with nc.Block() as block:
            @block.sync
            def _(sp):
                for dst, name in ((w1, "w1_5"), (w2, "w2_5"), (b1, "b1_5"), (b2, "b2_5"), (shiftm, "shift5"),
                                  (tokens, "tokens5"), (scale, "scale5")):
                    c.load(sp, dst, ins[name])

            @block.tensor
            def _(pe):
                pe.wait_ge(c.loaded, c.load_count)
                with pe.Fori(0, B) as b:
                    pe_transpose_x(c, pe, b)
                    pe.wait_ge(c.A.empty, c.A.vacant(b, "before"))
                    out = c.A.slot("before")
                    pe.matmul(out[:, 0:D], shiftm[:, :], c.xn[:, 0, :], start=True, stop=True).then_inc(c.A.full, 1)
                    pe.wait_ge(c.vec_ready.sem, c.vec_ready.at(b, 1))
                    for k in range(KD):
                        for i in range(2):
                            pe.wait_ge(c.V.empty, c.V.vacant(b, ("m1", k, i)))
                            out = c.V.slot(("m1", k, i))
                            pe.matmul(out, c.xn[:, 0, k * P:(k + 1) * P], outer1[:, 2 * i:2 * i + 2, :],
                                                 start=True, stop=True).then_inc(c.V.full, 1)
                    pe.wait_ge(c.vec_ready.sem, c.vec_ready.at(b, 2))
                    for r in range(4):
                        pe.wait_ge(c.V.empty, c.V.vacant(b, ("m2", r)))
                        out = c.V.slot(("m2", r))
                        for k in range(KD):
                            last = pe.matmul(out[:, k * D:(k + 1) * D], c.xn[:, 0, k * P:(k + 1) * P],
                                             outer2[:, r, :, :], start=True, stop=True)
                        last.then_inc(c.V.full, 1)
                    pe.wait_ge(c.A.empty, c.A.copied(b, "xT"))
                    pe.wait_ge(c.V.empty, c.V.copied(b, ("m1", 1, 1)))
                    for i in range(FT // 2):
                        pe.wait_ge(c.A.empty, c.A.vacant(b, ("h", i)))
                        out = c.A.slot(("h", i))
                        for m in (2 * i, 2 * i + 1):
                            last = mm(pe, out[:, (m - 2 * i) * S:(m - 2 * i + 1) * S],
                                      [(w1b[:, k, m * P:(m + 1) * P], c.xT[:, k, :]) for k in range(KD)])
                        last.then_inc(c.A.full, 1)
                    pe.wait_ge(c.A.empty, c.A.copied(b, ("h", FT // 2 - 1)))
                    pe.wait_ge(c.V.empty, c.V.copied(b, ("m2", 3)))
                    pe_project_out(c, pe, b, [lambda t, f=f: hT[:, f, t * P:(t + 1) * P] for f in range(FT)],
                                   [w2b[:, f, :] for f in range(FT)], [b2[0:1, :]])

            @block.vector
            def _(dve):
                dve.wait_ge(c.loaded, c.load_count)
                dve.tensor_scalar(tokens[:, :], tokens[:, :], scale[:, 0:1], None, ALU.mult)
                dve.drain()
                with dve.Fori(0, B) as b:
                    dve.wait_ge(c.A.empty, c.A.copied(b, "before"))
                    for a in range(4):
                        last = dve.tensor_scalar(outer1[:, a, :], before[:, :], tokens[:, a:a + 1], None, ALU.mult)
                    last.then_inc(c.vec_ready.sem, 1)
                    for a in range(4):
                        last = dve.tensor_scalar(outer2[:, :, a, :], before[:, :].rearrange("p (o r) -> p r o", r=4),
                                                 tokens[:, 4 + a:5 + a], None, ALU.mult)
                    last.then_inc(c.vec_ready.sem, 1)
                    for k in range(KD):
                        for i in range(2):
                            dve.wait_ge(c.V.full, c.V.filled(b, ("m1", k, i)))
                            m = c.V.slot(("m1", k, i))
                            dve.tensor_tensor(w1b[:, k, i * S:(i + 1) * S], m, w1[:, k, i * S:(i + 1) * S], ALU.add).then_inc(c.V.empty, 1)
                    for r in range(4):
                        dve.wait_ge(c.V.full, c.V.filled(b, ("m2", r)))
                        m = c.V.slot(("m2", r)).rearrange("p (k d) -> p k d", d=D)
                        dve.tensor_tensor(w2b[:, 2 * r:2 * r + 2, :], m, w2[:, 2 * r:2 * r + 2, :], ALU.add).then_inc(c.V.empty, 1)
                    dve_residual_norm(c, dve, b)

            @block.scalar
            def _(act):
                with act.Fori(0, B) as b:
                    act_fetch_x(c, act, b)
                    act_transposed_x(c, act, b)
                    act.wait_ge(c.A.full, c.A.filled(b, "before"))
                    src = c.A.slot("before")
                    act.activation(before[:, :], src[:, 0:D], ACT.Copy).then_inc(c.A.empty, 1)
                    for i in range(FT // 2):
                        act.wait_ge(c.A.full, c.A.filled(b, ("h", i)))
                        src = c.A.slot(("h", i))
                        for m in (2 * i, 2 * i + 1):
                            last = act.activation(hT[:, m, :], src[:, (m - 2 * i) * S:(m - 2 * i + 1) * S], ACT.Gelu,
                                                  bias=b1[:, m:m + 1])
                        last.then_inc(c.A.empty, 1)

            @block.gpsimd
            def _(pool):
                with pool.Fori(0, B) as b:
                    pool_rstd(c, pool, b, 0)
        c.finish()



def layer_l2_attn(nc, c, ins):
    with ExitStack() as ctx:
        sb = allocator(nc, ctx, "l2_attn")
        wq, wk = sb("wq", [P, KD, NG * P]), sb("wk", [P, KD, NG * P])
        wv, wo, wn = sb("wv", [P, KD, D]), sb("wo", [P, KD, D]), sb("wn", [P, KD, H])
        qbias, kbias = sb("qbias", [P, NG]), sb("kbias", [P, NG])
        vbias, obias, nbias = sb("vbias", [1, D]), sb("obias", [1, D]), sb("nbias", [1, H])
        qT, kT = sb("qT", [P, NG, S]), sb("kT", [P, NG, S])
        oT, expn = sb("oT", [P, KD, S]), sb("expn", [P, T, H])
        c.causal01 = sb("causal01", [P, S])
        alloc_attention(c, sb, S + OFF_LEN, 16, T, D, False)
        c.per_o = 4
        begin(c, A=1 + 4 + 2 + H + 1, V=H + 2, O=NG, x_here=1, var_ready=1, rstd_ready=1, heads_ready=NG)
        c.expect_setup(0)

        with nc.Block() as block:
            @block.sync
            def _(sp):
                for dst, name in ((wq, "wq6"), (wk, "wk6"), (wv, "wv6"), (wo, "wo6"), (wn, "wn6"), (qbias, "qbias6"),
                                  (kbias, "kbias6"), (vbias, "vbias6"), (obias, "obias6"), (nbias, "nbias6"),
                                  (c.causal01, "causal01")):
                    c.load(sp, dst, ins[name])

            @block.tensor
            def _(pe):
                pe.wait_ge(c.loaded, c.load_count)
                with pe.Fori(0, B) as b:
                    pe_transpose_x(c, pe, b)
                    pe.wait_ge(c.A.empty, c.A.copied(b, "xT"))
                    for name, w in (("q", wq), ("k", wk)):
                        for i in range(2):
                            pe.wait_ge(c.A.empty, c.A.vacant(b, (name, i)))
                            out = c.A.slot((name, i))
                            for g in (2 * i, 2 * i + 1):
                                last = mm(pe, out[:, (g - 2 * i) * S:(g - 2 * i + 1) * S],
                                          [(w[:, k, g * P:(g + 1) * P], c.xT[:, k, :]) for k in range(KD)])
                            last.then_inc(c.A.full, 1)
                    for name, w, bias, n in (("v", wv, vbias, D), ("n", wn, nbias, H)):
                        pe.wait_ge(c.A.empty, c.A.vacant(b, name))
                        out = c.A.slot(name)
                        for t in range(T):
                            last = mm(pe, out[:, t * n:(t + 1) * n],
                                      [(c.xT[:, k, t * P:(t + 1) * P], w[:, k, :]) for k in range(KD)]
                                      + [(c.ones[0:1, 0:P], bias[0:1, :])])
                        last.then_inc(c.A.full, 1)
                    for h in range(H + 1):
                        if h < H:
                            if h == 0:
                                pe.wait_ge(c.A.empty, c.A.copied(b, ("k", 1)))
                            pe_causal_scores(c, pe, b, h, head16(kT, h), head16(qT, h), c.V, False)
                        if h:
                            pe_values(c, pe, b, h - 1, c.e[(h - 1) % 2], c.v, 16, True,
                                      [(c.V, ("d", h - 1)), (c.A, ("o", h - 1))])
                    pe_transpose_attn(c, pe, b, c.on, D)
                    pe.wait_ge(c.A.empty, c.A.copied(b, ("oT", 0)))
                    pe_project_out(c, pe, b, [lambda t, k=k: oT[:, k, t * P:(t + 1) * P] for k in range(KD)],
                                   [wo[:, k, :] for k in range(KD)], [obias[0:1, :]])

            @block.vector
            def _(dve):
                with dve.Fori(0, B) as b:
                    for h in range(H):
                        dve.wait_ge(c.V.full, c.V.filled(b, ("d", h)))
                        d = c.V.slot(("d", h))
                        dve.tensor_tensor(c.e[h % 2][:, 0:S], d, c.causal01[:, :], ALU.mult).then_inc(c.V.empty, 1)
                        if h == 0:
                            dve.wait_ge(c.A.empty, c.A.copied(b, "n"))
                        if h % 4 == 0 and h:
                            dve_heads_out(c, dve, b, h // 4 - 1, 16, 16, given=expn)
                    dve_heads_out(c, dve, b, 3, 16, 16, given=expn)
                    dve_residual_norm(c, dve, b)

            @block.scalar
            def _(act):
                act.wait_ge(c.loaded, c.load_count)
                with act.Fori(0, B) as b:
                    act_fetch_x(c, act, b)
                    act_transposed_x(c, act, b)
                    for name, dst, bias in (("q", qT, qbias), ("k", kT, kbias)):
                        for i in range(2):
                            act.wait_ge(c.A.full, c.A.filled(b, (name, i)))
                            src = c.A.slot((name, i))
                            for g in (2 * i, 2 * i + 1):
                                last = act.activation(dst[:, g, :], src[:, (g - 2 * i) * S:(g - 2 * i + 1) * S],
                                                      ACT.Identity, bias=bias[:, g:g + 1])
                            last.then_inc(c.A.empty, 1)
                    act.wait_ge(c.A.full, c.A.filled(b, "v"))
                    src = c.A.slot("v")
                    act.activation(c.v[:, :, :, :].rearrange("p t h d -> p (t h d)"), src, ACT.Copy).then_inc(c.A.empty, 1)
                    act.wait_ge(c.A.full, c.A.filled(b, "n"))
                    src = c.A.slot("n")
                    act.activation(expn[:, :, :].rearrange("p t h -> p (t h)"), src[:, 0:T * H], ACT.Exp, scale=-1.0).then_inc(c.A.empty, 1)
                    for h in range(H):
                        act.wait_ge(c.A.full, c.A.filled(b, ("o", h)))
                        src = c.A.slot(("o", h))
                        act.activation(c.e[h % 2][:, S:S + OFF_LEN], src[:, 0:OFF_LEN], ACT.Copy).then_inc(c.A.empty, 1)
                    act_transposed_attn(c, act, b, oT, D)

            @block.gpsimd
            def _(pool):
                with pool.Fori(0, B) as b:
                    pool_rstd(c, pool, b, 0)
        c.finish()



KT2 = 2 * T
HD = 64
INNER = H * HD


def layer_l2_xattn(nc, c, ins):
    with ExitStack() as ctx:
        sb = allocator(nc, ctx, "l2_xattn")
        IT = INNER // P
        QUADS, QT = 4, 2
        wq, wk, wv = (sb(n, [P, KD, INNER]) for n in ("wq", "wk", "wv"))
        wo = sb("wo", [P, IT, D])
        gain, shiftc = sb("gain", [P, 2, KD]), sb("shiftc", [P, 2, KD])
        mask_col8 = sb("mask_col8", [P, B * T], mybir.dt.uint8)
        hide_row, hide_col = sb("hide_row", [1, B * S], BF16), sb("hide_col", [P, B * T])
        hide = sb("hide", [P, T])
        ones16 = sb("ones16", [1, P], BF16)
        qT = sb("qT", [P, 2, QT, S])
        kT = sb("kT", [P, 2, QT, 2 * S])
        alloc_attention(c, sb, KT2 * S, HD + 1, KT2, INNER, True, k=64)
        mask_row8 = c.e[0][0:1, 0:B * S // 4].bitcast(mybir.dt.uint8)
        shifts = [c.shift, sb("shift_b", [P, S], BF16)]
        c.mraw = sb("mraw", [P, T, H, 2])
        c.per_o = 1
        oT = kT[:, :, :, :].rearrange("p u q s -> p (u q s)").rearrange("p (m s) -> p m s", s=S)
        begin(c, A=KD + QUADS * (1 + QT + 1) + KT2 + H * KT2 // 2 + IT // 2, V=2 + H * T * 2 + 2, O=H,
              ctx_here=1, x_here=1, var_ready=3, rstd_ready=3, heads_ready=H, parts_ready=QUADS)
        c.expect_setup(1)
        slot = lambda h: h // 4 % 2
        qh = lambda h: qT[64 * (h % 2):64 * (h % 2) + 64, slot(h), h % 4 // 2, :]
        kh = lambda h: kT[64 * (h % 2):64 * (h % 2) + 64, slot(h), h % 4 // 2, :]
        c.shifth = lambda h: shifts[slot(h)][64 * (h % 2):64 * (h % 2) + 64, :]

        with nc.Block() as block:
            @block.sync
            def _(sp):
                for dst, name in ((mask_row8, "mask_row7"), (mask_col8, "mask_col7"), (gain, "gain7"), (shiftc, "shift7"),
                                  (c.sel, "sel64"), (wq, "wq7"), (wk, "wk7"), (wv, "wv7"), (wo, "wo7")):
                    c.load(sp, dst, ins[name])

            @block.tensor
            def _(pe):
                pe.wait_ge(c.loaded, c.load_count)
                pe.wait_ge(c.setup_done, c.setup_dones)
                with pe.Fori(0, B) as b:
                    for k in range(KD):
                        pe.wait_ge(c.V.empty, c.V.vacant(b, ("zx", k)))
                        out = c.V.slot(("zx", k))
                        pe.wait_ge(c.x_here.sem, c.x_here.at(b, 1))
                        for t in range(T):
                            last = pe.transpose(out[:, t * P:(t + 1) * P], c.xn[:, t, k * P:(k + 1) * P], c.ident[:, :])
                        last.then_inc(c.V.full, 1)
                    for k in range(KD):
                        pe.wait_ge(c.A.empty, c.A.vacant(b, ("zc", k)))
                        out = c.A.slot(("zc", k))
                        pe.wait_ge(c.ctx_here.sem, c.ctx_here.at(b, 1))
                        for t in range(T):
                            last = pe.transpose(out[:, t * P:(t + 1) * P], c.ctxn[:, t, k * P:(k + 1) * P], c.ident[:, :])
                        last.then_inc(c.A.full, 1)

                    def quad(g):
                        pe.wait_ge(c.A.empty, c.A.vacant(b, ("q", g)))
                        out = c.A.slot(("q", g))
                        for m in range(QT):
                            cols = slice((g * QT + m) * P, (g * QT + m + 1) * P)
                            last = mm(pe, out[:, m * S:(m + 1) * S], [(wq[:, k, cols], c.xT[:, k, :]) for k in range(KD)])
                        last.then_inc(c.A.full, 1)
                        for m in range(QT):
                            cols = slice((g * QT + m) * P, (g * QT + m + 1) * P)
                            pe.wait_ge(c.A.empty, c.A.vacant(b, ("k", g, m)))
                            out = c.A.slot(("k", g, m))
                            for half, zT in ((0, c.cT), (1, c.xT)):
                                last = mm(pe, out[:, half * S:(half + 1) * S], [(wk[:, k, cols], zT[:, k, :]) for k in range(KD)])
                            last.then_inc(c.A.full, 1)
                        pe.wait_ge(c.A.empty, c.A.copied(b, ("k", g, QT - 1)))
                        for h in range(4 * g, 4 * g + 4):
                            for qt in range(T):
                                pe_max_scores(c, pe, b, h, qt, kh(h), qh(h),
                                              [(0, 0, S, (ones16[0:1, :], hide_row[0:1, bass.ds(b * S, S)]))], True)
                                pe_max_scores(c, pe, b, h, qt, kh(h), qh(h), [(0, S, S, None)])
                        pe.wait_ge(c.A.empty, c.A.vacant(b, ("shift", g)))
                        out = c.A.slot(("shift", g))
                        pe.wait_ge(c.parts_ready.sem, c.parts_ready.at(b, g + 1))
                        for t in range(T):
                            last = pe.transpose(out[:, t * P:(t + 1) * P], c.parts[:, t, :], c.ident[:, :])
                        last.then_inc(c.A.full, 1)

                    pe.wait_ge(c.A.empty, c.A.copied(b, ("zc", 1)))
                    pe.wait_ge(c.V.empty, c.V.copied(b, ("zx", 1)))
                    for kt in range(KT2):
                        pe.wait_ge(c.A.empty, c.A.vacant(b, ("v", kt)))
                        out = c.A.slot(("v", kt))
                        zT = c.cT if kt < T else c.xT
                        for i in range(2):
                            last = mm(pe, out[:, i * S:(i + 1) * S],
                                      [(zT[:, k, kt % T * P:(kt % T + 1) * P], wv[:, k, i * S:(i + 1) * S]) for k in range(KD)])
                        last.then_inc(c.A.full, 1)
                    quad(0)
                    for h in range(H + 1):
                        if h < H:
                            if h % 4 == 0:
                                if h + 4 < H:
                                    quad(h // 4 + 1)
                                pe.wait_ge(c.A.empty, c.A.copied(b, ("shift", h // 4)))
                            pe_scores(c, pe, b, h, kh(h), qh(h), KT2)
                        if h:
                            pe_values(c, pe, b, h - 1, c.e[(h - 1) % 2], c.v, HD + 1, False,
                                      [(c.A, ("s", h - 1, KT2 // 2 - 1))])
                    pe_transpose_attn(c, pe, b, c.on, INNER)
                    pe.wait_ge(c.A.empty, c.A.copied(b, ("oT", IT // 2 - 1)))
                    pe_project_out(c, pe, b, [lambda t, m=m: oT[:, m, t * P:(t + 1) * P] for m in range(IT)],
                                   [wo[:, m, :] for m in range(IT)])

            @block.vector
            def _(dve):
                dve.wait_ge(c.loaded, c.load_count)
                dve.tensor_scalar(hide_row[:, :], mask_row8[:, :], 1.0, 1e30, ALU.subtract, ALU.mult)
                dve.tensor_scalar(hide_col[:, :], mask_col8[:, :], 1.0, 1e30, ALU.subtract, ALU.mult)
                dve.memset(ones16[:, :], 1.0)
                dve.memset(c.parts[:, :, :], 0.0)
                dve.memset(c.mraw[:, :, :, :], 0.0)
                dve.memset(c.v[:, :, :, HD:HD + 1], 1.0)
                dve.drain().then_inc(c.setup_done, 1)
                with dve.Fori(0, B) as b:
                    here = bass.ds(b * T, T)
                    dve_norm(c, dve, b, 0, c.x[:, here, :], c.xn).then_inc(c.x_here.sem, 1)
                    dve_norm(c, dve, b, 1, c.ctx[:, here, :], c.ctxn).then_inc(c.ctx_here.sem, 1)
                    for k in range(KD):
                        dve.wait_ge(c.V.full, c.V.filled(b, ("zx", k)))
                        src = c.V.slot(("zx", k))
                        dve.tensor_scalar(c.xT[:, k, :], src, gain[:, 1, k:k + 1], shiftc[:, 1, k:k + 1],
                                                      ALU.mult, ALU.add).then_inc(c.V.empty, 1)
                    for g in range(QUADS + 1):
                        if g < QUADS:
                            for h in range(4 * g, 4 * g + 4):
                                for qt in range(T):
                                    for j in range(2):
                                        dve.wait_ge(c.V.full, c.V.filled(b, ("m", h, qt, j * S)))
                                        s = c.V.slot(("m", h, qt, j * S))
                                        dve.tensor_reduce(c.mraw[:, qt, h, j:j + 1], s, AX, ALU.max).then_inc(c.V.empty, 1)
                            dve.drain()
                            dve_shift_parts(c, dve)
                        if g:
                            for h in range(4 * g - 5 if g > 1 else 0, 4 * g - 1 if g < QUADS else H):
                                dve_heads_out(c, dve, b, h, HD, HD + 1)
                    dve_residual_norm(c, dve, b, 2)

            @block.scalar
            def _(act):
                act.wait_ge(c.loaded, c.load_count)
                act.wait_ge(c.setup_done, c.setup_dones)
                with act.Fori(0, B) as b:
                    alone(c, act)
                    act.activation(hide[:, :], hide_col[:, bass.ds(b * T, T)], ACT.Copy)
                    for k in range(KD):
                        act.wait_ge(c.A.full, c.A.filled(b, ("zc", k)))
                        src = c.A.slot(("zc", k))
                        act.activation(c.cT[:, k, :], src[:, 0:S], ACT.Identity,
                                                   bias=shiftc[:, 0, k:k + 1], scale=gain[:, 0, k:k + 1]).then_inc(c.A.empty, 1)
                    act.drain()
                    for kt in range(KT2):
                        act.wait_ge(c.A.full, c.A.filled(b, ("v", kt)))
                        src = c.A.slot(("v", kt)).rearrange("p (h d) -> p h d", d=HD)
                        act.activation(c.v[:, kt, :, 0:HD], src, ACT.Copy).then_inc(c.A.empty, 1)

                    def quad(g):
                        act.wait_ge(c.A.full, c.A.filled(b, ("q", g)))
                        src = c.A.slot(("q", g))
                        act.activation(qT[:, g % 2, :, :].rearrange("p m s -> p (m s)"), src, ACT.Copy).then_inc(c.A.empty, 1)
                        for m in range(QT):
                            act.wait_ge(c.A.full, c.A.filled(b, ("k", g, m)))
                            src = c.A.slot(("k", g, m))
                            act.activation(kT[:, g % 2, m, :], src, ACT.Copy).then_inc(c.A.empty, 1)
                        act.wait_ge(c.A.full, c.A.filled(b, ("shift", g)))
                        src = c.A.slot(("shift", g))
                        act.activation(shifts[g % 2][:, :], src[:, 0:S], ACT.Copy).then_inc(c.A.empty, 1)

                    quad(0)
                    for h in range(H):
                        if h % 4 == 0 and h + 4 < H:
                            quad(h // 4 + 1)
                        for j in range(KT2 // 2):
                            act.wait_ge(c.A.full, c.A.filled(b, ("s", h, j)))
                            src = c.A.slot(("s", h, j))
                            e = c.e[h % 2]
                            if j < T // 2:
                                for kt in (2 * j, 2 * j + 1):
                                    last = act.activation(e[:, kt * S:(kt + 1) * S], src[:, (kt - 2 * j) * S:(kt - 2 * j + 1) * S],
                                                          ACT.Exp, bias=hide[:, kt:kt + 1], scale=HD ** -0.5)
                            else:
                                last = act.activation(e[:, 2 * j * S:2 * (j + 1) * S], src, ACT.Exp, scale=HD ** -0.5)
                            last.then_inc(c.A.empty, 1)
                    act_transposed_attn(c, act, b, oT, INNER)

            @block.gpsimd
            def _(pool):
                with pool.Fori(0, B) as b:
                    for j in range(3):
                        pool_rstd(c, pool, b, j)
        c.finish()



def dve_scales(c, dve, peak, scale, inv):
    dve.tensor_scalar(scale, peak, 1e-6, 1.0 / 127.0, ALU.max, ALU.mult)
    dve.drain()
    dve.reciprocal(inv, scale)
    dve.drain()


def layer_l2_ffn(nc, c, ins):
    with ExitStack() as ctx:
        sb = allocator(nc, ctx, "l2_ffn")
        FT = 8
        w1, w2 = sb("w1", [P, KD, FT * P]), sb("w2", [P, FT, D])
        w1q, w2q = sb("w1q", [P, KD, FT * P], BF16), sb("w2q", [P, FT, D], BF16)
        b1, b1s, b2 = sb("b1", [P, FT]), sb("b1s", [P, FT]), sb("b2", [1, D])
        peak, peaks = sb("peak", [P, 4]), sb("peaks", [P, 4])
        scale, inv = sb("scale", [P, 4]), sb("inv", [P, 4])
        out1, out2 = sb("out1", [P, 1]), sb("out2", [P, 1])
        magic = sb("magic", [P, 1])
        xr, xq = sb("xr", [P, KD, S]), sb("xq", [P, KD, S], BF16)
        h = sb("h", [P, B, FT, S])
        hbatch = sb("hbatch", [P, 1])
        hr, hq = sb("hr", [P, FT, S]), sb("hq", [P, FT, S], BF16)
        with nc.Block() as block:
            c.expect_setup(3)
            first = c.setup_dones

            @block.sync
            def _(sp):
                for dst, name in ((w1, "w1_8"), (w2, "w2_8"), (b1, "b1_8"), (b2, "b2_8")):
                    c.load(sp, dst, ins[name])

            @block.vector
            def _(dve):
                dve.wait_ge(c.loaded, c.load_count)
                dve.memset(magic[:, :], MAGIC)
                dve.memset(peak[:, :], 0.0)
                dve.drain()
                for i, src in enumerate((c.x, w1, w2)):
                    dve.tensor_reduce(peak[:, i:i + 1], src[:, :, :], mybir.AxisListType.XY, ALU.max,
                                      apply_absolute_value=True)
                dve.drain().then_inc(c.setup_done, 1)
                dve.wait_ge(c.setup_done, first - 1)
                dve_scales(c, dve, peaks[:, 0:3], scale[:, 0:3], inv[:, 0:3])
                dve.tensor_tensor(out1[:, :], scale[:, 0:1], scale[:, 1:2], ALU.mult)
                dve.drain()
                dve.tensor_scalar(b1s[:, :], b1[:, :], out1[:, 0:1], None, ALU.mult)
                for w, wq, i in ((w1, w1q, 1), (w2, w2q, 2)):
                    dve.tensor_scalar(w[:, :, :], w[:, :, :], inv[:, i:i + 1], MAGIC, ALU.mult, ALU.add)
                    dve.drain()
                    dve.tensor_scalar(wq[:, :, :], w[:, :, :], MAGIC, None, ALU.subtract)
                dve.drain().then_inc(c.setup_done, 1)

            @block.gpsimd
            def _(pool):
                pool.wait_ge(c.setup_done, first - 2)
                pool.partition_all_reduce(peaks[:, 0:3], peak[:, 0:3], P, RMAX).then_inc(c.setup_done, 1)

        begin(c, A=2 + FT // 2, V=0, O=0, x_here=1, vec_ready=1)
        with nc.Block() as block:
            @block.tensor
            def _(pe):
                with pe.Fori(0, B) as b:
                    pe_transpose_x_halves(c, pe, b)
                    pe.wait_ge(c.vec_ready.sem, c.vec_ready.at(b, 1))
                    for i in range(FT // 2):
                        pe.wait_ge(c.A.empty, c.A.vacant(b, ("h", i)))
                        out = c.A.slot(("h", i))
                        for m in (2 * i, 2 * i + 1):
                            last = mm(pe, out[:, (m - 2 * i) * S:(m - 2 * i + 1) * S],
                                      [(w1q[:, k, m * P:(m + 1) * P], xq[:, k, :]) for k in range(KD)])
                        last.then_inc(c.A.full, 1)

            @block.scalar
            def _(act):
                with act.Fori(0, B) as b:
                    act_fetch_x(c, act, b)
                    for k in range(KD):
                        act.wait_ge(c.A.full, c.A.filled(b, ("xT", k)))
                        src = c.A.slot(("xT", k))[:, 0:S]
                        act.activation(xr[:, k, :], src, ACT.Identity, bias=magic[:, 0:1], scale=inv[:, 0:1]).then_inc(c.A.empty, 1)
                    for i in range(FT // 2):
                        act.wait_ge(c.A.full, c.A.filled(b, ("h", i)))
                        src = c.A.slot(("h", i))
                        for m in (2 * i, 2 * i + 1):
                            alone(c, act)
                            last = act.activation(h[:, bass.ds(b, 1), m, :], src[:, (m - 2 * i) * S:(m - 2 * i + 1) * S],
                                                  ACT.Gelu, bias=b1s[:, m:m + 1], scale=out1[:, 0:1])
                        last.then_inc(c.A.empty, 1)

            @block.vector
            def _(dve):
                with dve.Fori(0, B) as b:
                    dve.wait_ge(c.A.empty, c.A.copied(b, ("xT", KD - 1)))
                    dve.tensor_scalar(xq[:, :, :], xr[:, :, :], MAGIC, None, ALU.subtract).then_inc(c.vec_ready.sem, 1)
                    dve.wait_ge(c.A.empty, c.A.copied(b, ("h", FT // 2 - 1)))
                    alone(c, dve)
                    dve.tensor_reduce(hbatch[:, :], h[:, bass.ds(b, 1), :, :], mybir.AxisListType.XYZ, ALU.max,
                                      apply_absolute_value=True)
                    dve.drain()
                    dve.tensor_tensor(peak[:, 3:4], peak[:, 3:4], hbatch[:, :], ALU.max)
                    dve.drain()
        c.finish()

        with nc.Block() as block:
            c.expect_setup(2)
            second = c.setup_dones

            @block.gpsimd
            def _(pool):
                pool.partition_all_reduce(peaks[:, 3:4], peak[:, 3:4], P, RMAX).then_inc(c.setup_done, 1)

            @block.vector
            def _(dve):
                dve.wait_ge(c.setup_done, second - 1)
                dve_scales(c, dve, peaks[:, 3:4], scale[:, 3:4], inv[:, 3:4])
                dve.tensor_tensor(out2[:, :], scale[:, 2:3], scale[:, 3:4], ALU.mult)
                dve.drain().then_inc(c.setup_done, 1)

        begin(c, A=0, V=2, O=0, var_ready=1, rstd_ready=1, exp_in=1, vec_ready=1)
        with nc.Block() as block:
            @block.tensor
            def _(pe):
                with pe.Fori(0, B) as b:
                    pe.wait_ge(c.vec_ready.sem, c.vec_ready.at(b, 1))
                    pe_project_out(c, pe, b, [lambda t, f=f: hq[:, f, t * P:(t + 1) * P] for f in range(FT)],
                                   [w2q[:, f, :] for f in range(FT)], [b2[0:1, :]])

            @block.scalar
            def _(act):
                with act.Fori(0, B) as b:
                    alone(c, act)
                    act.activation(hr[:, :, :].rearrange("p f s -> p (f s)"),
                                   h[:, bass.ds(b, 1), :, :].rearrange("p b f s -> p (b f s)"), ACT.Identity,
                                   bias=magic[:, 0:1], scale=inv[:, 3:4]).then_inc(c.exp_in.sem, 1)
                    act.wait_ge(c.vec_ready.sem, c.vec_ready.at(b, 1))

            @block.vector
            def _(dve):
                with dve.Fori(0, B) as b:
                    dve.wait_ge(c.exp_in.sem, c.exp_in.at(b, 1))
                    dve.tensor_scalar(hq[:, :, :], hr[:, :, :], MAGIC, None, ALU.subtract).then_inc(c.vec_ready.sem, 1)
                    for i in range(2):
                        dve.wait_ge(c.V.full, c.V.filled(b, ("y", i)))
                        y = c.V.slot(("y", i))
                        last = dve.tensor_scalar(c.r[:, 2 * i:2 * i + 2, :].rearrange("p t d -> p (t d)"), y,
                                                 out2[:, 0:1], None, ALU.mult)
                        last.then_inc(c.V.empty, 1)
                    dve.drain()
                    dve.tensor_tensor(c.r[:, :, :], c.r[:, :, :], c.x[:, bass.ds(b * T, T), :], ALU.add)
                    dve.drain()
                    dve_norm(c, dve, b, 0, c.r, c.x[:, bass.ds(b * T, T), :])

            @block.gpsimd
            def _(pool):
                with pool.Fori(0, B) as b:
                    pool_rstd(c, pool, b, 0)
        c.finish()



def layer_l3_attn(nc, c, ins):
    with ExitStack() as ctx:
        sb = allocator(nc, ctx, "l3_attn")
        wq, wk = sb("wq", [P, KD, NG * P]), sb("wk", [P, KD, NG * P])
        wv, wo = sb("wv", [P, KD, D]), sb("wo", [P, KD, D])
        rope = sb("rope", [P, S])
        qT, kT = sb("qT", [P, NG, S]), sb("kT", [P, NG, S])
        oT = sb("oT", [P, KD, S])
        alloc_attention(c, sb, T * S, 17, T, D, True)
        c.mraw = sb("mraw", [P, T, H, 1])
        c.per_o = 4
        begin(c, A=1 + 1 + 1 + 2 * H + 1, V=2 * NG + H * T + 2, O=NG,
              x_here=1, var_ready=1, rstd_ready=1, heads_ready=NG, parts_ready=1)
        c.expect_setup(1)

        with nc.Block() as block:
            @block.sync
            def _(sp):
                for dst, name in ((wq, "wq9"), (wk, "wk9"), (wv, "wv9"), (wo, "wo9"), (rope, "rope9"), (c.sel, "sel32")):
                    c.load(sp, dst, ins[name])

            @block.tensor
            def _(pe):
                pe.wait_ge(c.loaded, c.load_count)
                pe.wait_ge(c.setup_done, c.setup_dones)
                with pe.Fori(0, B) as b:
                    pe_transpose_x(c, pe, b)
                    pe.wait_ge(c.A.empty, c.A.copied(b, "xT"))
                    for name, w in (("q", wq), ("k", wk)):
                        for g in range(NG):
                            pe.wait_ge(c.V.empty, c.V.vacant(b, (name, g)))
                            out = c.V.slot((name, g))
                            mm(pe, out, [(w[:, k, g * P:(g + 1) * P], c.xT[:, k, :]) for k in range(KD)]).then_inc(c.V.full, 1)
                    pe.wait_ge(c.A.empty, c.A.vacant(b, "v"))
                    out = c.A.slot("v")
                    for t in range(T):
                        last = mm(pe, out[:, t * D:(t + 1) * D],
                                  [(c.xT[:, k, t * P:(t + 1) * P], wv[:, k, :]) for k in range(KD)])
                    last.then_inc(c.A.full, 1)
                    pe.wait_ge(c.V.empty, c.V.copied(b, ("k", NG - 1)))
                    for h in range(H):
                        for qt in range(T):
                            pe_max_scores(c, pe, b, h, qt, head16(kT, h), head16(qT, h), [(0, 0, S, None)])
                    pe_transpose_shift(c, pe, b)
                    pe.wait_ge(c.A.empty, c.A.copied(b, "shift"))
                    for h in range(H + 1):
                        if h < H:
                            pe_scores(c, pe, b, h, head16(kT, h), head16(qT, h), T)
                        if h:
                            pe_values(c, pe, b, h - 1, c.e[(h - 1) % 2], c.v, 17, False, [(c.A, ("s", h - 1, 1))])
                    pe_transpose_attn(c, pe, b, c.on, D)
                    pe.wait_ge(c.A.empty, c.A.copied(b, ("oT", 0)))
                    pe_project_out(c, pe, b, [lambda t, k=k: oT[:, k, t * P:(t + 1) * P] for k in range(KD)],
                                   [wo[:, k, :] for k in range(KD)])

            @block.vector
            def _(dve):
                dve.wait_ge(c.loaded, c.load_count)
                dve.memset(c.parts[:, :, :], 0.0)
                dve.memset(c.v[:, :, :, 16:17], 1.0)
                dve.drain().then_inc(c.setup_done, 1)
                with dve.Fori(0, B) as b:
                    for name, dst in (("q", qT), ("k", kT)):
                        for g in range(NG):
                            dve.wait_ge(c.V.full, c.V.filled(b, (name, g)))
                            src = c.V.slot((name, g))
                            dve.tensor_tensor(dst[:, g, :], src, rope[:, :], ALU.mult).then_inc(c.V.empty, 1)
                    for h in range(H):
                        for qt in range(T):
                            dve.wait_ge(c.V.full, c.V.filled(b, ("m", h, qt, 0)))
                            s = c.V.slot(("m", h, qt, 0))
                            dve.tensor_reduce(c.mraw[:, qt, h, :], s, AX, ALU.max).then_inc(c.V.empty, 1)
                    dve.drain()
                    dve_shift_parts(c, dve)
                    for g in range(NG):
                        dve_heads_out(c, dve, b, g, 16, 17)
                    dve_residual_norm(c, dve, b)

            @block.scalar
            def _(act):
                with act.Fori(0, B) as b:
                    act_fetch_x(c, act, b)
                    act_transposed_x(c, act, b)
                    act.wait_ge(c.A.full, c.A.filled(b, "v"))
                    src = c.A.slot("v")
                    act.activation(c.v[:, :, :, 0:16].rearrange("p t h d -> p (t h) d"),
                                               src.rearrange("p (a d) -> p a d", d=16), ACT.Copy).then_inc(c.A.empty, 1)
                    act_transposed_shift(c, act, b)
                    for h in range(H):
                        for j in range(2):
                            act.wait_ge(c.A.full, c.A.filled(b, ("s", h, j)))
                            src = c.A.slot(("s", h, j))
                            act.activation(c.e[h % 2][:, 2 * j * S:2 * (j + 1) * S], src, ACT.Exp, scale=0.25).then_inc(c.A.empty, 1)
                    act_transposed_attn(c, act, b, oT, D)

            @block.gpsimd
            def _(pool):
                with pool.Fori(0, B) as b:
                    pool_rstd(c, pool, b, 0)
        c.finish()



CLIP = 11.0


def layer_l3_xattn(nc, c, ins):
    with ExitStack() as ctx:
        sb = allocator(nc, ctx, "l3_xattn")
        IT = INNER // P
        wq, wk, wv = (sb(n, [P, KD, INNER]) for n in ("wq", "wk", "wv"))
        wo, obias = sb("wo", [P, IT, D]), sb("obias", [1, D])
        gain, shiftc = sb("gain", [P, 2, KD]), sb("shiftc", [P, 2, KD])
        qT, kT = sb("qT", [P, IT, S]), sb("kT", [P, IT, S])
        alloc_attention(c, sb, T * S, HD + 1, T, INNER, False)
        c.per_o = 1
        begin(c, A=2 + 2 * (IT // 2) + T + IT // 2, V=H * T + 2, O=H, ctx_here=1, x_here=1, var_ready=3, rstd_ready=3,
              heads_ready=H, exp_in=H, exp_ready=H)
        c.expect_setup(1)
        oT = kT
        pair = lambda tile, h: tile[64 * (h % 2):64 * (h % 2) + 64, h // 2, :]

        with nc.Block() as block:
            @block.sync
            def _(sp):
                for dst, name in ((gain, "gain10"), (shiftc, "shift10"), (wq, "wq10"), (wk, "wk10"), (wv, "wv10"),
                                  (wo, "wo10"), (obias, "obias10")):
                    c.load(sp, dst, ins[name])

            @block.tensor
            def _(pe):
                pe.wait_ge(c.loaded, c.load_count)
                pe.wait_ge(c.setup_done, c.setup_dones)
                with pe.Fori(0, B) as b:
                    for name, src, here in (("zx", c.xn, c.x_here), ("zc", c.ctxn, c.ctx_here)):
                        pe.wait_ge(c.A.empty, c.A.vacant(b, name))
                        out = c.A.slot(name)
                        pe.wait_ge(here.sem, here.at(b, 1))
                        for k in range(KD):
                            for t in range(T):
                                last = pe.transpose(out[:, k * S + t * P:k * S + (t + 1) * P], src[:, t, k * P:(k + 1) * P], c.ident[:, :])
                        last.then_inc(c.A.full, 1)
                    pe.wait_ge(c.A.empty, c.A.copied(b, "zc"))
                    for name, w, zT in (("q", wq, c.xT), ("k", wk, c.cT)):
                        for i in range(IT // 2):
                            pe.wait_ge(c.A.empty, c.A.vacant(b, (name, i)))
                            out = c.A.slot((name, i))
                            for m in (2 * i, 2 * i + 1):
                                last = mm(pe, out[:, (m - 2 * i) * S:(m - 2 * i + 1) * S],
                                          [(w[:, k, m * P:(m + 1) * P], zT[:, k, :]) for k in range(KD)])
                            last.then_inc(c.A.full, 1)
                    for t in range(T):
                        pe.wait_ge(c.A.empty, c.A.vacant(b, ("v", t)))
                        out = c.A.slot(("v", t))
                        for i in range(2):
                            last = mm(pe, out[:, i * S:(i + 1) * S],
                                      [(c.cT[:, k, t * P:(t + 1) * P], wv[:, k, i * S:(i + 1) * S]) for k in range(KD)])
                        last.then_inc(c.A.full, 1)
                    pe.wait_ge(c.A.empty, c.A.copied(b, ("k", IT // 2 - 1)))
                    for h in range(H + 1):
                        if h < H:
                            for t in range(T):
                                pe.wait_ge(c.V.empty, c.V.vacant(b, ("s", h, t)))
                                out = c.V.slot(("s", h, t))
                                pe.matmul(out, pair(kT, h)[:, t * P:(t + 1) * P], pair(qT, h), start=True, stop=True).then_inc(c.V.full, 1)
                        if h == 1:
                            pe.wait_ge(c.A.empty, c.A.copied(b, ("v", T - 1)))
                        if h:
                            pe.wait_ge(c.exp_ready.sem, c.exp_ready.at(b, h))
                            pe_values(c, pe, b, h - 1, c.e[(h - 1) % 2], c.v, HD + 1, False, [])
                    pe_transpose_attn(c, pe, b, c.on, INNER)
                    pe.wait_ge(c.A.empty, c.A.copied(b, ("oT", IT // 2 - 1)))
                    pe_project_out(c, pe, b, [lambda t, m=m: oT[:, m, t * P:(t + 1) * P] for m in range(IT)],
                                   [wo[:, m, :] for m in range(IT)], [obias[0:1, :]])

            @block.vector
            def _(dve):
                dve.memset(c.v[:, :, :, HD:HD + 1], 1.0)
                dve.drain().then_inc(c.setup_done, 1)
                with dve.Fori(0, B) as b:
                    here = bass.ds(b * T, T)
                    dve_norm(c, dve, b, 0, c.x[:, here, :], c.xn).then_inc(c.x_here.sem, 1)
                    dve_norm(c, dve, b, 1, c.ctx[:, here, :], c.ctxn).then_inc(c.ctx_here.sem, 1)
                    bound = CLIP * HD ** 0.5
                    for h in range(H):
                        for t in range(T):
                            dve.wait_ge(c.V.full, c.V.filled(b, ("s", h, t)))
                            s = c.V.slot(("s", h, t))
                            dve.tensor_scalar(c.e[h % 2][:, t * S:(t + 1) * S], s, bound, -bound, ALU.min, ALU.max).then_inc(c.V.empty, 1)
                        dve.drain().then_inc(c.exp_in.sem, 1)
                        if h > 1:
                            dve_heads_out(c, dve, b, h - 2, HD, HD + 1)
                    for h in (H - 2, H - 1):
                        dve_heads_out(c, dve, b, h, HD, HD + 1)
                    dve_residual_norm(c, dve, b, 2)

            @block.scalar
            def _(act):
                act.wait_ge(c.loaded, c.load_count)
                with act.Fori(0, B) as b:
                    for name, dst, i in (("zx", c.xT, 1), ("zc", c.cT, 0)):
                        act.wait_ge(c.A.full, c.A.filled(b, name))
                        src = c.A.slot(name)
                        for k in range(KD):
                            last = act.activation(dst[:, k, :], src[:, k * S:(k + 1) * S], ACT.Identity,
                                                  bias=shiftc[:, i, k:k + 1], scale=gain[:, i, k:k + 1])
                        last.then_inc(c.A.empty, 1)
                    for name, dst in (("q", qT), ("k", kT)):
                        for i in range(IT // 2):
                            act.wait_ge(c.A.full, c.A.filled(b, (name, i)))
                            src = c.A.slot((name, i))
                            act.activation(dst[:, 2 * i:2 * i + 2, :].rearrange("p m s -> p (m s)"), src, ACT.Copy).then_inc(c.A.empty, 1)
                    for t in range(T):
                        act.wait_ge(c.A.full, c.A.filled(b, ("v", t)))
                        src = c.A.slot(("v", t)).rearrange("p (h d) -> p h d", d=HD)
                        act.activation(c.v[:, t, :, 0:HD], src, ACT.Copy).then_inc(c.A.empty, 1)
                    for h in range(H):
                        act.wait_ge(c.exp_in.sem, c.exp_in.at(b, h + 1))
                        act.activation(c.e[h % 2][:, :], c.e[h % 2][:, :], ACT.Exp, scale=HD ** -0.5).then_inc(c.exp_ready.sem, 1)
                    act_transposed_attn(c, act, b, oT, INNER)

            @block.gpsimd
            def _(pool):
                with pool.Fori(0, B) as b:
                    for j in range(3):
                        pool_rstd(c, pool, b, j)
        c.finish()



def layer_l3_ffn(nc, c, ins):
    with ExitStack() as ctx:
        sb = allocator(nc, ctx, "l3_ffn")
        FT, STAGES = 8, 10
        HIDDEN = FT * P
        up, down = sb("up", [P, KD + 1, HIDDEN]), sb("down", [P, KD, HIDDEN])
        upw = [sb(f"upw{i}", [P, 2, HIDDEN]) for i in range(2)]
        downw = [sb(f"downw{i}", [P, 2, HIDDEN]) for i in range(2)]
        ta, tb, da, db = (sb(n, [P, HIDDEN]) for n in ("ta", "tb", "da", "db"))
        w2 = sb("w2", [P, FT, D])
        ubias, obias = sb("ubias", [P, FT]), sb("obias", [1, 2, D])
        hT = sb("hT", [P, FT, S])
        zeroed, up_stage, down_stage, pool_step = (ctx.enter_context(nc.semaphore(n)) for n in (
            "up_zeroed", "up_stage", "down_stage", "pool_step"))
        weights = [ctx.enter_context(nc.semaphore(f"butterfly_weights{i}")) for i in range(2)]
        c.setup_fulls += 1

        def stage(eng, y, w, s, a, b2):
            nb = HIDDEN // (2 * s)
            v = y.rearrange("p (n c s) -> p n c s", c=2, s=s)
            wide = [y.shape[0], nb, 2, s]
            n = y.shape[0]
            view = lambda t: t.rearrange("p (n c s) -> p n c s", c=2, s=s)
            eng.tensor_tensor(view(a[0:n, :]), view(w[0:n, 0, :]), v[:, :, 0:1, :].to_broadcast(wide), ALU.mult)
            eng.tensor_tensor(view(b2[0:n, :]), view(w[0:n, 1, :]), v[:, :, 1:2, :].to_broadcast(wide), ALU.mult)

        with nc.Block() as block:
            @block.sync
            def _(sp):
                for dst, name in ((ubias, "ubias11"), (obias, "obias11")):
                    c.load(sp, dst, ins[name])
                sp.dma_start(up[:, 0:KD, :], ins["up11"]).then_inc(c.loaded, 16)
                sp.dma_start(down[:, :, :], ins["down11"]).then_inc(c.loaded, 16)
                c.load_count += 32
                sp.wait_ge(zeroed, 1)
                sp.dma_start(up[0:1, KD, :], ins["upb11"]).then_inc(c.loaded, 16)
                c.load_count += 16
                sp.wait_ge(c.loaded, c.load_count)
                for st in range(STAGES):
                    if st > 1:
                        sp.wait_ge(up_stage, st - 1)
                        sp.wait_ge(down_stage, st - 1)
                    for dst, name in ((upw, "upw11"), (downw, "downw11")):
                        src = ins[name][st:st + 1, :, :].to_broadcast([P, 2, HIDDEN])
                        sp.dma_start(dst[st % 2][:, :, :], src).then_inc(weights[st % 2], 16)

            @block.vector
            def _(dve):
                dve.memset(up[:, KD, :], 0.0).then_inc(zeroed, 1)
                dve.wait_ge(c.loaded, c.load_count)
                for st in range(STAGES):
                    dve.wait_ge(weights[st % 2], 32 * (st // 2 + 1))
                    for k in range(KD + 1):
                        y = up[:, k, :] if k < KD else up[0:1, k, :]
                        n = P if k < KD else 1
                        stage(dve, y, upw[st % 2], 2 ** st, ta, tb)
                        dve.drain()
                        last = dve.tensor_tensor(y, ta[0:n, :], tb[0:n, :], ALU.add)
                        dve.drain()
                    dve.drain().then_inc(up_stage, 1)

            @block.gpsimd
            def _(pool):
                pool.wait_ge(c.loaded, c.load_count)
                done = 0
                for st in range(STAGES):
                    pool.wait_ge(weights[st % 2], 32 * (st // 2 + 1))
                    for k in range(KD):
                        y = down[:, k, :]
                        stage(pool, y, downw[st % 2], 2 ** (STAGES - 1 - st), da, db)
                        pool.drain().then_inc(pool_step, 1)
                        done += 1
                        pool.wait_ge(pool_step, done)
                        pool.tensor_tensor(y, da[:, :], db[:, :], ALU.add)
                        pool.drain().then_inc(pool_step, 1)
                        done += 1
                        pool.wait_ge(pool_step, done)
                    pool.sem_inc(down_stage, 1)

        c.expect_setup(1)
        with nc.Block() as block:
            @block.tensor
            def _(pe):
                for f in range(FT):
                    for o in range(KD):
                        last = pe.transpose(c.psA[:, f // 4, f % 4 * D + o * P:f % 4 * D + (o + 1) * P],
                                            down[:, o, f * P:(f + 1) * P], c.ident[:, :])
                last.then_inc(c.setup_full, 1)

            @block.scalar
            def _(act):
                act.wait_ge(c.setup_full, c.setup_fulls)
                for i in range(2):
                    last = act.activation(w2[:, 4 * i:4 * i + 4, :].rearrange("p f d -> p (f d)"), c.psA[:, i, :], ACT.Copy)
                act.drain().then_inc(c.setup_done, 1)

        begin(c, A=2 + FT // 2, V=2, O=0, x_here=1, var_ready=1, rstd_ready=1)
        with nc.Block() as block:
            @block.tensor
            def _(pe):
                pe.wait_ge(c.setup_done, c.setup_dones)
                with pe.Fori(0, B) as b:
                    pe_transpose_x_halves(c, pe, b)
                    pe.wait_ge(c.A.empty, c.A.copied(b, ("xT", KD - 1)))
                    for i in range(FT // 2):
                        pe.wait_ge(c.A.empty, c.A.vacant(b, ("h", i)))
                        out = c.A.slot(("h", i))
                        for m in (2 * i, 2 * i + 1):
                            last = mm(pe, out[:, (m - 2 * i) * S:(m - 2 * i + 1) * S],
                                      [(up[:, k, m * P:(m + 1) * P], c.xT[:, k, :]) for k in range(KD)]
                                      + [(up[0:1, KD, m * P:(m + 1) * P], c.ones[0:1, 0:S])])
                        last.then_inc(c.A.full, 1)
                    pe.wait_ge(c.A.empty, c.A.copied(b, ("h", FT // 2 - 1)))
                    pe_project_out(c, pe, b, [lambda t, f=f: hT[:, f, t * P:(t + 1) * P] for f in range(FT)],
                                   [w2[:, f, :] for f in range(FT)], [obias[0:1, 0, :], obias[0:1, 1, :]])

            @block.vector
            def _(dve):
                with dve.Fori(0, B) as b:
                    dve_residual_norm(c, dve, b)

            @block.scalar
            def _(act):
                with act.Fori(0, B) as b:
                    act_fetch_x(c, act, b)
                    for k in range(KD):
                        act.wait_ge(c.A.full, c.A.filled(b, ("xT", k)))
                        act.activation(c.xT[:, k, :], c.A.slot(("xT", k))[:, 0:S], ACT.Copy).then_inc(c.A.empty, 1)
                    for i in range(FT // 2):
                        act.wait_ge(c.A.full, c.A.filled(b, ("h", i)))
                        src = c.A.slot(("h", i))
                        for m in (2 * i, 2 * i + 1):
                            last = act.activation(hT[:, m, :], src[:, (m - 2 * i) * S:(m - 2 * i + 1) * S], ACT.Gelu,
                                                  bias=ubias[:, m:m + 1])
                        last.then_inc(c.A.empty, 1)

            @block.gpsimd
            def _(pool):
                with pool.Fori(0, B) as b:
                    pool_rstd(c, pool, b, 0)
        c.finish()


LAYERS = [layer_l0_attn, layer_l0_xattn, layer_l0_ffn, layer_l1_attn, layer_l1_xattn, layer_l1_ffn, layer_l2_attn,
          layer_l2_xattn, layer_l2_ffn, layer_l3_attn, layer_l3_xattn, layer_l3_ffn]


def build(nc, ins, out):
    with ExitStack() as ctx:
        sb = allocator(nc, ctx, "all")

        def sem(name):
            return ctx.enter_context(nc.semaphore(name))

        c = Core()
        c.x = sb("x", [P, B * T, D])
        c.xn = sb("xn", [P, T, D])
        c.xT = sb("xT", [P, KD, S])
        c.ctx = sb("ctx", [P, B * T, D])
        c.ctxn = sb("ctxn", [P, T, D])
        c.cT = sb("cT", [P, KD, S])
        c.r = sb("r", [P, T, D])
        c.stats = sb("stats", [P, T, 6])
        c.meanvar = sb("meanvar", [P, T, 2])
        c.vareps = sb("vareps", [P, T])
        c.rstd = sb("rstd", [P, T])
        c.minus_half = sb("minus_half", [P, T])
        c.ones = sb("ones", [1, S])
        c.ident = sb("ident", [P, P])
        c.ident16 = sb("ident16", [P, P], BF16)
        c.causal_kq = sb("causal_kq", [P, S], BF16)
        c.causal_qk = sb("causal_qk", [P, P], BF16)
        c.psA = ctx.enter_context(nc.psum_tensor("psA", [P, SLOTS, 1024], F32))
        c.psV = ctx.enter_context(nc.psum_tensor("psV", [P, SLOTS, 512], F32))
        c.psO = ctx.enter_context(nc.psum_tensor("psO", [P, SLOTS, 512], F32))
        c.A = Ring(nc, ctx, "A", "act_slot", c.psA)
        c.V = Ring(nc, ctx, "V", "dve_slot", c.psV)
        c.O = Ring(nc, ctx, "O", "heads_slot", c.psO)
        names = ("x_here", "ctx_here", "var_ready", "rstd_ready", "heads_ready", "parts_ready",
                 "exp_in", "exp_ready", "feat_ready", "step_ready", "vec_ready")
        signals = [Signal(nc, ctx, n) for n in names]
        c.signals = dict(zip(names, signals))
        (c.x_here, c.ctx_here, c.var_ready, c.rstd_ready, c.heads_ready, c.parts_ready,
         c.exp_in, c.exp_ready, c.feat_ready, c.step_ready, c.vec_ready) = signals
        c.marker = sem("marker")
        c.loaded = sem("loaded")
        c.setup_full = sem("setup_full")
        c.setup_done = sem("setup_done")
        c.stored = sem("stored")
        c.load_count = 0
        c.setup_dones = c.setup_fulls = 0

        def load(sp, dst, src):
            sp.dma_start(dst[tuple(slice(None) for _ in dst.shape)], src).then_inc(c.loaded, 16)
            c.load_count += 16

        def expect_setup(n):
            c.setup_dones += n

        def finish():
            for r in (c.A, c.V, c.O):
                r.end()
            for s in signals:
                s.end()

        c.load, c.expect_setup, c.finish = load, expect_setup, finish

        with nc.Block() as block:
            @block.sync
            def _(sp):
                x_view = ins["x"].rearrange("b (t p) d -> p (b t) d", p=P)
                load(sp, c.x, x_view)
                load(sp, c.ctx, ins["ctx"].rearrange("b (t p) d -> p (b t) d", p=P))
                for dst, name in ((c.ident, "ident"), (c.ident16, "ident16"), (c.causal_kq, "causal_kq"),
                                  (c.causal_qk, "causal_qk")):
                    load(sp, dst, ins[name])
                sp.wait_ge(c.loaded, c.load_count)

            @block.gpsimd
            def _(pool):
                pool.memset(c.minus_half[:, :], -0.5)
                pool.memset(c.ones[:, :], 1.0)

            @block.scalar
            def _(act):
                act.sem_inc(c.A.empty, SLOTS)

            @block.vector
            def _(dve):
                dve.sem_inc(c.V.empty, SLOTS)
                dve.sem_inc(c.O.empty, SLOTS)

        for i in PHASES:
            LAYERS[i](nc, c, ins)

        with nc.Block() as block:
            @block.sync
            def _(sp):
                sp.dma_start(out.rearrange("b (t p) d -> p (b t) d", p=P), c.x[:, :, :]).then_inc(c.stored, 16)
                sp.wait_ge(c.stored, 16)



def kernel(**inputs):
    import ml_dtypes
    import concourse.bacc as bacc
    from concourse.bass_utils import run_bass_kernel_spmd as run

    bf16 = ml_dtypes.bfloat16
    a = {k: np.asarray(v) for k, v in inputs.items()}

    def tiled(w):
        return w.reshape(w.shape[0] // P, P, *w.shape[1:]).swapaxes(0, 1)

    def row(v):
        return v.reshape(1, -1)

    def col(v):
        return v.reshape(-1, P).T

    def strips(w):
        out = np.zeros((w.shape[0], H, 32), w.dtype)
        out[:, :, 0:16] = w.reshape(w.shape[0], H, 16)
        return out.reshape(w.shape[0], H * 32)

    def block_diagonal(m):
        out = np.zeros((P, P), m.dtype)
        for i in range(0, P, 16):
            out[i:i + 16, i:i + 16] = m.T
        return out

    i = np.arange(P)
    lower = i[:, None] >= i[None, :]
    arrays = {
        "x": a["x"],
        "ctx": a["ctx_1024"],
        "ident": np.eye(P, dtype=np.float32),
        "ident16": np.eye(P, dtype=bf16),
        "causal_qk": np.where(lower, 0.0, -1e30).astype(bf16),
        "causal_kq": np.tile(np.where(lower.T, 0.0, -1e30), (1, T)).astype(bf16),
        "causal01": np.tile(np.where(lower.T, 1.0, 0.0), (1, T)).astype(np.float32),
        "sel32": np.tile((i[:, None] % H == np.arange(H)[None, :])[:, :, None], (1, 1, P)).astype(bf16),
    }
    w = a["L0_attn_w_qkv"]
    arrays["wqk0"] = tiled(w[0:2 * D])
    arrays["maps0"] = np.stack([block_diagonal(a["L0_attn_wq_map"]), block_diagonal(a["L0_attn_wk_map"])], axis=1)
    arrays["wv0"] = tiled(w[2 * D:].T)
    arrays["wo0"] = tiled(a["L0_attn_w_out"].T)
    arrays["fbias0"] = row(np.concatenate([np.tile(a["L0_attn_bq_map"], H), np.tile(a["L0_attn_bk_map"], H)]))
    for k, w in (("wq1", "w_q"), ("wk1", "w_k")):
        arrays[k] = tiled(strips(a["L0_xattn_" + w]))
    arrays["wv1"], arrays["wo1"] = tiled(a["L0_xattn_w_v"]), tiled(a["L0_xattn_w_o"])
    arrays["qbias1"], arrays["kbias1"] = col(strips(row(a["L0_xattn_b_q"]))), col(strips(row(a["L0_xattn_b_k"])))
    arrays["vbias1"], arrays["obias1"] = row(a["L0_xattn_b_v"]), row(a["L0_xattn_b_o"])

    arrays["wg2"], arrays["gbias2"] = tiled(a["L0_ffn_Wg"]), row(a["L0_ffn_bg"])
    arrays["rank2"] = np.tile(np.arange(8, 0, -1, dtype=np.float32), (P, T, 1))
    arrays["b1_2"], arrays["b2_2"] = col(a["L0_ffn_b1"]), a["L0_ffn_b2"]
    arrays["w1_2"] = a["L0_ffn_W1"].reshape(8, 2, P, 512).transpose(2, 0, 1, 3)
    arrays["w2_2"] = a["L0_ffn_W2"].reshape(8, 4, P, D).transpose(2, 0, 1, 3)

    for k, w in (("wq3", "query"), ("wk3", "key"), ("wv3", "value")):
        arrays[k] = tiled(a["L1_attn_W_" + w])

    arrays["w1_5"], arrays["w2_5"] = tiled(a["L1_ffn_W1"].T), tiled(a["L1_ffn_W2"].T)
    arrays["b1_5"], arrays["b2_5"] = col(a["L1_ffn_b1"]), row(a["L1_ffn_b2"])
    arrays["shift5"] = np.eye(P, k=1, dtype=np.float32)
    arrays["tokens5"] = (i[:, None] == np.arange(2, 17, 2)[None, :]).astype(np.float32)
    arrays["scale5"] = np.broadcast_to(a["L1_ffn_scale"].reshape(1, 1), (P, 1))

    w, v = a["L2_attn_Wqk"], a["L2_attn_bqk"]
    arrays["wq6"], arrays["wk6"] = tiled(strips(w[:, 0:D])), tiled(strips(w[:, D:]))
    arrays["qbias6"], arrays["kbias6"] = col(strips(row(v[0:D]))), col(strips(row(v[D:])))
    arrays["wv6"], arrays["wo6"], arrays["wn6"] = (tiled(a["L2_attn_" + n]) for n in ("Wv", "Wo", "Wn"))
    arrays["vbias6"], arrays["obias6"], arrays["nbias6"] = (row(a["L2_attn_" + n]) for n in ("bv", "bo", "bn"))
    def norm_cols(l, ctx):
        return np.stack([col(a[ctx]), col(a[l])], axis=1)

    m = a["mask_BxS2_bf1"].view(np.uint8)
    arrays["mask_row7"], arrays["mask_col7"] = row(m), col(m)
    arrays["gain7"], arrays["shift7"] = norm_cols("L2_xattn_gl", "L2_xattn_gm"), norm_cols("L2_xattn_bl", "L2_xattn_bm")
    arrays["sel64"] = ((i[:, None] % 64 < 32)[:, :, None] & (i[:, None] % H == np.arange(H)[None, :])[:, :, None]
                       & np.ones((1, 1, P), bool)).astype(bf16)
    for k in "qkvo":
        arrays[f"w{k}7"] = tiled(a["L2_xattn_W" + k])

    arrays["w1_8"], arrays["w2_8"] = tiled(a["L2_ffn_w1"].T), tiled(a["L2_ffn_w2"].T)
    arrays["b1_8"], arrays["b2_8"] = col(a["L2_ffn_b1"]), row(a["L2_ffn_b2"])

    for k, w in (("wq9", "Wq"), ("wk9", "Wk")):
        w = a["L3_attn_" + w].T.reshape(D, H, 8, 2)
        arrays[k] = tiled(strips(np.stack([w[..., 0], w[..., 0]], axis=-1).reshape(D, D)))
    arrays["wv9"], arrays["wo9"] = tiled(a["L3_attn_Wv"].T), tiled(a["L3_attn_Wo"].T)
    freqs = np.exp(np.arange(0, 16, 2, dtype=np.float32) * np.float32(-np.log(10000.0) / 16))
    angles = (np.arange(S, dtype=np.float32)[:, None] * freqs[None, :]).T
    rope = np.zeros((32, S), np.float32)
    rope[0:16:2], rope[1:16:2] = np.cos(angles), -np.sin(angles)
    arrays["rope9"] = np.tile(rope, (4, 1))

    arrays["gain10"] = norm_cols("L3_xattn_ln_l_w", "L3_xattn_ln_c_w")
    arrays["shift10"] = norm_cols("L3_xattn_ln_l_b", "L3_xattn_ln_c_b")
    w = a["L3_xattn_Wkv"]
    arrays["wq10"], arrays["wk10"], arrays["wv10"] = tiled(a["L3_xattn_Wq"]), tiled(w[:, 0:INNER]), tiled(w[:, INNER:])
    arrays["wo10"], arrays["obias10"] = tiled(a["L3_xattn_Wo"]), row(a["L3_xattn_bo"])

    def stage_weights(w, transposed):
        out = []
        for st in range(w.shape[0]):
            m = w[st].reshape(-1, 2 ** st, 2, 2)
            out.append(m.transpose((2, 0, 3, 1) if transposed else (3, 0, 2, 1)).reshape(2, -1))
        return np.stack(out[::-1] if transposed else out)

    arrays["upw11"] = stage_weights(a["L3_ffn_up_weights"], False)
    arrays["downw11"] = stage_weights(a["L3_ffn_down_weights"], True)
    arrays["up11"], arrays["upb11"] = tiled(a["L3_ffn_W_exp"]), row(a["L3_ffn_b_exp"])
    arrays["down11"] = tiled(a["L3_ffn_W_con"].T)
    arrays["ubias11"] = col(a["L3_ffn_up_bias"])
    arrays["obias11"] = np.stack([a["L3_ffn_b_con"], a["L3_ffn_down_bias"]])[None]

    nc = bacc.Bacc("TRN2", target_bir_lowering=False, num_devices=1)
    arrays = {f"in_{k}": np.ascontiguousarray(v) for k, v in arrays.items()}
    ins = {k[3:]: nc.dram_tensor(k, v.shape, mybir.dt.from_np(v.dtype), kind="ExternalInput").ap()
           for k, v in arrays.items()}
    out = nc.dram_tensor("out", (B, S, D), F32, kind="ExternalOutput").ap()
    build(nc, ins, out)
    result = run(nc, [arrays], core_ids=[0])
    return result.results[0]["out"]
```

```python
from contextlib import ExitStack

import numpy as np

import concourse.bass as bass
from concourse import mybir

F32 = mybir.dt.float32
BF16 = mybir.dt.bfloat16
ALU = mybir.AluOpType
ACT = mybir.ActivationFunctionType
AX = mybir.AxisListType.X
RMAX = bass.bass_isa.ReduceOp.max

P = 128
B, S, D = 4, 512, 256
T = S // P
KD = D // P
H = 16
NG = 4
EPS = 1e-5
CREDIT = 4
MAGIC = 12582912.0
PHASES = range(0, 12)


class Ring:

    def __init__(self, nc, ctx, short, name, psum):
        self.full = ctx.enter_context(nc.semaphore(f"{name}_full"))
        self.empty = ctx.enter_context(nc.semaphore(f"{name}_empty"))
        self.psum, self.base, self.short = psum, 0, short

    def begin(self, per_batch, slots):
        assert per_batch % slots == 0, per_batch
        self.n, self.slots, self.keys, self.taken = per_batch, slots, [], 0
        self.tiles = self.psum.shape[1] // slots // S

    def end(self):
        assert len(self.keys) == self.taken == self.n, (len(self.keys), self.taken, self.n)
        self.base += B * self.n

    def vacant(self, b, key):
        self.keys.append(key)
        return b * self.n + (self.base + len(self.keys) + CREDIT - self.slots)

    def filled(self, b, key):
        assert self.keys[self.taken] == key, (key, self.keys[self.taken])
        self.taken += 1
        return b * self.n + (self.base + self.taken)

    def reading(self, b, key):
        return b * self.n + (self.base + self.keys.index(key) + 1)

    def copied(self, b, key):
        return b * self.n + (self.base + self.keys.index(key) + 1 + CREDIT)

    def slot(self, key):
        width = self.psum.shape[1] // self.slots
        at = self.keys.index(key) % self.slots * width
        return self.psum[:, at:at + width]


class Signal:

    def __init__(self, nc, ctx, name):
        self.sem = ctx.enter_context(nc.semaphore(name))
        self.base, self.n = 0, 0

    def begin(self, per_batch):
        self.n = per_batch

    def end(self):
        self.base += B * self.n
        self.n = 0

    def at(self, b, k):
        return b * self.n + (self.base + k)


class Core:
    pass


def allocator(nc, ctx, layer):
    def sb(name, shape, dt=F32):
        return ctx.enter_context(nc.sbuf_tensor(f"{layer}_{name}", shape, dt))
    return sb


def alone(c, eng):
    eng.sem_inc(c.marker, 1)


def mm(pe, out, pairs, start=True):
    for i, (lhsT, rhs) in enumerate(pairs):
        last = pe.matmul(out, lhsT, rhs, start=start and i == 0, stop=i == len(pairs) - 1)
    return last


def begin(c, a_slots=2, v_slots=2, **counts):
    for ring, slots in ((c.A, a_slots), (c.V, v_slots), (c.O, 2)):
        ring.begin(counts.pop(ring.short), slots)
    for name, n in counts.items():
        c.signals[name].begin(n)



def act_fetch_x(c, act, b):
    alone(c, act)
    act.activation(c.xn[:, :, :], c.x[:, bass.ds(b * T, T), :], ACT.Copy).then_inc(c.x_here.sem, 1)


def pe_transpose_x(c, pe, b):
    pe.wait_ge(c.A.empty, c.A.vacant(b, "xT"))
    out = c.A.slot("xT")
    pe.wait_ge(c.x_here.sem, c.x_here.at(b, 1))
    for k in range(KD):
        for t in range(T):
            last = pe.transpose(out[:, k * S + t * P:k * S + (t + 1) * P], c.xn[:, t, k * P:(k + 1) * P], c.ident[:, :])
    last.then_inc(c.A.full, 1)


def pe_transpose_x_halves(c, pe, b):
    for k in range(KD):
        pe.wait_ge(c.A.empty, c.A.vacant(b, ("xT", k)))
        out = c.A.slot(("xT", k))
        pe.wait_ge(c.x_here.sem, c.x_here.at(b, 1))
        for t in range(T):
            last = pe.transpose(out[:, t * P:(t + 1) * P], c.xn[:, t, k * P:(k + 1) * P], c.ident[:, :])
        last.then_inc(c.A.full, 1)


def act_transposed_x(c, act, b):
    act.wait_ge(c.A.full, c.A.filled(b, "xT"))
    act.activation(c.xT[:, :, :].rearrange("p k s -> p (k s)"), c.A.slot("xT"), ACT.Copy).then_inc(c.A.empty, 1)


def act_transposed_x_halves(c, act, b):
    for k in range(KD):
        act.wait_ge(c.A.full, c.A.filled(b, ("xT", k)))
        act.activation(c.xT[:, k, :], c.A.slot(("xT", k))[:, 0:S], ACT.Copy).then_inc(c.A.empty, 1)


def pe_transpose_ctx(c, pe, b):
    pe.wait_ge(c.A.empty, c.A.vacant(b, "cT"))
    out = c.A.slot("cT")
    pe.wait_ge(c.ctx_here.sem, c.ctx_here.at(b, 1))
    for k in range(KD):
        for t in range(T):
            last = pe.transpose(out[:, k * S + t * P:k * S + (t + 1) * P], c.ctxn[:, t, k * P:(k + 1) * P], c.ident[:, :])
    last.then_inc(c.A.full, 1)


def act_fetch_ctx(c, act, b):
    alone(c, act)
    act.activation(c.ctxn[:, :, :], c.ctx[:, bass.ds(b * T, T), :], ACT.Copy).then_inc(c.ctx_here.sem, 1)


def act_transposed_ctx(c, act, b):
    act.wait_ge(c.A.full, c.A.filled(b, "cT"))
    act.activation(c.cT[:, :, :].rearrange("p k s -> p (k s)"), c.A.slot("cT"), ACT.Copy).then_inc(c.A.empty, 1)


def pe_transpose_ctx_halves(c, pe, b):
    for k in range(KD):
        pe.wait_ge(c.A.empty, c.A.vacant(b, ("cT", k)))
        out = c.A.slot(("cT", k))
        pe.wait_ge(c.ctx_here.sem, c.ctx_here.at(b, 1))
        for t in range(T):
            last = pe.transpose(out[:, t * P:(t + 1) * P], c.ctxn[:, t, k * P:(k + 1) * P], c.ident[:, :])
        last.then_inc(c.A.full, 1)


def act_transposed_ctx_halves(c, act, b):
    for k in range(KD):
        act.wait_ge(c.A.full, c.A.filled(b, ("cT", k)))
        act.activation(c.cT[:, k, :], c.A.slot(("cT", k))[:, 0:S], ACT.Copy).then_inc(c.A.empty, 1)


def dve_norm(c, dve, b, j, src, dst):
    for t in range(T):
        dve.bn_stats(c.stats[:, t, :], src[:, t, :])
    dve.drain()
    for t in range(T):
        dve.bn_aggr(c.meanvar[:, t, :], c.stats[:, t, :])
    dve.drain()
    dve.tensor_scalar(c.vareps[:, :], c.meanvar[:, :, 1], EPS, None, ALU.add).then_inc(c.var_ready.sem, 1)
    dve.wait_ge(c.rstd_ready.sem, c.rstd_ready.at(b, j + 1))
    alone(c, dve)
    for t in range(T):
        last = dve.tensor_scalar(dst[:, t, :], src[:, t, :], c.meanvar[:, t, 0:1], c.rstd[:, t:t + 1],
                                 ALU.subtract, ALU.mult)
    return last


def pool_rstd(c, pool, b, j):
    pool.wait_ge(c.var_ready.sem, c.var_ready.at(b, j + 1))
    alone(c, pool)
    pool.tensor_tensor(c.rstd[:, :], c.vareps[:, :], c.minus_half[:, :], ALU.pow).then_inc(c.rstd_ready.sem, 1)


def dve_residual_norm(c, dve, b, norm=0):
    dve.drain()
    for i in range(2):
        dve.wait_ge(c.V.full, c.V.filled(b, ("y", i)))
        y = c.V.slot(("y", i)).rearrange("p (t d) -> p t d", d=D)
        last = dve.tensor_tensor(c.r[:, 2 * i:2 * i + 2, :], y, c.x[:, bass.ds(b * T + 2 * i, 2), :], ALU.add)
        last.then_inc(c.V.empty, 1)
    dve.drain()
    dve_norm(c, dve, b, norm, c.r, c.x[:, bass.ds(b * T, T), :])


def pe_project_out(c, pe, b, lhs, rhs, bias=None):
    for i in range(2):
        pe.wait_ge(c.V.empty, c.V.vacant(b, ("y", i)))
        out = c.V.slot(("y", i))
        for t in (2 * i, 2 * i + 1):
            pairs = [(l(t), r) for l, r in zip(lhs, rhs)]
            if bias is not None:
                pairs += [(c.ones[0:1, 0:P], v) for v in bias]
            last = mm(pe, out[:, (t - 2 * i) * D:(t - 2 * i + 1) * D], pairs)
        last.then_inc(c.V.full, 1)


def pe_transpose_attn(c, pe, b, on, width):
    n = c.A.tiles
    for m in range(width // P // n):
        pe.wait_ge(c.A.empty, c.A.vacant(b, ("oT", m)))
        out = c.A.slot(("oT", m))
        if m == 0:
            pe.wait_ge(c.heads_ready.sem, c.heads_ready.at(b, c.heads_ready.n))
        for k in range(n):
            for t in range(T):
                last = pe.transpose(out[:, k * S + t * P:k * S + (t + 1) * P],
                                    on[:, t, (n * m + k) * P:(n * m + k + 1) * P], c.ident[:, :])
        last.then_inc(c.A.full, 1)


def act_transposed_attn(c, act, b, oT, width):
    n = c.A.tiles
    for m in range(width // P // n):
        act.wait_ge(c.A.full, c.A.filled(b, ("oT", m)))
        src = c.A.slot(("oT", m))
        act.activation(oT[:, n * m:n * (m + 1), :].rearrange("p k s -> p (k s)"), src, ACT.Copy).then_inc(c.A.empty, 1)


OFF_AT = {0: 0, 2: 384, 1: 512}
OFF_LEN = 768


def causal_at(kt, qt):
    return qt * P if kt == qt else S + OFF_AT[kt] + (qt - kt - 1) * P


def pe_causal_scores(c, pe, b, h, kh, qh, diag_ring, softmax):
    pe.wait_ge(diag_ring.empty, diag_ring.vacant(b, ("d", h)))
    out = diag_ring.slot(("d", h))
    if softmax:
        pe.matmul(out[:, 0:S], c.ident16[:, :], c.causal_kq[:, :], start=True, stop=False)
        pe.matmul(out[:, 0:S], c.selh(h), c.shifth(h), start=False, stop=False)
    for t in range(T):
        cols = slice(t * P, (t + 1) * P)
        last = pe.matmul(out[:, cols], kh[:, cols], qh[:, cols], start=not softmax, stop=not softmax or t == T - 1)
    last.then_inc(diag_ring.full, 1)
    pe.wait_ge(c.A.empty, c.A.vacant(b, ("o", h)))
    out = c.A.slot(("o", h))
    for kts in ((0, 2), (1,)):
        if softmax:
            for kt in kts:
                n = S - (kt + 1) * P
                pe.matmul(out[:, OFF_AT[kt]:OFF_AT[kt] + n], c.selh(h), c.shifth(h)[:, S - n:S], start=kt == kts[0],
                          stop=False)
        for kt in kts:
            n = S - (kt + 1) * P
            last = pe.matmul(out[:, OFF_AT[kt]:OFF_AT[kt] + n], kh[:, kt * P:(kt + 1) * P], qh[:, S - n:S],
                             start=not softmax, stop=not softmax or kt == kts[-1])
    last.then_inc(c.A.full, 1)


def pe_scores(c, pe, b, h, kh, qh, kts):
    for j in range(kts // 2):
        pe.wait_ge(c.A.empty, c.A.vacant(b, ("s", h, j)))
        out = c.A.slot(("s", h, j))
        for i in range(2):
            kt = 2 * j + i
            pe.matmul(out[:, i * S:(i + 1) * S], c.selh(h), c.shifth(h), start=True, stop=False)
            last = pe.matmul(out[:, i * S:(i + 1) * S], kh[:, kt * P:(kt + 1) * P], qh, start=False, stop=True)
        last.then_inc(c.A.full, 1)


def pe_values(c, pe, b, h, e, v, vw, causal, last_jobs):
    g, i = divmod(h, c.per_o)
    if i == 0:
        pe.wait_ge(c.O.empty, c.O.vacant(b, ("O", g)))
        c.o_slot = c.O.slot(("O", g))
    for ring, key in last_jobs:
        pe.wait_ge(ring.empty, ring.copied(b, key))
    for qt in range(T):
        kts = range(qt + 1) if causal else range(v.shape[1])
        at = (qt * c.per_o + i) * vw
        for kt in kts:
            w = e[:, causal_at(kt, qt):causal_at(kt, qt) + P] if causal else e[:, kt * S + qt * P:kt * S + (qt + 1) * P]
            last = pe.matmul(c.o_slot[:, at:at + vw], w, v[:, kt, h, 0:vw], start=kt == 0, stop=kt == kts[-1])
    if i == c.per_o - 1:
        last.then_inc(c.O.full, 1)


def pe_max_scores(c, pe, b, h, qt, kh, qh, parts, by_register=False):
    pe.wait_ge(c.V.empty, c.V.vacant(b, ("m", h, qt, parts[0][1])))
    out = c.V.slot(("m", h, qt, parts[0][1]))
    if by_register:
        alone(c, pe)
    for at, k0, n, hide in parts:
        if hide is not None:
            pe.matmul(out[:, at:at + n], hide[0], hide[1], start=True, stop=False)
        last = pe.matmul(out[:, at:at + n], qh[:, qt * P:(qt + 1) * P], kh[:, k0:k0 + n], start=hide is None, stop=True)
    last.then_inc(c.V.full, 1)


def pe_project_values(c, pe, b, xT, wv, bias=None):
    for i in range(2):
        pe.wait_ge(c.V.empty, c.V.vacant(b, ("v", i)))
        out = c.V.slot(("v", i))
        for t in (2 * i, 2 * i + 1):
            pairs = [(xT[:, k, t * P:(t + 1) * P], wv[:, k, :]) for k in range(KD)]
            if bias is not None:
                pairs.append((c.ones[0:1, 0:P], bias))
            last = mm(pe, out[:, (t - 2 * i) * D:(t - 2 * i + 1) * D], pairs)
        last.then_inc(c.V.full, 1)


def dve_values(c, dve, b):
    for i in range(2):
        dve.wait_ge(c.V.full, c.V.filled(b, ("v", i)))
        src = c.V.slot(("v", i)).rearrange("p (t h d) -> p t h d", t=2, d=16)
        for t in range(2):
            last = dve.tensor_copy(c.v[:, 2 * i + t, :, 0:16], src[:, t, :, :])
        last.then_inc(c.V.empty, 1)


def dve_shift_parts(c, dve):
    nmax, hi = c.nmax, c.nmax16
    dve.tensor_reduce(nmax[:, :, :], c.mraw[:, :, :, :], AX, ALU.max, negate=True)
    dve.drain()
    dve.tensor_copy(hi[:, :, :], nmax[:, :, :])
    dve.drain()
    dst = c.parts[:, :, :].rearrange("p t (c w) -> p t c w", w=32)
    for cc in range(4):
        dve.tensor_copy(dst[:, :, cc, 0:H], hi[:, :, :])
        last = dve.tensor_tensor(dst[:, :, cc, H:2 * H], nmax[:, :, :], hi[:, :, :], ALU.subtract)
    last.then_inc(c.parts_ready.sem, 1)


def pe_transpose_shift(c, pe, b):
    pe.wait_ge(c.A.empty, c.A.vacant(b, "shift"))
    out = c.A.slot("shift")
    pe.wait_ge(c.parts_ready.sem, c.parts_ready.at(b, 1))
    for t in range(T):
        last = pe.transpose(out[:, t * P:(t + 1) * P], c.parts[:, t, :], c.ident[:, :])
    last.then_inc(c.A.full, 1)


def act_transposed_shift(c, act, b):
    act.wait_ge(c.A.full, c.A.filled(b, "shift"))
    act.activation(c.shift[:, :], c.A.slot("shift")[:, 0:S], ACT.Copy).then_inc(c.A.empty, 1)


def head16(tile, h):
    return tile[32 * (h % 4):32 * (h % 4) + 32, h // 4, :]


def head64(tile, h):
    return tile[64 * (h % 2):64 * (h % 2) + 64, h // 2, :]


def alloc_attention(c, sb, e_len, vw, kts, o_width, softmax, k=32):
    c.e = [sb(f"e{i}", [P, e_len]) for i in range(2)]
    c.v = sb("v", [P, kts, H, vw])
    c.on = sb("on", [P, T, o_width])
    c.rec = sb("rec", [P, T, H])
    if softmax:
        c.nmax = sb("nmax", [P, T, H])
        c.nmax16 = sb("nmax16", [P, T, H], BF16)
        c.parts = sb("parts", [P, T, P])
        c.shift = sb("shift", [P, S], BF16)
        sel = c.sel = sb("sel", [P, H, P], BF16)
        c.selh = lambda h: sel[k * (h % (P // k)):k * (h % (P // k)) + k, h, :]
        c.shifth = lambda h: c.shift[k * (h % (P // k)):k * (h % (P // k)) + k, :]


LAG = 2
AHEAD = 3


def spread_heads(copy, dst, src, heads, width):
    for i, h in enumerate(heads):
        rows = slice(width * i, width * (i + 1))
        last = copy(dst[rows, h, :], src[rows, :], rows)
    return last


def alloc_softmax(c, sb, keys, width, o_width, span=T):
    c.width, c.per_o, c.span = width, P // width, span
    c.p = [sb(f"p{i}", [P, keys * P]) for i in range(LAG + 1)]
    c.pTs = sb("pTs", [P, c.per_o + 1, keys, span * P])
    c.v = sb("v", [P, keys, H, width])
    c.oraw = sb("oraw", [P, 2, span * P])
    c.on = sb("on", [P, T, o_width])
    c.nmax = sb("nmax", [P, LAG + 2])
    c.rsum = sb("rsum", [P, T, H])
    c.rec = sb("rec", [P, span, c.per_o])
    c.chunks = [(g, q0) for g in range(H // c.per_o) for q0 in range(0, T, span)]
    c.units = [(g * c.per_o + m, q0 + q) for g, q0 in c.chunks for m in range(c.per_o) for q in range(span)]


def pT_of_run(c, run):
    return c.pTs[:, run % (c.per_o + 1), :, :]


def pe_attend(c, pe, b, keys, scores, causal=False, before_unit=None):
    size = c.per_o * c.span
    for i in range(len(c.units) + LAG + 4):
        if i < len(c.units):
            if before_unit is not None:
                before_unit(i)
            h, qt = c.units[i]
            pe.wait_ge(c.A.empty, c.A.vacant(b, ("s", h, qt)))
            scores(c.A.slot(("s", h, qt)), h, qt).then_inc(c.A.full, 1)
        if LAG <= i < len(c.units) + LAG:
            h, qt = c.units[i - LAG]
            n = qt + 1 if causal else keys
            for j in range(0, n, T):
                pe.wait_ge(c.V.empty, c.V.vacant(b, ("pT", h, qt, j)))
                if j == 0:
                    pe.wait_ge(c.A.empty, c.A.copied(b, ("s", h, qt)))
                out = c.V.slot(("pT", h, qt, j))
                for k in range(j, min(j + T, n)):
                    last = pe.transpose(out[:, (k - j) * P:(k - j + 1) * P],
                                        c.p[(i - LAG) % (LAG + 1)][:, k * P:(k + 1) * P], c.ident[:, :])
                last.then_inc(c.V.full, 1)
        done, rest = divmod(i - LAG, size)
        if done > 0 and rest == 0:
            g, q0 = c.chunks[done - 1]
            pe.wait_ge(c.O.empty, c.O.vacant(b, ("O", g, q0)))
            h, qt = c.units[done * size - 1]
            pe.wait_ge(c.V.empty, c.V.copied(b, ("pT", h, qt, (keys - 1) // T * T)))
            out = c.O.slot(("O", g, q0))
            for k in range(keys):
                cols = slice(k * P if causal else 0, c.span * P)
                for m in range(c.per_o):
                    last = pe.matmul(out[m * c.width:(m + 1) * c.width, cols], c.v[:, k, g * c.per_o + m, :],
                                     pT_of_run(c, (done - 1) * c.per_o + m)[:, k, cols], start=k == 0,
                                     stop=k == keys - 1)
            last.then_inc(c.O.full, 1)
        if done > 0 and rest == 2:
            g, q0 = c.chunks[done - 1]
            pe.wait_ge(c.V.empty, c.V.vacant(b, ("o", g, q0)))
            pe.wait_ge(c.O.empty, c.O.copied(b, ("O", g, q0)))
            out = c.V.slot(("o", g, q0))
            for t in range(c.span):
                cols = slice(t * P, (t + 1) * P)
                last = pe.transpose(out[:, cols], c.oraw[:, (done - 1) % 2, cols], c.ident[:, :])
            last.then_inc(c.V.full, 1)


def dve_attend(c, dve, b, keys, hd, causal=False):
    size = c.per_o * c.span
    for i in range(len(c.units) + LAG + 4):
        if i < len(c.units):
            h, qt = c.units[i]
            n = qt + 1 if causal else keys
            dve.wait_ge(c.A.full, c.A.reading(b, ("s", h, qt)))
            at = i % (LAG + 2)
            dve.tensor_reduce(c.nmax[:, at:at + 1], c.A.slot(("s", h, qt))[:, 0:n * P], AX, ALU.max,
                              negate=True).then_inc(c.max_ready.sem, 1)
        if LAG <= i < len(c.units) + LAG:
            h, qt = c.units[i - LAG]
            n = qt + 1 if causal else keys
            run, at = divmod(i - LAG, c.span)
            if at == 0 and run > c.per_o:
                dve.wait_ge(c.O.full, c.O.reading(b, ("O", *c.chunks[(run - c.per_o - 1) // c.per_o])))
            for j in range(0, n, T):
                dve.wait_ge(c.V.full, c.V.filled(b, ("pT", h, qt, j)))
                m = min(T, n - j)
                src = c.V.slot(("pT", h, qt, j))[:, 0:m * P].rearrange("p (k q) -> p k q", q=P)
                dve.tensor_copy(pT_of_run(c, run)[:, j:j + m, at * P:(at + 1) * P], src).then_inc(c.V.empty, 1)
        done, rest = divmod(i - LAG, size)
        if done > 0 and rest == 1:
            g, q0 = c.chunks[done - 1]
            dve.wait_ge(c.O.full, c.O.filled(b, ("O", g, q0)))
            dve.tensor_copy(c.oraw[:, (done - 1) % 2, :], c.O.slot(("O", g, q0))[:, 0:c.span * P]).then_inc(c.O.empty, 1)
            dve.reciprocal(c.rec[:, :, :], c.rsum[:, q0:q0 + c.span, g * c.per_o:(g + 1) * c.per_o])
        if done > 0 and rest == 2:
            g, q0 = c.chunks[done - 1]
            dve.drain()
            dve.wait_ge(c.V.full, c.V.filled(b, ("o", g, q0)))
            o = c.V.slot(("o", g, q0)).rearrange("p (t i w) -> p t i w", i=c.per_o, w=c.width)
            for t in range(c.span):
                dst = c.on[:, q0 + t, g * c.per_o * hd:(g + 1) * c.per_o * hd].rearrange("p (i d) -> p i d", d=hd)
                last = dve.tensor_tensor(dst, o[:, t, :, 0:hd],
                                         c.rec[:, t, :].unsqueeze(2).to_broadcast([P, c.per_o, hd]), ALU.mult)
            last.then_inc(c.V.empty, 1)
            dve.drain().then_inc(c.heads_ready.sem, 1)


def act_attend(c, act, b, keys, causal=False, before_unit=None):
    for i, (h, qt) in enumerate(c.units):
        if before_unit is not None:
            before_unit(i)
        n = (qt + 1 if causal else keys) * P
        at = i % (LAG + 2)
        c.A.filled(b, ("s", h, qt))
        act.wait_ge(c.max_ready.sem, c.max_ready.at(b, i + 1))
        act.activation(c.p[i % (LAG + 1)][:, 0:n], c.A.slot(("s", h, qt))[:, 0:n], ACT.Exp,
                       bias=c.nmax[:, at:at + 1], accum_out=c.rsum[:, qt, h:h + 1]).then_inc(c.A.empty, 1)



def alloc_linear(c, sb):
    c.v = sb("v", [P, T, H, 32])
    c.qm = sb("qm", [P, H, S])
    c.e = sb("e", [P, 3, NG * P])
    c.sums = sb("sums", [P, 2, (T - 1) * P])
    c.oraw = sb("oraw", [P, 2, S])
    c.on = sb("on", [P, T, D])
    c.rec = sb("rec", [P, T, 4])
    c.causal01 = sb("causal01", [P, 4 * P])
    c.blocks = sb("blocks", [P, (T - 1) * P])


def pe_linear(c, pe, b, q, k, kn):
    for u in range(NG * T + 4):
        g, t = divmod(u, T)
        if g < NG:
            if t == 0:
                pe.wait_ge(c.V.empty, c.V.vacant(b, ("sums", g)))
                out = c.V.slot(("sums", g))
                v = c.v[:, :, 4 * g:4 * g + 4, :].rearrange("p t h d -> p t (h d)")
                for upto in range(1, T):
                    last = mm(pe, out[:, (upto - 1) * P:upto * P], [(kn(g, j), v[:, j, :]) for j in range(upto)])
                last.then_inc(c.V.full, 1)
            pe.wait_ge(c.V.empty, c.V.vacant(b, ("d", g, t)))
            cols = slice(t * P, (t + 1) * P)
            pe.matmul(c.V.slot(("d", g, t)).rearrange("p (h q) -> p h q", q=P), k(g)[:, cols],
                      c.qm[:, 4 * g:4 * g + 4, cols], start=True, stop=True).then_inc(c.V.full, 1)
        if 0 < u <= NG * T:
            g, t = divmod(u - 1, T)
            cols = slice(t * P, (t + 1) * P)
            if t == 0:
                pe.wait_ge(c.O.empty, c.O.vacant(b, ("O", g)))
            pe.wait_ge(c.V.empty, c.V.copied(b, ("d", g, t)))
            out = c.O.slot(("O", g))
            if t:
                pe.matmul(out[:, cols], c.sums[:, g % 2, (t - 1) * P:t * P], q(g)[:, cols], start=True, stop=False)
            for m in range(4):
                last = pe.matmul(out[32 * m:32 * m + 32, cols], c.v[:, t, 4 * g + m, :],
                                 c.e[:, (u - 1) % 3, m * P:(m + 1) * P], start=t == 0, stop=True)
            if t == T - 1:
                last.then_inc(c.O.full, 1)
        g, rest = divmod(u - T, T)
        if g >= 0 and rest == 2:
            pe.wait_ge(c.V.empty, c.V.vacant(b, ("o", g)))
            pe.wait_ge(c.O.empty, c.O.copied(b, ("O", g)))
            out = c.V.slot(("o", g))
            for t in range(T):
                last = pe.transpose(out[:, t * P:(t + 1) * P], c.oraw[:, g % 2, t * P:(t + 1) * P], c.ident[:, :])
            last.then_inc(c.V.full, 1)


def dve_linear(c, dve, b, factors):
    for u in range(NG * T + 4):
        g, t = divmod(u, T)
        if g < NG:
            if t == 0:
                dve.wait_ge(c.V.full, c.V.filled(b, ("sums", g)))
                dve.tensor_tensor(c.sums[:, g % 2, :], c.V.slot(("sums", g))[:, 0:(T - 1) * P], c.blocks[:, :],
                                  ALU.mult).then_inc(c.V.empty, 1)
            dve.wait_ge(c.V.full, c.V.filled(b, ("d", g, t)))
            dve.tensor_tensor(c.e[:, u % 3, :], c.V.slot(("d", g, t)), c.causal01[:, :], ALU.mult).then_inc(c.V.empty, 1)
        g, rest = divmod(u - T, T)
        if g >= 0 and rest == 1:
            dve.wait_ge(c.O.full, c.O.filled(b, ("O", g)))
            dve.tensor_copy(c.oraw[:, g % 2, :], c.O.slot(("O", g))).then_inc(c.O.empty, 1)
        if g >= 0 and rest == 2:
            dve.wait_ge(c.V.full, c.V.filled(b, ("o", g)))
            o = c.V.slot(("o", g)).rearrange("p (t i w) -> p t i w", i=4, w=32)
            rec = factors(g, o)
            for t in range(T):
                dst = c.on[:, t, g * 64:(g + 1) * 64].rearrange("p (i d) -> p i d", d=16)
                last = dve.tensor_tensor(dst, o[:, t, :, 0:16], rec[:, t, :].unsqueeze(2).to_broadcast([P, 4, 16]), ALU.mult)
            last.then_inc(c.V.empty, 1)
            dve.drain().then_inc(c.heads_ready.sem, 1)


def dve_heads_out(c, dve, b, g, hd, vw, floor=None, given=None):
    n = c.per_o
    dve.wait_ge(c.O.full, c.O.filled(b, ("O", g)))
    o = c.O.slot(("O", g))[:, 0:T * n * vw].rearrange("p (t i w) -> p t i w", i=n, w=vw)
    hs = slice(g * n, (g + 1) * n)
    if given is None:
        rec = c.rec[:, :, hs]
        if floor is not None:
            dve.tensor_scalar(rec, o[:, :, :, hd], floor, None, ALU.max)
            dve.drain()
            dve.reciprocal(rec, rec)
        else:
            dve.reciprocal(rec, o[:, :, :, hd])
        dve.drain()
    else:
        rec = given[:, :, hs]
    for t in range(T):
        dst = c.on[:, t, g * n * hd:(g + 1) * n * hd].rearrange("p (i d) -> p i d", d=hd)
        last = dve.tensor_tensor(dst, o[:, t, :, 0:hd], rec[:, t, :].unsqueeze(2).to_broadcast([P, n, hd]), ALU.mult)
    last.then_inc(c.O.empty, 1)
    dve.drain().then_inc(c.heads_ready.sem, 1)



def layer_l0_attn(nc, c, ins):
    with ExitStack() as ctx:
        sb = allocator(nc, ctx, "l0_attn")
        FW = 2 * 2 * D
        wqk = sb("wqk", [P, 4, D])
        maps = sb("maps", [P, 2, P])
        wv = sb("wv", [P, KD, D])
        wo = sb("wo", [P, KD, D])
        fbias = sb("fbias", [1, 2 * D])
        wc = sb("wc", [P, KD, 2 * D])
        feat = sb("feat", [P, T, FW])
        hi = sb("hi", [P, T, 2 * H])
        lo = sb("lo", [P, T, 2 * H])
        fsum = sb("fsum", [P, T, 4 * H])
        fT = sb("fT", [P, 2, NG, S])
        oT = sb("oT", [P, KD, S])
        alloc_linear(c, sb)
        begin(c, A=1 + NG + 1, V=T + 2 + NG * (T + 2) + 2, O=NG, x_here=1, var_ready=1, rstd_ready=1, heads_ready=NG,
              exp_in=T, exp_ready=T, feat_ready=T)
        c.expect_setup(3)
        c.setup_fulls += 1

        with nc.Block() as block:
            @block.sync
            def _(sp):
                for dst, name in ((wqk, "wqk0"), (maps, "maps0"), (wv, "wv0"), (wo, "wo0"), (fbias, "fbias0"),
                                  (c.causal01, "causal01"), (c.blocks, "blocks")):
                    c.load(sp, dst, ins[name])

            @block.tensor
            def _(pe):
                pe.wait_ge(c.loaded, c.load_count)
                for m in range(4):
                    for k in range(KD):
                        last = pe.matmul(c.psO[:, k * S + m * P:k * S + (m + 1) * P], wqk[:, m, k * P:(k + 1) * P],
                                         maps[:, m // 2, :], start=True, stop=True)
                last.then_inc(c.setup_full, 1)
                pe.wait_ge(c.setup_done, c.setup_dones)
                with pe.Fori(0, B) as b:
                    pe_transpose_x(c, pe, b)
                    pe.wait_ge(c.A.empty, c.A.copied(b, "xT"))
                    for t in range(T):
                        pe.wait_ge(c.V.empty, c.V.vacant(b, ("p", t)))
                        out = c.V.slot(("p", t))
                        mm(pe, out, [(c.xT[:, k, t * P:(t + 1) * P], wc[:, k, :]) for k in range(KD)]
                                      + [(c.ones[0:1, 0:P], fbias[0:1, :])]).then_inc(c.V.full, 1)
                    pe_project_values(c, pe, b, c.xT, wv)
                    for g in range(NG):
                        pe.wait_ge(c.A.empty, c.A.vacant(b, ("fT", g)))
                        out = c.A.slot(("fT", g))
                        if g == 0:
                            pe.wait_ge(c.feat_ready.sem, c.feat_ready.at(b, T))
                        for w in range(2):
                            for t in range(T):
                                last = pe.transpose(out[:, w * S + t * P:w * S + (t + 1) * P],
                                                    feat[:, t, (w * NG + g) * P:(w * NG + g + 1) * P], c.ident[:, :])
                        last.then_inc(c.A.full, 1)
                    pe.wait_ge(c.A.empty, c.A.copied(b, ("fT", NG - 1)))
                    pe_linear(c, pe, b, lambda g: fT[:, 0, g, :], lambda g: fT[:, 1, g, :],
                              lambda g, t: feat[:, t, (NG + g) * P:(NG + g + 1) * P])
                    pe_transpose_attn(c, pe, b, c.on, D)
                    pe.wait_ge(c.A.empty, c.A.copied(b, ("oT", 0)))
                    pe_project_out(c, pe, b, [lambda t, k=k: oT[:, k, t * P:(t + 1) * P] for k in range(KD)],
                                   [wo[:, k, :] for k in range(KD)])

            @block.vector
            def _(dve):
                dve.wait_ge(c.setup_full, 1)
                dve.wait_ge(c.loaded, c.load_count)
                dve.tensor_copy(wc[:, :, :].rearrange("p k m -> p (k m)"), c.psO[:, :]).then_inc(c.setup_done, 1)
                with dve.Fori(0, B) as b:
                    for t in range(T):
                        dve.wait_ge(c.V.full, c.V.filled(b, ("p", t)))
                        p = c.V.slot(("p", t)).rearrange("p (h d) -> p h d", d=16)
                        f = feat[:, t, :].rearrange("p (h d) -> p h d", d=32)
                        dve.tensor_reduce(hi[:, t, :], p, AX, ALU.max)
                        dve.tensor_reduce(lo[:, t, :], p, AX, ALU.min)
                        dve.drain()
                        shape = [P, 2 * H, 16]
                        dve.tensor_tensor(f[:, :, 0:16], p, hi[:, t, :].unsqueeze(2).to_broadcast(shape), ALU.subtract)
                        last = dve.tensor_tensor(f[:, :, 16:32], lo[:, t, :].unsqueeze(2).to_broadcast(shape), p,
                                                 ALU.subtract)
                        last.then_inc(c.V.empty, 1)
                        dve.drain().then_inc(c.exp_in.sem, 1)
                    dve_values(c, dve, b)
                    for t in range(T):
                        f = feat[:, t, :].rearrange("p (h d) -> p h d", d=16)
                        dve.wait_ge(c.exp_ready.sem, c.exp_ready.at(b, t + 1))
                        dve.tensor_reduce(fsum[:, t, :], f, AX, ALU.add)
                        dve.drain()
                        dve.reciprocal(fsum[:, t, :], fsum[:, t, :])
                        dve.drain()
                        dve.tensor_tensor(
                            f, f, fsum[:, t, :].unsqueeze(2).to_broadcast([P, 4 * H, 16]), ALU.mult).then_inc(c.feat_ready.sem, 1)
                    def factors(g, o):
                        dve.tensor_scalar(c.rec[:, :, :], o[:, :, :, 16], 1e-6, None, ALU.max)
                        dve.drain()
                        dve.reciprocal(c.rec[:, :, :], c.rec[:, :, :])
                        dve.drain()
                        return c.rec

                    dve_linear(c, dve, b, factors)
                    dve_residual_norm(c, dve, b)

            @block.scalar
            def _(act):
                act.wait_ge(c.setup_done, c.setup_dones)
                with act.Fori(0, B) as b:
                    act_fetch_x(c, act, b)
                    act_transposed_x(c, act, b)
                    for t in range(T):
                        act.wait_ge(c.exp_in.sem, c.exp_in.at(b, t + 1))
                        act.activation(feat[:, t, :], feat[:, t, :], ACT.Exp).then_inc(c.exp_ready.sem, 1)
                    for g in range(NG):
                        act.wait_ge(c.A.full, c.A.filled(b, ("fT", g)))
                        src = c.A.slot(("fT", g))
                        act.activation(fT[:, :, g, :], src.rearrange("p (w s) -> p w s", s=S), ACT.Copy)
                        spread_heads(lambda dst, src, rows: act.activation(dst, src, ACT.Copy), c.qm, src[:, 0:S],
                                     range(4 * g, 4 * g + 4), 32).then_inc(c.A.empty, 1)
                    act_transposed_attn(c, act, b, oT, D)

            @block.gpsimd
            def _(pool):
                pool.memset(c.qm[:, :, :], 0.0).then_inc(c.setup_done, 1)
                pool.memset(c.v[:, :, :, 17:32], 0.0)
                pool.memset(c.v[:, :, :, 16:17], 1.0).then_inc(c.setup_done, 1)
                with pool.Fori(0, B) as b:
                    pool_rstd(c, pool, b, 0)
        c.finish()



def layer_l0_xattn(nc, c, ins):
    with ExitStack() as ctx:
        sb = allocator(nc, ctx, "l0_xattn")
        wq, wk = sb("wq", [P, KD, NG * P]), sb("wk", [P, KD, NG * P])
        wv, wo = sb("wv", [P, KD, D]), sb("wo", [P, KD, D])
        qbias, kbias = sb("qbias", [P, NG]), sb("kbias", [P, NG])
        vbias, obias = sb("vbias", [1, D]), sb("obias", [1, D])
        qm, kT = sb("qm", [P, H, S]), sb("kT", [P, NG, S])
        oT = sb("oT", [P, KD, S])
        alloc_softmax(c, sb, T, 32, D)
        begin(c, a_slots=4, A=KD + KD + NG + 2 + H * T + KD, V=NG + H * T + NG + 2, O=NG,
              x_here=1, ctx_here=1, var_ready=1, rstd_ready=1, heads_ready=NG, max_ready=H * T)
        c.expect_setup(1)

        with nc.Block() as block:
            @block.sync
            def _(sp):
                for dst, name in ((wq, "wq1"), (wk, "wk1"), (wv, "wv1"), (wo, "wo1"), (qbias, "qbias1"),
                                  (kbias, "kbias1"), (vbias, "vbias1"), (obias, "obias1")):
                    c.load(sp, dst, ins[name])

            @block.tensor
            def _(pe):
                pe.wait_ge(c.loaded, c.load_count)
                pe.wait_ge(c.setup_done, c.setup_dones)
                with pe.Fori(0, B) as b:
                    pe_transpose_x_halves(c, pe, b)
                    pe_transpose_ctx_halves(c, pe, b)
                    pe.wait_ge(c.A.empty, c.A.copied(b, ("xT", KD - 1)))
                    for g in range(NG):
                        pe.wait_ge(c.V.empty, c.V.vacant(b, ("q", g)))
                        out = c.V.slot(("q", g))
                        mm(pe, out, [(wq[:, k, g * P:(g + 1) * P], c.xT[:, k, :]) for k in range(KD)]).then_inc(c.V.full, 1)
                    pe.wait_ge(c.A.empty, c.A.copied(b, ("cT", KD - 1)))
                    for g in range(NG):
                        pe.wait_ge(c.A.empty, c.A.vacant(b, ("k", g)))
                        mm(pe, c.A.slot(("k", g)), [(wk[:, k, g * P:(g + 1) * P], c.cT[:, k, :]) for k in range(KD)]).then_inc(c.A.full, 1)
                    for i in range(2):
                        pe.wait_ge(c.A.empty, c.A.vacant(b, ("v", i)))
                        out = c.A.slot(("v", i))
                        for t in range(2):
                            cols = slice((2 * i + t) * P, (2 * i + t + 1) * P)
                            last = mm(pe, out[:, t * D:(t + 1) * D], [(c.cT[:, k, cols], wv[:, k, :]) for k in range(KD)]
                                      + [(c.ones[0:1, 0:P], vbias[0:1, :])])
                        last.then_inc(c.A.full, 1)
                    pe.wait_ge(c.V.empty, c.V.copied(b, ("q", NG - 1)))
                    pe.wait_ge(c.A.empty, c.A.copied(b, ("v", 1)))

                    def scores(out, h, qt):
                        n = qt * P
                        q = qm[:, h, n:n + P]
                        if qt:
                            pe.matmul(out[:, 0:n], q, kT[:, h // 4, 0:n], start=True, stop=True)
                        pe.matmul(out[:, n:n + P], c.ident16[:, :], c.causal_qk[:, :], start=True, stop=False)
                        return pe.matmul(out[:, n:n + P], q, kT[:, h // 4, n:n + P], start=False, stop=True)

                    pe_attend(c, pe, b, T, scores, causal=True)
                    pe_transpose_attn(c, pe, b, c.on, D)
                    pe.wait_ge(c.A.empty, c.A.copied(b, ("oT", KD - 1)))
                    pe_project_out(c, pe, b, [lambda t, k=k: oT[:, k, t * P:(t + 1) * P] for k in range(KD)],
                                   [wo[:, k, :] for k in range(KD)], [obias[0:1, :]])

            @block.vector
            def _(dve):
                dve.wait_ge(c.loaded, c.load_count)
                dve.memset(qm[:, :, :], 0.0)
                dve.memset(c.v[:, :, :, :], 0.0)
                dve.tensor_scalar(qbias[:, :], qbias[:, :], 0.25, None, ALU.mult)
                dve.drain().then_inc(c.setup_done, 1)
                with dve.Fori(0, B) as b:
                    for g in range(NG):
                        dve.wait_ge(c.V.full, c.V.filled(b, ("q", g)))
                        spread_heads(lambda dst, src, rows: dve.tensor_scalar(dst, src, 0.25, qbias[rows, g:g + 1],
                                                                              ALU.mult, ALU.add),
                                     qm, c.V.slot(("q", g)), range(4 * g, 4 * g + 4), 32).then_inc(c.V.empty, 1)
                    dve_attend(c, dve, b, T, 16, causal=True)
                    dve_residual_norm(c, dve, b)

            @block.scalar
            def _(act):
                with act.Fori(0, B) as b:
                    act_fetch_x(c, act, b)
                    act_fetch_ctx(c, act, b)
                    act_transposed_x_halves(c, act, b)
                    act_transposed_ctx_halves(c, act, b)
                    for g in range(NG):
                        act.wait_ge(c.A.full, c.A.filled(b, ("k", g)))
                        act.activation(kT[:, g, :], c.A.slot(("k", g)), ACT.Identity, bias=kbias[:, g:g + 1]).then_inc(c.A.empty, 1)
                    for i in range(2):
                        act.wait_ge(c.A.full, c.A.filled(b, ("v", i)))
                        act.activation(c.v[:, 2 * i:2 * i + 2, :, 0:16].rearrange("p t h d -> p (t h) d"),
                                       c.A.slot(("v", i)).rearrange("p (a d) -> p a d", d=16), ACT.Copy).then_inc(c.A.empty, 1)
                    act_attend(c, act, b, T, causal=True)
                    act_transposed_attn(c, act, b, oT, D)

            @block.gpsimd
            def _(pool):
                with pool.Fori(0, B) as b:
                    pool_rstd(c, pool, b, 0)
        c.finish()



def layer_l0_ffn(nc, c, ins):
    with ExitStack() as ctx:
        sb = allocator(nc, ctx, "l0_ffn")
        E, FT = 8, 4
        w1, w2 = sb("w1", [P, E, KD, FT * P]), sb("w2", [P, E, FT, D])
        wg, gbias = sb("wg", [P, KD, E]), sb("gbias", [1, E])
        b1, b2 = sb("b1", [P, E * FT]), sb("b2", [E, D])
        rank = sb("rank", [P, T, E])
        hT = [sb(f"hT{i}", [P, FT, S]) for i in range(2)]
        logits, probs, left = sb("logits", [P, T, E]), sb("probs", [P, T, E]), sb("left", [P, T, E])
        key, pick, mask = sb("key", [P, T, E]), sb("pick", [P, T, E]), sb("mask", [P, T, E])
        top = sb("top", [P, T])
        gates, gatesT, mixed_b2 = sb("gates", [P, T, P]), sb("gatesT", [P, S]), sb("mixed_b2", [P, T, D])
        begin(c, A=4 + 2 * E, V=2 * E, O=0, x_here=1, var_ready=1, rstd_ready=1, exp_in=1, exp_ready=1, vec_ready=1)
        c.expect_setup(0)

        with nc.Block() as block:
            @block.sync
            def _(sp):
                for dst, name in ((wg, "wg2"), (gbias, "gbias2"), (rank, "rank2"), (b1, "b1_2"), (b2, "b2_2"),
                                  (w1, "w1_2"), (w2, "w2_2")):
                    c.load(sp, dst, ins[name])

            @block.tensor
            def _(pe):
                pe.wait_ge(c.loaded, c.load_count)
                with pe.Fori(0, B) as b:
                    pe_transpose_x(c, pe, b)
                    pe.wait_ge(c.A.empty, c.A.copied(b, "xT"))
                    pe.wait_ge(c.A.empty, c.A.vacant(b, "logits"))
                    out = c.A.slot("logits")
                    for t in range(T):
                        last = mm(pe, out[:, t * E:(t + 1) * E],
                                  [(c.xT[:, k, t * P:(t + 1) * P], wg[:, k, :]) for k in range(KD)]
                                  + [(c.ones[0:1, 0:P], gbias[0:1, :])])
                    last.then_inc(c.A.full, 1)

                    def up(e):
                        for i in range(2):
                            pe.wait_ge(c.A.empty, c.A.vacant(b, ("h", e, i)))
                            out = c.A.slot(("h", e, i))
                            for m in (2 * i, 2 * i + 1):
                                last = mm(pe, out[:, (m - 2 * i) * S:(m - 2 * i + 1) * S],
                                          [(w1[:, e, k, m * P:(m + 1) * P], c.xT[:, k, :]) for k in range(KD)])
                            last.then_inc(c.A.full, 1)

                    def down(e):
                        pe.wait_ge(c.A.empty, c.A.copied(b, ("h", e, 1)))
                        for i in range(2):
                            pe.wait_ge(c.V.empty, c.V.vacant(b, ("o", e, i)))
                            out = c.V.slot(("o", e, i))
                            for t in (2 * i, 2 * i + 1):
                                last = mm(pe, out[:, (t - 2 * i) * D:(t - 2 * i + 1) * D],
                                          [(hT[e % 2][:, f, t * P:(t + 1) * P], w2[:, e, f, :]) for f in range(FT)])
                            last.then_inc(c.V.full, 1)

                    up(0)
                    pe.wait_ge(c.A.empty, c.A.vacant(b, "gatesT"))
                    out = c.A.slot("gatesT")
                    pe.wait_ge(c.vec_ready.sem, c.vec_ready.at(b, 1))
                    for t in range(T):
                        last = pe.transpose(out[:, t * P:(t + 1) * P], gates[:, t, :], c.ident[:, :])
                    last.then_inc(c.A.full, 1)
                    pe.wait_ge(c.A.empty, c.A.vacant(b, "mixed_b2"))
                    out = c.A.slot("mixed_b2")
                    pe.wait_ge(c.A.empty, c.A.copied(b, "gatesT"))
                    for t in range(T):
                        last = pe.matmul(out[:, t * D:(t + 1) * D], gatesT[0:E, t * P:(t + 1) * P], b2[0:E, :],
                                         start=True, stop=True)
                    last.then_inc(c.A.full, 1)
                    for e in range(E):
                        if e + 1 < E:
                            up(e + 1)
                        down(e)

            @block.vector
            def _(dve):
                dve.wait_ge(c.loaded, c.load_count)
                dve.memset(gates[:, :, :], 0.0)
                with dve.Fori(0, B) as b:
                    wide = [P, T, E]
                    dve.wait_ge(c.A.empty, c.A.copied(b, "logits"))
                    dve.tensor_reduce(top[:, :], logits[:, :, :], AX, ALU.max)
                    dve.drain()
                    dve.tensor_tensor(logits[:, :, :], logits[:, :, :],
                                                  top[:, :].unsqueeze(2).to_broadcast(wide), ALU.subtract).then_inc(c.exp_in.sem, 1)
                    dve.wait_ge(c.exp_ready.sem, c.exp_ready.at(b, 1))
                    dve.tensor_reduce(top[:, :], probs[:, :, :], AX, ALU.add)
                    dve.drain()
                    dve.reciprocal(top[:, :], top[:, :])
                    dve.drain()
                    dve.tensor_tensor(probs[:, :, :], probs[:, :, :], top[:, :].unsqueeze(2).to_broadcast(wide), ALU.mult)
                    dve.drain()
                    for i in range(2):
                        src = probs if i == 0 else left
                        dve.tensor_reduce(top[:, :], src[:, :, :], AX, ALU.max)
                        dve.drain()
                        dve.tensor_tensor(key[:, :, :], src[:, :, :], top[:, :].unsqueeze(2).to_broadcast(wide), ALU.is_equal)
                        dve.drain()
                        dve.tensor_tensor(key[:, :, :], key[:, :, :], rank[:, :, :], ALU.mult)
                        dve.drain()
                        dve.tensor_reduce(top[:, :], key[:, :, :], AX, ALU.max)
                        dve.drain()
                        dst = mask if i == 0 else pick
                        dve.tensor_tensor(dst[:, :, :], key[:, :, :], top[:, :].unsqueeze(2).to_broadcast(wide), ALU.is_equal)
                        dve.drain()
                        if i == 0:
                            dve.scalar_tensor_tensor(left[:, :, :], mask[:, :, :], -2.0, probs[:, :, :], ALU.mult, ALU.add)
                            dve.drain()
                    dve.tensor_tensor(mask[:, :, :], mask[:, :, :], pick[:, :, :], ALU.add)
                    dve.drain()
                    dve.tensor_tensor(mask[:, :, :], mask[:, :, :], probs[:, :, :], ALU.mult)
                    dve.drain()
                    dve.tensor_reduce(top[:, :], mask[:, :, :], AX, ALU.add)
                    dve.drain()
                    dve.tensor_scalar(top[:, :], top[:, :], 1e-9, None, ALU.add)
                    dve.drain()
                    dve.reciprocal(top[:, :], top[:, :])
                    dve.drain()
                    dve.tensor_tensor(gates[:, :, 0:E], mask[:, :, :],
                                                     top[:, :].unsqueeze(2).to_broadcast(wide), ALU.mult).then_inc(c.vec_ready.sem, 1)
                    dve.wait_ge(c.A.empty, c.A.copied(b, "mixed_b2"))
                    dve.tensor_tensor(c.r[:, :, :], mixed_b2[:, :, :], c.x[:, bass.ds(b * T, T), :], ALU.add)
                    dve.drain()
                    for e in range(E):
                        for i in range(2):
                            dve.wait_ge(c.V.full, c.V.filled(b, ("o", e, i)))
                            o = c.V.slot(("o", e, i))
                            for t in (2 * i, 2 * i + 1):
                                last = dve.scalar_tensor_tensor(c.r[:, t, :], o[:, (t - 2 * i) * D:(t - 2 * i + 1) * D],
                                                                gates[:, t, e:e + 1], c.r[:, t, :], ALU.mult, ALU.add)
                            last.then_inc(c.V.empty, 1)
                        dve.drain()
                    dve_norm(c, dve, b, 0, c.r, c.x[:, bass.ds(b * T, T), :])

            @block.scalar
            def _(act):
                with act.Fori(0, B) as b:
                    act_fetch_x(c, act, b)
                    act_transposed_x(c, act, b)
                    act.wait_ge(c.A.full, c.A.filled(b, "logits"))
                    src = c.A.slot("logits")
                    act.activation(logits[:, :, :].rearrange("p t e -> p (t e)"), src[:, 0:T * E], ACT.Copy).then_inc(c.A.empty, 1)
                    act.wait_ge(c.exp_in.sem, c.exp_in.at(b, 1))
                    act.activation(probs[:, :, :], logits[:, :, :], ACT.Exp, scale=0.2).then_inc(c.exp_ready.sem, 1)

                    def gelu(e):
                        for i in range(2):
                            act.wait_ge(c.A.full, c.A.filled(b, ("h", e, i)))
                            src = c.A.slot(("h", e, i))
                            for m in (2 * i, 2 * i + 1):
                                last = act.activation(hT[e % 2][:, m, :], src[:, (m - 2 * i) * S:(m - 2 * i + 1) * S],
                                                      ACT.Gelu, bias=b1[:, e * FT + m:e * FT + m + 1])
                            last.then_inc(c.A.empty, 1)

                    gelu(0)
                    act.wait_ge(c.A.full, c.A.filled(b, "gatesT"))
                    src = c.A.slot("gatesT")
                    act.activation(gatesT[:, :], src[:, 0:S], ACT.Copy).then_inc(c.A.empty, 1)
                    act.wait_ge(c.A.full, c.A.filled(b, "mixed_b2"))
                    src = c.A.slot("mixed_b2")
                    act.activation(mixed_b2[:, :, :].rearrange("p t d -> p (t d)"), src, ACT.Copy).then_inc(c.A.empty, 1)
                    for e in range(1, E):
                        gelu(e)

            @block.gpsimd
            def _(pool):
                with pool.Fori(0, B) as b:
                    pool_rstd(c, pool, b, 0)
        c.finish()



def layer_l1_attn(nc, c, ins):
    with ExitStack() as ctx:
        sb = allocator(nc, ctx, "l1_attn")
        wq, wk, wv = (sb(n, [P, KD, D]) for n in ("wq", "wk", "wv"))
        qT, kT, v = sb("qT", [P, KD, S]), sb("kT", [P, KD, S]), sb("v", [P, T, D])
        e, eT = sb("e", [P, T, S]), sb("eT", [P, T, S])
        nmax, rsum = sb("nmax", [P, T]), sb("rsum", [P, T])
        begin(c, A=6, V=6, O=0, x_here=1, var_ready=1, rstd_ready=1, exp_in=T, exp_ready=T)
        c.expect_setup(0)

        with nc.Block() as block:
            @block.sync
            def _(sp):
                for dst, name in ((wq, "wq3"), (wk, "wk3"), (wv, "wv3")):
                    c.load(sp, dst, ins[name])

            @block.tensor
            def _(pe):
                pe.wait_ge(c.loaded, c.load_count)
                with pe.Fori(0, B) as b:
                    pe_transpose_x(c, pe, b)
                    pe.wait_ge(c.A.empty, c.A.copied(b, "xT"))
                    for name, w in (("q", wq), ("k", wk)):
                        pe.wait_ge(c.A.empty, c.A.vacant(b, name))
                        out = c.A.slot(name)
                        for m in range(KD):
                            last = mm(pe, out[:, m * S:(m + 1) * S],
                                      [(w[:, k, m * P:(m + 1) * P], c.xT[:, k, :]) for k in range(KD)])
                        last.then_inc(c.A.full, 1)
                    pe.wait_ge(c.A.empty, c.A.vacant(b, "v"))
                    out = c.A.slot("v")
                    for t in range(T):
                        last = mm(pe, out[:, t * D:(t + 1) * D],
                                  [(c.xT[:, k, t * P:(t + 1) * P], wv[:, k, :]) for k in range(KD)])
                    last.then_inc(c.A.full, 1)
                    pe.wait_ge(c.A.empty, c.A.copied(b, "k"))
                    for t in range(T):
                        pe.wait_ge(c.V.empty, c.V.vacant(b, ("s", t)))
                        out = c.V.slot(("s", t))
                        mm(pe, out, [(kT[:, k, t * P:(t + 1) * P], qT[:, k, :]) for k in range(KD)]).then_inc(c.V.full, 1)
                    for i in range(2):
                        pe.wait_ge(c.A.empty, c.A.vacant(b, ("eT", i)))
                        out = c.A.slot(("eT", i))
                        if i == 0:
                            pe.wait_ge(c.exp_ready.sem, c.exp_ready.at(b, T))
                        for q in (2 * i, 2 * i + 1):
                            for t in range(T):
                                last = pe.transpose(out[:, (q - 2 * i) * S + t * P:(q - 2 * i) * S + (t + 1) * P],
                                                    e[:, t, q * P:(q + 1) * P], c.ident[:, :])
                        last.then_inc(c.A.full, 1)
                    pe.wait_ge(c.A.empty, c.A.copied(b, ("eT", 1)))
                    pe_project_out(c, pe, b, [lambda t, q=q: eT[:, q, t * P:(t + 1) * P] for q in range(T)],
                                   [v[:, q, :] for q in range(T)])

            @block.vector
            def _(dve):
                with dve.Fori(0, B) as b:
                    for t in range(T):
                        dve.wait_ge(c.V.full, c.V.filled(b, ("s", t)))
                        s = c.V.slot(("s", t))
                        dve.tensor_reduce(nmax[:, t:t + 1], s, AX, ALU.max)
                        dve.drain()
                        dve.tensor_scalar(e[:, t, :], s, nmax[:, t:t + 1], None, ALU.subtract).then_inc(c.V.empty, 1)
                        dve.drain().then_inc(c.exp_in.sem, 1)
                    for t in range(T):
                        dve.wait_ge(c.exp_ready.sem, c.exp_ready.at(b, t + 1))
                        dve.tensor_reduce(rsum[:, t:t + 1], e[:, t, :], AX, ALU.add)
                    dve.drain()
                    dve.reciprocal(rsum[:, :], rsum[:, :])
                    dve.drain()
                    for i in range(2):
                        dve.wait_ge(c.V.full, c.V.filled(b, ("y", i)))
                        y = c.V.slot(("y", i))
                        for t in (2 * i, 2 * i + 1):
                            last = dve.tensor_scalar(c.r[:, t, :], y[:, (t - 2 * i) * D:(t - 2 * i + 1) * D],
                                                     rsum[:, t:t + 1], None, ALU.mult)
                        last.then_inc(c.V.empty, 1)
                    dve.drain()
                    dve.tensor_tensor(c.r[:, :, :], c.r[:, :, :], c.x[:, bass.ds(b * T, T), :], ALU.add)
                    dve.drain()
                    dve_norm(c, dve, b, 0, c.r, c.x[:, bass.ds(b * T, T), :])

            @block.scalar
            def _(act):
                with act.Fori(0, B) as b:
                    act_fetch_x(c, act, b)
                    act_transposed_x(c, act, b)
                    for name, dst in (("q", qT), ("k", kT), ("v", v)):
                        act.wait_ge(c.A.full, c.A.filled(b, name))
                        src = c.A.slot(name)
                        act.activation(dst[:, :, :].rearrange("p a s -> p (a s)"), src, ACT.Copy).then_inc(c.A.empty, 1)
                    for t in range(T):
                        act.wait_ge(c.exp_in.sem, c.exp_in.at(b, t + 1))
                        act.activation(e[:, t, :], e[:, t, :], ACT.Exp, scale=1.0 / 16).then_inc(c.exp_ready.sem, 1)
                    for i in range(2):
                        act.wait_ge(c.A.full, c.A.filled(b, ("eT", i)))
                        src = c.A.slot(("eT", i))
                        act.activation(eT[:, 2 * i:2 * i + 2, :].rearrange("p a s -> p (a s)"), src, ACT.Copy).then_inc(c.A.empty, 1)

            @block.gpsimd
            def _(pool):
                with pool.Fori(0, B) as b:
                    pool_rstd(c, pool, b, 0)
        c.finish()



def layer_l1_xattn(nc, c, ins):
    with ExitStack() as ctx:
        sb = allocator(nc, ctx, "l1_xattn")
        lin, gate = sb("lin", [P, T, S]), sb("gate", [P, T, S])
        begin(c, A=4, V=2, O=0, x_here=1, ctx_here=1, var_ready=1, rstd_ready=1, vec_ready=2)

        with nc.Block() as block:
            @block.tensor
            def _(pe):
                with pe.Fori(0, B) as b:
                    pe_transpose_x(c, pe, b)
                    pe_transpose_ctx(c, pe, b)
                    pe.wait_ge(c.A.empty, c.A.copied(b, "cT"))
                    for i in range(2):
                        pe.wait_ge(c.A.empty, c.A.vacant(b, ("h", i)))
                        out = c.A.slot(("h", i))
                        for f in (2 * i, 2 * i + 1):
                            last = mm(pe, out[:, (f - 2 * i) * S:(f - 2 * i + 1) * S],
                                      [(c.cT[:, k, f * P:(f + 1) * P], c.xT[:, k, :]) for k in range(KD)])
                        last.then_inc(c.A.full, 1)
                    pe.wait_ge(c.vec_ready.sem, c.vec_ready.at(b, 2))
                    alone(c, pe)
                    pe_project_out(c, pe, b, [lambda t, f=f: gate[:, f, t * P:(t + 1) * P] for f in range(T)],
                                   [c.ctx[:, bass.ds(b * T + f, 1), :] for f in range(T)])

            @block.vector
            def _(dve):
                with dve.Fori(0, B) as b:
                    for i in range(2):
                        dve.wait_ge(c.A.empty, c.A.copied(b, ("h", i)))
                        sl = slice(2 * i, 2 * i + 2)
                        dve.tensor_tensor(gate[:, sl, :], gate[:, sl, :], lin[:, sl, :], ALU.mult).then_inc(c.vec_ready.sem, 1)
                    dve_residual_norm(c, dve, b)

            @block.scalar
            def _(act):
                with act.Fori(0, B) as b:
                    act_fetch_x(c, act, b)
                    act_fetch_ctx(c, act, b)
                    act_transposed_x(c, act, b)
                    act_transposed_ctx(c, act, b)
                    for i in range(2):
                        act.wait_ge(c.A.full, c.A.filled(b, ("h", i)))
                        src = c.A.slot(("h", i))
                        sl = slice(2 * i, 2 * i + 2)
                        act.activation(gate[:, sl, :].rearrange("p a s -> p (a s)"), src, ACT.Gelu)
                        act.activation(lin[:, sl, :].rearrange("p a s -> p (a s)"), src, ACT.Copy).then_inc(c.A.empty, 1)

            @block.gpsimd
            def _(pool):
                with pool.Fori(0, B) as b:
                    pool_rstd(c, pool, b, 0)
        c.finish()



def layer_l1_ffn(nc, c, ins):
    with ExitStack() as ctx:
        sb = allocator(nc, ctx, "l1_ffn")
        FT = 8
        w1, w2 = sb("w1", [P, KD, FT * P]), sb("w2", [P, FT, D])
        w1b, w2b = sb("w1b", [P, KD, FT * P]), sb("w2b", [P, FT, D])
        b1, b2 = sb("b1", [P, FT]), sb("b2", [1, D])
        shiftm, tokens, scale = sb("shiftm", [P, P]), sb("tokens", [P, 8]), sb("scale", [P, 1])
        before = sb("before", [P, D])
        outer1, outer2 = sb("outer1", [P, 4, D]), sb("outer2", [P, 4, 4, D // 4])
        hT = sb("hT", [P, FT, S])
        begin(c, A=6, V=10, O=0, x_here=1, var_ready=1, rstd_ready=1, vec_ready=2)
        c.expect_setup(0)

        with nc.Block() as block:
            @block.sync
            def _(sp):
                for dst, name in ((w1, "w1_5"), (w2, "w2_5"), (b1, "b1_5"), (b2, "b2_5"), (shiftm, "shift5"),
                                  (tokens, "tokens5"), (scale, "scale5")):
                    c.load(sp, dst, ins[name])

            @block.tensor
            def _(pe):
                pe.wait_ge(c.loaded, c.load_count)
                with pe.Fori(0, B) as b:
                    pe_transpose_x(c, pe, b)
                    pe.wait_ge(c.A.empty, c.A.vacant(b, "before"))
                    out = c.A.slot("before")
                    pe.matmul(out[:, 0:D], shiftm[:, :], c.xn[:, 0, :], start=True, stop=True).then_inc(c.A.full, 1)
                    pe.wait_ge(c.vec_ready.sem, c.vec_ready.at(b, 1))
                    for k in range(KD):
                        for i in range(2):
                            pe.wait_ge(c.V.empty, c.V.vacant(b, ("m1", k, i)))
                            out = c.V.slot(("m1", k, i))
                            pe.matmul(out, c.xn[:, 0, k * P:(k + 1) * P], outer1[:, 2 * i:2 * i + 2, :],
                                                 start=True, stop=True).then_inc(c.V.full, 1)
                    pe.wait_ge(c.vec_ready.sem, c.vec_ready.at(b, 2))
                    for r in range(4):
                        pe.wait_ge(c.V.empty, c.V.vacant(b, ("m2", r)))
                        out = c.V.slot(("m2", r))
                        for k in range(KD):
                            last = pe.matmul(out[:, k * D:(k + 1) * D], c.xn[:, 0, k * P:(k + 1) * P],
                                             outer2[:, r, :, :], start=True, stop=True)
                        last.then_inc(c.V.full, 1)
                    pe.wait_ge(c.A.empty, c.A.copied(b, "xT"))
                    pe.wait_ge(c.V.empty, c.V.copied(b, ("m1", 1, 1)))
                    for i in range(FT // 2):
                        pe.wait_ge(c.A.empty, c.A.vacant(b, ("h", i)))
                        out = c.A.slot(("h", i))
                        for m in (2 * i, 2 * i + 1):
                            last = mm(pe, out[:, (m - 2 * i) * S:(m - 2 * i + 1) * S],
                                      [(w1b[:, k, m * P:(m + 1) * P], c.xT[:, k, :]) for k in range(KD)])
                        last.then_inc(c.A.full, 1)
                    pe.wait_ge(c.A.empty, c.A.copied(b, ("h", FT // 2 - 1)))
                    pe.wait_ge(c.V.empty, c.V.copied(b, ("m2", 3)))
                    pe_project_out(c, pe, b, [lambda t, f=f: hT[:, f, t * P:(t + 1) * P] for f in range(FT)],
                                   [w2b[:, f, :] for f in range(FT)], [b2[0:1, :]])

            @block.vector
            def _(dve):
                dve.wait_ge(c.loaded, c.load_count)
                dve.tensor_scalar(tokens[:, :], tokens[:, :], scale[:, 0:1], None, ALU.mult)
                dve.drain()
                with dve.Fori(0, B) as b:
                    dve.wait_ge(c.A.empty, c.A.copied(b, "before"))
                    for a in range(4):
                        last = dve.tensor_scalar(outer1[:, a, :], before[:, :], tokens[:, a:a + 1], None, ALU.mult)
                    last.then_inc(c.vec_ready.sem, 1)
                    for a in range(4):
                        last = dve.tensor_scalar(outer2[:, :, a, :], before[:, :].rearrange("p (o r) -> p r o", r=4),
                                                 tokens[:, 4 + a:5 + a], None, ALU.mult)
                    last.then_inc(c.vec_ready.sem, 1)
                    for k in range(KD):
                        for i in range(2):
                            dve.wait_ge(c.V.full, c.V.filled(b, ("m1", k, i)))
                            m = c.V.slot(("m1", k, i))
                            dve.tensor_tensor(w1b[:, k, i * S:(i + 1) * S], m, w1[:, k, i * S:(i + 1) * S], ALU.add).then_inc(c.V.empty, 1)
                    for r in range(4):
                        dve.wait_ge(c.V.full, c.V.filled(b, ("m2", r)))
                        m = c.V.slot(("m2", r)).rearrange("p (k d) -> p k d", d=D)
                        dve.tensor_tensor(w2b[:, 2 * r:2 * r + 2, :], m, w2[:, 2 * r:2 * r + 2, :], ALU.add).then_inc(c.V.empty, 1)
                    dve_residual_norm(c, dve, b)

            @block.scalar
            def _(act):
                with act.Fori(0, B) as b:
                    act_fetch_x(c, act, b)
                    act_transposed_x(c, act, b)
                    act.wait_ge(c.A.full, c.A.filled(b, "before"))
                    src = c.A.slot("before")
                    act.activation(before[:, :], src[:, 0:D], ACT.Copy).then_inc(c.A.empty, 1)
                    for i in range(FT // 2):
                        act.wait_ge(c.A.full, c.A.filled(b, ("h", i)))
                        src = c.A.slot(("h", i))
                        for m in (2 * i, 2 * i + 1):
                            last = act.activation(hT[:, m, :], src[:, (m - 2 * i) * S:(m - 2 * i + 1) * S], ACT.Gelu,
                                                  bias=b1[:, m:m + 1])
                        last.then_inc(c.A.empty, 1)

            @block.gpsimd
            def _(pool):
                with pool.Fori(0, B) as b:
                    pool_rstd(c, pool, b, 0)
        c.finish()



def layer_l2_attn(nc, c, ins):
    with ExitStack() as ctx:
        sb = allocator(nc, ctx, "l2_attn")
        wq, wk = sb("wq", [P, KD, NG * P]), sb("wk", [P, KD, NG * P])
        wv, wo, wn = sb("wv", [P, KD, D]), sb("wo", [P, KD, D]), sb("wn", [P, KD, H])
        qbias, kbias = sb("qbias", [P, NG]), sb("kbias", [P, NG])
        vbias, obias, nbias = sb("vbias", [1, D]), sb("obias", [1, D]), sb("nbias", [1, H])
        qT, kT, kn = sb("qT", [P, NG, S]), sb("kT", [P, NG, S]), sb("kn", [P, NG, T, P])
        oT, expn = sb("oT", [P, KD, S]), sb("expn", [P, T, H])
        alloc_linear(c, sb)
        begin(c, A=1 + 4 + 2 + 2 + 1, V=NG * (T + 2) + 2, O=NG, x_here=1, var_ready=1, rstd_ready=1, heads_ready=NG)
        c.expect_setup(2)

        with nc.Block() as block:
            @block.sync
            def _(sp):
                for dst, name in ((wq, "wq6"), (wk, "wk6"), (wv, "wv6"), (wo, "wo6"), (wn, "wn6"), (qbias, "qbias6"),
                                  (kbias, "kbias6"), (vbias, "vbias6"), (obias, "obias6"), (nbias, "nbias6"),
                                  (c.causal01, "causal01"), (c.blocks, "blocks")):
                    c.load(sp, dst, ins[name])

            @block.tensor
            def _(pe):
                pe.wait_ge(c.loaded, c.load_count)
                pe.wait_ge(c.setup_done, c.setup_dones)
                with pe.Fori(0, B) as b:
                    pe_transpose_x(c, pe, b)
                    pe.wait_ge(c.A.empty, c.A.copied(b, "xT"))
                    for name, w in (("q", wq), ("k", wk)):
                        for i in range(2):
                            pe.wait_ge(c.A.empty, c.A.vacant(b, (name, i)))
                            out = c.A.slot((name, i))
                            for g in (2 * i, 2 * i + 1):
                                last = mm(pe, out[:, (g - 2 * i) * S:(g - 2 * i + 1) * S],
                                          [(w[:, k, g * P:(g + 1) * P], c.xT[:, k, :]) for k in range(KD)])
                            last.then_inc(c.A.full, 1)
                    for name, w, bias, n in (("v", wv, vbias, D), ("n", wn, nbias, H)):
                        pe.wait_ge(c.A.empty, c.A.vacant(b, name))
                        out = c.A.slot(name)
                        for t in range(T):
                            last = mm(pe, out[:, t * n:(t + 1) * n],
                                      [(c.xT[:, k, t * P:(t + 1) * P], w[:, k, :]) for k in range(KD)]
                                      + [(c.ones[0:1, 0:P], bias[0:1, :])])
                        last.then_inc(c.A.full, 1)
                    pe.wait_ge(c.A.empty, c.A.copied(b, ("k", 1)))
                    for i in range(2):
                        pe.wait_ge(c.A.empty, c.A.vacant(b, ("kn", i)))
                        out = c.A.slot(("kn", i))
                        for g in (2 * i, 2 * i + 1):
                            for t in range(T):
                                at = ((g - 2 * i) * T + t) * P
                                last = pe.transpose(out[:, at:at + P], kT[:, g, t * P:(t + 1) * P], c.ident[:, :])
                        last.then_inc(c.A.full, 1)
                    pe.wait_ge(c.A.empty, c.A.copied(b, ("kn", 1)))
                    pe_linear(c, pe, b, lambda g: qT[:, g, :], lambda g: kT[:, g, :], lambda g, t: kn[:, g, t, :])
                    pe_transpose_attn(c, pe, b, c.on, D)
                    pe.wait_ge(c.A.empty, c.A.copied(b, ("oT", 0)))
                    pe_project_out(c, pe, b, [lambda t, k=k: oT[:, k, t * P:(t + 1) * P] for k in range(KD)],
                                   [wo[:, k, :] for k in range(KD)], [obias[0:1, :]])

            @block.vector
            def _(dve):
                dve.memset(c.v[:, :, :, :], 0.0).then_inc(c.setup_done, 1)
                dve.wait_ge(c.loaded, c.load_count)
                with dve.Fori(0, B) as b:
                    def factors(g, o):
                        if g == 0:
                            dve.wait_ge(c.A.empty, c.A.copied(b, "n"))
                        return expn[:, :, 4 * g:4 * g + 4]

                    dve_linear(c, dve, b, factors)
                    dve_residual_norm(c, dve, b)

            @block.scalar
            def _(act):
                act.wait_ge(c.loaded, c.load_count)
                act.wait_ge(c.setup_done, c.setup_dones)
                with act.Fori(0, B) as b:
                    act_fetch_x(c, act, b)
                    act_transposed_x(c, act, b)
                    for name, dst, bias in (("q", qT, qbias), ("k", kT, kbias)):
                        for i in range(2):
                            act.wait_ge(c.A.full, c.A.filled(b, (name, i)))
                            src = c.A.slot((name, i))
                            for g in (2 * i, 2 * i + 1):
                                last = act.activation(dst[:, g, :], src[:, (g - 2 * i) * S:(g - 2 * i + 1) * S],
                                                      ACT.Identity, bias=bias[:, g:g + 1])
                                if name == "q":
                                    last = spread_heads(
                                        lambda dst, src, rows: act.activation(dst, src, ACT.Identity, bias=bias[rows, g:g + 1]),
                                        c.qm, src[:, (g - 2 * i) * S:(g - 2 * i + 1) * S], range(4 * g, 4 * g + 4), 32)
                            last.then_inc(c.A.empty, 1)
                    act.wait_ge(c.A.full, c.A.filled(b, "v"))
                    src = c.A.slot("v")
                    act.activation(c.v[:, :, :, 0:16].rearrange("p t h d -> p (t h) d"),
                                   src.rearrange("p (a d) -> p a d", d=16), ACT.Copy).then_inc(c.A.empty, 1)
                    act.wait_ge(c.A.full, c.A.filled(b, "n"))
                    src = c.A.slot("n")
                    act.activation(expn[:, :, :].rearrange("p t h -> p (t h)"), src[:, 0:T * H], ACT.Exp, scale=-1.0).then_inc(c.A.empty, 1)
                    for i in range(2):
                        act.wait_ge(c.A.full, c.A.filled(b, ("kn", i)))
                        act.activation(kn[:, 2 * i:2 * i + 2, :, :].rearrange("p g t d -> p (g t d)"),
                                       c.A.slot(("kn", i)), ACT.Copy).then_inc(c.A.empty, 1)
                    act_transposed_attn(c, act, b, oT, D)

            @block.gpsimd
            def _(pool):
                pool.memset(c.qm[:, :, :], 0.0).then_inc(c.setup_done, 1)
                with pool.Fori(0, B) as b:
                    pool_rstd(c, pool, b, 0)
        c.finish()



KT2 = 2 * T
HD = 64
INNER = H * HD


def layer_l2_xattn(nc, c, ins):
    with ExitStack() as ctx:
        sb = allocator(nc, ctx, "l2_xattn")
        IT = INNER // P
        PAIRS = H // 2
        wq, wk, wv = (sb(n, [P, KD, INNER]) for n in ("wq", "wk", "wv"))
        wo = sb("wo", [P, IT, D])
        gain, shiftc = sb("gain", [P, 2, KD]), sb("shiftc", [P, 2, KD])
        mask_row8 = sb("mask_row8", [1, B * S], mybir.dt.uint8)
        hide_rows, hide = sb("hide_rows", [P, B, S], BF16), sb("hide", [P, S], BF16)
        ones16 = sb("ones16", [P, P], BF16)
        qm = sb("qm", [P, 4, S])
        kT = sb("kT", [P, 2, 2 * S])
        alloc_softmax(c, sb, KT2, HD, INNER, span=2)
        oT = c.pTs[:, :, :, :].rearrange("p r k q -> p (r k q)")[:, 0:IT * S].rearrange("p (m s) -> p m s", s=S)
        begin(c, A=KD + KT2 + 2 * PAIRS + H * T + IT // 2, V=KD + H * T * 2 + 2 * PAIRS + 2, O=2 * PAIRS,
              ctx_here=1, x_here=1, var_ready=3, rstd_ready=3, heads_ready=2 * PAIRS, max_ready=H * T)
        c.expect_setup(1)

        with nc.Block() as block:
            @block.sync
            def _(sp):
                for dst, name in ((mask_row8, "mask_row7"), (gain, "gain7"), (shiftc, "shift7"),
                                  (wq, "wq7"), (wk, "wk7"), (wv, "wv7"), (wo, "wo7")):
                    c.load(sp, dst, ins[name])

            @block.tensor
            def _(pe):
                pe.wait_ge(c.loaded, c.load_count)
                pe.wait_ge(c.setup_done, c.setup_dones)
                with pe.Fori(0, B) as b:
                    for k in range(KD):
                        pe.wait_ge(c.V.empty, c.V.vacant(b, ("zx", k)))
                        out = c.V.slot(("zx", k))
                        pe.wait_ge(c.x_here.sem, c.x_here.at(b, 1))
                        for t in range(T):
                            last = pe.transpose(out[:, t * P:(t + 1) * P], c.xn[:, t, k * P:(k + 1) * P], c.ident[:, :])
                        last.then_inc(c.V.full, 1)
                    for k in range(KD):
                        pe.wait_ge(c.A.empty, c.A.vacant(b, ("zc", k)))
                        out = c.A.slot(("zc", k))
                        pe.wait_ge(c.ctx_here.sem, c.ctx_here.at(b, 1))
                        for t in range(T):
                            last = pe.transpose(out[:, t * P:(t + 1) * P], c.ctxn[:, t, k * P:(k + 1) * P], c.ident[:, :])
                        last.then_inc(c.A.full, 1)

                    def project_pair(i):
                        g, rest = divmod(i + AHEAD, 2 * T)
                        if 0 < g < PAIRS and rest == 0:
                            pe_pair(g)

                    def pe_pair(g):
                        cols = slice(g * P, (g + 1) * P)
                        pe.wait_ge(c.A.empty, c.A.vacant(b, ("q", g)))
                        mm(pe, c.A.slot(("q", g))[:, 0:S], [(wq[:, k, cols], c.xT[:, k, :]) for k in range(KD)]).then_inc(c.A.full, 1)
                        pe.wait_ge(c.A.empty, c.A.vacant(b, ("k", g)))
                        out = c.A.slot(("k", g))
                        for half, zT in ((0, c.cT), (1, c.xT)):
                            last = mm(pe, out[:, half * S:(half + 1) * S], [(wk[:, k, cols], zT[:, k, :]) for k in range(KD)])
                        last.then_inc(c.A.full, 1)

                    pe.wait_ge(c.A.empty, c.A.copied(b, ("zc", 1)))
                    pe.wait_ge(c.V.empty, c.V.copied(b, ("zx", 1)))
                    for kt in range(KT2):
                        pe.wait_ge(c.A.empty, c.A.vacant(b, ("v", kt)))
                        out = c.A.slot(("v", kt))
                        zT = c.cT if kt < T else c.xT
                        for i in range(2):
                            last = mm(pe, out[:, i * S:(i + 1) * S],
                                      [(zT[:, k, kt % T * P:(kt % T + 1) * P], wv[:, k, i * S:(i + 1) * S]) for k in range(KD)])
                        last.then_inc(c.A.full, 1)
                    pe_pair(0)

                    def scores(out, h, qt):
                        g = h // 2
                        if qt == 0:
                            pe.wait_ge(c.A.empty, c.A.copied(b, ("k", g)))
                        q = qm[:, h % 4, qt * P:(qt + 1) * P]
                        pe.matmul(out[:, 0:S], ones16[:, :], hide[:, :], start=True, stop=False)
                        pe.matmul(out[:, 0:S], q, kT[:, g % 2, 0:S], start=False, stop=True)
                        return pe.matmul(out[:, S:2 * S], q, kT[:, g % 2, S:2 * S], start=True, stop=True)

                    pe_attend(c, pe, b, KT2, scores, before_unit=project_pair)
                    pe_transpose_attn(c, pe, b, c.on, INNER)
                    pe.wait_ge(c.A.empty, c.A.copied(b, ("oT", IT // 2 - 1)))
                    pe_project_out(c, pe, b, [lambda t, m=m: oT[:, m, t * P:(t + 1) * P] for m in range(IT)],
                                   [wo[:, m, :] for m in range(IT)])

            @block.vector
            def _(dve):
                dve.wait_ge(c.loaded, c.load_count)
                dve.memset(hide_rows[:, :, :], 0.0)
                dve.drain()
                dve.tensor_scalar(hide_rows[0:1, :, :].rearrange("p b s -> p (b s)"), mask_row8[:, :], 1.0, 1e30,
                                  ALU.subtract, ALU.mult)
                dve.memset(ones16[:, :], 1.0)
                dve.memset(qm[:, :, :], 0.0)
                dve.drain().then_inc(c.setup_done, 1)
                with dve.Fori(0, B) as b:
                    here = bass.ds(b * T, T)
                    dve_norm(c, dve, b, 0, c.x[:, here, :], c.xn).then_inc(c.x_here.sem, 1)
                    dve_norm(c, dve, b, 1, c.ctx[:, here, :], c.ctxn).then_inc(c.ctx_here.sem, 1)
                    for k in range(KD):
                        dve.wait_ge(c.V.full, c.V.filled(b, ("zx", k)))
                        src = c.V.slot(("zx", k))
                        dve.tensor_scalar(c.xT[:, k, :], src, gain[:, 1, k:k + 1], shiftc[:, 1, k:k + 1],
                                                      ALU.mult, ALU.add).then_inc(c.V.empty, 1)
                    dve_attend(c, dve, b, KT2, HD)
                    dve_residual_norm(c, dve, b, 2)

            @block.scalar
            def _(act):
                act.wait_ge(c.loaded, c.load_count)
                act.wait_ge(c.setup_done, c.setup_dones)
                with act.Fori(0, B) as b:
                    alone(c, act)
                    act.activation(hide[:, :], hide_rows[:, bass.ds(b, 1), :].rearrange("p b s -> p (b s)"), ACT.Copy)
                    for k in range(KD):
                        act.wait_ge(c.A.full, c.A.filled(b, ("zc", k)))
                        src = c.A.slot(("zc", k))
                        act.activation(c.cT[:, k, :], src[:, 0:S], ACT.Identity,
                                                   bias=shiftc[:, 0, k:k + 1], scale=gain[:, 0, k:k + 1]).then_inc(c.A.empty, 1)
                    act.drain()
                    for kt in range(KT2):
                        act.wait_ge(c.A.full, c.A.filled(b, ("v", kt)))
                        src = c.A.slot(("v", kt)).rearrange("p (h d) -> p h d", d=HD)
                        act.activation(c.v[:, kt, :, 0:HD], src, ACT.Copy).then_inc(c.A.empty, 1)

                    def act_pair(g):
                        act.wait_ge(c.A.full, c.A.filled(b, ("q", g)))
                        src = c.A.slot(("q", g))
                        spread_heads(lambda dst, src, rows: act.activation(dst, src, ACT.Copy, scale=HD ** -0.5),
                                     qm, src[:, 0:S], (2 * g % 4, 2 * g % 4 + 1), HD).then_inc(c.A.empty, 1)
                        act.wait_ge(c.A.full, c.A.filled(b, ("k", g)))
                        act.activation(kT[:, g % 2, :], c.A.slot(("k", g)), ACT.Copy).then_inc(c.A.empty, 1)

                    def copy_pair(i):
                        g, rest = divmod(i + AHEAD, 2 * T)
                        if 0 < g < PAIRS and rest == 0:
                            act_pair(g)

                    act_pair(0)
                    act_attend(c, act, b, KT2, before_unit=copy_pair)
                    act_transposed_attn(c, act, b, oT, INNER)

            @block.gpsimd
            def _(pool):
                with pool.Fori(0, B) as b:
                    for j in range(3):
                        pool_rstd(c, pool, b, j)
        c.finish()



def dve_scales(c, dve, peak, scale, inv):
    dve.tensor_scalar(scale, peak, 1e-6, 1.0 / 127.0, ALU.max, ALU.mult)
    dve.drain()
    dve.reciprocal(inv, scale)
    dve.drain()


def layer_l2_ffn(nc, c, ins):
    with ExitStack() as ctx:
        sb = allocator(nc, ctx, "l2_ffn")
        FT = 8
        w1, w2 = sb("w1", [P, KD, FT * P]), sb("w2", [P, FT, D])
        w1q, w2q = sb("w1q", [P, KD, FT * P], BF16), sb("w2q", [P, FT, D], BF16)
        b1, b1s, b2 = sb("b1", [P, FT]), sb("b1s", [P, FT]), sb("b2", [1, D])
        peak, peaks = sb("peak", [P, 4]), sb("peaks", [P, 4])
        scale, inv = sb("scale", [P, 4]), sb("inv", [P, 4])
        out1, out2 = sb("out1", [P, 1]), sb("out2", [P, 1])
        magic = sb("magic", [P, 1])
        xr, xq = sb("xr", [P, KD, S]), sb("xq", [P, KD, S], BF16)
        h = sb("h", [P, B, FT, S])
        hbatch = sb("hbatch", [P, 1])
        hr, hq = sb("hr", [P, FT, S]), sb("hq", [P, FT, S], BF16)
        with nc.Block() as block:
            c.expect_setup(3)
            first = c.setup_dones

            @block.sync
            def _(sp):
                for dst, name in ((w1, "w1_8"), (w2, "w2_8"), (b1, "b1_8"), (b2, "b2_8")):
                    c.load(sp, dst, ins[name])

            @block.vector
            def _(dve):
                dve.wait_ge(c.loaded, c.load_count)
                dve.memset(magic[:, :], MAGIC)
                dve.memset(peak[:, :], 0.0)
                dve.drain()
                for i, src in enumerate((c.x, w1, w2)):
                    dve.tensor_reduce(peak[:, i:i + 1], src[:, :, :], mybir.AxisListType.XY, ALU.max,
                                      apply_absolute_value=True)
                dve.drain().then_inc(c.setup_done, 1)
                dve.wait_ge(c.setup_done, first - 1)
                dve_scales(c, dve, peaks[:, 0:3], scale[:, 0:3], inv[:, 0:3])
                dve.tensor_tensor(out1[:, :], scale[:, 0:1], scale[:, 1:2], ALU.mult)
                dve.drain()
                dve.tensor_scalar(b1s[:, :], b1[:, :], out1[:, 0:1], None, ALU.mult)
                for w, wq, i in ((w1, w1q, 1), (w2, w2q, 2)):
                    dve.tensor_scalar(w[:, :, :], w[:, :, :], inv[:, i:i + 1], MAGIC, ALU.mult, ALU.add)
                    dve.drain()
                    dve.tensor_scalar(wq[:, :, :], w[:, :, :], MAGIC, None, ALU.subtract)
                dve.drain().then_inc(c.setup_done, 1)

            @block.gpsimd
            def _(pool):
                pool.wait_ge(c.setup_done, first - 2)
                pool.partition_all_reduce(peaks[:, 0:3], peak[:, 0:3], P, RMAX).then_inc(c.setup_done, 1)

        begin(c, A=2 + FT // 2, V=0, O=0, x_here=1, vec_ready=1)
        with nc.Block() as block:
            @block.tensor
            def _(pe):
                with pe.Fori(0, B) as b:
                    pe_transpose_x_halves(c, pe, b)
                    pe.wait_ge(c.vec_ready.sem, c.vec_ready.at(b, 1))
                    for i in range(FT // 2):
                        pe.wait_ge(c.A.empty, c.A.vacant(b, ("h", i)))
                        out = c.A.slot(("h", i))
                        for m in (2 * i, 2 * i + 1):
                            last = mm(pe, out[:, (m - 2 * i) * S:(m - 2 * i + 1) * S],
                                      [(w1q[:, k, m * P:(m + 1) * P], xq[:, k, :]) for k in range(KD)])
                        last.then_inc(c.A.full, 1)

            @block.scalar
            def _(act):
                with act.Fori(0, B) as b:
                    act_fetch_x(c, act, b)
                    for k in range(KD):
                        act.wait_ge(c.A.full, c.A.filled(b, ("xT", k)))
                        src = c.A.slot(("xT", k))[:, 0:S]
                        act.activation(xr[:, k, :], src, ACT.Identity, bias=magic[:, 0:1], scale=inv[:, 0:1]).then_inc(c.A.empty, 1)
                    for i in range(FT // 2):
                        act.wait_ge(c.A.full, c.A.filled(b, ("h", i)))
                        src = c.A.slot(("h", i))
                        for m in (2 * i, 2 * i + 1):
                            alone(c, act)
                            last = act.activation(h[:, bass.ds(b, 1), m, :], src[:, (m - 2 * i) * S:(m - 2 * i + 1) * S],
                                                  ACT.Gelu, bias=b1s[:, m:m + 1], scale=out1[:, 0:1])
                        last.then_inc(c.A.empty, 1)

            @block.vector
            def _(dve):
                with dve.Fori(0, B) as b:
                    dve.wait_ge(c.A.empty, c.A.copied(b, ("xT", KD - 1)))
                    dve.tensor_scalar(xq[:, :, :], xr[:, :, :], MAGIC, None, ALU.subtract).then_inc(c.vec_ready.sem, 1)
                    dve.wait_ge(c.A.empty, c.A.copied(b, ("h", FT // 2 - 1)))
                    alone(c, dve)
                    dve.tensor_reduce(hbatch[:, :], h[:, bass.ds(b, 1), :, :], mybir.AxisListType.XYZ, ALU.max,
                                      apply_absolute_value=True)
                    dve.drain()
                    dve.tensor_tensor(peak[:, 3:4], peak[:, 3:4], hbatch[:, :], ALU.max)
                    dve.drain()
        c.finish()

        with nc.Block() as block:
            c.expect_setup(2)
            second = c.setup_dones

            @block.gpsimd
            def _(pool):
                pool.partition_all_reduce(peaks[:, 3:4], peak[:, 3:4], P, RMAX).then_inc(c.setup_done, 1)

            @block.vector
            def _(dve):
                dve.wait_ge(c.setup_done, second - 1)
                dve_scales(c, dve, peaks[:, 3:4], scale[:, 3:4], inv[:, 3:4])
                dve.tensor_tensor(out2[:, :], scale[:, 2:3], scale[:, 3:4], ALU.mult)
                dve.drain().then_inc(c.setup_done, 1)

        begin(c, A=0, V=2, O=0, var_ready=1, rstd_ready=1, exp_in=1, vec_ready=1)
        with nc.Block() as block:
            @block.tensor
            def _(pe):
                with pe.Fori(0, B) as b:
                    pe.wait_ge(c.vec_ready.sem, c.vec_ready.at(b, 1))
                    pe_project_out(c, pe, b, [lambda t, f=f: hq[:, f, t * P:(t + 1) * P] for f in range(FT)],
                                   [w2q[:, f, :] for f in range(FT)], [b2[0:1, :]])

            @block.scalar
            def _(act):
                with act.Fori(0, B) as b:
                    alone(c, act)
                    act.activation(hr[:, :, :].rearrange("p f s -> p (f s)"),
                                   h[:, bass.ds(b, 1), :, :].rearrange("p b f s -> p (b f s)"), ACT.Identity,
                                   bias=magic[:, 0:1], scale=inv[:, 3:4]).then_inc(c.exp_in.sem, 1)
                    act.wait_ge(c.vec_ready.sem, c.vec_ready.at(b, 1))

            @block.vector
            def _(dve):
                with dve.Fori(0, B) as b:
                    dve.wait_ge(c.exp_in.sem, c.exp_in.at(b, 1))
                    dve.tensor_scalar(hq[:, :, :], hr[:, :, :], MAGIC, None, ALU.subtract).then_inc(c.vec_ready.sem, 1)
                    for i in range(2):
                        dve.wait_ge(c.V.full, c.V.filled(b, ("y", i)))
                        y = c.V.slot(("y", i))
                        last = dve.tensor_scalar(c.r[:, 2 * i:2 * i + 2, :].rearrange("p t d -> p (t d)"), y,
                                                 out2[:, 0:1], None, ALU.mult)
                        last.then_inc(c.V.empty, 1)
                    dve.drain()
                    dve.tensor_tensor(c.r[:, :, :], c.r[:, :, :], c.x[:, bass.ds(b * T, T), :], ALU.add)
                    dve.drain()
                    dve_norm(c, dve, b, 0, c.r, c.x[:, bass.ds(b * T, T), :])

            @block.gpsimd
            def _(pool):
                with pool.Fori(0, B) as b:
                    pool_rstd(c, pool, b, 0)
        c.finish()



def layer_l3_attn(nc, c, ins):
    with ExitStack() as ctx:
        sb = allocator(nc, ctx, "l3_attn")
        wq, wk = sb("wq", [P, KD, NG * P]), sb("wk", [P, KD, NG * P])
        wv, wo = sb("wv", [P, KD, D]), sb("wo", [P, KD, D])
        rope, qrope = sb("rope", [P, S]), sb("qrope", [P, S])
        qm, kT = sb("qm", [P, H, S]), sb("kT", [P, NG, S])
        oT = sb("oT", [P, KD, S])
        alloc_softmax(c, sb, T, 32, D)
        begin(c, a_slots=4, A=KD + H * T + KD, V=2 * NG + 2 + H * T + NG + 2, O=NG,
              x_here=1, var_ready=1, rstd_ready=1, heads_ready=NG, max_ready=H * T)
        c.expect_setup(1)

        with nc.Block() as block:
            @block.sync
            def _(sp):
                for dst, name in ((wq, "wq9"), (wk, "wk9"), (wv, "wv9"), (wo, "wo9"), (rope, "rope9"), (qrope, "qrope9")):
                    c.load(sp, dst, ins[name])

            @block.tensor
            def _(pe):
                pe.wait_ge(c.loaded, c.load_count)
                pe.wait_ge(c.setup_done, c.setup_dones)
                with pe.Fori(0, B) as b:
                    pe_transpose_x_halves(c, pe, b)
                    pe.wait_ge(c.A.empty, c.A.copied(b, ("xT", KD - 1)))
                    for name, w in (("q", wq), ("k", wk)):
                        for g in range(NG):
                            pe.wait_ge(c.V.empty, c.V.vacant(b, (name, g)))
                            out = c.V.slot((name, g))
                            mm(pe, out, [(w[:, k, g * P:(g + 1) * P], c.xT[:, k, :]) for k in range(KD)]).then_inc(c.V.full, 1)
                    pe_project_values(c, pe, b, c.xT, wv)
                    pe.wait_ge(c.V.empty, c.V.copied(b, ("v", 1)))

                    def scores(out, h, qt):
                        return pe.matmul(out[:, 0:S], qm[:, h, qt * P:(qt + 1) * P], kT[:, h // 4, :], start=True, stop=True)

                    pe_attend(c, pe, b, T, scores)
                    pe_transpose_attn(c, pe, b, c.on, D)
                    pe.wait_ge(c.A.empty, c.A.copied(b, ("oT", KD - 1)))
                    pe_project_out(c, pe, b, [lambda t, k=k: oT[:, k, t * P:(t + 1) * P] for k in range(KD)],
                                   [wo[:, k, :] for k in range(KD)])

            @block.vector
            def _(dve):
                dve.wait_ge(c.loaded, c.load_count)
                dve.memset(qm[:, :, :], 0.0)
                dve.memset(c.v[:, :, :, :], 0.0)
                dve.drain().then_inc(c.setup_done, 1)
                with dve.Fori(0, B) as b:
                    for g in range(NG):
                        dve.wait_ge(c.V.full, c.V.filled(b, ("q", g)))
                        spread_heads(lambda dst, src, rows: dve.tensor_tensor(dst, src, qrope[rows, :], ALU.mult),
                                     qm, c.V.slot(("q", g)), range(4 * g, 4 * g + 4), 32).then_inc(c.V.empty, 1)
                    for g in range(NG):
                        dve.wait_ge(c.V.full, c.V.filled(b, ("k", g)))
                        dve.tensor_tensor(kT[:, g, :], c.V.slot(("k", g)), rope[:, :], ALU.mult).then_inc(c.V.empty, 1)
                    dve_values(c, dve, b)
                    dve_attend(c, dve, b, T, 16)
                    dve_residual_norm(c, dve, b)

            @block.scalar
            def _(act):
                with act.Fori(0, B) as b:
                    act_fetch_x(c, act, b)
                    act_transposed_x_halves(c, act, b)
                    act_attend(c, act, b, T)
                    act_transposed_attn(c, act, b, oT, D)

            @block.gpsimd
            def _(pool):
                with pool.Fori(0, B) as b:
                    pool_rstd(c, pool, b, 0)
        c.finish()



CLIP = 11.0


def layer_l3_xattn(nc, c, ins):
    with ExitStack() as ctx:
        sb = allocator(nc, ctx, "l3_xattn")
        IT = INNER // P
        wq, wk, wv = (sb(n, [P, KD, INNER]) for n in ("wq", "wk", "wv"))
        wo, obias = sb("wo", [P, IT, D]), sb("obias", [1, D])
        gain, shiftc = sb("gain", [P, 2, KD]), sb("shiftc", [P, 2, KD])
        PAIRS = H // 2
        qm, kT = sb("qm", [P, H, S]), sb("kT", [P, IT, S])
        v = sb("v", [P, T, H, HD])
        e = sb("e", [P, 4, T, S])
        half, total = sb("half", [P, 2, 2, S]), sb("total", [P, 4, S])
        ones = sb("ones", [P, HD])
        rec = sb("rec", [P, S])
        oT = kT
        begin(c, A=2 + 2 * (IT // 2) + T, V=H * T + 2, O=2 * PAIRS, ctx_here=1, x_here=1, var_ready=3, rstd_ready=3,
              exp_in=H, exp_ready=H, sums_ready=H)
        c.expect_setup(1)

        with nc.Block() as block:
            @block.sync
            def _(sp):
                for dst, name in ((gain, "gain10"), (shiftc, "shift10"), (wq, "wq10"), (wk, "wk10"), (wv, "wv10"),
                                  (wo, "wo10"), (obias, "obias10")):
                    c.load(sp, dst, ins[name])

            @block.tensor
            def _(pe):
                pe.wait_ge(c.loaded, c.load_count)
                pe.wait_ge(c.setup_done, c.setup_dones)
                with pe.Fori(0, B) as b:
                    for name, src, here in (("zx", c.xn, c.x_here), ("zc", c.ctxn, c.ctx_here)):
                        pe.wait_ge(c.A.empty, c.A.vacant(b, name))
                        out = c.A.slot(name)
                        pe.wait_ge(here.sem, here.at(b, 1))
                        for k in range(KD):
                            for t in range(T):
                                last = pe.transpose(out[:, k * S + t * P:k * S + (t + 1) * P], src[:, t, k * P:(k + 1) * P], c.ident[:, :])
                        last.then_inc(c.A.full, 1)
                    pe.wait_ge(c.A.empty, c.A.copied(b, "zc"))
                    for name, w, zT in (("q", wq, c.xT), ("k", wk, c.cT)):
                        for i in range(IT // 2):
                            pe.wait_ge(c.A.empty, c.A.vacant(b, (name, i)))
                            out = c.A.slot((name, i))
                            for m in (2 * i, 2 * i + 1):
                                last = mm(pe, out[:, (m - 2 * i) * S:(m - 2 * i + 1) * S],
                                          [(w[:, k, m * P:(m + 1) * P], zT[:, k, :]) for k in range(KD)])
                            last.then_inc(c.A.full, 1)
                    for t in range(T):
                        pe.wait_ge(c.A.empty, c.A.vacant(b, ("v", t)))
                        out = c.A.slot(("v", t))
                        for i in range(2):
                            last = mm(pe, out[:, i * S:(i + 1) * S],
                                      [(c.cT[:, k, t * P:(t + 1) * P], wv[:, k, i * S:(i + 1) * S]) for k in range(KD)])
                        last.then_inc(c.A.full, 1)
                    pe.wait_ge(c.A.empty, c.A.copied(b, ("k", IT // 2 - 1)))
                    pe.wait_ge(c.A.empty, c.A.copied(b, ("v", T - 1)))
                    for step in range(H + 2):
                        if step < H:
                            h = step
                            for t in range(T):
                                pe.wait_ge(c.V.empty, c.V.vacant(b, ("s", h, t)))
                                pe.matmul(c.V.slot(("s", h, t)), kT[:, h // 2, t * P:(t + 1) * P], qm[:, h, :],
                                          start=True, stop=True).then_inc(c.V.full, 1)
                        if step >= 3 and step % 2:
                            g = (step - 3) // 2
                            pe.wait_ge(c.O.empty, c.O.vacant(b, ("sum", g)))
                            pe.wait_ge(c.sums_ready.sem, c.sums_ready.at(b, 2 * g + 2))
                            out = c.O.slot(("sum", g))
                            for m in range(2):
                                last = pe.matmul(out[m * HD:(m + 1) * HD, :], ones[:, :], total[:, (2 * g + m) % 4, :],
                                                 start=True, stop=True)
                            last.then_inc(c.O.full, 1)
                            pe.wait_ge(c.O.empty, c.O.vacant(b, ("O", g)))
                            out = c.O.slot(("O", g))
                            for k in range(T):
                                for m in range(2):
                                    last = pe.matmul(out[m * HD:(m + 1) * HD, :], v[:, k, 2 * g + m, :],
                                                     e[:, (2 * g + m) % 4, k, :], start=k == 0, stop=k == T - 1)
                            last.then_inc(c.O.full, 1)
                    pe.wait_ge(c.O.empty, c.O.copied(b, ("O", PAIRS - 1)))
                    pe_project_out(c, pe, b, [lambda t, m=m: oT[:, m, t * P:(t + 1) * P] for m in range(IT)],
                                   [wo[:, m, :] for m in range(IT)], [obias[0:1, :]])

            @block.vector
            def _(dve):
                dve.memset(ones[:, :], 1.0)
                dve.memset(qm[:, :, :], 0.0)
                dve.drain().then_inc(c.setup_done, 1)
                with dve.Fori(0, B) as b:
                    here = bass.ds(b * T, T)
                    dve_norm(c, dve, b, 0, c.x[:, here, :], c.xn).then_inc(c.x_here.sem, 1)
                    dve_norm(c, dve, b, 1, c.ctx[:, here, :], c.ctxn).then_inc(c.ctx_here.sem, 1)
                    bound = CLIP * HD ** 0.5
                    for step in range(H + 2):
                        if step < H:
                            h = step
                            for t in range(T):
                                dve.wait_ge(c.V.full, c.V.filled(b, ("s", h, t)))
                                last = dve.tensor_scalar(e[:, h % 4, t, :], c.V.slot(("s", h, t)), bound, -bound, ALU.min, ALU.max)
                                last.then_inc(c.V.empty, 1)
                            dve.drain().then_inc(c.exp_in.sem, 1)
                        if step >= 3 and step % 2:
                            g = (step - 3) // 2
                            dve.drain()
                            dve.wait_ge(c.O.full, c.O.filled(b, ("sum", g)))
                            dve.reciprocal(rec[:, :], c.O.slot(("sum", g))).then_inc(c.O.empty, 1)
                            dve.drain()
                            dve.wait_ge(c.O.full, c.O.filled(b, ("O", g)))
                            dve.tensor_tensor(oT[:, g, :], c.O.slot(("O", g)), rec[:, :], ALU.mult).then_inc(c.O.empty, 1)
                    dve_residual_norm(c, dve, b, 2)

            @block.scalar
            def _(act):
                act.wait_ge(c.loaded, c.load_count)
                act.wait_ge(c.setup_done, c.setup_dones)
                with act.Fori(0, B) as b:
                    for name, dst, i in (("zx", c.xT, 1), ("zc", c.cT, 0)):
                        act.wait_ge(c.A.full, c.A.filled(b, name))
                        src = c.A.slot(name)
                        for k in range(KD):
                            last = act.activation(dst[:, k, :], src[:, k * S:(k + 1) * S], ACT.Identity,
                                                  bias=shiftc[:, i, k:k + 1], scale=gain[:, i, k:k + 1])
                        last.then_inc(c.A.empty, 1)
                    for i in range(IT // 2):
                        act.wait_ge(c.A.full, c.A.filled(b, ("q", i)))
                        src = c.A.slot(("q", i))
                        for m in range(2):
                            last = spread_heads(lambda dst, src, rows: act.activation(dst, src, ACT.Copy), qm,
                                                src[:, m * S:(m + 1) * S], (4 * i + 2 * m, 4 * i + 2 * m + 1), HD)
                        last.then_inc(c.A.empty, 1)
                    for name, dst in (("k", kT),):
                        for i in range(IT // 2):
                            act.wait_ge(c.A.full, c.A.filled(b, (name, i)))
                            src = c.A.slot((name, i))
                            act.activation(dst[:, 2 * i:2 * i + 2, :].rearrange("p m s -> p (m s)"), src, ACT.Copy).then_inc(c.A.empty, 1)
                    for t in range(T):
                        act.wait_ge(c.A.full, c.A.filled(b, ("v", t)))
                        src = c.A.slot(("v", t)).rearrange("p (h d) -> p h d", d=HD)
                        act.activation(v[:, t, :, :], src, ACT.Copy).then_inc(c.A.empty, 1)
                    for h in range(H):
                        act.wait_ge(c.exp_in.sem, c.exp_in.at(b, h + 1))
                        act.activation(e[:, h % 4, :, :], e[:, h % 4, :, :], ACT.Exp, scale=HD ** -0.5).then_inc(c.exp_ready.sem, 1)

            @block.gpsimd
            def _(pool):
                with pool.Fori(0, B) as b:
                    for j in range(2):
                        pool_rstd(c, pool, b, j)
                    for h in range(H):
                        pool.wait_ge(c.exp_ready.sem, c.exp_ready.at(b, h + 1))
                        alone(c, pool)
                        w = e[:, h % 4, :, :].rearrange("p (i t) s -> p i t s", t=2)
                        pool.tensor_tensor(half[:, h % 2, :, :], w[:, :, 0, :], w[:, :, 1, :], ALU.add)
                        pool.drain()
                        pool.tensor_tensor(total[:, h % 4, :], half[:, h % 2, 0, :], half[:, h % 2, 1, :],
                                           ALU.add).then_inc(c.sums_ready.sem, 1)
                    pool_rstd(c, pool, b, 2)
        c.finish()



def layer_l3_ffn(nc, c, ins):
    with ExitStack() as ctx:
        sb = allocator(nc, ctx, "l3_ffn")
        FT, STAGES = 8, 10
        HIDDEN = FT * P
        up, down = sb("up", [P, KD + 1, HIDDEN]), sb("down", [P, KD, HIDDEN])
        upw = [sb(f"upw{i}", [P, 2, HIDDEN]) for i in range(2)]
        downw = [sb(f"downw{i}", [P, 2, HIDDEN]) for i in range(2)]
        ta, tb, da, db = (sb(n, [P, HIDDEN]) for n in ("ta", "tb", "da", "db"))
        w2 = sb("w2", [P, FT, D])
        ubias, obias = sb("ubias", [P, FT]), sb("obias", [1, 2, D])
        hT = sb("hT", [P, FT, S])
        zeroed, up_stage, down_stage, pool_step = (ctx.enter_context(nc.semaphore(n)) for n in (
            "up_zeroed", "up_stage", "down_stage", "pool_step"))
        weights = [ctx.enter_context(nc.semaphore(f"butterfly_weights{i}")) for i in range(2)]
        c.setup_fulls += 1

        def stage(eng, y, w, s, a, b2):
            nb = HIDDEN // (2 * s)
            v = y.rearrange("p (n c s) -> p n c s", c=2, s=s)
            wide = [y.shape[0], nb, 2, s]
            n = y.shape[0]
            view = lambda t: t.rearrange("p (n c s) -> p n c s", c=2, s=s)
            eng.tensor_tensor(view(a[0:n, :]), view(w[0:n, 0, :]), v[:, :, 0:1, :].to_broadcast(wide), ALU.mult)
            eng.tensor_tensor(view(b2[0:n, :]), view(w[0:n, 1, :]), v[:, :, 1:2, :].to_broadcast(wide), ALU.mult)

        with nc.Block() as block:
            @block.sync
            def _(sp):
                for dst, name in ((ubias, "ubias11"), (obias, "obias11")):
                    c.load(sp, dst, ins[name])
                sp.dma_start(up[:, 0:KD, :], ins["up11"]).then_inc(c.loaded, 16)
                sp.dma_start(down[:, :, :], ins["down11"]).then_inc(c.loaded, 16)
                c.load_count += 32
                sp.wait_ge(zeroed, 1)
                sp.dma_start(up[0:1, KD, :], ins["upb11"]).then_inc(c.loaded, 16)
                c.load_count += 16
                sp.wait_ge(c.loaded, c.load_count)
                for st in range(STAGES):
                    if st > 1:
                        sp.wait_ge(up_stage, st - 1)
                        sp.wait_ge(down_stage, st - 1)
                    for dst, name in ((upw, "upw11"), (downw, "downw11")):
                        src = ins[name][st:st + 1, :, :].to_broadcast([P, 2, HIDDEN])
                        sp.dma_start(dst[st % 2][:, :, :], src).then_inc(weights[st % 2], 16)

            @block.vector
            def _(dve):
                dve.memset(up[:, KD, :], 0.0).then_inc(zeroed, 1)
                dve.wait_ge(c.loaded, c.load_count)
                for st in range(STAGES):
                    dve.wait_ge(weights[st % 2], 32 * (st // 2 + 1))
                    for k in range(KD + 1):
                        y = up[:, k, :] if k < KD else up[0:1, k, :]
                        n = P if k < KD else 1
                        stage(dve, y, upw[st % 2], 2 ** st, ta, tb)
                        dve.drain()
                        last = dve.tensor_tensor(y, ta[0:n, :], tb[0:n, :], ALU.add)
                        dve.drain()
                    dve.drain().then_inc(up_stage, 1)

            @block.gpsimd
            def _(pool):
                pool.wait_ge(c.loaded, c.load_count)
                done = 0
                for st in range(STAGES):
                    pool.wait_ge(weights[st % 2], 32 * (st // 2 + 1))
                    for k in range(KD):
                        y = down[:, k, :]
                        stage(pool, y, downw[st % 2], 2 ** (STAGES - 1 - st), da, db)
                        pool.drain().then_inc(pool_step, 1)
                        done += 1
                        pool.wait_ge(pool_step, done)
                        pool.tensor_tensor(y, da[:, :], db[:, :], ALU.add)
                        pool.drain().then_inc(pool_step, 1)
                        done += 1
                        pool.wait_ge(pool_step, done)
                    pool.sem_inc(down_stage, 1)

        c.expect_setup(1)
        with nc.Block() as block:
            @block.tensor
            def _(pe):
                for f in range(FT):
                    for o in range(KD):
                        last = pe.transpose(c.psA[:, f * D + o * P:f * D + (o + 1) * P],
                                            down[:, o, f * P:(f + 1) * P], c.ident[:, :])
                last.then_inc(c.setup_full, 1)

            @block.scalar
            def _(act):
                act.wait_ge(c.setup_full, c.setup_fulls)
                for i in range(2):
                    last = act.activation(w2[:, 4 * i:4 * i + 4, :].rearrange("p f d -> p (f d)"), c.psA[:, i * 1024:(i + 1) * 1024], ACT.Copy)
                act.drain().then_inc(c.setup_done, 1)

        begin(c, A=2 + FT // 2, V=2, O=0, x_here=1, var_ready=1, rstd_ready=1)
        with nc.Block() as block:
            @block.tensor
            def _(pe):
                pe.wait_ge(c.setup_done, c.setup_dones)
                with pe.Fori(0, B) as b:
                    pe_transpose_x_halves(c, pe, b)
                    pe.wait_ge(c.A.empty, c.A.copied(b, ("xT", KD - 1)))
                    for i in range(FT // 2):
                        pe.wait_ge(c.A.empty, c.A.vacant(b, ("h", i)))
                        out = c.A.slot(("h", i))
                        for m in (2 * i, 2 * i + 1):
                            last = mm(pe, out[:, (m - 2 * i) * S:(m - 2 * i + 1) * S],
                                      [(up[:, k, m * P:(m + 1) * P], c.xT[:, k, :]) for k in range(KD)]
                                      + [(up[0:1, KD, m * P:(m + 1) * P], c.ones[0:1, 0:S])])
                        last.then_inc(c.A.full, 1)
                    pe.wait_ge(c.A.empty, c.A.copied(b, ("h", FT // 2 - 1)))
                    pe_project_out(c, pe, b, [lambda t, f=f: hT[:, f, t * P:(t + 1) * P] for f in range(FT)],
                                   [w2[:, f, :] for f in range(FT)], [obias[0:1, 0, :], obias[0:1, 1, :]])

            @block.vector
            def _(dve):
                with dve.Fori(0, B) as b:
                    dve_residual_norm(c, dve, b)

            @block.scalar
            def _(act):
                with act.Fori(0, B) as b:
                    act_fetch_x(c, act, b)
                    for k in range(KD):
                        act.wait_ge(c.A.full, c.A.filled(b, ("xT", k)))
                        act.activation(c.xT[:, k, :], c.A.slot(("xT", k))[:, 0:S], ACT.Copy).then_inc(c.A.empty, 1)
                    for i in range(FT // 2):
                        act.wait_ge(c.A.full, c.A.filled(b, ("h", i)))
                        src = c.A.slot(("h", i))
                        for m in (2 * i, 2 * i + 1):
                            last = act.activation(hT[:, m, :], src[:, (m - 2 * i) * S:(m - 2 * i + 1) * S], ACT.Gelu,
                                                  bias=ubias[:, m:m + 1])
                        last.then_inc(c.A.empty, 1)

            @block.gpsimd
            def _(pool):
                with pool.Fori(0, B) as b:
                    pool_rstd(c, pool, b, 0)
        c.finish()


LAYERS = [layer_l0_attn, layer_l0_xattn, layer_l0_ffn, layer_l1_attn, layer_l1_xattn, layer_l1_ffn, layer_l2_attn,
          layer_l2_xattn, layer_l2_ffn, layer_l3_attn, layer_l3_xattn, layer_l3_ffn]


def build(nc, ins, out):
    with ExitStack() as ctx:
        sb = allocator(nc, ctx, "all")

        def sem(name):
            return ctx.enter_context(nc.semaphore(name))

        c = Core()
        c.x = sb("x", [P, B * T, D])
        c.xn = sb("xn", [P, T, D])
        c.xT = sb("xT", [P, KD, S])
        c.ctx = sb("ctx", [P, B * T, D])
        c.ctxn = sb("ctxn", [P, T, D])
        c.cT = sb("cT", [P, KD, S])
        c.r = sb("r", [P, T, D])
        c.stats = sb("stats", [P, T, 6])
        c.meanvar = sb("meanvar", [P, T, 2])
        c.vareps = sb("vareps", [P, T])
        c.rstd = sb("rstd", [P, T])
        c.minus_half = sb("minus_half", [P, T])
        c.ones = sb("ones", [1, S])
        c.ident = sb("ident", [P, P])
        c.ident16 = sb("ident16", [P, P], BF16)
        c.causal_kq = sb("causal_kq", [P, S], BF16)
        c.causal_qk = sb("causal_qk", [P, P], BF16)
        c.psA = ctx.enter_context(nc.psum_tensor("psA", [P, 2048], F32))
        c.psV = ctx.enter_context(nc.psum_tensor("psV", [P, 1024], F32))
        c.psO = ctx.enter_context(nc.psum_tensor("psO", [P, 1024], F32))
        c.A = Ring(nc, ctx, "A", "act_slot", c.psA)
        c.V = Ring(nc, ctx, "V", "dve_slot", c.psV)
        c.O = Ring(nc, ctx, "O", "heads_slot", c.psO)
        names = ("x_here", "ctx_here", "var_ready", "rstd_ready", "heads_ready", "parts_ready",
                 "max_ready", "sums_ready", "exp_in", "exp_ready", "feat_ready", "step_ready", "vec_ready")
        signals = [Signal(nc, ctx, n) for n in names]
        c.signals = dict(zip(names, signals))
        (c.x_here, c.ctx_here, c.var_ready, c.rstd_ready, c.heads_ready, c.parts_ready,
         c.max_ready, c.sums_ready, c.exp_in, c.exp_ready, c.feat_ready, c.step_ready, c.vec_ready) = signals
        c.marker = sem("marker")
        c.loaded = sem("loaded")
        c.setup_full = sem("setup_full")
        c.setup_done = sem("setup_done")
        c.stored = sem("stored")
        c.load_count = 0
        c.setup_dones = c.setup_fulls = 0

        def load(sp, dst, src):
            sp.dma_start(dst[tuple(slice(None) for _ in dst.shape)], src).then_inc(c.loaded, 16)
            c.load_count += 16

        def expect_setup(n):
            c.setup_dones += n

        def finish():
            for r in (c.A, c.V, c.O):
                r.end()
            for s in signals:
                s.end()

        c.load, c.expect_setup, c.finish = load, expect_setup, finish

        with nc.Block() as block:
            @block.sync
            def _(sp):
                x_view = ins["x"].rearrange("b (t p) d -> p (b t) d", p=P)
                load(sp, c.x, x_view)
                load(sp, c.ctx, ins["ctx"].rearrange("b (t p) d -> p (b t) d", p=P))
                for dst, name in ((c.ident, "ident"), (c.ident16, "ident16"), (c.causal_kq, "causal_kq"),
                                  (c.causal_qk, "causal_qk")):
                    load(sp, dst, ins[name])
                sp.wait_ge(c.loaded, c.load_count)

            @block.gpsimd
            def _(pool):
                pool.memset(c.minus_half[:, :], -0.5)
                pool.memset(c.ones[:, :], 1.0)

            @block.scalar
            def _(act):
                act.sem_inc(c.A.empty, CREDIT)

            @block.vector
            def _(dve):
                dve.sem_inc(c.V.empty, CREDIT)
                dve.sem_inc(c.O.empty, CREDIT)

        for i in PHASES:
            LAYERS[i](nc, c, ins)

        with nc.Block() as block:
            @block.sync
            def _(sp):
                sp.dma_start(out.rearrange("b (t p) d -> p (b t) d", p=P), c.x[:, :, :]).then_inc(c.stored, 16)
                sp.wait_ge(c.stored, 16)



def kernel(**inputs):
    import ml_dtypes
    import concourse.bacc as bacc
    from concourse.bass_utils import run_bass_kernel_spmd as run

    bf16 = ml_dtypes.bfloat16
    a = {k: np.asarray(v) for k, v in inputs.items()}

    def tiled(w):
        return w.reshape(w.shape[0] // P, P, *w.shape[1:]).swapaxes(0, 1)

    def row(v):
        return v.reshape(1, -1)

    def col(v):
        return v.reshape(-1, P).T

    def strips(w):
        out = np.zeros((w.shape[0], H, 32), w.dtype)
        out[:, :, 0:16] = w.reshape(w.shape[0], H, 16)
        return out.reshape(w.shape[0], H * 32)

    def block_diagonal(m):
        out = np.zeros((P, P), m.dtype)
        for i in range(0, P, 16):
            out[i:i + 16, i:i + 16] = m.T
        return out

    i = np.arange(P)
    lower = i[:, None] >= i[None, :]
    arrays = {
        "x": a["x"],
        "ctx": a["ctx_1024"],
        "ident": np.eye(P, dtype=np.float32),
        "ident16": np.eye(P, dtype=bf16),
        "causal_qk": np.where(lower, 0.0, -1e30).astype(bf16),
        "causal_kq": np.tile(np.where(lower.T, 0.0, -1e30), (1, T)).astype(bf16),
        "blocks": np.tile((i[:, None] // 32 == i[None, :] // 32).astype(np.float32), (1, T - 1)),
        "causal01": np.tile(np.where(lower.T, 1.0, 0.0), (1, T)).astype(np.float32),
        "sel32": np.tile((i[:, None] % H == np.arange(H)[None, :])[:, :, None], (1, 1, P)).astype(bf16),
    }
    w = a["L0_attn_w_qkv"]
    arrays["wqk0"] = tiled(w[0:2 * D])
    arrays["maps0"] = np.stack([block_diagonal(a["L0_attn_wq_map"]), block_diagonal(a["L0_attn_wk_map"])], axis=1)
    arrays["wv0"] = tiled(w[2 * D:].T)
    arrays["wo0"] = tiled(a["L0_attn_w_out"].T)
    arrays["fbias0"] = row(np.concatenate([np.tile(a["L0_attn_bq_map"], H), np.tile(a["L0_attn_bk_map"], H)]))
    for k, w in (("wq1", "w_q"), ("wk1", "w_k")):
        arrays[k] = tiled(strips(a["L0_xattn_" + w]))
    arrays["wv1"], arrays["wo1"] = tiled(a["L0_xattn_w_v"]), tiled(a["L0_xattn_w_o"])
    arrays["qbias1"], arrays["kbias1"] = col(strips(row(a["L0_xattn_b_q"]))), col(strips(row(a["L0_xattn_b_k"])))
    arrays["vbias1"], arrays["obias1"] = row(a["L0_xattn_b_v"]), row(a["L0_xattn_b_o"])

    arrays["wg2"], arrays["gbias2"] = tiled(a["L0_ffn_Wg"]), row(a["L0_ffn_bg"])
    arrays["rank2"] = np.tile(np.arange(8, 0, -1, dtype=np.float32), (P, T, 1))
    arrays["b1_2"], arrays["b2_2"] = col(a["L0_ffn_b1"]), a["L0_ffn_b2"]
    arrays["w1_2"] = a["L0_ffn_W1"].reshape(8, 2, P, 512).transpose(2, 0, 1, 3)
    arrays["w2_2"] = a["L0_ffn_W2"].reshape(8, 4, P, D).transpose(2, 0, 1, 3)

    for k, w in (("wq3", "query"), ("wk3", "key"), ("wv3", "value")):
        arrays[k] = tiled(a["L1_attn_W_" + w])

    arrays["w1_5"], arrays["w2_5"] = tiled(a["L1_ffn_W1"].T), tiled(a["L1_ffn_W2"].T)
    arrays["b1_5"], arrays["b2_5"] = col(a["L1_ffn_b1"]), row(a["L1_ffn_b2"])
    arrays["shift5"] = np.eye(P, k=1, dtype=np.float32)
    arrays["tokens5"] = (i[:, None] == np.arange(2, 17, 2)[None, :]).astype(np.float32)
    arrays["scale5"] = np.broadcast_to(a["L1_ffn_scale"].reshape(1, 1), (P, 1))

    w, v = a["L2_attn_Wqk"], a["L2_attn_bqk"]
    arrays["wq6"], arrays["wk6"] = tiled(strips(w[:, 0:D])), tiled(strips(w[:, D:]))
    arrays["qbias6"], arrays["kbias6"] = col(strips(row(v[0:D]))), col(strips(row(v[D:])))
    arrays["wv6"], arrays["wo6"], arrays["wn6"] = (tiled(a["L2_attn_" + n]) for n in ("Wv", "Wo", "Wn"))
    arrays["vbias6"], arrays["obias6"], arrays["nbias6"] = (row(a["L2_attn_" + n]) for n in ("bv", "bo", "bn"))
    def norm_cols(l, ctx):
        return np.stack([col(a[ctx]), col(a[l])], axis=1)

    m = a["mask_BxS2_bf1"].view(np.uint8)
    arrays["mask_row7"], arrays["mask_col7"] = row(m), col(m)
    arrays["gain7"], arrays["shift7"] = norm_cols("L2_xattn_gl", "L2_xattn_gm"), norm_cols("L2_xattn_bl", "L2_xattn_bm")
    arrays["sel64"] = ((i[:, None] % 64 < 32)[:, :, None] & (i[:, None] % H == np.arange(H)[None, :])[:, :, None]
                       & np.ones((1, 1, P), bool)).astype(bf16)
    for k in "qkvo":
        arrays[f"w{k}7"] = tiled(a["L2_xattn_W" + k])

    arrays["w1_8"], arrays["w2_8"] = tiled(a["L2_ffn_w1"].T), tiled(a["L2_ffn_w2"].T)
    arrays["b1_8"], arrays["b2_8"] = col(a["L2_ffn_b1"]), row(a["L2_ffn_b2"])

    for k, w in (("wq9", "Wq"), ("wk9", "Wk")):
        w = a["L3_attn_" + w].T.reshape(D, H, 8, 2)
        arrays[k] = tiled(strips(np.stack([w[..., 0], w[..., 0]], axis=-1).reshape(D, D)))
    arrays["wv9"], arrays["wo9"] = tiled(a["L3_attn_Wv"].T), tiled(a["L3_attn_Wo"].T)
    freqs = np.exp(np.arange(0, 16, 2, dtype=np.float32) * np.float32(-np.log(10000.0) / 16))
    angles = (np.arange(S, dtype=np.float32)[:, None] * freqs[None, :]).T
    rope = np.zeros((32, S), np.float32)
    rope[0:16:2], rope[1:16:2] = np.cos(angles), -np.sin(angles)
    arrays["rope9"], arrays["qrope9"] = np.tile(rope, (4, 1)), np.tile(rope * np.float32(0.25), (4, 1))

    arrays["gain10"] = norm_cols("L3_xattn_ln_l_w", "L3_xattn_ln_c_w")
    arrays["shift10"] = norm_cols("L3_xattn_ln_l_b", "L3_xattn_ln_c_b")
    w = a["L3_xattn_Wkv"]
    arrays["wq10"], arrays["wk10"], arrays["wv10"] = tiled(a["L3_xattn_Wq"]), tiled(w[:, 0:INNER]), tiled(w[:, INNER:])
    arrays["wo10"], arrays["obias10"] = tiled(a["L3_xattn_Wo"]), row(a["L3_xattn_bo"])

    def stage_weights(w, transposed):
        out = []
        for st in range(w.shape[0]):
            m = w[st].reshape(-1, 2 ** st, 2, 2)
            out.append(m.transpose((2, 0, 3, 1) if transposed else (3, 0, 2, 1)).reshape(2, -1))
        return np.stack(out[::-1] if transposed else out)

    arrays["upw11"] = stage_weights(a["L3_ffn_up_weights"], False)
    arrays["downw11"] = stage_weights(a["L3_ffn_down_weights"], True)
    arrays["up11"], arrays["upb11"] = tiled(a["L3_ffn_W_exp"]), row(a["L3_ffn_b_exp"])
    arrays["down11"] = tiled(a["L3_ffn_W_con"].T)
    arrays["ubias11"] = col(a["L3_ffn_up_bias"])
    arrays["obias11"] = np.stack([a["L3_ffn_b_con"], a["L3_ffn_down_bias"]])[None]

    nc = bacc.Bacc("TRN2", target_bir_lowering=False, num_devices=1)
    arrays = {f"in_{k}": np.ascontiguousarray(v) for k, v in arrays.items()}
    ins = {k[3:]: nc.dram_tensor(k, v.shape, mybir.dt.from_np(v.dtype), kind="ExternalInput").ap()
           for k, v in arrays.items()}
    out = nc.dram_tensor("out", (B, S, D), F32, kind="ExternalOutput").ap()
    build(nc, ins, out)
    result = run(nc, [arrays], core_ids=[0])
    return result.results[0]["out"]
```

```python
from contextlib import ExitStack

import numpy as np

import concourse.bass as bass
from concourse import mybir

F32 = mybir.dt.float32
BF16 = mybir.dt.bfloat16
ALU = mybir.AluOpType
ACT = mybir.ActivationFunctionType
AX = mybir.AxisListType.X
RMAX = bass.bass_isa.ReduceOp.max

P = 128
B, S, D = 4, 512, 256
T = S // P
KD = D // P
H = 16
NG = 4
EPS = 1e-5
MATRICES, CONTEXT = 2, 3
CREDIT = 4
MAGIC = 12582912.0
PHASES = range(0, 12)


class Ring:

    def __init__(self, nc, ctx, short, name, psum):
        self.full = ctx.enter_context(nc.semaphore(f"{name}_full"))
        self.empty = ctx.enter_context(nc.semaphore(f"{name}_empty"))
        self.psum, self.base, self.short = psum, 0, short

    def begin(self, per_batch, slots):
        assert per_batch % slots == 0, per_batch
        self.n, self.slots, self.keys, self.taken = per_batch, slots, [], 0
        self.tiles = self.psum.shape[1] // slots // S

    def end(self):
        assert len(self.keys) == self.taken == self.n, (len(self.keys), self.taken, self.n)
        self.base += B * self.n

    def vacant(self, b, key):
        self.keys.append(key)
        return b * self.n + (self.base + len(self.keys) + CREDIT - self.slots)

    def filled(self, b, key):
        assert self.keys[self.taken] == key, (key, self.keys[self.taken])
        self.taken += 1
        return b * self.n + (self.base + self.taken)

    def reading(self, b, key):
        return b * self.n + (self.base + self.keys.index(key) + 1)

    def copied(self, b, key):
        return b * self.n + (self.base + self.keys.index(key) + 1 + CREDIT)

    def slot(self, key):
        width = self.psum.shape[1] // self.slots
        at = self.keys.index(key) % self.slots * width
        return self.psum[:, at:at + width]


class Signal:

    def __init__(self, nc, ctx, name):
        self.sem = ctx.enter_context(nc.semaphore(name))
        self.base, self.n = 0, 0

    def begin(self, per_batch):
        self.n = per_batch

    def end(self):
        self.base += B * self.n
        self.n = 0

    def once_more(self):
        self.base += 1

    def at(self, b, k):
        return b * self.n + (self.base + k)


class Core:
    pass


def allocator(nc, ctx, layer):
    def sb(name, shape, dt=F32):
        return ctx.enter_context(nc.sbuf_tensor(f"{layer}_{name}", shape, dt))
    return sb


def alone(c, eng):
    eng.sem_inc(c.marker, 1)


def mm(pe, out, pairs, start=True):
    for i, (lhsT, rhs) in enumerate(pairs):
        last = pe.matmul(out, lhsT, rhs, start=start and i == 0, stop=i == len(pairs) - 1)
    return last


def begin(c, a_slots=2, v_slots=2, **counts):
    for ring, slots in ((c.A, a_slots), (c.V, v_slots), (c.O, 2)):
        ring.begin(counts.pop(ring.short), slots)
    for name, n in counts.items():
        c.signals[name].begin(n)



def act_fetch_x(c, act, b):
    alone(c, act)
    act.activation(c.xn[:, :, :], c.x[:, bass.ds(b * T, T), :], ACT.Copy).then_inc(c.x_here.sem, 1)


def pe_transpose_x(c, pe, b):
    pe.wait_ge(c.A.empty, c.A.vacant(b, "xT"))
    out = c.A.slot("xT")
    pe.wait_ge(c.x_here.sem, c.x_here.at(b, 1))
    for k in range(KD):
        for t in range(T):
            last = pe.transpose(out[:, k * S + t * P:k * S + (t + 1) * P], c.xn[:, t, k * P:(k + 1) * P], c.ident[:, :])
    last.then_inc(c.A.full, 1)


def pe_transpose_x_halves(c, pe, b):
    for k in range(KD):
        pe.wait_ge(c.A.empty, c.A.vacant(b, ("xT", k)))
        out = c.A.slot(("xT", k))
        pe.wait_ge(c.x_here.sem, c.x_here.at(b, 1))
        for t in range(T):
            last = pe.transpose(out[:, t * P:(t + 1) * P], c.xn[:, t, k * P:(k + 1) * P], c.ident[:, :])
        last.then_inc(c.A.full, 1)


def act_transposed_x(c, act, b):
    act.wait_ge(c.A.full, c.A.filled(b, "xT"))
    act.activation(c.xT[:, :, :].rearrange("p k s -> p (k s)"), c.A.slot("xT"), ACT.Copy).then_inc(c.A.empty, 1)


def act_transposed_x_halves(c, act, b):
    for k in range(KD):
        act.wait_ge(c.A.full, c.A.filled(b, ("xT", k)))
        act.activation(c.xT[:, k, :], c.A.slot(("xT", k))[:, 0:S], ACT.Copy).then_inc(c.A.empty, 1)


def pe_transpose_ctx(c, pe, b):
    pe.wait_ge(c.A.empty, c.A.vacant(b, "cT"))
    out = c.A.slot("cT")
    pe.wait_ge(c.ctx_here.sem, c.ctx_here.at(b, 1))
    for k in range(KD):
        for t in range(T):
            last = pe.transpose(out[:, k * S + t * P:k * S + (t + 1) * P], c.ctxn[:, t, k * P:(k + 1) * P], c.ident[:, :])
    last.then_inc(c.A.full, 1)


def act_fetch_ctx(c, act, b):
    alone(c, act)
    act.activation(c.ctxn[:, :, :], c.ctx[:, bass.ds(b * T, T), :], ACT.Copy).then_inc(c.ctx_here.sem, 1)


def act_transposed_ctx(c, act, b):
    act.wait_ge(c.A.full, c.A.filled(b, "cT"))
    act.activation(c.cT[:, :, :].rearrange("p k s -> p (k s)"), c.A.slot("cT"), ACT.Copy).then_inc(c.A.empty, 1)


def pe_transpose_ctx_halves(c, pe, b):
    for k in range(KD):
        pe.wait_ge(c.A.empty, c.A.vacant(b, ("cT", k)))
        out = c.A.slot(("cT", k))
        pe.wait_ge(c.ctx_here.sem, c.ctx_here.at(b, 1))
        for t in range(T):
            last = pe.transpose(out[:, t * P:(t + 1) * P], c.ctxn[:, t, k * P:(k + 1) * P], c.ident[:, :])
        last.then_inc(c.A.full, 1)


def act_transposed_ctx_halves(c, act, b):
    for k in range(KD):
        act.wait_ge(c.A.full, c.A.filled(b, ("cT", k)))
        act.activation(c.cT[:, k, :], c.A.slot(("cT", k))[:, 0:S], ACT.Copy).then_inc(c.A.empty, 1)


def dve_norm(c, dve, b, j, src, dst):
    for t in range(T):
        dve.bn_stats(c.stats[:, t, :], src[:, t, :])
    dve.drain()
    for t in range(T):
        dve.bn_aggr(c.meanvar[:, t, :], c.stats[:, t, :])
    dve.drain()
    dve.tensor_scalar(c.vareps[:, :], c.meanvar[:, :, 1], EPS, None, ALU.add).then_inc(c.var_ready.sem, 1)
    dve.wait_ge(c.rstd_ready.sem, c.rstd_ready.at(b, j + 1))
    alone(c, dve)
    for t in range(T):
        last = dve.tensor_scalar(dst[:, t, :], src[:, t, :], c.meanvar[:, t, 0:1], c.rstd[:, t:t + 1],
                                 ALU.subtract, ALU.mult)
    return last


def pool_rstd(c, pool, b, j):
    pool.wait_ge(c.var_ready.sem, c.var_ready.at(b, j + 1))
    alone(c, pool)
    pool.tensor_tensor(c.rstd[:, :], c.vareps[:, :], c.minus_half[:, :], ALU.pow).then_inc(c.rstd_ready.sem, 1)


def dve_norm_ahead(c, dve, b):
    dve_norm(c, dve, b, 1, c.xc[:, bass.ds(b * T + T, T), :], c.xn).then_inc(c.x_here.sem, 1)


def dve_residual_norm(c, dve, b, norm=0):
    dve.drain()
    for i in range(2):
        dve.wait_ge(c.V.full, c.V.filled(b, ("y", i)))
        y = c.V.slot(("y", i)).rearrange("p (t d) -> p t d", d=D)
        last = dve.tensor_tensor(c.r[:, 2 * i:2 * i + 2, :], y, c.x[:, bass.ds(b * T + 2 * i, 2), :], ALU.add)
        last.then_inc(c.V.empty, 1)
    dve.drain()
    dve_norm(c, dve, b, norm, c.r, c.x[:, bass.ds(b * T, T), :])


def pe_project_out(c, pe, b, lhs, rhs, bias=None):
    for i in range(2):
        pe.wait_ge(c.V.empty, c.V.vacant(b, ("y", i)))
        out = c.V.slot(("y", i))
        for t in (2 * i, 2 * i + 1):
            pairs = [(l(t), r) for l, r in zip(lhs, rhs)]
            if bias is not None:
                pairs += [(c.ones[0:1, 0:P], v) for v in bias]
            last = mm(pe, out[:, (t - 2 * i) * D:(t - 2 * i + 1) * D], pairs)
        last.then_inc(c.V.full, 1)


def pe_transpose_attn(c, pe, b, on, width):
    n = c.A.tiles
    for m in range(width // P // n):
        pe.wait_ge(c.A.empty, c.A.vacant(b, ("oT", m)))
        out = c.A.slot(("oT", m))
        if m == 0:
            pe.wait_ge(c.heads_ready.sem, c.heads_ready.at(b, c.heads_ready.n))
        for k in range(n):
            for t in range(T):
                last = pe.transpose(out[:, k * S + t * P:k * S + (t + 1) * P],
                                    on[:, t, (n * m + k) * P:(n * m + k + 1) * P], c.ident[:, :])
        last.then_inc(c.A.full, 1)


def act_transposed_attn(c, act, b, oT, width):
    n = c.A.tiles
    for m in range(width // P // n):
        act.wait_ge(c.A.full, c.A.filled(b, ("oT", m)))
        src = c.A.slot(("oT", m))
        act.activation(oT[:, n * m:n * (m + 1), :].rearrange("p k s -> p (k s)"), src, ACT.Copy).then_inc(c.A.empty, 1)


def pe_project_values(c, pe, b, xT, wv, bias=None):
    for i in range(2):
        pe.wait_ge(c.V.empty, c.V.vacant(b, ("v", i)))
        out = c.V.slot(("v", i))
        for t in (2 * i, 2 * i + 1):
            pairs = [(xT[:, k, t * P:(t + 1) * P], wv[:, k, :]) for k in range(KD)]
            if bias is not None:
                pairs.append((c.ones[0:1, 0:P], bias))
            last = mm(pe, out[:, (t - 2 * i) * D:(t - 2 * i + 1) * D], pairs)
        last.then_inc(c.V.full, 1)


def dve_values(c, dve, b):
    for i in range(2):
        dve.wait_ge(c.V.full, c.V.filled(b, ("v", i)))
        src = c.V.slot(("v", i)).rearrange("p (t h d) -> p t h d", t=2, d=16)
        for t in range(2):
            last = dve.tensor_copy(c.v[:, 2 * i + t, :, 0:16], src[:, t, :, :])
        last.then_inc(c.V.empty, 1)


AHEAD = 3


def spread_heads(copy, dst, src, heads, width):
    for i, h in enumerate(heads):
        rows = slice(width * i, width * (i + 1))
        last = copy(dst[rows, h, :], src[rows, :], rows)
    return last


def alloc_softmax(c, sb, keys, width, o_width, span=T, lag=3):
    c.width, c.per_o, c.span, c.lag = width, P // width, span, lag
    c.p = [sb(f"p{i}", [P, keys * P]) for i in range(lag + 1)]
    c.pTs = sb("pTs", [P, c.per_o + 1, keys, span * P])
    c.v = sb("v", [P, keys, H, width])
    c.oraw = sb("oraw", [P, 2, span * P])
    c.on = sb("on", [P, T, o_width])
    c.nmax = sb("nmax", [P, lag + 2])
    c.rsum = sb("rsum", [P, T, H])
    c.rec = sb("rec", [P, span, c.per_o])
    c.chunks = [(g, q0) for g in range(H // c.per_o) for q0 in range(0, T, span)]
    c.units = [(g * c.per_o + m, q0 + q) for g, q0 in c.chunks for m in range(c.per_o) for q in range(span)]


def pT_of_run(c, run):
    return c.pTs[:, run % (c.per_o + 1), :, :]


def pe_attend(c, pe, b, keys, scores, causal=False, before_unit=None):
    size = c.per_o * c.span
    for i in range(len(c.units) + c.lag + 4):
        done, rest = divmod(i - c.lag, size)
        if done > 0 and rest == 3:
            g, q0 = c.chunks[done - 1]
            pe.wait_ge(c.O.empty, c.O.vacant(b, ("o", g, q0)))
            pe.wait_ge(c.O.empty, c.O.copied(b, ("O", g, q0)))
            out = c.O.slot(("o", g, q0))
            for t in range(c.span):
                cols = slice(t * P, (t + 1) * P)
                last = pe.transpose(out[:, cols], c.oraw[:, (done - 1) % 2, cols], c.ident[:, :])
            last.then_inc(c.O.full, 1)
        if i < len(c.units):
            if before_unit is not None:
                before_unit(i)
            h, qt = c.units[i]
            pe.wait_ge(c.A.empty, c.A.vacant(b, ("s", h, qt)))
            scores(c.A.slot(("s", h, qt)), h, qt).then_inc(c.A.full, 1)
        if c.lag <= i < len(c.units) + c.lag:
            h, qt = c.units[i - c.lag]
            n = qt + 1 if causal else keys
            for j in range(0, n, T):
                pe.wait_ge(c.V.empty, c.V.vacant(b, ("pT", h, qt, j)))
                if j == 0:
                    pe.wait_ge(c.A.empty, c.A.copied(b, ("s", h, qt)))
                out = c.V.slot(("pT", h, qt, j))
                for k in range(j, min(j + T, n)):
                    last = pe.transpose(out[:, (k - j) * P:(k - j + 1) * P],
                                        c.p[(i - c.lag) % (c.lag + 1)][:, k * P:(k + 1) * P], c.ident[:, :])
                last.then_inc(c.V.full, 1)
        if done > 0 and rest == 0:
            g, q0 = c.chunks[done - 1]
            pe.wait_ge(c.O.empty, c.O.vacant(b, ("O", g, q0)))
            h, qt = c.units[done * size - 1]
            pe.wait_ge(c.V.empty, c.V.copied(b, ("pT", h, qt, (keys - 1) // T * T)))
            out = c.O.slot(("O", g, q0))
            for k in range(keys):
                cols = slice(k * P if causal else 0, c.span * P)
                for m in range(c.per_o):
                    last = pe.matmul(out[m * c.width:(m + 1) * c.width, cols], c.v[:, k, g * c.per_o + m, :],
                                     pT_of_run(c, (done - 1) * c.per_o + m)[:, k, cols], start=k == 0,
                                     stop=k == keys - 1)
            last.then_inc(c.O.full, 1)


def dve_attend(c, dve, b, keys, hd, causal=False, before_unit=None):
    size = c.per_o * c.span
    for i in range(len(c.units) + c.lag + 4):
        done, rest = divmod(i - c.lag, size)
        if done > 0 and rest == 3:
            g, q0 = c.chunks[done - 1]
            dve.drain()
            dve.wait_ge(c.O.full, c.O.filled(b, ("o", g, q0)))
            o = c.O.slot(("o", g, q0))[:, 0:c.span * P].rearrange("p (t i w) -> p t i w", i=c.per_o, w=c.width)
            for t in range(c.span):
                dst = c.on[:, q0 + t, g * c.per_o * hd:(g + 1) * c.per_o * hd].rearrange("p (i d) -> p i d", d=hd)
                last = dve.tensor_tensor(dst, o[:, t, :, 0:hd],
                                         c.rec[:, t, :].unsqueeze(2).to_broadcast([P, c.per_o, hd]), ALU.mult)
            last.then_inc(c.O.empty, 1)
            dve.drain().then_inc(c.heads_ready.sem, 1)
        if i < len(c.units):
            if before_unit is not None:
                before_unit(i)
            h, qt = c.units[i]
            n = qt + 1 if causal else keys
            dve.wait_ge(c.A.full, c.A.reading(b, ("s", h, qt)))
            at = i % (c.lag + 2)
            dve.tensor_reduce(c.nmax[:, at:at + 1], c.A.slot(("s", h, qt))[:, 0:n * P], AX, ALU.max,
                              negate=True).then_inc(c.max_ready.sem, 1)
        if c.lag <= i < len(c.units) + c.lag:
            h, qt = c.units[i - c.lag]
            n = qt + 1 if causal else keys
            run, at = divmod(i - c.lag, c.span)
            if at == 0 and run > c.per_o:
                dve.wait_ge(c.O.full, c.O.reading(b, ("O", *c.chunks[(run - c.per_o - 1) // c.per_o])))
            for j in range(0, n, T):
                dve.wait_ge(c.V.full, c.V.filled(b, ("pT", h, qt, j)))
                m = min(T, n - j)
                src = c.V.slot(("pT", h, qt, j))[:, 0:m * P].rearrange("p (k q) -> p k q", q=P)
                dve.tensor_copy(pT_of_run(c, run)[:, j:j + m, at * P:(at + 1) * P], src).then_inc(c.V.empty, 1)
        if done > 0 and rest == 1:
            g, q0 = c.chunks[done - 1]
            dve.wait_ge(c.O.full, c.O.filled(b, ("O", g, q0)))
            dve.tensor_copy(c.oraw[:, (done - 1) % 2, :], c.O.slot(("O", g, q0))[:, 0:c.span * P]).then_inc(c.O.empty, 1)
            dve.reciprocal(c.rec[:, :, :], c.rsum[:, q0:q0 + c.span, g * c.per_o:(g + 1) * c.per_o])


def act_attend(c, act, b, keys, causal=False):
    for i, (h, qt) in enumerate(c.units):
        n = (qt + 1 if causal else keys) * P
        at = i % (c.lag + 2)
        c.A.filled(b, ("s", h, qt))
        act.wait_ge(c.max_ready.sem, c.max_ready.at(b, i + 1))
        act.activation(c.p[i % (c.lag + 1)][:, 0:n], c.A.slot(("s", h, qt))[:, 0:n], ACT.Exp,
                       bias=c.nmax[:, at:at + 1], accum_out=c.rsum[:, qt, h:h + 1]).then_inc(c.A.empty, 1)



def alloc_linear(c, sb):
    c.v = sb("v", [P, T, H, 32])
    c.qm = sb("qm", [P, H, S])
    c.e = sb("e", [P, 3, NG * P])
    c.sums = sb("sums", [P, 2, (T - 1) * P])
    c.oraw = sb("oraw", [P, 2, S])
    c.on = sb("on", [P, T, D])
    c.rec = sb("rec", [P, T, 4])
    c.causal01 = sb("causal01", [P, 4 * P])
    c.blocks = sb("blocks", [P, (T - 1) * P])


def pe_linear(c, pe, b, q, k, kn, before_scores=None):
    for u in range(NG * T + 4):
        g, t = divmod(u, T)
        if g < NG:
            if t == 0:
                pe.wait_ge(c.V.empty, c.V.vacant(b, ("sums", g)))
                out = c.V.slot(("sums", g))
                v = c.v[:, :, 4 * g:4 * g + 4, :].rearrange("p t h d -> p t (h d)")
                for upto in range(1, T):
                    last = mm(pe, out[:, (upto - 1) * P:upto * P], [(kn(g, j), v[:, j, :]) for j in range(upto)])
                last.then_inc(c.V.full, 1)
            if u == 0 and before_scores is not None:
                before_scores()
            pe.wait_ge(c.V.empty, c.V.vacant(b, ("d", g, t)))
            cols = slice(t * P, (t + 1) * P)
            pe.matmul(c.V.slot(("d", g, t)).rearrange("p (h q) -> p h q", q=P), k(g)[:, cols],
                      c.qm[:, 4 * g:4 * g + 4, cols], start=True, stop=True).then_inc(c.V.full, 1)
        if 0 < u <= NG * T:
            g, t = divmod(u - 1, T)
            cols = slice(t * P, (t + 1) * P)
            if t == 0:
                pe.wait_ge(c.O.empty, c.O.vacant(b, ("O", g)))
            pe.wait_ge(c.V.empty, c.V.copied(b, ("d", g, t)))
            out = c.O.slot(("O", g))
            if t:
                pe.matmul(out[:, cols], c.sums[:, g % 2, (t - 1) * P:t * P], q(g)[:, cols], start=True, stop=False)
            for m in range(4):
                last = pe.matmul(out[32 * m:32 * m + 32, cols], c.v[:, t, 4 * g + m, :],
                                 c.e[:, (u - 1) % 3, m * P:(m + 1) * P], start=t == 0, stop=True)
            if t == T - 1:
                last.then_inc(c.O.full, 1)
        g, rest = divmod(u - T, T)
        if g >= 0 and rest == 2:
            pe.wait_ge(c.V.empty, c.V.vacant(b, ("o", g)))
            pe.wait_ge(c.O.empty, c.O.copied(b, ("O", g)))
            out = c.V.slot(("o", g))
            for t in range(T):
                last = pe.transpose(out[:, t * P:(t + 1) * P], c.oraw[:, g % 2, t * P:(t + 1) * P], c.ident[:, :])
            last.then_inc(c.V.full, 1)


def dve_linear(c, dve, b, factors):
    for u in range(NG * T + 4):
        g, t = divmod(u, T)
        if g < NG:
            if t == 0:
                dve.wait_ge(c.V.full, c.V.filled(b, ("sums", g)))
                dve.tensor_tensor(c.sums[:, g % 2, :], c.V.slot(("sums", g))[:, 0:(T - 1) * P], c.blocks[:, :],
                                  ALU.mult).then_inc(c.V.empty, 1)
            dve.wait_ge(c.V.full, c.V.filled(b, ("d", g, t)))
            dve.tensor_tensor(c.e[:, u % 3, :], c.V.slot(("d", g, t)), c.causal01[:, :], ALU.mult).then_inc(c.V.empty, 1)
        g, rest = divmod(u - T, T)
        if g >= 0 and rest == 1:
            dve.wait_ge(c.O.full, c.O.filled(b, ("O", g)))
            dve.tensor_copy(c.oraw[:, g % 2, :], c.O.slot(("O", g))).then_inc(c.O.empty, 1)
        if g >= 0 and rest == 2:
            dve.wait_ge(c.V.full, c.V.filled(b, ("o", g)))
            o = c.V.slot(("o", g)).rearrange("p (t i w) -> p t i w", i=4, w=32)
            rec = factors(g, o)
            for t in range(T):
                dst = c.on[:, t, g * 64:(g + 1) * 64].rearrange("p (i d) -> p i d", d=16)
                last = dve.tensor_tensor(dst, o[:, t, :, 0:16], rec[:, t, :].unsqueeze(2).to_broadcast([P, 4, 16]), ALU.mult)
            last.then_inc(c.V.empty, 1)
            dve.drain().then_inc(c.heads_ready.sem, 1)



def layer_l0_attn(nc, c, ins):
    with ExitStack() as ctx:
        sb = allocator(nc, ctx, "l0_attn")
        FW = 2 * 2 * D
        wqk = sb("wqk", [P, 4, D])
        maps = sb("maps", [P, 2, P])
        wv = sb("wv", [P, KD, D])
        wo = sb("wo", [P, KD, D])
        fbias = sb("fbias", [1, 2 * D])
        wc = sb("wc", [P, KD, 2 * D])
        feat = sb("feat", [P, T, FW])
        hi = sb("hi", [P, T, 2 * H])
        lo = sb("lo", [P, T, 2 * H])
        fsum = sb("fsum", [P, T, 4 * H])
        fT = sb("fT", [P, 2, NG, S])
        oT = sb("oT", [P, KD, S])
        alloc_linear(c, sb)
        begin(c, A=1 + T + 1, V=T + 2 + NG * (T + 2) + 2, O=NG, x_here=1, var_ready=1, rstd_ready=1, heads_ready=NG,
              exp_in=T, exp_ready=T, feat_ready=T)
        c.expect_setup(3)
        c.setup_fulls += 1

        with nc.Block() as block:
            @block.sync
            def _(sp):
                for dst, name in ((wqk, "wqk0"), (maps, "maps0"), (wv, "wv0"), (wo, "wo0"), (fbias, "fbias0"),
                                  (c.causal01, "causal01"), (c.blocks, "blocks")):
                    c.load(sp, dst, ins[name])
                c.load_part(sp, CONTEXT, c.ctx[:, :, :], ins["ctx"].rearrange("b (t p) d -> p (b t) d", p=P))

            @block.tensor
            def _(pe):
                pe.wait_ge(c.loaded, c.load_count)
                for m in range(4):
                    for k in range(KD):
                        last = pe.matmul(c.psO[:, k * S + m * P:k * S + (m + 1) * P], wqk[:, m, k * P:(k + 1) * P],
                                         maps[:, m // 2, :], start=True, stop=True)
                last.then_inc(c.setup_full, 1)
                pe.wait_ge(c.setup_done, c.setup_dones)
                with pe.Fori(0, B) as b:
                    pe_transpose_x(c, pe, b)
                    pe.wait_ge(c.A.empty, c.A.copied(b, "xT"))
                    for t in range(T):
                        pe.wait_ge(c.V.empty, c.V.vacant(b, ("p", t)))
                        out = c.V.slot(("p", t))
                        mm(pe, out, [(c.xT[:, k, t * P:(t + 1) * P], wc[:, k, :]) for k in range(KD)]
                                      + [(c.ones[0:1, 0:P], fbias[0:1, :])]).then_inc(c.V.full, 1)
                    pe_project_values(c, pe, b, c.xT, wv)
                    for t in range(T):
                        pe.wait_ge(c.A.empty, c.A.vacant(b, ("fT", t)))
                        out = c.A.slot(("fT", t))
                        pe.wait_ge(c.feat_ready.sem, c.feat_ready.at(b, t + 1))
                        for m in range(2 * NG):
                            last = pe.transpose(out[:, m * P:(m + 1) * P], feat[:, t, m * P:(m + 1) * P], c.ident[:, :])
                        last.then_inc(c.A.full, 1)
                    def features_transposed():
                        pe.wait_ge(c.A.empty, c.A.copied(b, ("fT", T - 1)))

                    pe_linear(c, pe, b, lambda g: fT[:, 0, g, :], lambda g: fT[:, 1, g, :],
                              lambda g, t: feat[:, t, (NG + g) * P:(NG + g + 1) * P], features_transposed)
                    pe_transpose_attn(c, pe, b, c.on, D)
                    pe.wait_ge(c.A.empty, c.A.copied(b, ("oT", 0)))
                    pe_project_out(c, pe, b, [lambda t, k=k: oT[:, k, t * P:(t + 1) * P] for k in range(KD)],
                                   [wo[:, k, :] for k in range(KD)])

            @block.vector
            def _(dve):
                dve.wait_ge(c.setup_full, 1)
                dve.wait_ge(c.loaded, c.load_count)
                dve.tensor_copy(wc[:, :, :].rearrange("p k m -> p (k m)"), c.psO[:, :]).then_inc(c.setup_done, 1)
                def map_features(b, t):
                    dve.wait_ge(c.V.full, c.V.filled(b, ("p", t)))
                    p = c.V.slot(("p", t)).rearrange("p (h d) -> p h d", d=16)
                    f = feat[:, t, :].rearrange("p (h d) -> p h d", d=32)
                    dve.tensor_reduce(hi[:, t, :], p, AX, ALU.max)
                    dve.tensor_reduce(lo[:, t, :], p, AX, ALU.min)
                    dve.drain()
                    shape = [P, 2 * H, 16]
                    dve.tensor_tensor(f[:, :, 0:16], p, hi[:, t, :].unsqueeze(2).to_broadcast(shape), ALU.subtract)
                    last = dve.tensor_tensor(f[:, :, 16:32], lo[:, t, :].unsqueeze(2).to_broadcast(shape), p, ALU.subtract)
                    last.then_inc(c.V.empty, 1)
                    dve.drain().then_inc(c.exp_in.sem, 1)

                def normalise_features(b, t):
                    f = feat[:, t, :].rearrange("p (h d) -> p h d", d=16)
                    dve.wait_ge(c.exp_ready.sem, c.exp_ready.at(b, t + 1))
                    dve.tensor_reduce(fsum[:, t, :], f, AX, ALU.add)
                    dve.drain()
                    dve.reciprocal(fsum[:, t, :], fsum[:, t, :])
                    dve.drain()
                    dve.tensor_tensor(
                        f, f, fsum[:, t, :].unsqueeze(2).to_broadcast([P, 4 * H, 16]), ALU.mult).then_inc(c.feat_ready.sem, 1)

                with dve.Fori(0, B) as b:
                    for t in range(T):
                        map_features(b, t)
                        if t:
                            normalise_features(b, t - 1)
                    dve_values(c, dve, b)
                    normalise_features(b, T - 1)
                    def factors(g, o):
                        dve.tensor_scalar(c.rec[:, :, :], o[:, :, :, 16], 1e-6, None, ALU.max)
                        dve.drain()
                        dve.reciprocal(c.rec[:, :, :], c.rec[:, :, :])
                        dve.drain()
                        return c.rec

                    dve_linear(c, dve, b, factors)
                    dve_residual_norm(c, dve, b)

            @block.scalar
            def _(act):
                act.wait_ge(c.setup_done, c.setup_dones)
                with act.Fori(0, B) as b:
                    act_fetch_x(c, act, b)
                    act_transposed_x(c, act, b)
                    for t in range(T):
                        act.wait_ge(c.exp_in.sem, c.exp_in.at(b, t + 1))
                        act.activation(feat[:, t, :], feat[:, t, :], ACT.Exp).then_inc(c.exp_ready.sem, 1)
                    heads = c.qm[:, :, :].rearrange("p (g i) s -> p g i s", i=4)
                    for t in range(T):
                        act.wait_ge(c.A.full, c.A.filled(b, ("fT", t)))
                        src = c.A.slot(("fT", t)).rearrange("p (w g s) -> p w g s", w=2, s=P)
                        cols = slice(t * P, (t + 1) * P)
                        act.activation(fT[:, 0, :, cols], src[:, 0, :, :], ACT.Copy)
                        act.activation(fT[:, 1, :, cols], src[:, 1, :, :], ACT.Copy)
                        for i in range(4):
                            rows = slice(32 * i, 32 * i + 32)
                            last = act.activation(heads[rows, :, i, cols], src[rows, 0, :, :], ACT.Copy)
                        last.then_inc(c.A.empty, 1)
                    act_transposed_attn(c, act, b, oT, D)

            @block.gpsimd
            def _(pool):
                pool.memset(c.qm[:, :, :], 0.0).then_inc(c.setup_done, 1)
                pool.memset(c.v[:, :, :, 17:32], 0.0)
                pool.memset(c.v[:, :, :, 16:17], 1.0).then_inc(c.setup_done, 1)
                with pool.Fori(0, B) as b:
                    pool_rstd(c, pool, b, 0)
        c.finish()



def layer_l0_xattn(nc, c, ins):
    with ExitStack() as ctx:
        sb = allocator(nc, ctx, "l0_xattn")
        wq, wk = sb("wq", [P, KD, NG * P]), sb("wk", [P, KD, NG * P])
        wv, wo = sb("wv", [P, KD, D]), sb("wo", [P, KD, D])
        qbias, kbias = sb("qbias", [P, NG]), sb("kbias", [P, NG])
        vbias, obias = sb("vbias", [1, D]), sb("obias", [1, D])
        qm, kT = sb("qm", [P, H, S]), sb("kT", [P, NG, S])
        oT = sb("oT", [P, KD, S])
        alloc_softmax(c, sb, T, 32, D)
        begin(c, a_slots=4, A=KD + KD + NG + 2 + H * T + KD, V=NG + H * T + 2, O=2 * NG,
              x_here=1, ctx_here=1, var_ready=1, rstd_ready=1, heads_ready=NG, max_ready=H * T)
        c.expect_setup(2)

        with nc.Block() as block:
            @block.sync
            def _(sp):
                for dst, name in ((qbias, "qbias1"), (kbias, "kbias1"), (vbias, "vbias1"), (obias, "obias1")):
                    c.load(sp, dst, ins[name])
                for part, dst, name in ((0, wq, "wq1"), (1, wk, "wk1"), (1, wv, "wv1"), (1, wo, "wo1")):
                    c.load_part(sp, part, dst[:, :, :], ins[name])

            @block.tensor
            def _(pe):
                pe.wait_ge(c.loaded, c.load_count)
                with pe.Fori(0, B) as b:
                    pe_transpose_x_halves(c, pe, b)
                    pe_transpose_ctx_halves(c, pe, b)
                    pe.wait_ge(c.A.empty, c.A.copied(b, ("xT", KD - 1)))
                    pe.wait_ge(c.arrived[0], c.arrivals[0])
                    for g in range(NG):
                        pe.wait_ge(c.V.empty, c.V.vacant(b, ("q", g)))
                        out = c.V.slot(("q", g))
                        mm(pe, out, [(wq[:, k, g * P:(g + 1) * P], c.xT[:, k, :]) for k in range(KD)]).then_inc(c.V.full, 1)
                    pe.wait_ge(c.A.empty, c.A.copied(b, ("cT", KD - 1)))
                    pe.wait_ge(c.arrived[1], c.arrivals[1])
                    for g in range(NG):
                        pe.wait_ge(c.A.empty, c.A.vacant(b, ("k", g)))
                        mm(pe, c.A.slot(("k", g)), [(wk[:, k, g * P:(g + 1) * P], c.cT[:, k, :]) for k in range(KD)]).then_inc(c.A.full, 1)
                    for i in range(2):
                        pe.wait_ge(c.A.empty, c.A.vacant(b, ("v", i)))
                        out = c.A.slot(("v", i))
                        for t in range(2):
                            cols = slice((2 * i + t) * P, (2 * i + t + 1) * P)
                            last = mm(pe, out[:, t * D:(t + 1) * D], [(c.cT[:, k, cols], wv[:, k, :]) for k in range(KD)]
                                      + [(c.ones[0:1, 0:P], vbias[0:1, :])])
                        last.then_inc(c.A.full, 1)
                    pe.wait_ge(c.V.empty, c.V.copied(b, ("q", NG - 1)))
                    pe.wait_ge(c.A.empty, c.A.copied(b, ("v", 1)))

                    def scores(out, h, qt):
                        n = qt * P
                        q = qm[:, h, n:n + P]
                        if qt:
                            pe.matmul(out[:, 0:n], q, kT[:, h // 4, 0:n], start=True, stop=True)
                        pe.matmul(out[:, n:n + P], c.ident16[:, :], c.causal_qk[:, :], start=True, stop=False)
                        return pe.matmul(out[:, n:n + P], q, kT[:, h // 4, n:n + P], start=False, stop=True)

                    pe.wait_ge(c.setup_done, c.setup_dones)
                    pe_attend(c, pe, b, T, scores, causal=True)
                    pe_transpose_attn(c, pe, b, c.on, D)
                    pe.wait_ge(c.A.empty, c.A.copied(b, ("oT", KD - 1)))
                    pe_project_out(c, pe, b, [lambda t, k=k: oT[:, k, t * P:(t + 1) * P] for k in range(KD)],
                                   [wo[:, k, :] for k in range(KD)], [obias[0:1, :]])

            @block.vector
            def _(dve):
                dve.wait_ge(c.loaded, c.load_count)
                dve.tensor_scalar(qbias[:, :], qbias[:, :], 0.25, None, ALU.mult)
                dve.drain().then_inc(c.setup_done, 1)
                dve.wait_ge(c.setup_done, c.setup_dones)
                with dve.Fori(0, B) as b:
                    for g in range(NG):
                        dve.wait_ge(c.V.full, c.V.filled(b, ("q", g)))
                        spread_heads(lambda dst, src, rows: dve.tensor_scalar(dst, src, 0.25, qbias[rows, g:g + 1],
                                                                              ALU.mult, ALU.add),
                                     qm, c.V.slot(("q", g)), range(4 * g, 4 * g + 4), 32).then_inc(c.V.empty, 1)
                    dve_attend(c, dve, b, T, 16, causal=True)
                    dve_residual_norm(c, dve, b)

            @block.scalar
            def _(act):
                act.wait_ge(c.loaded, c.load_count)
                act.wait_ge(c.arrived[CONTEXT], c.arrivals[CONTEXT])
                with act.Fori(0, B) as b:
                    act_fetch_x(c, act, b)
                    act_fetch_ctx(c, act, b)
                    act_transposed_x_halves(c, act, b)
                    act_transposed_ctx_halves(c, act, b)
                    for g in range(NG):
                        act.wait_ge(c.A.full, c.A.filled(b, ("k", g)))
                        act.activation(kT[:, g, :], c.A.slot(("k", g)), ACT.Identity, bias=kbias[:, g:g + 1]).then_inc(c.A.empty, 1)
                    act.wait_ge(c.setup_done, c.setup_dones)
                    for i in range(2):
                        act.wait_ge(c.A.full, c.A.filled(b, ("v", i)))
                        act.activation(c.v[:, 2 * i:2 * i + 2, :, 0:16].rearrange("p t h d -> p (t h) d"),
                                       c.A.slot(("v", i)).rearrange("p (a d) -> p a d", d=16), ACT.Copy).then_inc(c.A.empty, 1)
                    act_attend(c, act, b, T, causal=True)
                    act_transposed_attn(c, act, b, oT, D)

            @block.gpsimd
            def _(pool):
                pool.memset(c.v[:, :, :, :], 0.0)
                pool.memset(qm[:, :, :], 0.0)
                pool.drain().then_inc(c.setup_done, 1)
                with pool.Fori(0, B) as b:
                    pool_rstd(c, pool, b, 0)
        c.finish()



HIDDEN, STAGES = 1024, 10


def alloc_butterfly(c, nc, ctx, sb):
    c.up, c.down = sb("up", [P, KD + 1, HIDDEN]), sb("down", [P, KD, HIDDEN])
    c.pair_weights = [sb(f"pair_weights{i}", [P, 2, HIDDEN]) for i in range(2)]
    c.lower, c.upper = sb("lower", [P, HIDDEN]), sb("upper", [P, HIDDEN])
    c.weights_here = [ctx.enter_context(nc.semaphore(f"pair_weights_here{i}")) for i in range(2)]
    c.stage_done, c.pool_step = ctx.enter_context(nc.semaphore("stage_done")), ctx.enter_context(nc.semaphore("pool_step"))
    c.stages = [("upw11", st, 2 ** st) for st in range(STAGES)]
    c.stages += [("downw11", st, 2 ** (STAGES - 1 - st)) for st in range(STAGES)]


def sync_butterfly(c, sp, ins):
    c.load_part(sp, MATRICES, c.up[:, 0:KD, :], ins["up11"])
    c.load_part(sp, MATRICES, c.up[0:1, KD, :], ins["upb11"])
    c.load_part(sp, MATRICES, c.down[:, :, :], ins["down11"])
    for n, (name, st, _) in enumerate(c.stages):
        if n > 1:
            sp.wait_ge(c.stage_done, n - 1)
        src = ins[name][st:st + 1, :, :].to_broadcast([P, 2, HIDDEN])
        sp.dma_start(c.pair_weights[n % 2][:, :, :], src).then_inc(c.weights_here[n % 2], 16)
    sp.wait_ge(c.stage_done, len(c.stages))
    sp.dma_start(c.mixed_up[:, 0:KD, :], c.up[:, 0:KD, :]).then_inc(c.stored, 16)
    sp.dma_start(c.mixed_up[0:1, KD, :], c.up[0:1, KD, :]).then_inc(c.stored, 16)
    sp.dma_start(c.mixed_down, c.down[:, :, :]).then_inc(c.stored, 16)
    c.stores += 48
    sp.wait_ge(c.stored, c.stores)


def pool_butterfly(c, pool, n):
    name, _, s = c.stages[n]
    pool.wait_ge(c.weights_here[n % 2], 16 * (n // 2 + 1))
    w = c.pair_weights[n % 2]
    rows = [c.up[:, 0, :], c.up[:, 1, :], c.up[0:1, KD, :]] if name == "upw11" else [c.down[:, 0, :], c.down[:, 1, :]]
    for y in rows:
        v = y.rearrange("p (n c s) -> p n c s", c=2, s=s)
        m = y.shape[0]
        wide = [m, HIDDEN // (2 * s), 2, s]
        for i, dst in enumerate((c.lower, c.upper)):
            pool.tensor_tensor(dst[0:m, :].rearrange("p (n c s) -> p n c s", c=2, s=s),
                               w[0:m, i, :].rearrange("p (n c s) -> p n c s", c=2, s=s),
                               v[:, :, i:i + 1, :].to_broadcast(wide), ALU.mult)
        pool.drain().then_inc(c.pool_step, 1)
        c.pool_steps += 1
        pool.wait_ge(c.pool_step, c.pool_steps)
        pool.tensor_tensor(y, c.lower[0:m, :], c.upper[0:m, :], ALU.add)
        pool.drain().then_inc(c.pool_step, 1)
        c.pool_steps += 1
        pool.wait_ge(c.pool_step, c.pool_steps)
    pool.sem_inc(c.stage_done, 1)


def layer_l0_ffn(nc, c, ins):
    with ExitStack() as ctx:
        sb = allocator(nc, ctx, "l0_ffn")
        E, FT = 8, 4
        w1, w2 = sb("w1", [P, E, KD, FT * P]), sb("w2", [P, E, FT, D])
        wg, gbias = sb("wg", [P, KD, E]), sb("gbias", [1, E])
        b1, b2 = sb("b1", [P, E * FT]), sb("b2", [E, D])
        rank = sb("rank", [P, T, E])
        hT = [sb(f"hT{i}", [P, FT, S]) for i in range(2)]
        logits, probs, left = sb("logits", [P, T, E]), sb("probs", [P, T, E]), sb("left", [P, T, E])
        key, pick, mask = sb("key", [P, T, E]), sb("pick", [P, T, E]), sb("mask", [P, T, E])
        top = sb("top", [P, T])
        gates, gatesT, mixed_b2 = sb("gates", [P, T, P]), sb("gatesT", [P, S]), sb("mixed_b2", [P, T, D])
        begin(c, A=4 + 2 * E, V=2 * E, O=0, x_here=1, var_ready=1, rstd_ready=1, exp_in=1, exp_ready=1, vec_ready=1)
        alloc_butterfly(c, nc, ctx, sb)
        c.expect_setup(0)

        with nc.Block() as block:
            @block.sync
            def _(sp):
                for dst, name in ((wg, "wg2"), (gbias, "gbias2"), (rank, "rank2"), (b1, "b1_2"), (b2, "b2_2")):
                    c.load(sp, dst, ins[name])
                for part, es in enumerate((slice(0, 1), slice(1, 3), slice(3, E))):
                    c.load_part(sp, part, w1[:, es, :, :], ins["w1_2"][:, es, :, :])
                    c.load_part(sp, part, w2[:, es, :, :], ins["w2_2"][:, es, :, :])
                sync_butterfly(c, sp, ins)

            @block.tensor
            def _(pe):
                pe.wait_ge(c.loaded, c.load_count)
                with pe.Fori(0, B) as b:
                    pe_transpose_x(c, pe, b)
                    pe.wait_ge(c.A.empty, c.A.copied(b, "xT"))
                    pe.wait_ge(c.A.empty, c.A.vacant(b, "logits"))
                    out = c.A.slot("logits")
                    for t in range(T):
                        last = mm(pe, out[:, t * E:(t + 1) * E],
                                  [(c.xT[:, k, t * P:(t + 1) * P], wg[:, k, :]) for k in range(KD)]
                                  + [(c.ones[0:1, 0:P], gbias[0:1, :])])
                    last.then_inc(c.A.full, 1)

                    def up(e):
                        part = 0 if e < 1 else 1 if e < 3 else 2
                        pe.wait_ge(c.arrived[part], c.arrivals[part])
                        for i in range(2):
                            pe.wait_ge(c.A.empty, c.A.vacant(b, ("h", e, i)))
                            out = c.A.slot(("h", e, i))
                            for m in (2 * i, 2 * i + 1):
                                last = mm(pe, out[:, (m - 2 * i) * S:(m - 2 * i + 1) * S],
                                          [(w1[:, e, k, m * P:(m + 1) * P], c.xT[:, k, :]) for k in range(KD)])
                            last.then_inc(c.A.full, 1)

                    def down(e):
                        pe.wait_ge(c.A.empty, c.A.copied(b, ("h", e, 1)))
                        for i in range(2):
                            pe.wait_ge(c.V.empty, c.V.vacant(b, ("o", e, i)))
                            out = c.V.slot(("o", e, i))
                            for t in (2 * i, 2 * i + 1):
                                last = mm(pe, out[:, (t - 2 * i) * D:(t - 2 * i + 1) * D],
                                          [(hT[e % 2][:, f, t * P:(t + 1) * P], w2[:, e, f, :]) for f in range(FT)])
                            last.then_inc(c.V.full, 1)

                    up(0)
                    pe.wait_ge(c.A.empty, c.A.vacant(b, "gatesT"))
                    out = c.A.slot("gatesT")
                    pe.wait_ge(c.vec_ready.sem, c.vec_ready.at(b, 1))
                    for t in range(T):
                        last = pe.transpose(out[:, t * P:(t + 1) * P], gates[:, t, :], c.ident[:, :])
                    last.then_inc(c.A.full, 1)
                    pe.wait_ge(c.A.empty, c.A.vacant(b, "mixed_b2"))
                    out = c.A.slot("mixed_b2")
                    pe.wait_ge(c.A.empty, c.A.copied(b, "gatesT"))
                    for t in range(T):
                        last = pe.matmul(out[:, t * D:(t + 1) * D], gatesT[0:E, t * P:(t + 1) * P], b2[0:E, :],
                                         start=True, stop=True)
                    last.then_inc(c.A.full, 1)
                    for e in range(E):
                        if e + 1 < E:
                            up(e + 1)
                        down(e)

            @block.vector
            def _(dve):
                dve.wait_ge(c.loaded, c.load_count)
                dve.memset(gates[:, :, :], 0.0)
                with dve.Fori(0, B) as b:
                    wide = [P, T, E]
                    dve.wait_ge(c.A.empty, c.A.copied(b, "logits"))
                    dve.tensor_reduce(top[:, :], logits[:, :, :], AX, ALU.max)
                    dve.drain()
                    dve.tensor_tensor(logits[:, :, :], logits[:, :, :],
                                                  top[:, :].unsqueeze(2).to_broadcast(wide), ALU.subtract).then_inc(c.exp_in.sem, 1)
                    dve.wait_ge(c.exp_ready.sem, c.exp_ready.at(b, 1))
                    dve.tensor_reduce(top[:, :], probs[:, :, :], AX, ALU.add)
                    dve.drain()
                    dve.reciprocal(top[:, :], top[:, :])
                    dve.drain()
                    dve.tensor_tensor(probs[:, :, :], probs[:, :, :], top[:, :].unsqueeze(2).to_broadcast(wide), ALU.mult)
                    dve.drain()
                    for i in range(2):
                        src = probs if i == 0 else left
                        dve.tensor_reduce(top[:, :], src[:, :, :], AX, ALU.max)
                        dve.drain()
                        dve.tensor_tensor(key[:, :, :], src[:, :, :], top[:, :].unsqueeze(2).to_broadcast(wide), ALU.is_equal)
                        dve.drain()
                        dve.tensor_tensor(key[:, :, :], key[:, :, :], rank[:, :, :], ALU.mult)
                        dve.drain()
                        dve.tensor_reduce(top[:, :], key[:, :, :], AX, ALU.max)
                        dve.drain()
                        dst = mask if i == 0 else pick
                        dve.tensor_tensor(dst[:, :, :], key[:, :, :], top[:, :].unsqueeze(2).to_broadcast(wide), ALU.is_equal)
                        dve.drain()
                        if i == 0:
                            dve.scalar_tensor_tensor(left[:, :, :], mask[:, :, :], -2.0, probs[:, :, :], ALU.mult, ALU.add)
                            dve.drain()
                    dve.tensor_tensor(mask[:, :, :], mask[:, :, :], pick[:, :, :], ALU.add)
                    dve.drain()
                    dve.tensor_tensor(mask[:, :, :], mask[:, :, :], probs[:, :, :], ALU.mult)
                    dve.drain()
                    dve.tensor_reduce(top[:, :], mask[:, :, :], AX, ALU.add)
                    dve.drain()
                    dve.tensor_scalar(top[:, :], top[:, :], 1e-9, None, ALU.add)
                    dve.drain()
                    dve.reciprocal(top[:, :], top[:, :])
                    dve.drain()
                    dve.tensor_tensor(gates[:, :, 0:E], mask[:, :, :],
                                                     top[:, :].unsqueeze(2).to_broadcast(wide), ALU.mult).then_inc(c.vec_ready.sem, 1)
                    dve.wait_ge(c.A.empty, c.A.copied(b, "mixed_b2"))
                    dve.tensor_tensor(c.r[:, :, :], mixed_b2[:, :, :], c.x[:, bass.ds(b * T, T), :], ALU.add)
                    dve.drain()
                    for e in range(E):
                        for i in range(2):
                            dve.wait_ge(c.V.full, c.V.filled(b, ("o", e, i)))
                            o = c.V.slot(("o", e, i))
                            for t in (2 * i, 2 * i + 1):
                                last = dve.scalar_tensor_tensor(c.r[:, t, :], o[:, (t - 2 * i) * D:(t - 2 * i + 1) * D],
                                                                gates[:, t, e:e + 1], c.r[:, t, :], ALU.mult, ALU.add)
                            last.then_inc(c.V.empty, 1)
                        dve.drain()
                    dve_norm(c, dve, b, 0, c.r, c.x[:, bass.ds(b * T, T), :])

            @block.scalar
            def _(act):
                with act.Fori(0, B) as b:
                    act_fetch_x(c, act, b)
                    act_transposed_x(c, act, b)
                    act.wait_ge(c.A.full, c.A.filled(b, "logits"))
                    src = c.A.slot("logits")
                    act.activation(logits[:, :, :].rearrange("p t e -> p (t e)"), src[:, 0:T * E], ACT.Copy).then_inc(c.A.empty, 1)
                    act.wait_ge(c.exp_in.sem, c.exp_in.at(b, 1))
                    act.activation(probs[:, :, :], logits[:, :, :], ACT.Exp, scale=0.2).then_inc(c.exp_ready.sem, 1)

                    def gelu(e):
                        for i in range(2):
                            act.wait_ge(c.A.full, c.A.filled(b, ("h", e, i)))
                            src = c.A.slot(("h", e, i))
                            for m in (2 * i, 2 * i + 1):
                                last = act.activation(hT[e % 2][:, m, :], src[:, (m - 2 * i) * S:(m - 2 * i + 1) * S],
                                                      ACT.Gelu, bias=b1[:, e * FT + m:e * FT + m + 1])
                            last.then_inc(c.A.empty, 1)

                    gelu(0)
                    act.wait_ge(c.A.full, c.A.filled(b, "gatesT"))
                    src = c.A.slot("gatesT")
                    act.activation(gatesT[:, :], src[:, 0:S], ACT.Copy).then_inc(c.A.empty, 1)
                    act.wait_ge(c.A.full, c.A.filled(b, "mixed_b2"))
                    src = c.A.slot("mixed_b2")
                    act.activation(mixed_b2[:, :, :].rearrange("p t d -> p (t d)"), src, ACT.Copy).then_inc(c.A.empty, 1)
                    for e in range(1, E):
                        gelu(e)

            @block.gpsimd
            def _(pool):
                pool.wait_ge(c.arrived[MATRICES], c.arrivals[MATRICES])
                c.pool_steps = 0
                quarter = len(c.stages) // B
                for b in range(B):
                    for n in range(b * quarter, (b + 1) * quarter):
                        pool_butterfly(c, pool, n)
                    pool_rstd(c, pool, b, 0)
        c.finish()



def layer_l1_attn(nc, c, ins):
    with ExitStack() as ctx:
        sb = allocator(nc, ctx, "l1_attn")
        wq, wk, wv = (sb(n, [P, KD, D]) for n in ("wq", "wk", "wv"))
        qT, kT, v = sb("qT", [P, KD, S]), sb("kT", [P, KD, S]), sb("v", [P, T, D])
        e, eT = sb("e", [P, T, S]), sb("eT", [P, T, S])
        nmax, rsum = sb("nmax", [P, T]), sb("rsum", [P, T])
        begin(c, A=6, V=6, O=0, x_here=1, var_ready=1, rstd_ready=1, exp_in=T, exp_ready=T)
        c.expect_setup(0)

        with nc.Block() as block:
            @block.sync
            def _(sp):
                for dst, name in ((wq, "wq3"), (wk, "wk3"), (wv, "wv3")):
                    c.load(sp, dst, ins[name])

            @block.tensor
            def _(pe):
                pe.wait_ge(c.loaded, c.load_count)
                with pe.Fori(0, B) as b:
                    pe_transpose_x(c, pe, b)
                    pe.wait_ge(c.A.empty, c.A.copied(b, "xT"))
                    for name, w in (("q", wq), ("k", wk)):
                        pe.wait_ge(c.A.empty, c.A.vacant(b, name))
                        out = c.A.slot(name)
                        for m in range(KD):
                            last = mm(pe, out[:, m * S:(m + 1) * S],
                                      [(w[:, k, m * P:(m + 1) * P], c.xT[:, k, :]) for k in range(KD)])
                        last.then_inc(c.A.full, 1)
                    pe.wait_ge(c.A.empty, c.A.vacant(b, "v"))
                    out = c.A.slot("v")
                    for t in range(T):
                        last = mm(pe, out[:, t * D:(t + 1) * D],
                                  [(c.xT[:, k, t * P:(t + 1) * P], wv[:, k, :]) for k in range(KD)])
                    last.then_inc(c.A.full, 1)
                    pe.wait_ge(c.A.empty, c.A.copied(b, "k"))
                    for t in range(T):
                        pe.wait_ge(c.V.empty, c.V.vacant(b, ("s", t)))
                        out = c.V.slot(("s", t))
                        mm(pe, out, [(kT[:, k, t * P:(t + 1) * P], qT[:, k, :]) for k in range(KD)]).then_inc(c.V.full, 1)
                    for i in range(2):
                        pe.wait_ge(c.A.empty, c.A.vacant(b, ("eT", i)))
                        out = c.A.slot(("eT", i))
                        if i == 0:
                            pe.wait_ge(c.exp_ready.sem, c.exp_ready.at(b, T))
                        for q in (2 * i, 2 * i + 1):
                            for t in range(T):
                                last = pe.transpose(out[:, (q - 2 * i) * S + t * P:(q - 2 * i) * S + (t + 1) * P],
                                                    e[:, t, q * P:(q + 1) * P], c.ident[:, :])
                        last.then_inc(c.A.full, 1)
                    pe.wait_ge(c.A.empty, c.A.copied(b, ("eT", 1)))
                    pe_project_out(c, pe, b, [lambda t, q=q: eT[:, q, t * P:(t + 1) * P] for q in range(T)],
                                   [v[:, q, :] for q in range(T)])

            @block.vector
            def _(dve):
                with dve.Fori(0, B) as b:
                    for t in range(T):
                        dve.wait_ge(c.V.full, c.V.filled(b, ("s", t)))
                        s = c.V.slot(("s", t))
                        dve.tensor_reduce(nmax[:, t:t + 1], s, AX, ALU.max)
                        dve.drain()
                        dve.tensor_scalar(e[:, t, :], s, nmax[:, t:t + 1], None, ALU.subtract).then_inc(c.V.empty, 1)
                        dve.drain().then_inc(c.exp_in.sem, 1)
                    for t in range(T):
                        dve.wait_ge(c.exp_ready.sem, c.exp_ready.at(b, t + 1))
                        dve.tensor_reduce(rsum[:, t:t + 1], e[:, t, :], AX, ALU.add)
                    dve.drain()
                    dve.reciprocal(rsum[:, :], rsum[:, :])
                    dve.drain()
                    for i in range(2):
                        dve.wait_ge(c.V.full, c.V.filled(b, ("y", i)))
                        y = c.V.slot(("y", i))
                        for t in (2 * i, 2 * i + 1):
                            last = dve.tensor_scalar(c.r[:, t, :], y[:, (t - 2 * i) * D:(t - 2 * i + 1) * D],
                                                     rsum[:, t:t + 1], None, ALU.mult)
                        last.then_inc(c.V.empty, 1)
                    dve.drain()
                    dve.tensor_tensor(c.r[:, :, :], c.r[:, :, :], c.x[:, bass.ds(b * T, T), :], ALU.add)
                    dve.drain()
                    dve_norm(c, dve, b, 0, c.r, c.x[:, bass.ds(b * T, T), :])

            @block.scalar
            def _(act):
                with act.Fori(0, B) as b:
                    act_fetch_x(c, act, b)
                    act_transposed_x(c, act, b)
                    for name, dst in (("q", qT), ("k", kT), ("v", v)):
                        act.wait_ge(c.A.full, c.A.filled(b, name))
                        src = c.A.slot(name)
                        act.activation(dst[:, :, :].rearrange("p a s -> p (a s)"), src, ACT.Copy).then_inc(c.A.empty, 1)
                    for t in range(T):
                        act.wait_ge(c.exp_in.sem, c.exp_in.at(b, t + 1))
                        act.activation(e[:, t, :], e[:, t, :], ACT.Exp, scale=1.0 / 16).then_inc(c.exp_ready.sem, 1)
                    for i in range(2):
                        act.wait_ge(c.A.full, c.A.filled(b, ("eT", i)))
                        src = c.A.slot(("eT", i))
                        act.activation(eT[:, 2 * i:2 * i + 2, :].rearrange("p a s -> p (a s)"), src, ACT.Copy).then_inc(c.A.empty, 1)

            @block.gpsimd
            def _(pool):
                with pool.Fori(0, B) as b:
                    pool_rstd(c, pool, b, 0)
        c.finish()



def layer_l1_xattn(nc, c, ins):
    with ExitStack() as ctx:
        sb = allocator(nc, ctx, "l1_xattn")
        lin, gate = sb("lin", [P, T, S]), sb("gate", [P, T, S])
        begin(c, A=4, V=2, O=0, x_here=1, ctx_here=1, var_ready=1, rstd_ready=1, vec_ready=2)

        with nc.Block() as block:
            @block.tensor
            def _(pe):
                with pe.Fori(0, B) as b:
                    pe_transpose_x(c, pe, b)
                    pe_transpose_ctx(c, pe, b)
                    pe.wait_ge(c.A.empty, c.A.copied(b, "cT"))
                    for i in range(2):
                        pe.wait_ge(c.A.empty, c.A.vacant(b, ("h", i)))
                        out = c.A.slot(("h", i))
                        for f in (2 * i, 2 * i + 1):
                            last = mm(pe, out[:, (f - 2 * i) * S:(f - 2 * i + 1) * S],
                                      [(c.cT[:, k, f * P:(f + 1) * P], c.xT[:, k, :]) for k in range(KD)])
                        last.then_inc(c.A.full, 1)
                    pe.wait_ge(c.vec_ready.sem, c.vec_ready.at(b, 2))
                    alone(c, pe)
                    pe_project_out(c, pe, b, [lambda t, f=f: gate[:, f, t * P:(t + 1) * P] for f in range(T)],
                                   [c.ctx[:, bass.ds(b * T + f, 1), :] for f in range(T)])

            @block.vector
            def _(dve):
                with dve.Fori(0, B) as b:
                    for i in range(2):
                        dve.wait_ge(c.A.empty, c.A.copied(b, ("h", i)))
                        sl = slice(2 * i, 2 * i + 2)
                        dve.tensor_tensor(gate[:, sl, :], gate[:, sl, :], lin[:, sl, :], ALU.mult).then_inc(c.vec_ready.sem, 1)
                    dve_residual_norm(c, dve, b)

            @block.scalar
            def _(act):
                with act.Fori(0, B) as b:
                    act_fetch_x(c, act, b)
                    act_fetch_ctx(c, act, b)
                    act_transposed_x(c, act, b)
                    act_transposed_ctx(c, act, b)
                    for i in range(2):
                        act.wait_ge(c.A.full, c.A.filled(b, ("h", i)))
                        src = c.A.slot(("h", i))
                        sl = slice(2 * i, 2 * i + 2)
                        act.activation(gate[:, sl, :].rearrange("p a s -> p (a s)"), src, ACT.Gelu)
                        act.activation(lin[:, sl, :].rearrange("p a s -> p (a s)"), src, ACT.Copy).then_inc(c.A.empty, 1)

            @block.gpsimd
            def _(pool):
                with pool.Fori(0, B) as b:
                    pool_rstd(c, pool, b, 0)
        c.finish()



def layer_l1_ffn(nc, c, ins):
    with ExitStack() as ctx:
        sb = allocator(nc, ctx, "l1_ffn")
        FT = 8
        w1, w2 = sb("w1", [P, KD, FT * P]), sb("w2", [P, FT, D])
        w1b, w2b = sb("w1b", [P, KD, FT * P]), sb("w2b", [P, FT, D])
        b1, b2 = sb("b1", [P, FT]), sb("b2", [1, D])
        shiftm, tokens, scale = sb("shiftm", [P, P]), sb("tokens", [P, 8]), sb("scale", [P, 1])
        before = sb("before", [P, D])
        outer1, outer2 = sb("outer1", [P, 4, D]), sb("outer2", [P, 4, 4, D // 4])
        hT = sb("hT", [P, FT, S])
        begin(c, A=6, V=10, O=0, x_here=1, var_ready=2, rstd_ready=2, vec_ready=2)
        c.expect_setup(0)

        with nc.Block() as block:
            @block.sync
            def _(sp):
                for dst, name in ((shiftm, "shift5"), (tokens, "tokens5"), (scale, "scale5"), (b1, "b1_5"), (b2, "b2_5")):
                    c.load(sp, dst, ins[name])
                for part, dst, name in ((0, w1, "w1_5"), (1, w2, "w2_5")):
                    c.load_part(sp, part, dst[:, :, :], ins[name])

            @block.tensor
            def _(pe):
                pe.wait_ge(c.loaded, c.load_count)
                with pe.Fori(0, B) as b:
                    pe_transpose_x(c, pe, b)
                    pe.wait_ge(c.A.empty, c.A.vacant(b, "before"))
                    out = c.A.slot("before")
                    pe.matmul(out[:, 0:D], shiftm[:, :], c.xn[:, 0, :], start=True, stop=True).then_inc(c.A.full, 1)
                    pe.wait_ge(c.vec_ready.sem, c.vec_ready.at(b, 1))
                    for k in range(KD):
                        for i in range(2):
                            pe.wait_ge(c.V.empty, c.V.vacant(b, ("m1", k, i)))
                            out = c.V.slot(("m1", k, i))
                            pe.matmul(out, c.xn[:, 0, k * P:(k + 1) * P], outer1[:, 2 * i:2 * i + 2, :],
                                                 start=True, stop=True).then_inc(c.V.full, 1)
                    pe.wait_ge(c.vec_ready.sem, c.vec_ready.at(b, 2))
                    for r in range(4):
                        pe.wait_ge(c.V.empty, c.V.vacant(b, ("m2", r)))
                        out = c.V.slot(("m2", r))
                        for k in range(KD):
                            last = pe.matmul(out[:, k * D:(k + 1) * D], c.xn[:, 0, k * P:(k + 1) * P],
                                             outer2[:, r, :, :], start=True, stop=True)
                        last.then_inc(c.V.full, 1)
                    pe.wait_ge(c.A.empty, c.A.copied(b, "xT"))
                    pe.wait_ge(c.V.empty, c.V.copied(b, ("m1", 1, 1)))
                    for i in range(FT // 2):
                        pe.wait_ge(c.A.empty, c.A.vacant(b, ("h", i)))
                        out = c.A.slot(("h", i))
                        for m in (2 * i, 2 * i + 1):
                            last = mm(pe, out[:, (m - 2 * i) * S:(m - 2 * i + 1) * S],
                                      [(w1b[:, k, m * P:(m + 1) * P], c.xT[:, k, :]) for k in range(KD)])
                        last.then_inc(c.A.full, 1)
                    pe.wait_ge(c.A.empty, c.A.copied(b, ("h", FT // 2 - 1)))
                    pe.wait_ge(c.V.empty, c.V.copied(b, ("m2", 3)))
                    pe_project_out(c, pe, b, [lambda t, f=f: hT[:, f, t * P:(t + 1) * P] for f in range(FT)],
                                   [w2b[:, f, :] for f in range(FT)], [b2[0:1, :]])

            @block.vector
            def _(dve):
                dve.wait_ge(c.loaded, c.load_count)
                dve.tensor_scalar(tokens[:, :], tokens[:, :], scale[:, 0:1], None, ALU.mult)
                dve.drain()
                with dve.Fori(0, B) as b:
                    dve.wait_ge(c.A.empty, c.A.copied(b, "before"))
                    for a in range(4):
                        last = dve.tensor_scalar(outer1[:, a, :], before[:, :], tokens[:, a:a + 1], None, ALU.mult)
                    last.then_inc(c.vec_ready.sem, 1)
                    for a in range(4):
                        last = dve.tensor_scalar(outer2[:, :, a, :], before[:, :].rearrange("p (o r) -> p r o", r=4),
                                                 tokens[:, 4 + a:5 + a], None, ALU.mult)
                    last.then_inc(c.vec_ready.sem, 1)
                    dve.wait_ge(c.arrived[0], c.arrivals[0])
                    for k in range(KD):
                        for i in range(2):
                            dve.wait_ge(c.V.full, c.V.filled(b, ("m1", k, i)))
                            m = c.V.slot(("m1", k, i))
                            dve.tensor_tensor(w1b[:, k, i * S:(i + 1) * S], m, w1[:, k, i * S:(i + 1) * S], ALU.add).then_inc(c.V.empty, 1)
                    dve.wait_ge(c.arrived[1], c.arrivals[1])
                    for r in range(4):
                        dve.wait_ge(c.V.full, c.V.filled(b, ("m2", r)))
                        m = c.V.slot(("m2", r)).rearrange("p (k d) -> p k d", d=D)
                        dve.tensor_tensor(w2b[:, 2 * r:2 * r + 2, :], m, w2[:, 2 * r:2 * r + 2, :], ALU.add).then_inc(c.V.empty, 1)
                    here = bass.ds(b * T, T)
                    dve_norm(c, dve, b, 0, c.ctx[:, here, :], c.ctx[:, here, :])
                    dve_residual_norm(c, dve, b, 1)

            @block.scalar
            def _(act):
                with act.Fori(0, B) as b:
                    act_fetch_x(c, act, b)
                    act_transposed_x(c, act, b)
                    act.wait_ge(c.A.full, c.A.filled(b, "before"))
                    src = c.A.slot("before")
                    act.activation(before[:, :], src[:, 0:D], ACT.Copy).then_inc(c.A.empty, 1)
                    for i in range(FT // 2):
                        act.wait_ge(c.A.full, c.A.filled(b, ("h", i)))
                        src = c.A.slot(("h", i))
                        for m in (2 * i, 2 * i + 1):
                            last = act.activation(hT[:, m, :], src[:, (m - 2 * i) * S:(m - 2 * i + 1) * S], ACT.Gelu,
                                                  bias=b1[:, m:m + 1])
                        last.then_inc(c.A.empty, 1)

            @block.gpsimd
            def _(pool):
                with pool.Fori(0, B) as b:
                    for j in range(2):
                        pool_rstd(c, pool, b, j)
        c.finish()



def layer_l2_attn(nc, c, ins):
    with ExitStack() as ctx:
        sb = allocator(nc, ctx, "l2_attn")
        wq, wk = sb("wq", [P, KD, NG * P]), sb("wk", [P, KD, NG * P])
        wv, wo, wn = sb("wv", [P, KD, D]), sb("wo", [P, KD, D]), sb("wn", [P, KD, H])
        qbias, kbias = sb("qbias", [P, NG]), sb("kbias", [P, NG])
        vbias, obias, nbias = sb("vbias", [1, D]), sb("obias", [1, D]), sb("nbias", [1, H])
        qT, kT, kn = sb("qT", [P, NG, S]), sb("kT", [P, NG, S]), sb("kn", [P, NG, T, P])
        oT, expn = sb("oT", [P, KD, S]), sb("expn", [P, T, H])
        alloc_linear(c, sb)
        begin(c, A=1 + 4 + 2 + 2 + 1, V=NG * (T + 2) + 2, O=NG, x_here=1, var_ready=1, rstd_ready=1, heads_ready=NG)
        c.expect_setup(2)

        with nc.Block() as block:
            @block.sync
            def _(sp):
                c.load_part(sp, 0, wq[:, :, :], ins["wq6"])
                for dst, name in ((qbias, "qbias6"), (kbias, "kbias6"), (vbias, "vbias6"), (obias, "obias6"), (nbias, "nbias6"),
                                  (c.causal01, "causal01"), (c.blocks, "blocks")):
                    c.load(sp, dst, ins[name])
                for dst, name in ((wk, "wk6"), (wv, "wv6"), (wo, "wo6"), (wn, "wn6")):
                    c.load_part(sp, 1, dst[:, :, :], ins[name])

            @block.tensor
            def _(pe):
                with pe.Fori(0, B) as b:
                    pe_transpose_x(c, pe, b)
                    pe.wait_ge(c.A.empty, c.A.copied(b, "xT"))
                    for part, (name, w) in enumerate((("q", wq), ("k", wk))):
                        pe.wait_ge(c.arrived[part], c.arrivals[part])
                        for i in range(2):
                            pe.wait_ge(c.A.empty, c.A.vacant(b, (name, i)))
                            out = c.A.slot((name, i))
                            for g in (2 * i, 2 * i + 1):
                                last = mm(pe, out[:, (g - 2 * i) * S:(g - 2 * i + 1) * S],
                                          [(w[:, k, g * P:(g + 1) * P], c.xT[:, k, :]) for k in range(KD)])
                            last.then_inc(c.A.full, 1)
                    pe.wait_ge(c.loaded, c.load_count)
                    for name, w, bias, n in (("v", wv, vbias, D), ("n", wn, nbias, H)):
                        pe.wait_ge(c.A.empty, c.A.vacant(b, name))
                        out = c.A.slot(name)
                        for t in range(T):
                            last = mm(pe, out[:, t * n:(t + 1) * n],
                                      [(c.xT[:, k, t * P:(t + 1) * P], w[:, k, :]) for k in range(KD)]
                                      + [(c.ones[0:1, 0:P], bias[0:1, :])])
                        last.then_inc(c.A.full, 1)
                    pe.wait_ge(c.A.empty, c.A.copied(b, ("k", 1)))
                    for i in range(2):
                        pe.wait_ge(c.A.empty, c.A.vacant(b, ("kn", i)))
                        out = c.A.slot(("kn", i))
                        for g in (2 * i, 2 * i + 1):
                            for t in range(T):
                                at = ((g - 2 * i) * T + t) * P
                                last = pe.transpose(out[:, at:at + P], kT[:, g, t * P:(t + 1) * P], c.ident[:, :])
                        last.then_inc(c.A.full, 1)
                    pe.wait_ge(c.A.empty, c.A.copied(b, ("kn", 1)))
                    pe.wait_ge(c.setup_done, c.setup_dones)
                    pe_linear(c, pe, b, lambda g: qT[:, g, :], lambda g: kT[:, g, :], lambda g, t: kn[:, g, t, :])
                    pe_transpose_attn(c, pe, b, c.on, D)
                    pe.wait_ge(c.A.empty, c.A.copied(b, ("oT", 0)))
                    pe_project_out(c, pe, b, [lambda t, k=k: oT[:, k, t * P:(t + 1) * P] for k in range(KD)],
                                   [wo[:, k, :] for k in range(KD)], [obias[0:1, :]])

            @block.vector
            def _(dve):
                dve.memset(c.v[:, :, :, :], 0.0).then_inc(c.setup_done, 1)
                dve.wait_ge(c.loaded, c.load_count)
                with dve.Fori(0, B) as b:
                    def factors(g, o):
                        if g == 0:
                            dve.wait_ge(c.A.empty, c.A.copied(b, "n"))
                        return expn[:, :, 4 * g:4 * g + 4]

                    dve_linear(c, dve, b, factors)
                    dve_residual_norm(c, dve, b)

            @block.scalar
            def _(act):
                act.wait_ge(c.loaded, c.load_count)
                with act.Fori(0, B) as b:
                    act_fetch_x(c, act, b)
                    act_transposed_x(c, act, b)
                    act.wait_ge(c.setup_done, c.setup_dones)
                    for name, dst, bias in (("q", qT, qbias), ("k", kT, kbias)):
                        for i in range(2):
                            act.wait_ge(c.A.full, c.A.filled(b, (name, i)))
                            src = c.A.slot((name, i))
                            for g in (2 * i, 2 * i + 1):
                                last = act.activation(dst[:, g, :], src[:, (g - 2 * i) * S:(g - 2 * i + 1) * S],
                                                      ACT.Identity, bias=bias[:, g:g + 1])
                                if name == "q":
                                    last = spread_heads(
                                        lambda dst, src, rows: act.activation(dst, src, ACT.Identity, bias=bias[rows, g:g + 1]),
                                        c.qm, src[:, (g - 2 * i) * S:(g - 2 * i + 1) * S], range(4 * g, 4 * g + 4), 32)
                            last.then_inc(c.A.empty, 1)
                    act.wait_ge(c.A.full, c.A.filled(b, "v"))
                    src = c.A.slot("v")
                    act.activation(c.v[:, :, :, 0:16].rearrange("p t h d -> p (t h) d"),
                                   src.rearrange("p (a d) -> p a d", d=16), ACT.Copy).then_inc(c.A.empty, 1)
                    act.wait_ge(c.A.full, c.A.filled(b, "n"))
                    src = c.A.slot("n")
                    act.activation(expn[:, :, :].rearrange("p t h -> p (t h)"), src[:, 0:T * H], ACT.Exp, scale=-1.0).then_inc(c.A.empty, 1)
                    for i in range(2):
                        act.wait_ge(c.A.full, c.A.filled(b, ("kn", i)))
                        act.activation(kn[:, 2 * i:2 * i + 2, :, :].rearrange("p g t d -> p (g t d)"),
                                       c.A.slot(("kn", i)), ACT.Copy).then_inc(c.A.empty, 1)
                    act_transposed_attn(c, act, b, oT, D)

            @block.gpsimd
            def _(pool):
                pool.memset(c.qm[:, :, :], 0.0).then_inc(c.setup_done, 1)
                with pool.Fori(0, B) as b:
                    pool_rstd(c, pool, b, 0)
        c.finish()



KT2 = 2 * T
HD = 64
INNER = H * HD


def layer_l2_xattn(nc, c, ins):
    with ExitStack() as ctx:
        sb = allocator(nc, ctx, "l2_xattn")
        IT = INNER // P
        PAIRS = H // 2
        wq, wk, wv = (sb(n, [P, KD, INNER]) for n in ("wq", "wk", "wv"))
        wo = sb("wo", [P, IT, D])
        gain, shiftc = sb("gain", [P, 2, KD]), sb("shiftc", [P, 2, KD])
        mask_row8 = sb("mask_row8", [1, B * S], mybir.dt.uint8)
        hide_row = sb("hide_row", [1, B, S], BF16)
        qm, km = sb("qm", [P, 4, S]), sb("km", [P, 4, 2 * S])
        alloc_softmax(c, sb, KT2, HD, INNER, span=2, lag=2)
        oT = c.pTs[:, :, :, :].rearrange("p r k q -> p (r k q)")[:, 0:IT * S].rearrange("p (m s) -> p m s", s=S)
        begin(c, A=2 * KD + KT2 + H * T + IT // 2, V=3 * PAIRS + H * T * 2 + 2, O=4 * PAIRS,
              ctx_here=1, x_here=1, var_ready=2, rstd_ready=2, heads_ready=2 * PAIRS, max_ready=H * T)
        c.expect_setup(2)

        with nc.Block() as block:
            @block.sync
            def _(sp):
                for dst, name in ((mask_row8, "mask_row7"), (gain, "gain7"), (shiftc, "shift7")):
                    c.load(sp, dst, ins[name])
                for part, dst, name in ((0, wv, "wv7"), (1, wq, "wq7"), (1, wk, "wk7"), (1, wo, "wo7")):
                    c.load_part(sp, part, dst[:, :, :], ins[name])

            @block.tensor
            def _(pe):
                pe.wait_ge(c.loaded, c.load_count)
                with pe.Fori(0, B) as b:
                    for name, src, here in (("zc", c.ctxn, c.ctx_here), ("zx", c.xn, c.x_here)):
                        for k in range(KD):
                            pe.wait_ge(c.A.empty, c.A.vacant(b, (name, k)))
                            out = c.A.slot((name, k))
                            pe.wait_ge(here.sem, here.at(b, 1))
                            for t in range(T):
                                last = pe.transpose(out[:, t * P:(t + 1) * P], src[:, t, k * P:(k + 1) * P], c.ident[:, :])
                            last.then_inc(c.A.full, 1)

                    def project_pair(i):
                        g, rest = divmod(i + AHEAD, 2 * T)
                        if 0 < g < PAIRS and rest == 0:
                            pe_pair(g)

                    def pe_pair(g):
                        cols = slice(g * P, (g + 1) * P)
                        pe.wait_ge(c.V.empty, c.V.vacant(b, ("q", g)))
                        mm(pe, c.V.slot(("q", g)), [(wq[:, k, cols], c.xT[:, k, :]) for k in range(KD)]).then_inc(c.V.full, 1)
                        for i, zT in enumerate((c.cT, c.xT)):
                            pe.wait_ge(c.V.empty, c.V.vacant(b, ("k", g, i)))
                            mm(pe, c.V.slot(("k", g, i)), [(wk[:, k, cols], zT[:, k, :]) for k in range(KD)]).then_inc(c.V.full, 1)

                    pe.wait_ge(c.A.empty, c.A.copied(b, ("zx", KD - 1)))
                    pe.wait_ge(c.arrived[0], c.arrivals[0])
                    for kt in range(KT2):
                        pe.wait_ge(c.A.empty, c.A.vacant(b, ("v", kt)))
                        out = c.A.slot(("v", kt))
                        zT = c.cT if kt < T else c.xT
                        for i in range(2):
                            last = mm(pe, out[:, i * S:(i + 1) * S],
                                      [(zT[:, k, kt % T * P:(kt % T + 1) * P], wv[:, k, i * S:(i + 1) * S]) for k in range(KD)])
                        last.then_inc(c.A.full, 1)
                    pe.wait_ge(c.arrived[1], c.arrivals[1])
                    pe_pair(0)

                    def scores(out, h, qt):
                        g = h // 2
                        if qt == 0:
                            pe.wait_ge(c.V.empty, c.V.copied(b, ("k", g, 1)))
                        q = qm[:, h % 4, qt * P:(qt + 1) * P]
                        pe.matmul(out[:, 0:S], q, km[:, h % 4, 0:S], start=True, stop=True)
                        return pe.matmul(out[:, S:2 * S], q, km[:, h % 4, S:2 * S], start=True, stop=True)

                    pe.wait_ge(c.setup_done, c.setup_dones)
                    pe_attend(c, pe, b, KT2, scores, before_unit=project_pair)
                    pe_transpose_attn(c, pe, b, c.on, INNER)
                    pe.wait_ge(c.A.empty, c.A.copied(b, ("oT", IT // 2 - 1)))
                    pe_project_out(c, pe, b, [lambda t, m=m: oT[:, m, t * P:(t + 1) * P] for m in range(IT)],
                                   [wo[:, m, :] for m in range(IT)])

            @block.vector
            def _(dve):
                dve_norm(c, dve, 0, 0, c.x[:, 0:T, :], c.xn).then_inc(c.x_here.sem, 1)
                dve.wait_ge(c.loaded, c.load_count)
                dve.tensor_scalar(hide_row[:, :, :].rearrange("p b s -> p (b s)"), mask_row8[:, :], 1.0, 1e30,
                                  ALU.subtract, ALU.mult)
                dve.drain().then_inc(c.setup_done, 1)
                dve.wait_ge(c.setup_done, c.setup_dones)
                with dve.Fori(0, B) as b:
                    def dve_pair(g):
                        dve.wait_ge(c.V.full, c.V.filled(b, ("q", g)))
                        spread_heads(lambda dst, src, rows: dve.tensor_scalar(dst, src, HD ** -0.5, None, ALU.mult), qm,
                                     c.V.slot(("q", g)), (2 * g % 4, 2 * g % 4 + 1), HD).then_inc(c.V.empty, 1)
                        for i in range(2):
                            dve.wait_ge(c.V.full, c.V.filled(b, ("k", g, i)))
                            spread_heads(lambda dst, src, rows: dve.tensor_copy(dst, src), km[:, :, i * S:(i + 1) * S],
                                         c.V.slot(("k", g, i)), (2 * g % 4, 2 * g % 4 + 1), HD).then_inc(c.V.empty, 1)

                    def copy_pair(i):
                        g, rest = divmod(i + AHEAD, 2 * T)
                        if 0 < g < PAIRS and rest == 0:
                            dve_pair(g)

                    dve_pair(0)
                    dve_attend(c, dve, b, KT2, HD, before_unit=copy_pair)
                    dve_norm_ahead(c, dve, b)
                    dve_residual_norm(c, dve, b, 2)

            @block.scalar
            def _(act):
                act.wait_ge(c.loaded, c.load_count)
                with act.Fori(0, B) as b:
                    act_fetch_ctx(c, act, b)
                    for name, dst, i in (("zc", c.cT, 0), ("zx", c.xT, 1)):
                        for k in range(KD):
                            act.wait_ge(c.A.full, c.A.filled(b, (name, k)))
                            act.activation(dst[:, k, :], c.A.slot((name, k))[:, 0:S], ACT.Identity,
                                           bias=shiftc[:, i, k:k + 1], scale=gain[:, i, k:k + 1]).then_inc(c.A.empty, 1)
                    act.wait_ge(c.setup_done, c.setup_dones)
                    for h in range(4):
                        row = HD * (1 - h % 2)
                        act.activation(km[row:row + 1, h, 0:S], hide_row[:, bass.ds(b, 1), :].rearrange("p b s -> p (b s)"),
                                       ACT.Copy)
                    act.drain()
                    for kt in range(KT2):
                        act.wait_ge(c.A.full, c.A.filled(b, ("v", kt)))
                        src = c.A.slot(("v", kt)).rearrange("p (h d) -> p h d", d=HD)
                        act.activation(c.v[:, kt, :, 0:HD], src, ACT.Copy).then_inc(c.A.empty, 1)

                    act_attend(c, act, b, KT2)
                    act_transposed_attn(c, act, b, oT, INNER)

            @block.gpsimd
            def _(pool):
                pool_rstd(c, pool, 0, 0)
                pool.memset(qm[:, :, :], 0.0)
                pool.memset(km[:, :, :], 0.0)
                pool.drain()
                for h in range(4):
                    row = HD * (1 - h % 2)
                    pool.memset(qm[row:row + 1, h, :], 1.0)
                pool.drain().then_inc(c.setup_done, 1)
                with pool.Fori(0, B) as b:
                    for j in (1, 2):
                        pool_rstd(c, pool, b, j)
        c.finish()
        for signal in (c.x_here, c.var_ready, c.rstd_ready):
            signal.once_more()



def dve_scales(c, dve, peak, scale, inv):
    dve.tensor_scalar(scale, peak, 1e-6, 1.0 / 127.0, ALU.max, ALU.mult)
    dve.drain()
    dve.reciprocal(inv, scale)
    dve.drain()


def layer_l2_ffn(nc, c, ins):
    with ExitStack() as ctx:
        sb = allocator(nc, ctx, "l2_ffn")
        FT = 8
        w1, w2 = sb("w1", [P, KD, FT * P]), sb("w2", [P, FT, D])
        w1q, w2q = sb("w1q", [P, KD, FT * P], BF16), sb("w2q", [P, FT, D], BF16)
        b1, b1s, b2 = sb("b1", [P, FT]), sb("b1s", [P, FT]), sb("b2", [1, D])
        peak, peaks = sb("peak", [P, 4]), sb("peaks", [P, 4])
        scale, inv = sb("scale", [P, 4]), sb("inv", [P, 4])
        out1, out2 = sb("out1", [P, 1]), sb("out2", [P, 1])
        magic = sb("magic", [P, 1])
        xr, xq = sb("xr", [P, KD, S]), sb("xq", [P, KD, S], BF16)
        h = sb("h", [P, B, FT, S])
        hbatch = sb("hbatch", [P, 1])
        minus_magic = sb("minus_magic", [P, 1])
        hr, hq = sb("hr", [P, FT, S]), sb("hq", [P, B, FT, S], BF16)
        with nc.Block() as block:
            c.expect_setup(3)
            first = c.setup_dones

            @block.sync
            def _(sp):
                for dst, name in ((w1, "w1_8"), (w2, "w2_8"), (b1, "b1_8"), (b2, "b2_8")):
                    c.load(sp, dst, ins[name])

            @block.vector
            def _(dve):
                dve.memset(magic[:, :], MAGIC)
                dve.memset(minus_magic[:, :], -MAGIC)
                dve.memset(peak[:, :], 0.0)
                dve.drain()
                for i, src in enumerate((c.x, w1, w2)):
                    if i == 1:
                        dve.wait_ge(c.loaded, c.load_count)
                    dve.tensor_reduce(peak[:, i:i + 1], src[:, :, :], mybir.AxisListType.XY, ALU.max,
                                      apply_absolute_value=True)
                dve.drain().then_inc(c.setup_done, 1)
                dve.wait_ge(c.setup_done, first - 1)
                dve_scales(c, dve, peaks[:, 0:3], scale[:, 0:3], inv[:, 0:3])
                dve.tensor_tensor(out1[:, :], scale[:, 0:1], scale[:, 1:2], ALU.mult)
                dve.drain()
                dve.tensor_scalar(b1s[:, :], b1[:, :], out1[:, 0:1], None, ALU.mult)
                for w, wq, i in ((w1, w1q, 1), (w2, w2q, 2)):
                    dve.tensor_scalar(w[:, :, :], w[:, :, :], inv[:, i:i + 1], MAGIC, ALU.mult, ALU.add)
                    dve.drain()
                    dve.tensor_scalar(wq[:, :, :], w[:, :, :], MAGIC, None, ALU.subtract)
                dve.drain().then_inc(c.setup_done, 1)

            @block.gpsimd
            def _(pool):
                pool.wait_ge(c.setup_done, first - 2)
                pool.partition_all_reduce(peaks[:, 0:3], peak[:, 0:3], P, RMAX).then_inc(c.setup_done, 1)

        begin(c, A=2 + FT // 2, V=0, O=0, x_here=1, vec_ready=1)
        with nc.Block() as block:
            @block.tensor
            def _(pe):
                with pe.Fori(0, B) as b:
                    pe_transpose_x_halves(c, pe, b)
                    pe.wait_ge(c.vec_ready.sem, c.vec_ready.at(b, 1))
                    for i in range(FT // 2):
                        pe.wait_ge(c.A.empty, c.A.vacant(b, ("h", i)))
                        out = c.A.slot(("h", i))
                        for m in (2 * i, 2 * i + 1):
                            last = mm(pe, out[:, (m - 2 * i) * S:(m - 2 * i + 1) * S],
                                      [(w1q[:, k, m * P:(m + 1) * P], xq[:, k, :]) for k in range(KD)])
                        last.then_inc(c.A.full, 1)

            @block.scalar
            def _(act):
                with act.Fori(0, B) as b:
                    act_fetch_x(c, act, b)
                    for k in range(KD):
                        act.wait_ge(c.A.full, c.A.filled(b, ("xT", k)))
                        src = c.A.slot(("xT", k))[:, 0:S]
                        act.activation(xr[:, k, :], src, ACT.Identity, bias=magic[:, 0:1], scale=inv[:, 0:1]).then_inc(c.A.empty, 1)
                    for i in range(FT // 2):
                        act.wait_ge(c.A.full, c.A.filled(b, ("h", i)))
                        src = c.A.slot(("h", i))
                        for m in (2 * i, 2 * i + 1):
                            alone(c, act)
                            last = act.activation(h[:, bass.ds(b, 1), m, :], src[:, (m - 2 * i) * S:(m - 2 * i + 1) * S],
                                                  ACT.Gelu, bias=b1s[:, m:m + 1], scale=out1[:, 0:1])
                        last.then_inc(c.A.empty, 1)

            @block.vector
            def _(dve):
                with dve.Fori(0, B) as b:
                    dve.wait_ge(c.A.empty, c.A.copied(b, ("xT", KD - 1)))
                    dve.tensor_scalar(xq[:, :, :], xr[:, :, :], MAGIC, None, ALU.subtract).then_inc(c.vec_ready.sem, 1)
                    dve.wait_ge(c.A.empty, c.A.copied(b, ("h", FT // 2 - 1)))
                    alone(c, dve)
                    dve.tensor_reduce(hbatch[:, :], h[:, bass.ds(b, 1), :, :], mybir.AxisListType.XYZ, ALU.max,
                                      apply_absolute_value=True)
                    dve.drain()
                    dve.tensor_tensor(peak[:, 3:4], peak[:, 3:4], hbatch[:, :], ALU.max)
                    dve.drain()
        c.finish()

        with nc.Block() as block:
            c.expect_setup(2)
            second = c.setup_dones

            @block.gpsimd
            def _(pool):
                pool.partition_all_reduce(peaks[:, 3:4], peak[:, 3:4], P, RMAX).then_inc(c.setup_done, 1)

            @block.vector
            def _(dve):
                dve.wait_ge(c.setup_done, second - 1)
                dve_scales(c, dve, peaks[:, 3:4], scale[:, 3:4], inv[:, 3:4])
                dve.tensor_tensor(out2[:, :], scale[:, 2:3], scale[:, 3:4], ALU.mult)
                dve.drain().then_inc(c.setup_done, 1)

        begin(c, A=0, V=2, O=0, var_ready=1, rstd_ready=1, vec_ready=1)
        with nc.Block() as block:
            @block.tensor
            def _(pe):
                with pe.Fori(0, B) as b:
                    pe.wait_ge(c.vec_ready.sem, c.vec_ready.at(b, 1))
                    pe_project_out(c, pe, b, [lambda t, f=f: hq[:, bass.ds(b, 1), f, t * P:(t + 1) * P].rearrange("p b s -> p (b s)") for f in range(FT)],
                                   [w2q[:, f, :] for f in range(FT)], [b2[0:1, :]])

            @block.scalar
            def _(act):
                with act.Fori(0, B) as b:
                    alone(c, act)
                    act.activation(hr[:, :, :].rearrange("p f s -> p (f s)"),
                                   h[:, bass.ds(b, 1), :, :].rearrange("p b f s -> p (b f s)"), ACT.Identity,
                                   bias=magic[:, 0:1], scale=inv[:, 3:4])
                    act.drain()
                    act.activation(hq[:, bass.ds(b, 1), :, :].rearrange("p b f s -> p (b f s)"),
                                   hr[:, :, :].rearrange("p f s -> p (f s)"), ACT.Identity,
                                   bias=minus_magic[:, 0:1]).then_inc(c.vec_ready.sem, 1)
                    act.drain()

            @block.vector
            def _(dve):
                with dve.Fori(0, B) as b:
                    dve.drain()
                    for i in range(2):
                        dve.wait_ge(c.V.full, c.V.filled(b, ("y", i)))
                        y = c.V.slot(("y", i))
                        last = dve.tensor_scalar(c.r[:, 2 * i:2 * i + 2, :].rearrange("p t d -> p (t d)"), y,
                                                 out2[:, 0:1], None, ALU.mult)
                        last.then_inc(c.V.empty, 1)
                    dve.drain()
                    dve.tensor_tensor(c.r[:, :, :], c.r[:, :, :], c.x[:, bass.ds(b * T, T), :], ALU.add)
                    dve.drain()
                    dve_norm(c, dve, b, 0, c.r, c.x[:, bass.ds(b * T, T), :])

            @block.gpsimd
            def _(pool):
                with pool.Fori(0, B) as b:
                    pool_rstd(c, pool, b, 0)
        c.finish()



def layer_l3_attn(nc, c, ins):
    with ExitStack() as ctx:
        sb = allocator(nc, ctx, "l3_attn")
        wq, wk = sb("wq", [P, KD, NG * P]), sb("wk", [P, KD, NG * P])
        wv, wo = sb("wv", [P, KD, D]), sb("wo", [P, KD, D])
        rope, qrope = sb("rope", [P, S]), sb("qrope", [P, S])
        qm, kT = sb("qm", [P, H, S]), sb("kT", [P, NG, S])
        oT = sb("oT", [P, KD, S])
        alloc_softmax(c, sb, T, 32, D)
        begin(c, a_slots=4, A=KD + H * T + KD, V=2 * NG + 2 + H * T + 2, O=2 * NG,
              x_here=1, var_ready=1, rstd_ready=1, heads_ready=NG, max_ready=H * T)
        c.expect_setup(1)

        with nc.Block() as block:
            @block.sync
            def _(sp):
                for part, dst, name in ((0, wq, "wq9"), (1, wk, "wk9"), (1, wv, "wv9"), (1, wo, "wo9")):
                    c.load_part(sp, part, dst[:, :, :], ins[name])
                    if part == 0:
                        c.load(sp, qrope, ins["qrope9"])
                        c.load(sp, rope, ins["rope9"])

            @block.tensor
            def _(pe):
                pe.wait_ge(c.loaded, c.load_count)
                with pe.Fori(0, B) as b:
                    pe_transpose_x_halves(c, pe, b)
                    pe.wait_ge(c.A.empty, c.A.copied(b, ("xT", KD - 1)))
                    for name, w in (("q", wq), ("k", wk)):
                        for g in range(NG):
                            pe.wait_ge(c.V.empty, c.V.vacant(b, (name, g)))
                            part = 0 if name == "q" else 1
                            pe.wait_ge(c.arrived[part], c.arrivals[part])
                            out = c.V.slot((name, g))
                            mm(pe, out, [(w[:, k, g * P:(g + 1) * P], c.xT[:, k, :]) for k in range(KD)]).then_inc(c.V.full, 1)
                    pe_project_values(c, pe, b, c.xT, wv)
                    pe.wait_ge(c.V.empty, c.V.copied(b, ("v", 1)))

                    def scores(out, h, qt):
                        return pe.matmul(out[:, 0:S], qm[:, h, qt * P:(qt + 1) * P], kT[:, h // 4, :], start=True, stop=True)

                    pe.wait_ge(c.setup_done, c.setup_dones)
                    pe_attend(c, pe, b, T, scores)
                    pe_transpose_attn(c, pe, b, c.on, D)
                    pe.wait_ge(c.A.empty, c.A.copied(b, ("oT", KD - 1)))
                    pe_project_out(c, pe, b, [lambda t, k=k: oT[:, k, t * P:(t + 1) * P] for k in range(KD)],
                                   [wo[:, k, :] for k in range(KD)])

            @block.vector
            def _(dve):
                dve.wait_ge(c.loaded, c.load_count)
                dve.wait_ge(c.setup_done, c.setup_dones)
                with dve.Fori(0, B) as b:
                    for g in range(NG):
                        dve.wait_ge(c.V.full, c.V.filled(b, ("q", g)))
                        spread_heads(lambda dst, src, rows: dve.tensor_tensor(dst, src, qrope[rows, :], ALU.mult),
                                     qm, c.V.slot(("q", g)), range(4 * g, 4 * g + 4), 32).then_inc(c.V.empty, 1)
                    for g in range(NG):
                        dve.wait_ge(c.V.full, c.V.filled(b, ("k", g)))
                        dve.tensor_tensor(kT[:, g, :], c.V.slot(("k", g)), rope[:, :], ALU.mult).then_inc(c.V.empty, 1)
                    dve_values(c, dve, b)
                    dve_attend(c, dve, b, T, 16)
                    dve_residual_norm(c, dve, b)

            @block.scalar
            def _(act):
                with act.Fori(0, B) as b:
                    act_fetch_x(c, act, b)
                    act_transposed_x_halves(c, act, b)
                    act_attend(c, act, b, T)
                    act_transposed_attn(c, act, b, oT, D)

            @block.gpsimd
            def _(pool):
                pool.memset(c.v[:, :, :, :], 0.0)
                pool.memset(qm[:, :, :], 0.0)
                pool.drain().then_inc(c.setup_done, 1)
                with pool.Fori(0, B) as b:
                    pool_rstd(c, pool, b, 0)
        c.finish()



CLIP = 11.0


def layer_l3_xattn(nc, c, ins):
    with ExitStack() as ctx:
        sb = allocator(nc, ctx, "l3_xattn")
        IT = INNER // P
        wq, wk, wv = (sb(n, [P, KD, INNER]) for n in ("wq", "wk", "wv"))
        wo, obias = sb("wo", [P, IT, D]), sb("obias", [1, D])
        gain, shiftc = sb("gain", [P, 2, KD]), sb("shiftc", [P, 2, KD])
        PAIRS = H // 2
        qm, kT = sb("qm", [P, H, S]), sb("kT", [P, IT, S])
        v = sb("v", [P, T, H, HD])
        e = sb("e", [P, 4, T, S])
        half, total = sb("half", [P, 2, 2, S]), sb("total", [P, 4, S])
        ones = sb("ones", [P, HD])
        rec = sb("rec", [P, S])
        oT = kT
        begin(c, A=2 + 2 * (IT // 2) + T, V=H * T + 2, O=2 * PAIRS, ctx_here=1, x_here=1, var_ready=2, rstd_ready=2,
              exp_in=H, exp_ready=H, sums_ready=H)
        c.expect_setup(2)

        with nc.Block() as block:
            @block.sync
            def _(sp):
                for dst, name in ((gain, "gain10"), (shiftc, "shift10"), (obias, "obias10")):
                    c.load(sp, dst, ins[name])
                for part, dst, name in ((0, wq, "wq10"), (1, wk, "wk10"), (2, wv, "wv10"), (2, wo, "wo10")):
                    c.load_part(sp, part, dst[:, :, :], ins[name])

            @block.tensor
            def _(pe):
                pe.wait_ge(c.loaded, c.load_count)
                with pe.Fori(0, B) as b:
                    for name, src, here in (("zc", c.ctxn, c.ctx_here), ("zx", c.xn, c.x_here)):
                        pe.wait_ge(c.A.empty, c.A.vacant(b, name))
                        out = c.A.slot(name)
                        pe.wait_ge(here.sem, here.at(b, 1))
                        for k in range(KD):
                            for t in range(T):
                                last = pe.transpose(out[:, k * S + t * P:k * S + (t + 1) * P], src[:, t, k * P:(k + 1) * P], c.ident[:, :])
                        last.then_inc(c.A.full, 1)
                    pe.wait_ge(c.A.empty, c.A.copied(b, "zx"))
                    for part, (name, w, zT) in enumerate((("q", wq, c.xT), ("k", wk, c.cT))):
                        pe.wait_ge(c.arrived[part], c.arrivals[part])
                        for i in range(IT // 2):
                            pe.wait_ge(c.A.empty, c.A.vacant(b, (name, i)))
                            out = c.A.slot((name, i))
                            for m in (2 * i, 2 * i + 1):
                                last = mm(pe, out[:, (m - 2 * i) * S:(m - 2 * i + 1) * S],
                                          [(w[:, k, m * P:(m + 1) * P], zT[:, k, :]) for k in range(KD)])
                            last.then_inc(c.A.full, 1)
                    pe.wait_ge(c.arrived[2], c.arrivals[2])
                    for t in range(T):
                        pe.wait_ge(c.A.empty, c.A.vacant(b, ("v", t)))
                        out = c.A.slot(("v", t))
                        for i in range(2):
                            last = mm(pe, out[:, i * S:(i + 1) * S],
                                      [(c.cT[:, k, t * P:(t + 1) * P], wv[:, k, i * S:(i + 1) * S]) for k in range(KD)])
                        last.then_inc(c.A.full, 1)
                    pe.wait_ge(c.A.empty, c.A.copied(b, ("k", IT // 2 - 1)))
                    pe.wait_ge(c.A.empty, c.A.copied(b, ("v", T - 1)))
                    pe.wait_ge(c.setup_done, c.setup_dones)
                    for step in range(H + 2):
                        if step < H:
                            h = step
                            for t in range(T):
                                pe.wait_ge(c.V.empty, c.V.vacant(b, ("s", h, t)))
                                pe.matmul(c.V.slot(("s", h, t)), kT[:, h // 2, t * P:(t + 1) * P], qm[:, h, :],
                                          start=True, stop=True).then_inc(c.V.full, 1)
                        if step >= 3 and step % 2:
                            g = (step - 3) // 2
                            pe.wait_ge(c.O.empty, c.O.vacant(b, ("sum", g)))
                            pe.wait_ge(c.sums_ready.sem, c.sums_ready.at(b, 2 * g + 2))
                            out = c.O.slot(("sum", g))
                            for m in range(2):
                                last = pe.matmul(out[m * HD:(m + 1) * HD, :], ones[:, :], total[:, (2 * g + m) % 4, :],
                                                 start=True, stop=True)
                            last.then_inc(c.O.full, 1)
                            pe.wait_ge(c.O.empty, c.O.vacant(b, ("O", g)))
                            out = c.O.slot(("O", g))
                            for k in range(T):
                                for m in range(2):
                                    last = pe.matmul(out[m * HD:(m + 1) * HD, :], v[:, k, 2 * g + m, :],
                                                     e[:, (2 * g + m) % 4, k, :], start=k == 0, stop=k == T - 1)
                            last.then_inc(c.O.full, 1)
                    pe.wait_ge(c.O.empty, c.O.copied(b, ("O", PAIRS - 1)))
                    pe_project_out(c, pe, b, [lambda t, m=m: oT[:, m, t * P:(t + 1) * P] for m in range(IT)],
                                   [wo[:, m, :] for m in range(IT)], [obias[0:1, :]])

            @block.vector
            def _(dve):
                dve.memset(ones[:, :], 1.0)
                dve.drain().then_inc(c.setup_done, 1)
                dve_norm(c, dve, 0, 0, c.x[:, 0:T, :], c.xn).then_inc(c.x_here.sem, 1)
                with dve.Fori(0, B) as b:
                    bound = CLIP * HD ** 0.5
                    for step in range(H + 2):
                        if step < H:
                            h = step
                            for t in range(T):
                                dve.wait_ge(c.V.full, c.V.filled(b, ("s", h, t)))
                                last = dve.tensor_scalar(e[:, h % 4, t, :], c.V.slot(("s", h, t)), bound, -bound, ALU.min, ALU.max)
                                last.then_inc(c.V.empty, 1)
                            dve.drain().then_inc(c.exp_in.sem, 1)
                        if step >= 3 and step % 2:
                            g = (step - 3) // 2
                            dve.drain()
                            dve.wait_ge(c.O.full, c.O.filled(b, ("sum", g)))
                            dve.reciprocal(rec[:, :], c.O.slot(("sum", g))).then_inc(c.O.empty, 1)
                            dve.drain()
                            dve.wait_ge(c.O.full, c.O.filled(b, ("O", g)))
                            dve.tensor_tensor(oT[:, g, :], c.O.slot(("O", g)), rec[:, :], ALU.mult).then_inc(c.O.empty, 1)
                    dve_norm_ahead(c, dve, b)
                    dve_residual_norm(c, dve, b, 2)

            @block.scalar
            def _(act):
                act.wait_ge(c.loaded, c.load_count)
                with act.Fori(0, B) as b:
                    act_fetch_ctx(c, act, b)
                    for name, dst, i in (("zc", c.cT, 0), ("zx", c.xT, 1)):
                        act.wait_ge(c.A.full, c.A.filled(b, name))
                        src = c.A.slot(name)
                        for k in range(KD):
                            last = act.activation(dst[:, k, :], src[:, k * S:(k + 1) * S], ACT.Identity,
                                                  bias=shiftc[:, i, k:k + 1], scale=gain[:, i, k:k + 1])
                        last.then_inc(c.A.empty, 1)
                    act.wait_ge(c.setup_done, c.setup_dones)
                    for i in range(IT // 2):
                        act.wait_ge(c.A.full, c.A.filled(b, ("q", i)))
                        src = c.A.slot(("q", i))
                        for m in range(2):
                            last = spread_heads(lambda dst, src, rows: act.activation(dst, src, ACT.Copy), qm,
                                                src[:, m * S:(m + 1) * S], (4 * i + 2 * m, 4 * i + 2 * m + 1), HD)
                        last.then_inc(c.A.empty, 1)
                    for i in range(IT // 2):
                        act.wait_ge(c.A.full, c.A.filled(b, ("k", i)))
                        src = c.A.slot(("k", i))
                        act.activation(kT[:, 2 * i:2 * i + 2, :].rearrange("p m s -> p (m s)"), src, ACT.Copy).then_inc(c.A.empty, 1)
                    for t in range(T):
                        act.wait_ge(c.A.full, c.A.filled(b, ("v", t)))
                        src = c.A.slot(("v", t)).rearrange("p (h d) -> p h d", d=HD)
                        act.activation(v[:, t, :, :], src, ACT.Copy).then_inc(c.A.empty, 1)
                    for h in range(H):
                        act.wait_ge(c.exp_in.sem, c.exp_in.at(b, h + 1))
                        act.activation(e[:, h % 4, :, :], e[:, h % 4, :, :], ACT.Exp, scale=HD ** -0.5).then_inc(c.exp_ready.sem, 1)

            @block.gpsimd
            def _(pool):
                pool_rstd(c, pool, 0, 0)
                pool.memset(qm[:, :, :], 0.0)
                pool.drain().then_inc(c.setup_done, 1)
                with pool.Fori(0, B) as b:
                    for h in range(H):
                        pool.wait_ge(c.exp_ready.sem, c.exp_ready.at(b, h + 1))
                        alone(c, pool)
                        w = e[:, h % 4, :, :].rearrange("p (i t) s -> p i t s", t=2)
                        pool.tensor_tensor(half[:, h % 2, :, :], w[:, :, 0, :], w[:, :, 1, :], ALU.add)
                        pool.drain()
                        pool.tensor_tensor(total[:, h % 4, :], half[:, h % 2, 0, :], half[:, h % 2, 1, :],
                                           ALU.add).then_inc(c.sums_ready.sem, 1)
                    for j in (1, 2):
                        pool_rstd(c, pool, b, j)
        c.finish()
        for signal in (c.x_here, c.var_ready, c.rstd_ready):
            signal.once_more()



def layer_l3_ffn(nc, c, ins):
    with ExitStack() as ctx:
        sb = allocator(nc, ctx, "l3_ffn")
        FT = HIDDEN // P
        up, down = sb("up", [P, KD + 1, HIDDEN]), sb("down", [P, KD, HIDDEN])
        w2 = sb("w2", [P, FT, D])
        ubias, obias = sb("ubias", [P, FT]), sb("obias", [1, 2, D])
        hT = sb("hT", [P, FT, S])
        c.setup_fulls += 1

        with nc.Block() as block:
            @block.sync
            def _(sp):
                for dst, name in ((ubias, "ubias11"), (obias, "obias11")):
                    c.load(sp, dst, ins[name])
                c.load_part(sp, 0, down[:, :, :], c.mixed_down)
                c.load_part(sp, 1, up[:, 0:KD, :], c.mixed_up[:, 0:KD, :])
                c.load_part(sp, 1, up[0:1, KD, :], c.mixed_up[0:1, KD, :])

            @block.tensor
            def _(pe):
                pe.wait_ge(c.arrived[0], c.arrivals[0])
                for f in range(FT):
                    for o in range(KD):
                        last = pe.transpose(c.psA[:, f * D + o * P:f * D + (o + 1) * P],
                                            down[:, o, f * P:(f + 1) * P], c.ident[:, :])
                last.then_inc(c.setup_full, 1)

            @block.scalar
            def _(act):
                act.wait_ge(c.setup_full, c.setup_fulls)
                for i in range(2):
                    last = act.activation(w2[:, 4 * i:4 * i + 4, :].rearrange("p f d -> p (f d)"), c.psA[:, i * 1024:(i + 1) * 1024], ACT.Copy)
                act.drain().then_inc(c.setup_done, 1)

        c.expect_setup(1)
        begin(c, A=2 + FT // 2, V=2, O=0, x_here=1, var_ready=1, rstd_ready=1)
        with nc.Block() as block:
            @block.tensor
            def _(pe):
                pe.wait_ge(c.setup_done, c.setup_dones)
                pe.wait_ge(c.loaded, c.load_count)
                pe.wait_ge(c.arrived[1], c.arrivals[1])
                with pe.Fori(0, B) as b:
                    pe_transpose_x_halves(c, pe, b)
                    pe.wait_ge(c.A.empty, c.A.copied(b, ("xT", KD - 1)))
                    for i in range(FT // 2):
                        pe.wait_ge(c.A.empty, c.A.vacant(b, ("h", i)))
                        out = c.A.slot(("h", i))
                        for m in (2 * i, 2 * i + 1):
                            last = mm(pe, out[:, (m - 2 * i) * S:(m - 2 * i + 1) * S],
                                      [(up[:, k, m * P:(m + 1) * P], c.xT[:, k, :]) for k in range(KD)]
                                      + [(up[0:1, KD, m * P:(m + 1) * P], c.ones[0:1, 0:S])])
                        last.then_inc(c.A.full, 1)
                    pe.wait_ge(c.A.empty, c.A.copied(b, ("h", FT // 2 - 1)))
                    pe_project_out(c, pe, b, [lambda t, f=f: hT[:, f, t * P:(t + 1) * P] for f in range(FT)],
                                   [w2[:, f, :] for f in range(FT)], [obias[0:1, 0, :], obias[0:1, 1, :]])

            @block.vector
            def _(dve):
                with dve.Fori(0, B) as b:
                    dve_residual_norm(c, dve, b)

            @block.scalar
            def _(act):
                with act.Fori(0, B) as b:
                    act_fetch_x(c, act, b)
                    for k in range(KD):
                        act.wait_ge(c.A.full, c.A.filled(b, ("xT", k)))
                        act.activation(c.xT[:, k, :], c.A.slot(("xT", k))[:, 0:S], ACT.Copy).then_inc(c.A.empty, 1)
                    for i in range(FT // 2):
                        act.wait_ge(c.A.full, c.A.filled(b, ("h", i)))
                        src = c.A.slot(("h", i))
                        for m in (2 * i, 2 * i + 1):
                            last = act.activation(hT[:, m, :], src[:, (m - 2 * i) * S:(m - 2 * i + 1) * S], ACT.Gelu,
                                                  bias=ubias[:, m:m + 1])
                        last.then_inc(c.A.empty, 1)

            @block.gpsimd
            def _(pool):
                with pool.Fori(0, B) as b:
                    pool_rstd(c, pool, b, 0)
        c.finish()


LAYERS = [layer_l0_attn, layer_l0_xattn, layer_l0_ffn, layer_l1_attn, layer_l1_xattn, layer_l1_ffn, layer_l2_attn,
          layer_l2_xattn, layer_l2_ffn, layer_l3_attn, layer_l3_xattn, layer_l3_ffn]


def build(nc, ins, out):
    with ExitStack() as ctx:
        sb = allocator(nc, ctx, "all")

        def sem(name):
            return ctx.enter_context(nc.semaphore(name))

        c = Core()
        c.xc = sb("xc", [P, 2 * B * T, D])
        c.x, c.ctx = c.xc[:, 0:B * T, :], c.xc[:, B * T:2 * B * T, :]
        c.xn = sb("xn", [P, T, D])
        c.xT = sb("xT", [P, KD, S])
        c.ctxn = sb("ctxn", [P, T, D])
        c.cT = sb("cT", [P, KD, S])
        c.r = sb("r", [P, T, D])
        c.stats = sb("stats", [P, T, 6])
        c.meanvar = sb("meanvar", [P, T, 2])
        c.vareps = sb("vareps", [P, T])
        c.rstd = sb("rstd", [P, T])
        c.minus_half = sb("minus_half", [P, T])
        c.ones = sb("ones", [1, S])
        c.ident = sb("ident", [P, P])
        c.ident16 = sb("ident16", [P, P], BF16)
        c.causal_qk = sb("causal_qk", [P, P], BF16)
        c.psA = ctx.enter_context(nc.psum_tensor("psA", [P, 2048], F32))
        c.psV = ctx.enter_context(nc.psum_tensor("psV", [P, 1024], F32))
        c.psO = ctx.enter_context(nc.psum_tensor("psO", [P, 1024], F32))
        c.A = Ring(nc, ctx, "A", "act_slot", c.psA)
        c.V = Ring(nc, ctx, "V", "dve_slot", c.psV)
        c.O = Ring(nc, ctx, "O", "heads_slot", c.psO)
        names = ("x_here", "ctx_here", "var_ready", "rstd_ready", "heads_ready",
                 "max_ready", "sums_ready", "exp_in", "exp_ready", "feat_ready", "vec_ready")
        signals = [Signal(nc, ctx, n) for n in names]
        c.signals = dict(zip(names, signals))
        (c.x_here, c.ctx_here, c.var_ready, c.rstd_ready, c.heads_ready,
         c.max_ready, c.sums_ready, c.exp_in, c.exp_ready, c.feat_ready, c.vec_ready) = signals
        c.marker = sem("marker")
        c.mixed_up = nc.dram_tensor("mixed_up", (P, KD + 1, HIDDEN), F32, kind="Internal").ap()
        c.mixed_down = nc.dram_tensor("mixed_down", (P, KD, HIDDEN), F32, kind="Internal").ap()
        c.loaded = sem("loaded")
        c.setup_full = sem("setup_full")
        c.setup_done = sem("setup_done")
        c.stored = sem("stored")
        c.load_count = c.stores = 0
        c.setup_dones = c.setup_fulls = 0

        def load(sp, dst, src):
            sp.dma_start(dst[tuple(slice(None) for _ in dst.shape)], src).then_inc(c.loaded, 16)
            c.load_count += 16

        c.arrived = [sem(f"arrived{i}") for i in range(1, 5)]
        c.arrivals = [0] * 4

        def load_part(sp, part, dst, src):
            sp.dma_start(dst, src).then_inc(c.arrived[part], 16)
            c.arrivals[part] += 16

        def expect_setup(n):
            c.setup_dones += n

        def finish():
            for r in (c.A, c.V, c.O):
                r.end()
            for s in signals:
                s.end()

        c.load, c.load_part, c.expect_setup, c.finish = load, load_part, expect_setup, finish

        with nc.Block() as block:
            @block.sync
            def _(sp):
                x_view = ins["x"].rearrange("b (t p) d -> p (b t) d", p=P)
                load(sp, c.x, x_view)
                for dst, name in ((c.ident, "ident"), (c.ident16, "ident16"),
                                  (c.causal_qk, "causal_qk")):
                    load(sp, dst, ins[name])
                sp.wait_ge(c.loaded, c.load_count)

            @block.gpsimd
            def _(pool):
                pool.memset(c.minus_half[:, :], -0.5)
                pool.memset(c.ones[:, :], 1.0)

            @block.scalar
            def _(act):
                act.sem_inc(c.A.empty, CREDIT)

            @block.vector
            def _(dve):
                dve.sem_inc(c.V.empty, CREDIT)
                dve.sem_inc(c.O.empty, CREDIT)

        for i in PHASES:
            LAYERS[i](nc, c, ins)

        with nc.Block() as block:
            @block.sync
            def _(sp):
                sp.dma_start(out.rearrange("b (t p) d -> p (b t) d", p=P), c.x[:, :, :]).then_inc(c.stored, 16)
                sp.wait_ge(c.stored, c.stores + 16)



def kernel(**inputs):
    import ml_dtypes
    import concourse.bacc as bacc
    from concourse.bass_utils import run_bass_kernel_spmd as run

    bf16 = ml_dtypes.bfloat16
    a = {k: np.asarray(v) for k, v in inputs.items()}

    def tiled(w):
        return w.reshape(w.shape[0] // P, P, *w.shape[1:]).swapaxes(0, 1)

    def row(v):
        return v.reshape(1, -1)

    def col(v):
        return v.reshape(-1, P).T

    def strips(w):
        out = np.zeros((w.shape[0], H, 32), w.dtype)
        out[:, :, 0:16] = w.reshape(w.shape[0], H, 16)
        return out.reshape(w.shape[0], H * 32)

    def block_diagonal(m):
        out = np.zeros((P, P), m.dtype)
        for i in range(0, P, 16):
            out[i:i + 16, i:i + 16] = m.T
        return out

    i = np.arange(P)
    lower = i[:, None] >= i[None, :]
    arrays = {
        "x": a["x"],
        "ctx": a["ctx_1024"],
        "ident": np.eye(P, dtype=np.float32),
        "ident16": np.eye(P, dtype=bf16),
        "causal_qk": np.where(lower, 0.0, -1e30).astype(bf16),
        "blocks": np.tile((i[:, None] // 32 == i[None, :] // 32).astype(np.float32), (1, T - 1)),
        "causal01": np.tile(np.where(lower.T, 1.0, 0.0), (1, T)).astype(np.float32),
    }
    w = a["L0_attn_w_qkv"]
    arrays["wqk0"] = tiled(w[0:2 * D])
    arrays["maps0"] = np.stack([block_diagonal(a["L0_attn_wq_map"]), block_diagonal(a["L0_attn_wk_map"])], axis=1)
    arrays["wv0"] = tiled(w[2 * D:].T)
    arrays["wo0"] = tiled(a["L0_attn_w_out"].T)
    arrays["fbias0"] = row(np.concatenate([np.tile(a["L0_attn_bq_map"], H), np.tile(a["L0_attn_bk_map"], H)]))
    for k, w in (("wq1", "w_q"), ("wk1", "w_k")):
        arrays[k] = tiled(strips(a["L0_xattn_" + w]))
    arrays["wv1"], arrays["wo1"] = tiled(a["L0_xattn_w_v"]), tiled(a["L0_xattn_w_o"])
    arrays["qbias1"], arrays["kbias1"] = col(strips(row(a["L0_xattn_b_q"]))), col(strips(row(a["L0_xattn_b_k"])))
    arrays["vbias1"], arrays["obias1"] = row(a["L0_xattn_b_v"]), row(a["L0_xattn_b_o"])

    arrays["wg2"], arrays["gbias2"] = tiled(a["L0_ffn_Wg"]), row(a["L0_ffn_bg"])
    arrays["rank2"] = np.tile(np.arange(8, 0, -1, dtype=np.float32), (P, T, 1))
    arrays["b1_2"], arrays["b2_2"] = col(a["L0_ffn_b1"]), a["L0_ffn_b2"]
    arrays["w1_2"] = a["L0_ffn_W1"].reshape(8, 2, P, 512).transpose(2, 0, 1, 3)
    arrays["w2_2"] = a["L0_ffn_W2"].reshape(8, 4, P, D).transpose(2, 0, 1, 3)

    for k, w in (("wq3", "query"), ("wk3", "key"), ("wv3", "value")):
        arrays[k] = tiled(a["L1_attn_W_" + w])

    arrays["w1_5"], arrays["w2_5"] = tiled(a["L1_ffn_W1"].T), tiled(a["L1_ffn_W2"].T)
    arrays["b1_5"], arrays["b2_5"] = col(a["L1_ffn_b1"]), row(a["L1_ffn_b2"])
    arrays["shift5"] = np.eye(P, k=1, dtype=np.float32)
    arrays["tokens5"] = (i[:, None] == np.arange(2, 17, 2)[None, :]).astype(np.float32)
    arrays["scale5"] = np.broadcast_to(a["L1_ffn_scale"].reshape(1, 1), (P, 1))

    w, v = a["L2_attn_Wqk"], a["L2_attn_bqk"]
    arrays["wq6"], arrays["wk6"] = tiled(strips(w[:, 0:D])), tiled(strips(w[:, D:]))
    arrays["qbias6"], arrays["kbias6"] = col(strips(row(v[0:D]))), col(strips(row(v[D:])))
    arrays["wv6"], arrays["wo6"], arrays["wn6"] = (tiled(a["L2_attn_" + n]) for n in ("Wv", "Wo", "Wn"))
    arrays["vbias6"], arrays["obias6"], arrays["nbias6"] = (row(a["L2_attn_" + n]) for n in ("bv", "bo", "bn"))
    def norm_cols(l, ctx):
        return np.stack([col(a[ctx]), col(a[l])], axis=1)

    m = a["mask_BxS2_bf1"].view(np.uint8)
    arrays["mask_row7"] = row(m)
    arrays["gain7"], arrays["shift7"] = norm_cols("L2_xattn_gl", "L2_xattn_gm"), norm_cols("L2_xattn_bl", "L2_xattn_bm")
    for k in "qkvo":
        arrays[f"w{k}7"] = tiled(a["L2_xattn_W" + k])

    arrays["w1_8"], arrays["w2_8"] = tiled(a["L2_ffn_w1"].T), tiled(a["L2_ffn_w2"].T)
    arrays["b1_8"], arrays["b2_8"] = col(a["L2_ffn_b1"]), row(a["L2_ffn_b2"])

    for k, w in (("wq9", "Wq"), ("wk9", "Wk")):
        w = a["L3_attn_" + w].T.reshape(D, H, 8, 2)
        arrays[k] = tiled(strips(np.stack([w[..., 0], w[..., 0]], axis=-1).reshape(D, D)))
    arrays["wv9"], arrays["wo9"] = tiled(a["L3_attn_Wv"].T), tiled(a["L3_attn_Wo"].T)
    freqs = np.exp(np.arange(0, 16, 2, dtype=np.float32) * np.float32(-np.log(10000.0) / 16))
    angles = (np.arange(S, dtype=np.float32)[:, None] * freqs[None, :]).T
    rope = np.zeros((32, S), np.float32)
    rope[0:16:2], rope[1:16:2] = np.cos(angles), -np.sin(angles)
    arrays["rope9"], arrays["qrope9"] = np.tile(rope, (4, 1)), np.tile(rope * np.float32(0.25), (4, 1))

    arrays["gain10"] = norm_cols("L3_xattn_ln_l_w", "L3_xattn_ln_c_w")
    arrays["shift10"] = norm_cols("L3_xattn_ln_l_b", "L3_xattn_ln_c_b")
    w = a["L3_xattn_Wkv"]
    arrays["wq10"], arrays["wk10"], arrays["wv10"] = tiled(a["L3_xattn_Wq"]), tiled(w[:, 0:INNER]), tiled(w[:, INNER:])
    arrays["wo10"], arrays["obias10"] = tiled(a["L3_xattn_Wo"]), row(a["L3_xattn_bo"])

    def stage_weights(w, transposed):
        out = []
        for st in range(w.shape[0]):
            m = w[st].reshape(-1, 2 ** st, 2, 2)
            out.append(m.transpose((2, 0, 3, 1) if transposed else (3, 0, 2, 1)).reshape(2, -1))
        return np.stack(out[::-1] if transposed else out)

    arrays["upw11"] = stage_weights(a["L3_ffn_up_weights"], False)
    arrays["downw11"] = stage_weights(a["L3_ffn_down_weights"], True)
    arrays["up11"], arrays["upb11"] = tiled(a["L3_ffn_W_exp"]), row(a["L3_ffn_b_exp"])
    arrays["down11"] = tiled(a["L3_ffn_W_con"].T)
    arrays["ubias11"] = col(a["L3_ffn_up_bias"])
    arrays["obias11"] = np.stack([a["L3_ffn_b_con"], a["L3_ffn_down_bias"]])[None]

    nc = bacc.Bacc("TRN2", target_bir_lowering=False, num_devices=1)
    arrays = {f"in_{k}": np.ascontiguousarray(v) for k, v in arrays.items()}
    ins = {k[3:]: nc.dram_tensor(k, v.shape, mybir.dt.from_np(v.dtype), kind="ExternalInput").ap()
           for k, v in arrays.items()}
    out = nc.dram_tensor("out", (B, S, D), F32, kind="ExternalOutput").ap()
    build(nc, ins, out)
    result = run(nc, [arrays], core_ids=[0])
    return result.results[0]["out"]
```
